# Optimizing a Trainium2 kernel written in Bass

```python
import numpy as np
import jax
import jax.numpy as jnp

def _softmax(x, axis=-1):
    return jax.nn.softmax(x, axis=axis)

def _gelu(x):
    return jax.nn.gelu(x, approximate=True)

def _silu(x):
    return jax.nn.silu(x)

def _sigmoid(x):
    return jax.nn.sigmoid(x)

def _layernorm(x, axis=-1, eps=1e-05):
    m = jnp.mean(x, axis=axis, keepdims=True)
    v = jnp.var(x, axis=axis, keepdims=True)
    return (x - m) / jnp.sqrt(v + eps)

def _scatter_add(tgt, idx, src, axis=0):
    return tgt.at[idx].add(src)

def _segment_sum(src, seg, n):
    return jax.ops.segment_sum(src, seg, n)
kernel_name = 'mk_decoder_postln_d2_seqx_r4_f3253f'

def setup_inputs(seed: int=0):
    np.random.seed(seed)
    _w = jnp.asarray

    def _rec_inputs():
        import jax
        import jax.numpy as jnp
        _rk = jax.random.key(seed)
        x = -0.0005207 + 1.001 * jax.random.normal(jax.random.fold_in(_rk, 1), (32, 100, 256), jnp.float32)
        _lenS = 100 - jax.random.randint(jax.random.fold_in(_rk, 7), (32,), 0, max(1, 100 // 4) + 1, jnp.int32)
        _lenS2 = 361 - jax.random.randint(jax.random.fold_in(_rk, 8), (32,), 0, max(1, 361 // 4) + 1, jnp.int32)
        _ctx_1024P = jax.random.normal(jax.random.fold_in(_rk, 11), (32, 16, 256), jnp.float32)
        _ctx_1024c = jax.random.dirichlet(jax.random.fold_in(_rk, 511), 0.3 * jnp.ones((16,), jnp.float32), (32, 361))
        _ctx_1024t = jnp.einsum('bsk,bkd->bsd', _ctx_1024c, _ctx_1024P)
        _ctx_1024t = _ctx_1024t * jax.lax.rsqrt(jnp.mean(jnp.square(_ctx_1024t)) + 1e-12) * 0.953939
        ctx_1024 = 2.81802e-05 + 1.00001 * (_ctx_1024t + 0.3 * jax.random.normal(jax.random.fold_in(_rk, 611), (32, 361, 256), jnp.float32))
        return (x, ctx_1024)
    x, ctx_1024 = _rec_inputs()

    def _L0_attn_setup():
        import jax, jax.numpy as jnp
        import numpy as np
        import math
        B, T, C = (2, 512, 256)
        H, L = (16, 64)
        DH = C // H
        DHE = DH // 2
        THETA = 10000.0

        def _rope_cache(t, dim):
            inv_freq = 1.0 / THETA ** (jnp.arange(0, dim, 2, dtype=jnp.float32) / dim)
            freqs = jnp.arange(t, dtype=jnp.float32)[:, None] * inv_freq[None, :]
            emb = jnp.concatenate((freqs, freqs), axis=-1)
            return (jnp.cos(emb), jnp.sin(emb))

        def _apply_rope(x, cos, sin):
            x1 = x[..., 0::2]
            x2 = x[..., 1::2]
            rot = jnp.stack((-x2, x1), axis=-1).reshape(x.shape)
            return x * cos[None, None] + rot * sin[None, None]
        key = jax.random.key(seed)
        ks = jax.random.split(key, 10)
        s = 0.02
        return {'x': jax.random.normal(ks[0], (B, T, C), jnp.float32), 'Wq_down': jax.random.normal(ks[1], (C, H * L), jnp.float32) * s, 'Wk_down': jax.random.normal(ks[2], (C, H * L), jnp.float32) * s, 'Wv_down': jax.random.normal(ks[3], (C, H * L), jnp.float32) * s, 'Wq_up_c': jax.random.normal(ks[4], (L, DHE), jnp.float32) * s, 'Wq_up_e': jax.random.normal(ks[5], (L, DHE), jnp.float32) * s, 'Wk_up_c': jax.random.normal(ks[6], (L, DHE), jnp.float32) * s, 'Wk_up_e': jax.random.normal(ks[7], (L, DHE), jnp.float32) * s, 'Wv_up': jax.random.normal(ks[8], (L, DH), jnp.float32) * s, 'Wc': jax.random.normal(ks[9], (C, C), jnp.float32) * s}
    _L0_attn_all = _L0_attn_setup()
    _L0_attn_in = {k: v for k, v in _L0_attn_all.items() if k in ('Wq_down', 'Wk_down', 'Wv_down', 'Wq_up_c', 'Wq_up_e', 'Wk_up_c', 'Wk_up_e', 'Wv_up', 'Wc')}
    del _L0_attn_all

    def _L0_xattn_setup():
        import jax, jax.numpy as jnp
        import numpy as np
        D_MODEL = 256
        N_HEAD = 8
        STRIDE = 8
        HEAD_DIM = D_MODEL // N_HEAD
        NEG_INF = jnp.float32(-1e+30)

        def _hepos_head_mask(src_len):
            src_idx = jnp.arange(src_len)
            h_idx = jnp.arange(N_HEAD)[:, None]
            m = (src_idx[None, :] - h_idx) % STRIDE != 0
            all_masked = jnp.all(m, axis=-1, keepdims=True)
            m = m.at[:, 0].set(jnp.where(all_masked[:, 0], False, m[:, 0]))
            return m
        key = jax.random.key(seed)
        ks = jax.random.split(key, 8)
        B, TGT, SRC = (2, 256, 2048)
        scale = 1.0 / np.sqrt(D_MODEL)
        return {'q': jax.random.normal(ks[0], (B, TGT, D_MODEL), jnp.float32), 'k': jax.random.normal(ks[1], (B, SRC, D_MODEL), jnp.float32), 'v': jax.random.normal(ks[2], (B, SRC, D_MODEL), jnp.float32), 'Wq': jax.random.normal(ks[3], (D_MODEL, D_MODEL), jnp.float32) * scale, 'bq': jnp.zeros((D_MODEL,), jnp.float32), 'Wk': jax.random.normal(ks[4], (D_MODEL, D_MODEL), jnp.float32) * scale, 'bk': jnp.zeros((D_MODEL,), jnp.float32), 'Wv': jax.random.normal(ks[5], (D_MODEL, D_MODEL), jnp.float32) * scale, 'bv': jnp.zeros((D_MODEL,), jnp.float32), 'Wo': jax.random.normal(ks[6], (D_MODEL, D_MODEL), jnp.float32) * scale, 'bo': jnp.zeros((D_MODEL,), jnp.float32)}
    _L0_xattn_all = _L0_xattn_setup()
    _L0_xattn_in = {k: v for k, v in _L0_xattn_all.items() if k in ('Wq', 'bq', 'Wk', 'bk', 'Wv', 'bv', 'Wo', 'bo')}
    del _L0_xattn_all

    def _L0_ffn_setup():
        import jax, jax.numpy as jnp
        import numpy as np
        E = 64
        K = 6
        CAP = 128
        ROUTE_SCALE = 1.0
        key = jax.random.key(seed)
        ks = jax.random.split(key, 9)
        B, S, D, I = (2, 256, 256, 176)
        SI = 2 * I
        s = 0.02
        return {'x': jax.random.normal(ks[0], (B, S, D), jnp.float32), 'gate_w': jax.random.normal(ks[1], (E, D), jnp.float32) * s, 'gate_b': jnp.zeros((E,), jnp.float32), 'w1': jax.random.normal(ks[2], (E, I, D), jnp.float32) * s, 'w2': jax.random.normal(ks[3], (E, D, I), jnp.float32) * s, 'w3': jax.random.normal(ks[4], (E, I, D), jnp.float32) * s, 'ws1': jax.random.normal(ks[5], (SI, D), jnp.float32) * s, 'ws2': jax.random.normal(ks[6], (D, SI), jnp.float32) * s, 'ws3': jax.random.normal(ks[7], (SI, D), jnp.float32) * s}
    _L0_ffn_all = _L0_ffn_setup()
    _L0_ffn_in = {k: v for k, v in _L0_ffn_all.items() if k in ('gate_w', 'gate_b', 'w1', 'w2', 'w3', 'ws1', 'ws2', 'ws3')}
    del _L0_ffn_all

    def _L1_attn_setup():
        import jax, jax.numpy as jnp
        import numpy as np
        B, L, D_MODEL, H = (4, 512, 256, 16)
        HD = D_MODEL // H
        EPS = 1e-06
        key = jax.random.key(seed)
        ks = jax.random.split(key, 9)
        s = 1.0 / np.sqrt(D_MODEL)
        return {'x': jax.random.normal(ks[0], (B, L, D_MODEL), dtype=jnp.float32), 'Wq': jax.random.normal(ks[1], (D_MODEL, D_MODEL), dtype=jnp.float32) * s, 'bq': jax.random.normal(ks[2], (D_MODEL,), dtype=jnp.float32) * 0.01, 'Wk': jax.random.normal(ks[3], (D_MODEL, D_MODEL), dtype=jnp.float32) * s, 'bk': jax.random.normal(ks[4], (D_MODEL,), dtype=jnp.float32) * 0.01, 'Wv': jax.random.normal(ks[5], (D_MODEL, D_MODEL), dtype=jnp.float32) * s, 'bv': jax.random.normal(ks[6], (D_MODEL,), dtype=jnp.float32) * 0.01, 'Wo': jax.random.normal(ks[7], (D_MODEL, D_MODEL), dtype=jnp.float32) * s, 'bo': jax.random.normal(ks[8], (D_MODEL,), dtype=jnp.float32) * 0.01}
    _L1_attn_all = _L1_attn_setup()
    _L1_attn_in = {k: v for k, v in _L1_attn_all.items() if k in ('Wq', 'bq', 'Wk', 'bk', 'Wv', 'bv', 'Wo', 'bo')}
    del _L1_attn_all

    def _L1_xattn_setup():
        import jax, jax.numpy as jnp
        import numpy as np
        D_MODEL = 256
        NUM_HEADS = 16
        HEAD_DIM = D_MODEL // NUM_HEADS
        SCALE = HEAD_DIM ** (-0.5)
        BIAS_LEN = 128
        ROPE_BASE = 10000.0
        LN_EPS = 1e-05

        def _layernorm(x, gamma, beta):
            mu = jnp.mean(x, axis=-1, keepdims=True)
            var = jnp.mean(jnp.square(x - mu), axis=-1, keepdims=True)
            return (x - mu) * jax.lax.rsqrt(var + LN_EPS) * gamma + beta

        def _rope(x, cos, sin):
            half = HEAD_DIM // 2
            c = cos[None, None, :, :]
            s = sin[None, None, :, :]
            x_even, x_odd = (x[..., :half], x[..., half:])
            return jnp.concatenate([x_even * c - x_odd * s, x_even * s + x_odd * c], axis=-1)

        def _temporal_bias(L_q, L_kv):
            pos = jnp.arange(BIAS_LEN, dtype=jnp.float32)
            dist = jnp.abs(pos[None, :] - pos[:, None])
            bias = jnp.exp(-dist * 0.1) - dist * 0.05
            if L_q <= BIAS_LEN and L_kv <= BIAS_LEN:
                return bias[:L_q, :L_kv]
            return jax.image.resize(bias, (L_q, L_kv), method='bilinear')
        key = jax.random.key(seed)
        ks = jax.random.split(key, 8)
        B, Lq, Lkv = (8, 128, 128)
        return {'decoder_hidden': jax.random.normal(ks[0], (B, Lq, D_MODEL), jnp.float32), 'encoder_output': jax.random.normal(ks[1], (B, Lkv, D_MODEL), jnp.float32), 'Wqkv': jax.random.normal(ks[2], (3 * D_MODEL, D_MODEL), jnp.float32) * 0.02, 'Wout': jax.random.normal(ks[3], (D_MODEL, D_MODEL), jnp.float32) * 0.02, 'b_out': jnp.zeros((D_MODEL,), jnp.float32), 'Wgate': jax.random.normal(ks[4], (D_MODEL, D_MODEL), jnp.float32) * 0.02, 'b_gate': jnp.zeros((D_MODEL,), jnp.float32), 'gamma': jnp.ones((D_MODEL,), jnp.float32), 'beta': jnp.zeros((D_MODEL,), jnp.float32)}
    _L1_xattn_all = _L1_xattn_setup()
    _L1_xattn_in = {k: v for k, v in _L1_xattn_all.items() if k in ('Wqkv', 'Wout', 'b_out', 'Wgate', 'b_gate', 'gamma', 'beta')}
    del _L1_xattn_all

    def _L1_ffn_setup():
        import jax, jax.numpy as jnp
        import numpy as np
        EPS_NORM = 1e-08
        EPS_Q = 1e-05

        def rmsnorm(x, w):
            v = jnp.mean(jnp.square(x.astype(jnp.float32)), axis=-1, keepdims=True)
            x_hat = x * jax.lax.rsqrt(v + EPS_NORM)
            return (x_hat * w).astype(x.dtype)

        def activation_quant(x):
            scale = 127.0 / jnp.clip(jnp.max(jnp.abs(x), axis=-1, keepdims=True), EPS_Q, None)
            return jnp.clip(jnp.round(x * scale), -128, 127) / scale

        def weight_quant(w):
            scale = 1.0 / jnp.clip(jnp.mean(jnp.abs(w)), EPS_Q, None)
            return jnp.clip(jnp.round(w * scale), -1, 1) / scale

        def bitlinear(x, norm_w, w):
            x_norm = rmsnorm(x, norm_w)
            x_q = x_norm + jax.lax.stop_gradient(activation_quant(x_norm) - x_norm)
            w_q = w + jax.lax.stop_gradient(weight_quant(w) - w)
            return jnp.einsum('bsd,hd->bsh', x_q, w_q)
        key = jax.random.key(seed)
        k1, k2, k3 = jax.random.split(key, 3)
        dim, hidden = (256, 1024)
        return {'x': jax.random.normal(k1, (4, 512, dim), dtype=jnp.float32), 'norm1_w': jnp.ones((dim,), jnp.float32), 'w1': jax.random.normal(k2, (hidden, dim), jnp.float32) * 0.02, 'act_scale': jnp.ones((1,), jnp.float32), 'act_bias': jnp.zeros((1,), jnp.float32), 'norm2_w': jnp.ones((hidden,), jnp.float32), 'w2': jax.random.normal(k3, (dim, hidden), jnp.float32) * 0.02}
    _L1_ffn_all = _L1_ffn_setup()
    _L1_ffn_in = {k: v for k, v in _L1_ffn_all.items() if k in ('norm1_w', 'w1', 'act_scale', 'act_bias', 'norm2_w', 'w2')}
    del _L1_ffn_all
    return {'x': x, 'ctx_1024': ctx_1024, 'L0_attn_Wq_down': _L0_attn_in['Wq_down'], 'L0_attn_Wk_down': _L0_attn_in['Wk_down'], 'L0_attn_Wv_down': _L0_attn_in['Wv_down'], 'L0_attn_Wq_up_c': _L0_attn_in['Wq_up_c'], 'L0_attn_Wq_up_e': _L0_attn_in['Wq_up_e'], 'L0_attn_Wk_up_c': _L0_attn_in['Wk_up_c'], 'L0_attn_Wk_up_e': _L0_attn_in['Wk_up_e'], 'L0_attn_Wv_up': _L0_attn_in['Wv_up'], 'L0_attn_Wc': _L0_attn_in['Wc'], 'L0_xattn_Wq': _L0_xattn_in['Wq'], 'L0_xattn_bq': _L0_xattn_in['bq'], 'L0_xattn_Wk': _L0_xattn_in['Wk'], 'L0_xattn_bk': _L0_xattn_in['bk'], 'L0_xattn_Wv': _L0_xattn_in['Wv'], 'L0_xattn_bv': _L0_xattn_in['bv'], 'L0_xattn_Wo': _L0_xattn_in['Wo'], 'L0_xattn_bo': _L0_xattn_in['bo'], 'L0_ffn_gate_w': _L0_ffn_in['gate_w'], 'L0_ffn_gate_b': _L0_ffn_in['gate_b'], 'L0_ffn_w1': _L0_ffn_in['w1'], 'L0_ffn_w2': _L0_ffn_in['w2'], 'L0_ffn_w3': _L0_ffn_in['w3'], 'L0_ffn_ws1': _L0_ffn_in['ws1'], 'L0_ffn_ws2': _L0_ffn_in['ws2'], 'L0_ffn_ws3': _L0_ffn_in['ws3'], 'L1_attn_Wq': _L1_attn_in['Wq'], 'L1_attn_bq': _L1_attn_in['bq'], 'L1_attn_Wk': _L1_attn_in['Wk'], 'L1_attn_bk': _L1_attn_in['bk'], 'L1_attn_Wv': _L1_attn_in['Wv'], 'L1_attn_bv': _L1_attn_in['bv'], 'L1_attn_Wo': _L1_attn_in['Wo'], 'L1_attn_bo': _L1_attn_in['bo'], 'L1_xattn_Wqkv': _L1_xattn_in['Wqkv'], 'L1_xattn_Wout': _L1_xattn_in['Wout'], 'L1_xattn_b_out': _L1_xattn_in['b_out'], 'L1_xattn_Wgate': _L1_xattn_in['Wgate'], 'L1_xattn_b_gate': _L1_xattn_in['b_gate'], 'L1_xattn_gamma': _L1_xattn_in['gamma'], 'L1_xattn_beta': _L1_xattn_in['beta'], 'L1_ffn_norm1_w': _L1_ffn_in['norm1_w'], 'L1_ffn_w1': _L1_ffn_in['w1'], 'L1_ffn_act_scale': _L1_ffn_in['act_scale'], 'L1_ffn_act_bias': _L1_ffn_in['act_bias'], 'L1_ffn_norm2_w': _L1_ffn_in['norm2_w'], 'L1_ffn_w2': _L1_ffn_in['w2']}

def reference(x, ctx_1024, L0_attn_Wq_down, L0_attn_Wk_down, L0_attn_Wv_down, L0_attn_Wq_up_c, L0_attn_Wq_up_e, L0_attn_Wk_up_c, L0_attn_Wk_up_e, L0_attn_Wv_up, L0_attn_Wc, L0_xattn_Wq, L0_xattn_bq, L0_xattn_Wk, L0_xattn_bk, L0_xattn_Wv, L0_xattn_bv, L0_xattn_Wo, L0_xattn_bo, L0_ffn_gate_w, L0_ffn_gate_b, L0_ffn_w1, L0_ffn_w2, L0_ffn_w3, L0_ffn_ws1, L0_ffn_ws2, L0_ffn_ws3, L1_attn_Wq, L1_attn_bq, L1_attn_Wk, L1_attn_bk, L1_attn_Wv, L1_attn_bv, L1_attn_Wo, L1_attn_bo, L1_xattn_Wqkv, L1_xattn_Wout, L1_xattn_b_out, L1_xattn_Wgate, L1_xattn_b_gate, L1_xattn_gamma, L1_xattn_beta, L1_ffn_norm1_w, L1_ffn_w1, L1_ffn_act_scale, L1_ffn_act_bias, L1_ffn_norm2_w, L1_ffn_w2):
    import jax
    import jax.numpy as jnp

    def _L0_attn_ref(x, Wq_down, Wk_down, Wv_down, Wq_up_c, Wq_up_e, Wk_up_c, Wk_up_e, Wv_up, Wc):
        import jax, jax.numpy as jnp
        import numpy as np
        import math
        B, T, C = (2, 512, 256)
        H, L = (16, 64)
        DH = C // H
        DHE = DH // 2
        THETA = 10000.0

        def _rope_cache(t, dim):
            inv_freq = 1.0 / THETA ** (jnp.arange(0, dim, 2, dtype=jnp.float32) / dim)
            freqs = jnp.arange(t, dtype=jnp.float32)[:, None] * inv_freq[None, :]
            emb = jnp.concatenate((freqs, freqs), axis=-1)
            return (jnp.cos(emb), jnp.sin(emb))

        def _apply_rope(x, cos, sin):
            x1 = x[..., 0::2]
            x2 = x[..., 1::2]
            rot = jnp.stack((-x2, x1), axis=-1).reshape(x.shape)
            return x * cos[None, None] + rot * sin[None, None]
        b, t, c = x.shape
        q_lat = (x @ Wq_down).reshape(b, t, H, L)
        k_lat = (x @ Wk_down).reshape(b, t, H, L)
        v_lat = (x @ Wv_down).reshape(b, t, H, L)
        q_c = jnp.einsum('bthl,ld->bhtd', q_lat, Wq_up_c)
        q_e = jnp.einsum('bthl,ld->bhtd', q_lat, Wq_up_e)
        k_c = jnp.einsum('bthl,ld->bhtd', k_lat, Wk_up_c)
        k_e = jnp.einsum('bthl,ld->bhtd', k_lat, Wk_up_e)
        v = jnp.einsum('bthl,ld->bhtd', v_lat, Wv_up)
        cos, sin = _rope_cache(t, DHE)
        q = jnp.concatenate([q_c, _apply_rope(q_e, cos, sin)], axis=-1)
        k = jnp.concatenate([k_c, _apply_rope(k_e, cos, sin)], axis=-1)
        scale = 1.0 / math.sqrt(DH)
        scores = jnp.einsum('bhqd,bhkd->bhqk', q, k) * scale
        causal = jnp.tril(jnp.ones((t, t), dtype=bool))
        scores = jnp.where(causal[None, None], scores, -jnp.inf)
        att = jax.nn.softmax(scores, axis=-1)
        y = jnp.einsum('bhqk,bhkd->bhqd', att, v)
        y = y.transpose(0, 2, 1, 3).reshape(b, t, c)
        return y @ Wc

    def _L0_xattn_ref(q, k, v, Wq, bq, Wk, bk, Wv, bv, Wo, bo):
        import jax, jax.numpy as jnp
        import numpy as np
        D_MODEL = 256
        N_HEAD = 8
        STRIDE = 8
        HEAD_DIM = D_MODEL // N_HEAD
        NEG_INF = jnp.float32(-1e+30)

        def _hepos_head_mask(src_len):
            src_idx = jnp.arange(src_len)
            h_idx = jnp.arange(N_HEAD)[:, None]
            m = (src_idx[None, :] - h_idx) % STRIDE != 0
            all_masked = jnp.all(m, axis=-1, keepdims=True)
            m = m.at[:, 0].set(jnp.where(all_masked[:, 0], False, m[:, 0]))
            return m
        B, tgt_len, _ = q.shape
        src_len = k.shape[1]
        Q = (q @ Wq + bq).reshape(B, tgt_len, N_HEAD, HEAD_DIM)
        K = (k @ Wk + bk).reshape(B, src_len, N_HEAD, HEAD_DIM)
        V = (v @ Wv + bv).reshape(B, src_len, N_HEAD, HEAD_DIM)
        scores = jnp.einsum('bthd,bshd->bhts', Q, K) / np.sqrt(HEAD_DIM)
        head_mask = _hepos_head_mask(src_len)
        scores = jnp.where(head_mask[None, :, None, :], NEG_INF, scores)
        attn = jax.nn.softmax(scores, axis=-1)
        out = jnp.einsum('bhts,bshd->bthd', attn, V).reshape(B, tgt_len, D_MODEL)
        return out @ Wo + bo

    def _L0_ffn_ref(x, gate_w, gate_b, w1, w2, w3, ws1, ws2, ws3):
        import jax, jax.numpy as jnp
        import numpy as np
        E = 64
        K = 6
        CAP = 128
        ROUTE_SCALE = 1.0
        shape = x.shape
        D = shape[-1]
        xf = x.reshape(-1, D)
        T = xf.shape[0]
        scores = jax.nn.softmax(xf @ gate_w.T, axis=-1)
        _, idx = jax.lax.top_k(scores + gate_b, K)
        weights = jnp.take_along_axis(scores, idx, axis=1) * ROUTE_SCALE
        flat_e = idx.reshape(-1)
        order = jnp.argsort(flat_e)
        se = flat_e[order]
        counts = jnp.bincount(flat_e, length=E)
        starts = jnp.cumsum(counts) - counts
        pos = jnp.arange(T * K) - starts[se]
        tok = order // K
        xb = jnp.zeros((E, CAP, D), xf.dtype).at[se, pos].set(xf[tok], mode='drop')
        h = jax.nn.silu(jnp.einsum('ecd,eid->eci', xb, w1)) * jnp.einsum('ecd,eid->eci', xb, w3)
        yb = jnp.einsum('eci,edi->ecd', h, w2)
        valid = (pos < CAP).astype(xf.dtype)
        contrib = yb[se, jnp.minimum(pos, CAP - 1)]
        wf = weights.reshape(-1)[order] * valid
        y = jnp.zeros_like(xf).at[tok].add(contrib * wf[:, None])
        z = jax.nn.silu(xf @ ws1.T) * (xf @ ws3.T) @ ws2.T
        return (y + z).reshape(shape)

    def _L1_attn_ref(x, Wq, bq, Wk, bk, Wv, bv, Wo, bo):
        import jax, jax.numpy as jnp
        import numpy as np
        B, L, D_MODEL, H = (4, 512, 256, 16)
        HD = D_MODEL // H
        EPS = 1e-06
        b, l, _ = x.shape
        s = l

        def proj(W, bias):
            return (x @ W.T + bias).reshape(b, l, H, HD).transpose(0, 2, 1, 3)
        q = jax.nn.sigmoid(proj(Wq, bq))
        k = jax.nn.sigmoid(proj(Wk, bk))
        v = proj(Wv, bv)
        sink_incoming = 1.0 / jnp.einsum('nhld,nhd->nhl', q + EPS, k.sum(axis=2) + EPS)
        source_outgoing = 1.0 / jnp.einsum('nhld,nhd->nhl', k + EPS, q.sum(axis=2) + EPS)
        conserved_sink = jnp.einsum('nhld,nhd->nhl', q + EPS, (k * source_outgoing[..., None]).sum(axis=2) + EPS)
        conserved_source = jnp.einsum('nhld,nhd->nhl', k + EPS, (q * sink_incoming[..., None]).sum(axis=2) + EPS)
        conserved_source = jnp.clip(conserved_source, -1.0, 1.0)
        sink_allocation = jax.nn.sigmoid(conserved_sink * (float(l) / float(s)))
        source_competition = jax.nn.softmax(conserved_source, axis=-1) * float(s)
        kv = jnp.einsum('nhld,nhlm->nhdm', k, v * source_competition[..., None])
        out = jnp.einsum('nhld,nhdm->nhlm', q * sink_incoming[..., None], kv)
        out = out * sink_allocation[..., None]
        out = out.transpose(0, 2, 1, 3).reshape(b, l, D_MODEL)
        return out @ Wo.T + bo

    def _L1_xattn_ref(decoder_hidden, encoder_output, Wqkv, Wout, b_out, Wgate, b_gate, gamma, beta):
        import jax, jax.numpy as jnp
        import numpy as np
        D_MODEL = 256
        NUM_HEADS = 16
        HEAD_DIM = D_MODEL // NUM_HEADS
        SCALE = HEAD_DIM ** (-0.5)
        BIAS_LEN = 128
        ROPE_BASE = 10000.0
        LN_EPS = 1e-05

        def _layernorm(x, gamma, beta):
            mu = jnp.mean(x, axis=-1, keepdims=True)
            var = jnp.mean(jnp.square(x - mu), axis=-1, keepdims=True)
            return (x - mu) * jax.lax.rsqrt(var + LN_EPS) * gamma + beta

        def _rope(x, cos, sin):
            half = HEAD_DIM // 2
            c = cos[None, None, :, :]
            s = sin[None, None, :, :]
            x_even, x_odd = (x[..., :half], x[..., half:])
            return jnp.concatenate([x_even * c - x_odd * s, x_even * s + x_odd * c], axis=-1)

        def _temporal_bias(L_q, L_kv):
            pos = jnp.arange(BIAS_LEN, dtype=jnp.float32)
            dist = jnp.abs(pos[None, :] - pos[:, None])
            bias = jnp.exp(-dist * 0.1) - dist * 0.05
            if L_q <= BIAS_LEN and L_kv <= BIAS_LEN:
                return bias[:L_q, :L_kv]
            return jax.image.resize(bias, (L_q, L_kv), method='bilinear')
        B, L_q, _ = decoder_hidden.shape
        L_kv = encoder_output.shape[1]
        residual = decoder_hidden
        q_in = _layernorm(decoder_hidden, gamma, beta)
        kv_in = _layernorm(encoder_output, gamma, beta)
        q = q_in @ Wqkv[:D_MODEL].T
        k = kv_in @ Wqkv[D_MODEL:2 * D_MODEL].T
        v = kv_in @ Wqkv[2 * D_MODEL:].T
        q = q.reshape(B, L_q, NUM_HEADS, HEAD_DIM).transpose(0, 2, 1, 3)
        k = k.reshape(B, L_kv, NUM_HEADS, HEAD_DIM).transpose(0, 2, 1, 3)
        v = v.reshape(B, L_kv, NUM_HEADS, HEAD_DIM).transpose(0, 2, 1, 3)
        L = max(L_q, L_kv)
        inv_freq = 1.0 / ROPE_BASE ** (jnp.arange(0, HEAD_DIM, 2, dtype=jnp.float32) / HEAD_DIM)
        freqs = jnp.arange(L, dtype=jnp.float32)[:, None] * inv_freq[None, :]
        cos, sin = (jnp.cos(freqs), jnp.sin(freqs))
        q = _rope(q, cos[:L_q], sin[:L_q])
        k = _rope(k, cos[:L_kv], sin[:L_kv])
        scores = jnp.einsum('bhqd,bhkd->bhqk', q, k) * SCALE
        scores = scores + _temporal_bias(L_q, L_kv)[None, None, :, :]
        attn = jax.nn.softmax(scores, axis=-1)
        attended = jnp.einsum('bhqk,bhkd->bhqd', attn, v)
        attended = attended.transpose(0, 2, 1, 3).reshape(B, L_q, D_MODEL)
        attended = attended @ Wout.T + b_out
        gate = jax.nn.sigmoid(attended @ Wgate.T + b_gate)
        output = gate * attended + (1.0 - gate) * residual
        return output

    def _L1_ffn_ref(x, norm1_w, w1, act_scale, act_bias, norm2_w, w2):
        import jax, jax.numpy as jnp
        import numpy as np
        EPS_NORM = 1e-08
        EPS_Q = 1e-05

        def rmsnorm(x, w):
            v = jnp.mean(jnp.square(x.astype(jnp.float32)), axis=-1, keepdims=True)
            x_hat = x * jax.lax.rsqrt(v + EPS_NORM)
            return (x_hat * w).astype(x.dtype)

        def activation_quant(x):
            scale = 127.0 / jnp.clip(jnp.max(jnp.abs(x), axis=-1, keepdims=True), EPS_Q, None)
            return jnp.clip(jnp.round(x * scale), -128, 127) / scale

        def weight_quant(w):
            scale = 1.0 / jnp.clip(jnp.mean(jnp.abs(w)), EPS_Q, None)
            return jnp.clip(jnp.round(w * scale), -1, 1) / scale

        def bitlinear(x, norm_w, w):
            x_norm = rmsnorm(x, norm_w)
            x_q = x_norm + jax.lax.stop_gradient(activation_quant(x_norm) - x_norm)
            w_q = w + jax.lax.stop_gradient(weight_quant(w) - w)
            return jnp.einsum('bsd,hd->bsh', x_q, w_q)
        h = bitlinear(x, norm1_w, w1)
        h = act_scale * jnp.square(jax.nn.relu(h)) + act_bias
        y = bitlinear(h, norm2_w, w2)
        return y
    x = _layernorm(x + _L0_attn_ref(x, L0_attn_Wq_down, L0_attn_Wk_down, L0_attn_Wv_down, L0_attn_Wq_up_c, L0_attn_Wq_up_e, L0_attn_Wk_up_c, L0_attn_Wk_up_e, L0_attn_Wv_up, L0_attn_Wc), axis=-1)
    x = _layernorm(x + _L0_xattn_ref(x, ctx_1024, ctx_1024, L0_xattn_Wq, L0_xattn_bq, L0_xattn_Wk, L0_xattn_bk, L0_xattn_Wv, L0_xattn_bv, L0_xattn_Wo, L0_xattn_bo), axis=-1)
    x = _layernorm(x + _L0_ffn_ref(x, L0_ffn_gate_w, L0_ffn_gate_b, L0_ffn_w1, L0_ffn_w2, L0_ffn_w3, L0_ffn_ws1, L0_ffn_ws2, L0_ffn_ws3), axis=-1)
    x = _layernorm(x + _L1_attn_ref(x, L1_attn_Wq, L1_attn_bq, L1_attn_Wk, L1_attn_bk, L1_attn_Wv, L1_attn_bv, L1_attn_Wo, L1_attn_bo), axis=-1)
    x = _layernorm(x + _L1_xattn_ref(x, ctx_1024, L1_xattn_Wqkv, L1_xattn_Wout, L1_xattn_b_out, L1_xattn_Wgate, L1_xattn_b_gate, L1_xattn_gamma, L1_xattn_beta), axis=-1)
    x = _layernorm(x + _L1_ffn_ref(x, L1_ffn_norm1_w, L1_ffn_w1, L1_ffn_act_scale, L1_ffn_act_bias, L1_ffn_norm2_w, L1_ffn_w2), axis=-1)
    return x

_drawn_inputs = setup_inputs


def setup_inputs(seed=0):
    import zlib

    import numpy as np

    out = dict(_drawn_inputs(seed))
    spreads = {'L0_xattn_bq': (0.0, 0.297),
     'L0_xattn_bk': (0.0, 0.8),
     'L0_xattn_bv': (0.0, 0.1),
     'L0_xattn_bo': (0.0, 0.1),
     'L0_ffn_gate_b': (0.0, 0.8),
     'L1_xattn_b_out': (0.0, 0.1),
     'L1_xattn_b_gate': (0.0, 0.41),
     'L1_xattn_gamma': (1.0, 0.6),
     'L1_xattn_beta': (0.0, 0.8),
     'L1_ffn_norm1_w': (1.0, 0.2),
     'L1_ffn_norm2_w': (1.0, 0.2)}
    factors = {'L0_attn_Wq_down': 8.0,
     'L0_attn_Wk_down': 8.0,
     'L0_attn_Wv_down': 8.0,
     'L0_attn_Wq_up_c': 8.0,
     'L0_attn_Wq_up_e': 8.0,
     'L0_attn_Wk_up_c': 8.0,
     'L0_attn_Wk_up_e': 8.0,
     'L0_attn_Wv_up': 8.0,
     'L0_attn_Wc': 8.0,
     'L0_ffn_gate_w': 8.0,
     'L0_ffn_w1': 8.0,
     'L0_ffn_w2': 8.0,
     'L0_ffn_w3': 8.0,
     'L0_ffn_ws1': 2.818,
     'L0_ffn_ws2': 2.8,
     'L0_ffn_ws3': 2.8,
     'L1_attn_Wq': 5.231,
     'L1_attn_bq': 8.0,
     'L1_attn_Wk': 4.522,
     'L1_attn_bk': 8.0,
     'L1_attn_bv': 6.254,
     'L1_attn_bo': 5.157,
     'L1_xattn_Wqkv': 2.829,
     'L1_xattn_Wout': 2.797,
     'L1_xattn_Wgate': 6.451}
    for name, (base, spread) in spreads.items():
        noise = np.random.default_rng([zlib.crc32(name.encode()), seed]).standard_normal(out[name].shape)
        drawn = base * np.exp(spread * noise) if base else spread * noise
        out[name] = jnp.asarray(drawn.astype(out[name].dtype))
    for name, factor in factors.items():
        out[name] = (out[name] * factor).astype(out[name].dtype)
    return out
```

```python
from contextlib import ExitStack

import numpy as np

import concourse.bass as bass
from concourse import mybir

F32 = mybir.dt.float32
F32R = mybir.dt.float32r
BF16 = mybir.dt.bfloat16
U32 = mybir.dt.uint32
ALU = mybir.AluOpType
ACT = mybir.ActivationFunctionType
AXIS_X = mybir.AxisListType.X

T = 100
D = 256
P = 128
KC = D // P
HEADS = 16
DH = D // HEADS
GROUPS = 4
HPG = HEADS // GROUPS
GW = HPG * T
LN_EPS = 1e-5
NEG = -1e30


def done(i, u, j=0, steps=1):
    return i * (2 * steps) + (2 * steps + 2 * j + u + 1)


def before(i, u, j=0, steps=1):
    return i * (2 * steps) + (2 * j + u + 1)


class Links:

    def __init__(self, eng, sem, i, per_iter):
        self.eng, self.sem, self.i, self.per_iter, self.k = eng, sem, i, per_iter, 0

    def add(self, ins):
        self.k += 1
        ins.then_inc(self.sem, 1)

    def wait(self, back=0):
        self.eng.wait_ge(self.sem, self.i * self.per_iter + (self.k - back))

    def end(self):
        assert self.k == self.per_iter, f"links in one iteration: {self.k}"


class Store:

    def __init__(self, nc, ctx, stage):
        self.nc, self.ctx, self.stage = nc, ctx, stage
        self.semaphores = []
        ctx.callback(self.end)

    def sb(self, name, shape, dt=F32):
        return self.ctx.enter_context(self.nc.sbuf_tensor(f"{self.stage}_{name}", shape, dt))

    def ps(self, name, shape, dt=F32):
        return self.ctx.enter_context(self.nc.psum_tensor(f"{self.stage}_{name}", shape, dt))

    def sem(self, name):
        self.semaphores.append(self.nc.alloc_semaphore(f"{self.stage}_{name}"))
        return self.semaphores[-1]

    def end(self):
        self.nc.clear_and_free_semaphores(self.semaphores)
        self.nc.all_engine_barrier()

    def sems(self, name):
        return [self.sem(f"{name}{u}") for u in range(2)]


class Norm:

    def __init__(self, s, nc, rows=T, tag="", lots=2):
        self.nc, self.rows = nc, rows
        tag = "ln" + tag + "_"
        self.stats = s.sb(tag + "stats", [rows, lots, 6])
        self.mv = s.sb(tag + "mv", [rows, lots, 2])
        self.spare = s.sb(tag + "spare", [rows, 1])
        self.var = s.sb(tag + "var", [rows, lots])
        self.rstd = s.sb(tag + "rstd", [rows, lots])
        self.power = s.sb(tag + "power", [rows, lots])
        self.var_ready = s.sem(tag + "var_ready")
        self.rstd_ready = s.sem(tag + "rstd_ready")
        self.power_set = s.sem(tag + "power_set")

    def set_power(self, pool):
        self.nc.gpsimd.memset(self.power[:], -0.5).then_inc(self.power_set, 1)
        pool.wait_ge(self.power_set, 1)

    def raise_power(self, pool, i):
        pool.wait_ge(self.var_ready, i + 1)
        self.nc.gpsimd.tensor_tensor(self.rstd[:], self.var[:], self.power[:], ALU.pow).then_inc(self.rstd_ready, 1)

    def steps_of(self, dve, links, i, sources, outs, out_ready):
        nc, mv = self.nc, self.mv
        for n, src in enumerate(sources):
            links.add(nc.vector.bn_stats(self.stats[:, n, :], src))
        links.wait()
        nc.vector.memset(self.spare[:], 0.0)
        for n in range(len(sources)):
            links.add(nc.vector.bn_aggr(mv[:, n, :], self.stats[:, n, :]))
        links.wait()
        nc.vector.tensor_scalar(self.var[:], mv[:, :, 1], LN_EPS, None, ALU.add).then_inc(self.var_ready, 1)
        dve.wait_ge(self.rstd_ready, i + 1)
        for n, (src, out) in enumerate(zip(sources, outs)):
            nc.vector.tensor_scalar(out, src, mv[:, n, 0:1], self.rstd[:, n:n + 1],
                                    ALU.subtract, ALU.mult).then_inc(out_ready, 1)

    def steps(self, dve, links, i, src, out, out_ready):
        self.steps_of(dve, links, i, [src[:, u, :] for u in range(2)], [out[:, u, :] for u in range(2)], out_ready)


def self_attention(nc, NB, x_in, x_out, w):
    with ExitStack() as ctx:
        s = Store(nc, ctx, "sa")
        down = s.sb("down", [64, 3, HEADS, D])
        up = s.sb("up", [64, 3, 32])
        wq = s.sb("wq", [P, 2, KC, D])
        wk = s.sb("wk", [P, 2, KC, D])
        wv = s.sb("wv", [P, KC, D])
        wc = s.sb("wc", [P, KC, D])
        cosT = s.sb("cosT", [P, T])
        sinT = s.sb("sinT", [P, T])
        head_mask = s.sb("head_mask", [P, 8])
        head_mask2 = s.sb("head_mask2", [P, 4])
        ident = s.sb("ident", [P, P])
        identb = s.sb("identb", [P, P], BF16)
        causalf = s.sb("causalf", [T, T])
        causal = s.sb("causal", [T, HPG, T], BF16)
        neg1 = s.sb("neg1", [T, T], F32R)
        x_t = s.sb("x_t", [T, 2, D])
        x_res = s.sb("x_res", [T, 2, D])
        xT = s.sb("xT", [P, 2, KC, T])
        qk_c = s.sb("qk_c", [P, 2, 2, KC, T])
        qk_s = s.sb("qk_s", [P, 2, 2, KC, T])
        qkT = s.sb("qkT", [P, 2, 2, KC, T])
        q_bd = s.sb("q_bd", [P, 2, KC, 8, T])
        v1 = s.sb("v1", [T, 2, GROUPS, P])
        mx = s.sb("mx", [T, 2, GW])
        nmax = s.sb("nmax", [T, 2, HPG])
        dmax = s.sb("dmax", [T, 2, HPG, T], F32R)
        prob = s.sb("prob", [T, 2, GW])
        own = s.sb("own", [P, 2, GW])
        nd = s.sb("nd", [P, 2, T])
        rec = s.sb("rec", [64, 2, T])
        yT = s.sb("yT", [P, 2, KC, T])
        r = s.sb("r", [T, 2, D])
        norm = Norm(s, nc)
        x_o = s.sb("x_o", [T, 2, D])
        S = [s.ps(f"S{u}", [P, 3, 512]) for u in range(2)]
        W = [s.ps(f"W{u}", [P, 512]) for u in range(2)]

        w_in = s.sem("weights_loaded")
        up_ready = s.sem("up_ready")
        fused = s.sem("fused_in_psum")
        fused_sb = s.sem("fused_in_sbuf")
        const_ready = s.sem("const_ready")
        x_loaded = s.sems("x_loaded")
        res_loaded = s.sems("res_loaded")
        stored = s.sems("stored")
        x_turned = s.sem("x_turned")
        xT_ready = s.sem("xT_ready")
        qkv_done = s.sem("qkv_done")
        v_ready = s.sem("v_ready")
        qk_rot = s.sem("qk_rot")
        qk_ready = s.sem("qk_ready")
        qbd_ready = s.sem("qbd_ready")
        scored = s.sem("scored")
        mx_copied = s.sem("mx_copied")
        mx_turned = s.sem("mx_turned")
        max_ready = s.sem("max_ready")
        shifted = s.sem("shifted")
        prob_ready = s.sem("prob_ready")
        av_done = s.sem("av_done")
        own_ready = s.sem("own_ready")
        yT_ready = s.sem("yT_ready")
        y_done = s.sem("y_done")
        r_ready = s.sem("r_ready")
        out_ready = s.sem("out_ready")
        vlink = s.sem("dve_link")
        alink = s.sem("act_link")
        plink = s.sem("pool_link")
        G = GROUPS

        with nc.Block() as block:

            @block.sync
            def _(sp):
                for k, name in enumerate(("L0_attn_Wq_down", "L0_attn_Wk_down", "L0_attn_Wv_down")):
                    sp.dma_start(down[:, k, :, :], w[name].rearrange("(h l) c -> l h c", l=64)).then_inc(w_in, 16)
                for k, (c_, e_) in enumerate((("Wq_up_c", "Wq_up_e"), ("Wk_up_c", "Wk_up_e"))):
                    sp.dma_start(up[:, k, 0:8], w["L0_attn_" + c_]).then_inc(w_in, 16)
                    sp.dma_start(up[:, k, 8:16], w["L0_attn_" + e_]).then_inc(w_in, 16)
                sp.dma_start(up[:, 2, 0:16], w["L0_attn_Wv_up"]).then_inc(w_in, 16)
                sp.dma_start(wc[:], w["L0_attn_Wc"].rearrange("(k p) n -> p k n", p=P)).then_inc(w_in, 16)
                sp.dma_start(cosT[:], w["cos_sa"]).then_inc(w_in, 16)
                sp.dma_start(sinT[:], w["sin_sa"]).then_inc(w_in, 16)
                sp.dma_start(head_mask[:], w["head_mask"]).then_inc(w_in, 16)
                sp.dma_start(head_mask2[:], w["head_mask2"]).then_inc(w_in, 16)
                sp.dma_start(ident[:], w["ident"]).then_inc(w_in, 16)
                sp.dma_start(causalf[:], w["causal"]).then_inc(w_in, 16)
                with sp.Fori(0, NB // 2) as i:
                    for u in range(2):
                        sp.wait_ge(x_turned, before(i, u))
                        sp.dma_start(x_t[:, u, :], x_in[2 * i + u]).then_inc(x_loaded[u], 16)
                    for u in range(2):
                        sp.wait_ge(r_ready, before(i, u))
                        sp.dma_start(x_res[:, u, :], x_in[2 * i + u]).then_inc(res_loaded[u], 16)

            W_ALL = 16 * 15

            @block.tensor
            def _(pe):
                for sem, steps in ((x_turned, 1), (qkv_done, 1), (scored, G), (mx_turned, G), (shifted, G),
                                   (av_done, G), (y_done, 1)):
                    pe.sem_inc(sem, 2 * steps)
                pe.wait_ge(w_in, W_ALL)
                pe.wait_ge(up_ready, 1)
                for k in range(3):
                    n = 32 if k < 2 else 16
                    if k:
                        pe.wait_ge(fused_sb, k)
                    for c in range(KC):
                        for h in range(HEADS):
                            last = nc.tensor.matmul(S[0][:, c, h * n:(h + 1) * n], down[:, k, h, c * P:(c + 1) * P],
                                                    up[:, k, 0:n], start=True, stop=True)
                    last.then_inc(fused, 1)
                pe.wait_ge(fused_sb, 3)
                pe.wait_ge(const_ready, 1)
                with pe.Fori(0, NB // 2) as i:
                    for u in range(2):
                        pe.wait_ge(x_loaded[u], 16 * i + 16)
                        pe.wait_ge(r_ready, before(i, u))
                        for c in range(KC):
                            last = nc.tensor.transpose(W[u][:, c * T:(c + 1) * T], x_t[:, u, c * P:(c + 1) * P],
                                                       ident[:T, :T])
                        last.then_inc(x_turned, 1)
                    for u in range(2):
                        pe.wait_ge(xT_ready, done(i, u))
                        pe.wait_ge(prob_ready, before(i, u, G - 1, G))
                        for k, wm in ((0, wq), (1, wk)):
                            for turned in range(2):
                                for g in range(KC):
                                    col = (turned * KC + g) * T
                                    for c in range(KC):
                                        nc.tensor.matmul(S[u][:, k, col:col + T], wm[:, turned, c, g * P:(g + 1) * P],
                                                         xT[:, u, c, :], start=(c == 0), stop=(c == KC - 1))
                        for c in range(KC):
                            last = nc.tensor.matmul(S[u][:T, 2, 0:D], xT[:, u, c, :], wv[:, c, :],
                                                    start=(c == 0), stop=(c == KC - 1))
                        last.then_inc(qkv_done, 1)

                    def attend(j):
                        for u in range(2):
                            pe.wait_ge(prob_ready, done(i, u, j, G))
                            pe.wait_ge(max_ready, done(i, u, j, G))
                            nc.tensor.matmul(W[u][:, 0:GW], v1[:, u, j, :], prob[:, u, :],
                                             start=True, stop=True).then_inc(av_done, 1)

                    for j in range(G):
                        bank = j % 3
                        for u in range(2):
                            if j == 0:
                                pe.wait_ge(qk_rot, done(i, u))
                                pe.wait_ge(v_ready, done(i, u))
                                pe.wait_ge(qbd_ready, done(i, u))
                            g, h0 = j // 2, 4 * (j % 2)
                            nc.tensor.matmul(S[u][:T, bank, 0:GW], qkT[:, u, 1, g, :],
                                             q_bd[:, u, g, h0:h0 + 4, :].rearrange("p h t -> p (h t)"),
                                             start=True, stop=False)
                            nc.tensor.matmul(S[u][:T, bank, 0:GW], identb[:T, :T],
                                             causal[:].rearrange("p h t -> p (h t)"), start=False, stop=True).then_inc(scored, 1)
                        if j:
                            attend(j - 1)
                        for u in range(2):
                            pe.wait_ge(mx_copied, done(i, u, j, G))
                            if j:
                                pe.wait_ge(own_ready, done(i, u, j - 1, G))
                            for h in range(HPG):
                                last = nc.tensor.transpose(W[u][:T, h * P:h * P + T], mx[:, u, h * T:(h + 1) * T],
                                                           ident[:T, :T])
                            last.then_inc(mx_turned, 1)
                        for u in range(2):
                            pe.wait_ge(max_ready, done(i, u, j, G))
                            nc.tensor.matmul(S[u][:T, bank, 0:GW], neg1[:], dmax[:, u, :, :].rearrange("p h t -> p (h t)"),
                                             start=False, stop=True, skip_group_check=True).then_inc(shifted, 1)
                    attend(G - 1)
                    for u in range(2):
                        pe.wait_ge(yT_ready, done(i, u, G - 1, G))
                        for c in range(KC):
                            last = nc.tensor.matmul(W[u][:T, 0:D], yT[:, u, c, :], wc[:, c, :],
                                                    start=(c == 0), stop=(c == KC - 1))
                        last.then_inc(y_done, 1)

            @block.scalar
            def _(act):
                act.sem_inc(xT_ready, 2)
                act.sem_inc(v_ready, 2)
                act.sem_inc(mx_copied, 2 * G)
                act.sem_inc(prob_ready, 2 * G)
                for u in range(2):
                    act.sem_inc(stored[u], 16)
                for k in range(3):
                    act.wait_ge(fused, k + 1)
                    for c in range(KC):
                        if k < 2:
                            src = S[0][:, c, :].rearrange("p (h n) -> p h n", n=32)
                            dst = (wq, wk)[k]
                            for t in range(2):
                                last = nc.scalar.activation(dst[:, t, c, :].rearrange("p (h n) -> p h n", n=16),
                                                            src[:, :, 16 * t:16 * t + 16], ACT.Copy)
                        else:
                            last = nc.scalar.activation(wv[:, c, :], S[0][:, c, 0:D], ACT.Copy)
                    last.then_inc(fused_sb, 1)
                with act.Fori(0, NB // 2) as i:
                    for u in range(2):
                        act.wait_ge(x_turned, done(i, u))
                        act.wait_ge(qkv_done, before(i, u))
                        nc.scalar.activation(xT[:, u, :, :].rearrange("p c t -> p (c t)"), W[u][:, 0:KC * T],
                                             ACT.Copy).then_inc(xT_ready, 1)
                    for u in range(2):
                        act.wait_ge(qkv_done, done(i, u))
                        act.wait_ge(av_done, before(i, u, G - 1, G))
                        nc.scalar.activation(v1[:, u, :, 0:64], S[u][:T, 2, 0:D].rearrange("p (g n) -> p g n", n=64),
                                             ACT.Copy).then_inc(v_ready, 1)
                    for j in range(G):
                        bank = j % 3
                        for u in range(2):
                            act.wait_ge(scored, done(i, u, j, G))
                            nc.scalar.activation(mx[:, u, :], S[u][:T, bank, 0:GW], ACT.Copy).then_inc(mx_copied, 1)
                        for u in range(2):
                            act.wait_ge(shifted, done(i, u, j, G))
                            if j:
                                act.wait_ge(av_done, done(i, u, j - 1, G))
                            nc.scalar.activation(prob[:, u, :], S[u][:T, bank, 0:GW], ACT.Exp,
                                                 scale=float(DH) ** -0.5).then_inc(prob_ready, 1)
                    for u in range(2):
                        act.wait_ge(out_ready, done(i, u))
                        act.dma_start(x_out[2 * i + u], x_o[:, u, :]).then_inc(stored[u], 16)
                for u in range(2):
                    act.wait_ge(stored[u], 16 * (NB // 2) + 16)

            @block.gpsimd
            def _(pool):
                pool.sem_inc(qk_ready, 2)
                pool.sem_inc(qbd_ready, 2)
                norm.set_power(pool)
                with pool.Fori(0, NB // 2) as i:
                    for u in range(2):
                        pool.wait_ge(qk_rot, done(i, u))
                        pool.wait_ge(scored, before(i, u, G - 1, G))
                        nc.gpsimd.tensor_tensor(qkT[:, u, :, :, :].rearrange("p a c t -> p (a c t)"),
                                                qk_c[:, u, :, :, :].rearrange("p a c t -> p (a c t)"),
                                                qk_s[:, u, :, :, :].rearrange("p a c t -> p (a c t)"),
                                                ALU.add).then_inc(qk_ready, 1)
                    for u in range(2):
                        pool.wait_ge(qk_ready, done(i, u))
                        pool.wait_ge(scored, before(i, u, G - 1, G))
                        for g in range(KC):
                            last = nc.gpsimd.tensor_tensor(q_bd[:, u, g, :, :],
                                                           qkT[:, u, 0, g, :].unsqueeze(1).to_broadcast([P, 8, T]),
                                                           head_mask[:].unsqueeze(2).to_broadcast([P, 8, T]), ALU.mult)
                        last.then_inc(qbd_ready, 1)
                    norm.raise_power(pool, i)

            @block.vector
            def _(dve):
                nc.vector.memset(v1[:], 1.0)
                nc.vector.memset(neg1[:].bitcast(F32), -1.0)
                for sem, steps in ((qk_rot, 1), (max_ready, G), (own_ready, G), (yT_ready, G), (r_ready, 1),
                                   (out_ready, 1)):
                    dve.sem_inc(sem, 2 * steps)
                dve.wait_ge(w_in, W_ALL)
                nc.vector.memset(up[:, 0:2, 16:24], 0.0)
                for k in range(2):
                    e = up[:, k, 8:16].rearrange("p (n two) -> p n two", two=2)
                    t = up[:, k, 24:32].rearrange("p (n two) -> p n two", two=2)
                    nc.vector.tensor_scalar(t[:, :, 0], e[:, :, 1], -1.0, None, ALU.mult)
                    last = nc.vector.tensor_copy(t[:, :, 1], e[:, :, 0])
                last.then_inc(up_ready, 1)
                nc.vector.tensor_copy(identb[:], ident[:])
                nc.vector.tensor_copy(causal[:], causalf[:].unsqueeze(1).to_broadcast([T, HPG, T])).then_inc(const_ready, 1)
                with dve.Fori(0, NB // 2) as i:
                    links = Links(dve, vlink, i, 2 * 3 * G + 2 * 2)
                    for u in range(2):
                        dve.wait_ge(qkv_done, done(i, u))
                        dve.wait_ge(qk_ready, before(i, u))
                        for k in range(2):
                            src = S[u][:, k, 0:4 * T].rearrange("p (r g t) -> p r g t", r=2, t=T)
                            nc.vector.tensor_tensor(qk_c[:, u, k, :, :], src[:, 0], cosT[:].unsqueeze(1).to_broadcast([P, KC, T]), ALU.mult)
                            last = nc.vector.tensor_tensor(qk_s[:, u, k, :, :], src[:, 1], sinT[:].unsqueeze(1).to_broadcast([P, KC, T]), ALU.mult)
                        last.then_inc(qk_rot, 1)

                    def normalise(j):
                        for u in range(2):
                            dve.wait_ge(av_done, done(i, u, j, G))
                            nc.vector.tensor_tensor(own[:, u, :].rearrange("p (h t) -> p h t", t=T),
                                                    W[u][:, 0:GW].rearrange("p (h t) -> p h t", t=T),
                                                    head_mask2[:].unsqueeze(2).to_broadcast([P, HPG, T]), ALU.mult)\
                                .then_inc(own_ready, 1)
                        for u in range(2):
                            dve.wait_ge(own_ready, done(i, u, j, G))
                            links.add(nc.vector.tensor_reduce(nd[:, u, :], own[:, u, :].rearrange("p (h t) -> p t h", t=T),
                                                              axis=AXIS_X, op=ALU.add))
                        links.wait()
                        for u in range(2):
                            links.add(nc.vector.reciprocal(rec[:, u, :], nd[64:128, u, :]))
                        links.wait()
                        o = 64 * (j % 2)
                        for u in range(2):
                            if j == 0:
                                dve.wait_ge(y_done, before(i, u))
                            nc.vector.tensor_tensor(yT[o:o + 64, u, j // 2, :], nd[0:64, u, :], rec[:, u, :],
                                                    ALU.mult).then_inc(yT_ready, 1)

                    for j in range(G):
                        if j:
                            normalise(j - 1)
                        for u in range(2):
                            dve.wait_ge(mx_turned, done(i, u, j, G))
                            links.add(nc.vector.tensor_reduce(nmax[:, u, :], W[u][:T, :].rearrange("p (h t) -> p h t", t=P)[:, :, 0:T],
                                                              axis=AXIS_X, op=ALU.max))
                        links.wait()
                        for u in range(2):
                            if j:
                                dve.wait_ge(shifted, done(i, u, j - 1, G))
                            nc.vector.tensor_tensor(dmax[:, u, :, :], ident[:T, :T].unsqueeze(1).to_broadcast([T, HPG, T]),
                                                    nmax[:, u, :].unsqueeze(2).to_broadcast([T, HPG, T]),
                                                    ALU.mult).then_inc(max_ready, 1)
                    normalise(G - 1)
                    for u in range(2):
                        dve.wait_ge(y_done, done(i, u))
                        dve.wait_ge(res_loaded[u], 16 * i + 16)
                        nc.vector.tensor_tensor(r[:, u, :], W[u][:T, 0:D], x_res[:, u, :], ALU.add).then_inc(r_ready, 1)
                    dve.wait_ge(r_ready, done(i, 1))
                    for u in range(2):
                        dve.wait_ge(stored[u], 16 * i + 16)
                    norm.steps(dve, links, i, r, x_o, out_ready)
                    links.end()
def cross_attention_strided(nc, NB, x_in, x_out, w, src_len):
    NH = 8
    HD = D // NH
    KPH = -(-src_len // NH)
    KFULL = src_len - (KPH - 1) * NH
    assert KFULL == 1
    SLOT = 64
    PAIRS = NH // 2
    VW = 96
    with ExitStack() as ctx:
        s = Store(nc, ctx, "xs")
        wq = s.sb("wq", [P, KC, D])
        wk = s.sb("wk", [P, KC, D])
        wv = s.sb("wv", [P, KC, D + 64])
        wo = s.sb("wo", [P, KC, D])
        bq = s.sb("bq", [P, KC])
        bk = s.sb("bk", [P, KC])
        bv = s.sb("bv", [P, KC])
        bo = s.sb("bo", [T, D])
        ident = s.sb("ident", [P, P])
        head_mask = s.sb("head_mask", [P, 4])
        x_t = s.sb("x_t", [T, 2, D])
        x_res = s.sb("x_res", [T, 2, D])
        x_bo = s.sb("x_bo", [T, 2, D])
        xT = s.sb("xT", [P, 2, KC, T])
        ctxT = s.sb("ctxT", [P, 2, KC, NH, SLOT])
        qT = s.sb("qT", [P, 2, KC, T])
        q_bd = s.sb("q_bd", [P, 2, KC, 4, T])
        kT = s.sb("kT", [P, 2, KC, NH, KPH])
        v_bd = s.sb("v_bd", [P, 2, PAIRS, VW])
        smax = s.sb("smax", [T, 2, NH])
        prob = s.sb("prob", [T, 2, NH, SLOT])
        pT = s.sb("pT", [P, 2, PAIRS, T])
        rec = s.sb("rec", [T, 2, NH])
        y = s.sb("y", [T, 2, D])
        yT = s.sb("yT", [P, 2, KC, T])
        r = s.sb("r", [T, 2, D])
        x_o = s.sb("x_o", [T, 2, D])
        norm = Norm(s, nc)
        B = [[s.ps(f"B{b}_{u}", [P, 512]) for b in range(4)] for u in range(2)]

        w_in = s.sem("weights_loaded")
        const_ready = s.sem("const_ready")
        x_loaded, res_loaded, ctx_loaded, stored = s.sems("x_loaded"), s.sems("res_loaded"), s.sems("ctx_loaded"), s.sems("stored")
        x_turned, xT_ready = s.sem("x_turned"), s.sem("xT_ready")
        qk_done, v_done = s.sem("qk_done"), s.sem("v_done")
        q_ready, k_ready, v_ready = s.sem("q_ready"), s.sem("k_ready"), s.sem("v_ready")
        qbd_ready = s.sem("qbd_ready")
        xbo_ready = s.sem("xbo_ready")
        scored = s.sem("scored")
        less_ready = s.sem("less_ready")
        prob_ready = s.sem("prob_ready")
        p_turned, pT_ready = s.sem("p_turned"), s.sem("pT_ready")
        av_done = s.sem("av_done")
        y_ready = s.sem("y_ready")
        y_turned, yT_ready = s.sem("y_turned"), s.sem("yT_ready")
        o_done, r_ready, out_ready = s.sem("o_done"), s.sem("r_ready"), s.sem("out_ready")
        vlink = s.sem("dve_link")

        loads = [(wq[:], w["L0_xattn_Wq"].rearrange("(k p) n -> p k n", p=P)),
                 (wk[:], w["L0_xattn_Wk"].rearrange("(k p) n -> p k n", p=P)),
                 (wv[:, :, 0:D], w["L0_xattn_Wv"].rearrange("(k p) n -> p k n", p=P)),
                 (wo[:], w["L0_xattn_Wo"].rearrange("(k p) n -> p k n", p=P)),
                 (bq[:], w["L0_xattn_bq"]), (bk[:], w["L0_xattn_bk"]), (bv[:], w["L0_xattn_bv"]),
                 (bo[:], w["L0_xattn_bo"].to_broadcast([T, D])),
                 (ident[:], w["ident"]), (head_mask[:], w["head_mask4"]),
                 (v_bd[:, 0], w["v_ones"]), (v_bd[:, 1], w["v_ones"])]
        W_ALL = 16 * len(loads)
        SC = float(1.0 / np.sqrt(np.float32(HD)))

        with nc.Block() as block:

            @block.sync
            def _(sp):
                for dst, src in loads:
                    sp.dma_start(dst, src).then_inc(w_in, 16)
                with sp.Fori(0, NB // 2) as i:
                    for u in range(2):
                        sp.wait_ge(x_turned, before(i, u))
                        sp.dma_start(x_t[:, u, :], x_in[2 * i + u]).then_inc(x_loaded[u], 16)
                        sp.wait_ge(v_done, before(i, u))
                        sp.dma_start(ctxT[:, u].rearrange("p k h s -> p k (h s)"), w["ctxT"][2 * i + u]).then_inc(ctx_loaded[u], 16)
                    for u in range(2):
                        sp.wait_ge(xbo_ready, before(i, u))
                        sp.dma_start(x_res[:, u, :], x_in[2 * i + u]).then_inc(res_loaded[u], 16)

            @block.tensor
            def _(pe):
                for sem in (x_turned, qk_done, v_done, scored, p_turned, av_done, y_turned, o_done):
                    pe.sem_inc(sem, 2)
                pe.wait_ge(w_in, W_ALL)
                pe.wait_ge(const_ready, 1)
                with pe.Fori(0, NB // 2) as i:
                    for u in range(2):
                        pe.wait_ge(x_loaded[u], 16 * i + 16)
                        pe.wait_ge(yT_ready, before(i, u))
                        for c in range(KC):
                            last = nc.tensor.transpose(B[u][3][:, c * T:(c + 1) * T], x_t[:, u, c * P:(c + 1) * P], ident[:T, :T])
                        last.then_inc(x_turned, 1)
                    for u in range(2):
                        pe.wait_ge(ctx_loaded[u], 16 * i + 16)
                        pe.wait_ge(less_ready, before(i, u))
                        pe.wait_ge(r_ready, before(i, u))
                        for g in range(KC):
                            for c in range(KC):
                                nc.tensor.matmul(B[u][g][:, 0:NH * KPH], wk[:, c, g * P:(g + 1) * P],
                                                 ctxT[:, u, c, :, 0:KPH], start=(c == 0), stop=(c == KC - 1))
                        pe.wait_ge(xT_ready, done(i, u))
                        pe.wait_ge(y_ready, before(i, u))
                        for g in range(KC):
                            for c in range(KC):
                                last = nc.tensor.matmul(B[u][2][:, g * T:(g + 1) * T], wq[:, c, g * P:(g + 1) * P],
                                                        xT[:, u, c, :], start=(c == 0), stop=(c == KC - 1))
                        last.then_inc(qk_done, 1)
                    for u in range(2):
                        for p in range(PAIRS):
                            for c in range(KC):
                                last = nc.tensor.matmul(B[u][3][:, p * P:(p + 1) * P],
                                                        ctxT[:, u, c, 2 * p:2 * p + 2, :].rearrange("p h s -> p (h s)"),
                                                        wv[:, c, 64 * p:64 * p + P], start=(c == 0), stop=(c == KC - 1))
                        last.then_inc(v_done, 1)
                    for u in range(2):
                        pe.wait_ge(qbd_ready, done(i, u))
                        pe.wait_ge(k_ready, done(i, u))
                        for h in range(NH):
                            last = nc.tensor.matmul(B[u][0][:T, h * KPH:(h + 1) * KPH], q_bd[:, u, h // 4, h % 4, :],
                                                    kT[:, u, h // 4, h, :], start=True, stop=True)
                        last.then_inc(scored, 1)
                    for u in range(2):
                        pe.wait_ge(prob_ready, done(i, u))
                        for p in range(PAIRS):
                            last = nc.tensor.transpose(B[u][1][:, p * T:(p + 1) * T],
                                                       prob[:, u, 2 * p:2 * p + 2, :].rearrange("p h s -> p (h s)"), ident[:T, :T])
                        last.then_inc(p_turned, 1)
                    for u in range(2):
                        pe.wait_ge(pT_ready, done(i, u))
                        pe.wait_ge(v_ready, done(i, u))
                        for p in range(PAIRS):
                            last = nc.tensor.matmul(B[u][2][:T, p * VW:(p + 1) * VW], pT[:, u, p, :], v_bd[:, u, p, :],
                                                    start=True, stop=True)
                        last.then_inc(av_done, 1)
                    for u in range(2):
                        pe.wait_ge(y_ready, done(i, u))
                        for c in range(KC):
                            last = nc.tensor.transpose(B[u][3][:, c * T:(c + 1) * T], y[:, u, c * P:(c + 1) * P], ident[:T, :T])
                        last.then_inc(y_turned, 1)
                    for u in range(2):
                        pe.wait_ge(yT_ready, done(i, u))
                        for c in range(KC):
                            last = nc.tensor.matmul(B[u][1][:T, 0:D], yT[:, u, c, :], wo[:, c, :],
                                                    start=(c == 0), stop=(c == KC - 1))
                        last.then_inc(o_done, 1)

            @block.scalar
            def _(act):
                for sem in (xT_ready, q_ready, k_ready, v_ready, prob_ready, pT_ready, yT_ready):
                    act.sem_inc(sem, 2)
                for u in range(2):
                    act.sem_inc(stored[u], 16)
                act.wait_ge(w_in, W_ALL)
                with act.Fori(0, NB // 2) as i:
                    for u in range(2):
                        act.wait_ge(x_turned, done(i, u))
                        nc.scalar.activation(xT[:, u, :, :].rearrange("p c t -> p (c t)"), B[u][3][:, 0:KC * T],
                                             ACT.Copy).then_inc(xT_ready, 1)
                    for u in range(2):
                        act.wait_ge(qk_done, done(i, u))
                        act.wait_ge(qbd_ready, before(i, u))
                        for g in range(KC):
                            last = nc.scalar.activation(qT[:, u, g, :], B[u][2][:, g * T:(g + 1) * T], ACT.Identity, bias=bq[:, g:g + 1])
                        last.then_inc(q_ready, 1)
                        for g in range(KC):
                            last = nc.scalar.activation(kT[:, u, g, :, :].rearrange("p h s -> p (h s)"), B[u][g][:, 0:NH * KPH],
                                                        ACT.Identity, bias=bk[:, g:g + 1])
                        last.then_inc(k_ready, 1)
                    for u in range(2):
                        act.wait_ge(v_done, done(i, u))
                        v = B[u][3][:, :].rearrange("p (n f) -> p n f", f=P)
                        nc.scalar.activation(v_bd[0:KPH, u, :, 0:HD], v[0:KPH, :, 0:HD], ACT.Copy)
                        nc.scalar.activation(v_bd[SLOT:SLOT + KPH, u, :, HD + 1:2 * HD + 1], v[SLOT:SLOT + KPH, :, HD:2 * HD],
                                             ACT.Copy).then_inc(v_ready, 1)
                    for u in range(2):
                        act.wait_ge(less_ready, done(i, u))
                        nc.scalar.activation(prob[:, u, :, 0:KPH - 1], prob[:, u, :, 0:KPH - 1], ACT.Exp, scale=SC)
                        nc.scalar.activation(prob[:, u, 0, KPH - 1:KPH], prob[:, u, 0, KPH - 1:KPH], ACT.Exp,
                                             scale=SC).then_inc(prob_ready, 1)
                    for u in range(2):
                        act.wait_ge(p_turned, done(i, u))
                        nc.scalar.activation(pT[:, u, :, :].rearrange("p n t -> p (n t)"), B[u][1][:, 0:PAIRS * T],
                                             ACT.Copy).then_inc(pT_ready, 1)
                    for u in range(2):
                        act.wait_ge(y_turned, done(i, u))
                        for g in range(KC):
                            last = nc.scalar.activation(yT[:, u, g, :], B[u][3][:, g * T:(g + 1) * T], ACT.Identity, bias=bv[:, g:g + 1])
                        last.then_inc(yT_ready, 1)
                    for u in range(2):
                        act.wait_ge(out_ready, done(i, u))
                        act.dma_start(x_out[2 * i + u], x_o[:, u, :]).then_inc(stored[u], 16)
                for u in range(2):
                    act.wait_ge(stored[u], 16 * (NB // 2) + 16)

            @block.gpsimd
            def _(pool):
                nc.gpsimd.memset(wv[:, :, D:D + 64], 0.0)
                nc.gpsimd.memset(prob[:], 0.0).then_inc(const_ready, 1)
                pool.sem_inc(qbd_ready, 2)
                pool.sem_inc(xbo_ready, 2)
                norm.set_power(pool)
                pool.wait_ge(w_in, W_ALL)
                with pool.Fori(0, NB // 2) as i:
                    for u in range(2):
                        pool.wait_ge(q_ready, done(i, u))
                        pool.wait_ge(scored, before(i, u))
                        for g in range(KC):
                            last = nc.gpsimd.tensor_tensor(q_bd[:, u, g, :, :],
                                                           qT[:, u, g, :].unsqueeze(1).to_broadcast([P, 4, T]),
                                                           head_mask[:].unsqueeze(2).to_broadcast([P, 4, T]), ALU.mult)
                        last.then_inc(qbd_ready, 1)
                    for u in range(2):
                        pool.wait_ge(res_loaded[u], 16 * i + 16)
                        pool.wait_ge(r_ready, before(i, u))
                        nc.gpsimd.tensor_tensor(x_bo[:, u, :], x_res[:, u, :], bo[:], ALU.add).then_inc(xbo_ready, 1)
                    norm.raise_power(pool, i)

            @block.vector
            def _(dve):
                for sem in (less_ready, y_ready, r_ready, out_ready):
                    dve.sem_inc(sem, 2)
                dve.wait_ge(const_ready, 1)
                with dve.Fori(0, NB // 2) as i:
                    links = Links(dve, vlink, i, 2 * 2 + 2 + 2 * 2)
                    for u in range(2):
                        dve.wait_ge(scored, done(i, u))
                        sc = B[u][0][:T, 0:NH * KPH].rearrange("p (h s) -> p h s", s=KPH)
                        links.add(nc.vector.tensor_reduce(smax[:, u, :], sc[:, :, 0:KPH - 1], axis=AXIS_X, op=ALU.max))
                    links.wait()
                    for u in range(2):
                        links.add(nc.vector.tensor_tensor(smax[:, u, 0:1], smax[:, u, 0:1], B[u][0][:T, KPH - 1:KPH], ALU.max))
                    links.wait()
                    for u in range(2):
                        sc = B[u][0][:T, 0:NH * KPH].rearrange("p (h s) -> p h s", s=KPH)
                        dve.wait_ge(p_turned, before(i, u))
                        nc.vector.tensor_tensor(prob[:, u, :, 0:KPH - 1], sc[:, :, 0:KPH - 1],
                                                smax[:, u, :].unsqueeze(2).to_broadcast([T, NH, KPH - 1]), ALU.subtract)
                        nc.vector.tensor_tensor(prob[:, u, 0, KPH - 1:KPH], sc[:, 0, KPH - 1:KPH], smax[:, u, 0:1],
                                                ALU.subtract).then_inc(less_ready, 1)
                    for u in range(2):
                        dve.wait_ge(av_done, done(i, u))
                        av = B[u][2][:T, 0:PAIRS * VW].rearrange("p (n c) -> p n c", c=VW)[:, :, 0:2 * (HD + 1)]\
                            .rearrange("p n (two c) -> p n two c", c=HD + 1)
                        links.add(nc.vector.reciprocal(rec[:, u, :].rearrange("p (n two) -> p n two", two=2), av[:, :, :, HD]))
                    links.wait()
                    for u in range(2):
                        av = B[u][2][:T, 0:PAIRS * VW].rearrange("p (n c) -> p n c", c=VW)[:, :, 0:2 * (HD + 1)]\
                            .rearrange("p n (two c) -> p n two c", c=HD + 1)
                        dve.wait_ge(y_turned, before(i, u))
                        nc.vector.tensor_tensor(y[:, u, :].rearrange("p (n two c) -> p n two c", two=2, c=HD), av[:, :, :, 0:HD],
                                                rec[:, u, :].rearrange("p (n two) -> p n two", two=2).unsqueeze(3).to_broadcast([T, PAIRS, 2, HD]),
                                                ALU.mult).then_inc(y_ready, 1)
                    for u in range(2):
                        dve.wait_ge(o_done, done(i, u))
                        dve.wait_ge(xbo_ready, done(i, u))
                        nc.vector.tensor_tensor(r[:, u, :], B[u][1][:T, 0:D], x_bo[:, u, :], ALU.add).then_inc(r_ready, 1)
                    dve.wait_ge(r_ready, done(i, 1))
                    for u in range(2):
                        dve.wait_ge(stored[u], 16 * i + 16)
                    norm.steps(dve, links, i, r, x_o, out_ready)
                    links.end()


EXPERTS = 64
TOPK = 6
CAP = 128
SLOTS = EXPERTS * CAP
FE = 176
FS = 352
HC = 88
FAR = 65536.0


def route(nc, NB, x_in, w, slot_rows, xz, slot_ids, slot_weights):
    with ExitStack() as ctx:
        s = Store(nc, ctx, "rt")
        gate = s.sb("gate", [P, KC, EXPERTS])
        gate_b = s.sb("gate_b", [T, EXPERTS])
        ws1 = s.sb("ws1", [P, KC, FS])
        ws3 = s.sb("ws3", [P, KC, FS])
        ws2 = s.sb("ws2", [HC, FS // HC, D])
        ident = s.sb("ident", [P, P])
        earlier = s.sb("earlier", [T, T])
        ones = s.sb("ones", [T, T])
        expert_no = s.sb("expert_no", [T, EXPERTS])
        first_slot = s.sb("first_slot", [T, EXPERTS])
        x_t = s.sb("x_t", [T, 2, D])
        xT = s.sb("xT", [P, 2, KC, T])
        nmax = s.sb("nmax", [T, 2])
        spare = s.sb("spare", [T, 1])
        esum = s.sb("esum", [T, 2])
        rec = s.sb("rec", [T, 2])
        e = s.sb("e", [T, 2, EXPERTS])
        probs = s.sb("probs", [T, 2, EXPERTS])
        biased = s.sb("biased", [T, 2, EXPERTS])
        top = s.sb("top", [T, 2, 8])
        top_i = s.sb("top_i", [T, 2, 8], U32)
        top_f = s.sb("top_f", [T, 2, TOPK])
        hot = s.sb("hot", [T, 2, TOPK, EXPERTS])
        chosen = s.sb("chosen", [T, 2, EXPERTS])
        sofar = s.sb("sofar", [T, 2, EXPERTS])
        over = s.sb("over", [T, 2, EXPERTS])
        slot_e = s.sb("slot_e", [T, 2, EXPERTS])
        picked = s.sb("picked", [T, 2, 2, TOPK, EXPERTS])
        slot_w = s.sb("slot_w", [T, 2, 2, TOPK])
        slot_u = s.sb("slot_u", [T, 2, TOPK], U32)
        gat_u = s.sb("gat_u", [T, 2, TOPK], U32)
        w_keep = s.sb("w_keep", [T, 2, TOPK])
        th = s.sb("th", [HC, 2, 4 * T])
        h1 = s.sb("h1", [HC, 2, 4 * T])
        hT = s.sb("hT", [HC, 2, 4, T])
        x_z = s.sb("x_z", [T, 2, D])
        zero = s.sb("zero", [P, 8, D])
        B = [[s.ps(f"B{b}_{u}", [P, 512]) for b in range(4)] for u in range(2)]

        w_in = s.sem("weights_loaded")
        scatter_over, routes_seen = s.sem("scatter_over"), s.sem("routes_seen")
        zero_set = s.sem("zero_set")
        zeroed = s.sem("slots_zeroed")
        ones_set = s.sem("ones_set")
        x_loaded, scattered, kept, z_stored = s.sems("x_loaded"), s.sems("scattered"), s.sems("routes_kept"), s.sems("z_stored")
        x_turned, xT_ready = s.sem("x_turned"), s.sem("xT_ready")
        gated, up_done, ranked, z_done = s.sem("gated"), s.sem("up_done"), s.sem("ranked"), s.sem("z_done")
        nmax_ready, chosen_ready, h_ready, routes_ready = s.sem("nmax_ready"), s.sem("chosen_ready"), s.sem("h_ready"), s.sem("routes_ready")
        gate_read = s.sem("gate_read")
        th_ready = s.sem("th_ready")
        xz_ready = s.sem("xz_ready")
        vlink = s.sem("dve_link")

        loads = [(gate[:], w["gate_wT"].rearrange("(k p) n -> p k n", p=P)),
                 (gate_b[:], w["gate_b"].to_broadcast([T, EXPERTS])),
                 (ws1[:], w["ws1T"].rearrange("(k p) n -> p k n", p=P)),
                 (ws3[:], w["ws3T"].rearrange("(k p) n -> p k n", p=P)),
                 (ws2[:], w["ws2T"].rearrange("(k p) n -> p k n", p=HC)),
                 (ident[:], w["ident"]), (earlier[:], w["earlier"]),
                 (expert_no[:], w["expert_no"]), (first_slot[:], w["first_slot"])]
        W_ALL = 16 * len(loads)

        with nc.Block() as block:

            @block.sync
            def _(sp):
                for dst, src in loads:
                    sp.dma_start(dst, src).then_inc(w_in, 16)
                sp.wait_ge(zero_set, 1)
                z = slot_rows.rearrange("(n p r) d -> n p r d", p=P, r=8)
                for n in range(SLOTS // (P * 8)):
                    sp.dma_start(z[n], zero[:]).then_inc(zeroed, 16)
                with sp.Fori(0, NB // 2) as i:
                    for u in range(2):
                        sp.wait_ge(xz_ready, before(i, u))
                        sp.wait_ge(scatter_over, before(i, u))
                        sp.dma_start(x_t[:, u, :], x_in[2 * i + u]).then_inc(x_loaded[u], 16)

            @block.tensor
            def _(pe):
                for sem in (x_turned, gated, up_done, ranked, z_done):
                    pe.sem_inc(sem, 2)
                pe.wait_ge(w_in, W_ALL)
                pe.wait_ge(ones_set, 1)
                with pe.Fori(0, NB // 2) as i:
                    for u in range(2):
                        pe.wait_ge(x_loaded[u], 16 * i + 16)
                        for c in range(KC):
                            last = nc.tensor.transpose(B[u][3][:, c * T:(c + 1) * T], x_t[:, u, c * P:(c + 1) * P], ident[:T, :T])
                        last.then_inc(x_turned, 1)
                    for u in range(2):
                        pe.wait_ge(xT_ready, done(i, u))
                        pe.wait_ge(xz_ready, before(i, u))
                        for c in range(KC):
                            last = nc.tensor.matmul(B[u][2][:T, 0:EXPERTS], xT[:, u, c, :], gate[:, c, :],
                                                    start=(c == 0), stop=(c == KC - 1))
                        last.then_inc(gated, 1)
                    for u in range(2):
                        for b, ws in ((0, ws1), (1, ws3)):
                            for m in range(FS // HC):
                                for c in range(KC):
                                    last = nc.tensor.matmul(B[u][b][:HC, m * T:(m + 1) * T], ws[:, c, m * HC:(m + 1) * HC],
                                                            xT[:, u, c, :], start=(c == 0), stop=(c == KC - 1))
                        last.then_inc(up_done, 1)
                    for u in range(2):
                        pe.wait_ge(chosen_ready, done(i, u))
                        nc.tensor.matmul(B[u][3][:T, 256:256 + EXPERTS], earlier[:], chosen[:, u, :], start=True, stop=False)
                        nc.tensor.matmul(B[u][3][:T, 256:256 + EXPERTS], ones[:], sofar[:, u, :], start=False,
                                         stop=True).then_inc(ranked, 1)
                    for u in range(2):
                        pe.wait_ge(h_ready, done(i, u))
                        for m in range(FS // HC):
                            last = nc.tensor.matmul(B[u][2][:T, 256:512], hT[:, u, m, :], ws2[:, m, :], start=(m == 0),
                                                    stop=(m == FS // HC - 1))
                        last.then_inc(z_done, 1)

            @block.scalar
            def _(act):
                for sem in (xT_ready, gate_read, th_ready):
                    act.sem_inc(sem, 2)
                for u in range(2):
                    act.sem_inc(z_stored[u], 16)
                    act.sem_inc(kept[u], 32)
                with act.Fori(0, NB // 2) as i:
                    for u in range(2):
                        act.wait_ge(x_turned, done(i, u))
                        act.wait_ge(up_done, before(i, u))
                        nc.scalar.activation(xT[:, u, :, :].rearrange("p c t -> p (c t)"), B[u][3][:, 0:KC * T],
                                             ACT.Copy).then_inc(xT_ready, 1)
                    for u in range(2):
                        act.wait_ge(nmax_ready, done(i, u))
                        nc.scalar.activation(e[:, u, :], B[u][2][:T, 0:EXPERTS], ACT.Exp, bias=nmax[:, u:u + 1],
                                             accum_out=esum[:, u:u + 1]).then_inc(gate_read, 1)
                    for u in range(2):
                        act.wait_ge(up_done, done(i, u))
                        act.wait_ge(h_ready, before(i, u))
                        nc.scalar.activation(th[:, u, :], B[u][0][:HC, 0:4 * T], ACT.Tanh, scale=0.5).then_inc(th_ready, 1)
                    for u in range(2):
                        act.wait_ge(routes_ready, done(i, u))
                        act.dma_start(slot_ids[2 * i + u], gat_u[:, u, :]).then_inc(kept[u], 16)
                        act.dma_start(slot_weights[2 * i + u], w_keep[:, u, :]).then_inc(kept[u], 16)
                    for u in range(2):
                        act.wait_ge(xz_ready, done(i, u))
                        act.dma_start(xz[2 * i + u], x_z[:, u, :]).then_inc(z_stored[u], 16)
                for u in range(2):
                    act.wait_ge(z_stored[u], 16 * (NB // 2) + 16)
                    act.wait_ge(kept[u], 32 * (NB // 2) + 32)

            @block.gpsimd
            def _(pool):
                pool.sem_inc(scatter_over, 2)
                nc.gpsimd.memset(ones[:], 1.0).then_inc(ones_set, 1)
                nc.gpsimd.memset(zero[:], 0.0).then_inc(zero_set, 1)
                pool.wait_ge(zeroed, 16 * (SLOTS // (P * 8)))
                with pool.Fori(0, NB // 2) as i:
                    for u in range(2):
                        pool.wait_ge(routes_ready, done(i, u))
                        pool.sem_inc(routes_seen, 1)
                        for k in range(TOPK):
                            nc.gpsimd.indirect_dma_start(slot_rows, bass.IndirectOffsetOnAxis(slot_u[:, u, k:k + 1], 0),
                                                         x_t[:, u, :], None, bounds_check=SLOTS - 1,
                                                         oob_is_err=False).then_inc(scattered[u], 16)
                    for u in range(2):
                        pool.wait_ge(scattered[u], 16 * TOPK * i + 16 * TOPK)
                        pool.sem_inc(scatter_over, 1)

            @block.vector
            def _(dve):
                for sem in (nmax_ready, chosen_ready, h_ready, routes_ready, xz_ready):
                    dve.sem_inc(sem, 2)
                nc.vector.memset(sofar[:], 0.0)
                dve.wait_ge(w_in, W_ALL)
                with dve.Fori(0, NB // 2) as i:
                    links = Links(dve, vlink, i, 30)
                    for u in range(2):
                        dve.wait_ge(gated, done(i, u))
                        nc.vector.tensor_reduce(nmax[:, u:u + 1], B[u][2][:T, 0:EXPERTS], axis=AXIS_X, op=ALU.max,
                                                negate=True).then_inc(nmax_ready, 1)
                    for u in range(2):
                        dve.wait_ge(gate_read, done(i, u))
                        links.add(nc.vector.reciprocal(rec[:, u:u + 1], esum[:, u:u + 1]))
                    links.wait()
                    for u in range(2):
                        links.add(nc.vector.tensor_scalar(probs[:, u, :], e[:, u, :], rec[:, u:u + 1], None, ALU.mult))
                    links.wait()
                    for u in range(2):
                        links.add(nc.vector.tensor_tensor(biased[:, u, :], probs[:, u, :], gate_b[:], ALU.add))
                    links.wait()
                    nc.vector.memset(spare[:], 0.0)
                    for u in range(2):
                        links.add(nc.vector.max(top[:, u, :], biased[:, u, :]))
                    links.wait()
                    nc.vector.memset(spare[:], 0.0)
                    for u in range(2):
                        links.add(nc.vector.max_index(top_i[:, u, :], top[:, u, :], biased[:, u, :]))
                    links.wait()
                    for u in range(2):
                        links.add(nc.vector.tensor_copy(top_f[:, u, :], top_i[:, u, 0:TOPK]))
                    links.wait()
                    for u in range(2):
                        links.add(nc.vector.tensor_tensor(hot[:, u, :, :], expert_no[:].unsqueeze(1).to_broadcast([T, TOPK, EXPERTS]),
                                                          top_f[:, u, :].unsqueeze(2).to_broadcast([T, TOPK, EXPERTS]), ALU.is_equal))
                    links.wait()
                    for u in range(2):
                        dve.wait_ge(ranked, before(i, u))
                        nc.vector.tensor_reduce(chosen[:, u, :], hot[:, u, :, :].rearrange("p k e -> p e k"), axis=AXIS_X,
                                                op=ALU.add).then_inc(chosen_ready, 1)
                        if u == 0:
                            dve.wait_ge(chosen_ready, done(i, 0))
                            dve.wait_ge(ranked, before(i, 1))
                            links.add(nc.vector.tensor_tensor(sofar[:, 1, :], sofar[:, 0, :], chosen[:, 0, :], ALU.add))
                            links.wait()
                    for u in range(2):
                        dve.wait_ge(th_ready, done(i, u))
                        links.add(nc.vector.scalar_tensor_tensor(h1[:, u, :], th[:, u, :], 1.0, B[u][0][:HC, 0:4 * T],
                                                                 ALU.add, ALU.mult))
                    links.wait()
                    for u in range(2):
                        dve.wait_ge(z_done, before(i, u))
                        nc.vector.scalar_tensor_tensor(hT[:, u, :, :].rearrange("p m t -> p (m t)"), h1[:, u, :], 0.5,
                                                       B[u][1][:HC, 0:4 * T], ALU.mult, ALU.mult).then_inc(h_ready, 1)
                    for u in range(2):
                        dve.wait_ge(ranked, done(i, u))
                        rank = B[u][3][:T, 256:256 + EXPERTS]
                        links.add(nc.vector.tensor_scalar(over[:, u, :], rank, float(CAP), FAR, ALU.is_ge, ALU.mult))
                        links.add(nc.vector.tensor_tensor(slot_e[:, u, :], rank, first_slot[:], ALU.add))
                    links.add(nc.vector.tensor_tensor(sofar[:, 0, :], sofar[:, 1, :], chosen[:, 1, :], ALU.add))
                    links.wait()
                    for u in range(2):
                        links.add(nc.vector.tensor_tensor(slot_e[:, u, :], slot_e[:, u, :], over[:, u, :], ALU.add))
                    links.wait()
                    for u in range(2):
                        for k, what in ((0, slot_e), (1, probs)):
                            links.add(nc.vector.tensor_tensor(picked[:, u, k, :, :], hot[:, u, :, :],
                                                              what[:, u, :].unsqueeze(1).to_broadcast([T, TOPK, EXPERTS]), ALU.mult))
                    links.wait()
                    for u in range(2):
                        links.add(nc.vector.tensor_reduce(slot_w[:, u, :, :], picked[:, u, :, :, :], axis=AXIS_X, op=ALU.add))
                    links.wait()
                    for u in range(2):
                        dve.wait_ge(scatter_over, before(i, u))
                        dve.wait_ge(kept[u], 32 * i + 32)
                        nc.vector.tensor_copy(slot_u[:, u, :], slot_w[:, u, 0, :])
                        nc.vector.tensor_scalar(gat_u[:, u, :], slot_w[:, u, 0, :], float(SLOTS - 1), None, ALU.min)
                        nc.vector.scalar_tensor_tensor(w_keep[:, u, :], slot_w[:, u, 0, :], float(SLOTS), slot_w[:, u, 1, :],
                                                       ALU.is_lt, ALU.mult).then_inc(routes_ready, 1)
                    for u in range(2):
                        dve.wait_ge(z_done, done(i, u))
                        dve.wait_ge(z_stored[u], 16 * i + 16)
                        nc.vector.tensor_tensor(x_z[:, u, :], B[u][2][:T, 256:512], x_t[:, u, :], ALU.add).then_inc(xz_ready, 1)
                    links.end()


def experts(nc, w, slot_rows, slot_out):
    with ExitStack() as ctx:
        s = Store(nc, ctx, "ex")
        ident = s.sb("ident", [P, P])
        w1 = s.sb("w1", [P, 2, KC, FE])
        w3 = s.sb("w3", [P, 2, KC, FE])
        w2 = s.sb("w2", [HC, 2, 2, D])
        x_t = s.sb("x_t", [P, 2, D])
        xT = s.sb("xT", [P, 2, KC, P])
        th = s.sb("th", [HC, 2, 2 * P])
        h1 = s.sb("h1", [HC, 2, 2 * P])
        hT = s.sb("hT", [HC, 2, 2, P])
        y = s.sb("y", [P, 2, D])
        B = [[s.ps(f"B{b}_{u}", [P, 512]) for b in range(4)] for u in range(2)]

        ident_in = s.sem("ident_loaded")
        up_loaded, down_loaded, x_loaded, stored = s.sems("up_loaded"), s.sems("down_loaded"), s.sems("x_loaded"), s.sems("stored")
        x_turned, xT_ready, up_done, y_done = s.sem("x_turned"), s.sem("xT_ready"), s.sem("up_done"), s.sem("y_done")
        th_ready, h1_ready, h_ready, y_ready = s.sem("th_ready"), s.sem("h1_ready"), s.sem("h_ready"), s.sem("y_ready")
        xs = slot_rows.rearrange("(e p) d -> e p d", p=P)
        ys = slot_out.rearrange("(e p) d -> e p d", p=P)

        with nc.Block() as block:

            @block.sync
            def _(sp):
                sp.dma_start(ident[:], w["ident"]).then_inc(ident_in, 16)
                with sp.Fori(0, EXPERTS // 2) as i:
                    for u in range(2):
                        sp.wait_ge(x_turned, before(i, u))
                        sp.dma_start(x_t[:, u, :], xs[2 * i + u]).then_inc(x_loaded[u], 16)
                        sp.wait_ge(up_done, before(i, u))
                        sp.dma_start(w1[:, u], w["w1T"][2 * i + u].rearrange("(k p) n -> p k n", p=P)).then_inc(up_loaded[u], 16)
                        sp.dma_start(w3[:, u], w["w3T"][2 * i + u].rearrange("(k p) n -> p k n", p=P)).then_inc(up_loaded[u], 16)
                        sp.wait_ge(y_done, before(i, u))
                        sp.dma_start(w2[:, u], w["w2T"][2 * i + u].rearrange("(k p) n -> p k n", p=HC)).then_inc(down_loaded[u], 16)

            @block.tensor
            def _(pe):
                for sem in (x_turned, up_done, y_done):
                    pe.sem_inc(sem, 2)
                pe.wait_ge(ident_in, 16)
                with pe.Fori(0, EXPERTS // 2) as i:
                    for u in range(2):
                        pe.wait_ge(x_loaded[u], 16 * i + 16)
                        pe.wait_ge(xT_ready, before(i, u))
                        for c in range(KC):
                            last = nc.tensor.transpose(B[u][3][:, c * P:(c + 1) * P], x_t[:, u, c * P:(c + 1) * P], ident[:])
                        last.then_inc(x_turned, 1)
                    for u in range(2):
                        pe.wait_ge(up_loaded[u], 32 * i + 32)
                        pe.wait_ge(xT_ready, done(i, u))
                        pe.wait_ge(h_ready, before(i, u))
                        for b, wu in ((0, w1), (1, w3)):
                            for m in range(2):
                                for c in range(KC):
                                    last = nc.tensor.matmul(B[u][b][:HC, m * P:(m + 1) * P], wu[:, u, c, m * HC:(m + 1) * HC],
                                                            xT[:, u, c, :], start=(c == 0), stop=(c == KC - 1))
                        last.then_inc(up_done, 1)
                    for u in range(2):
                        pe.wait_ge(down_loaded[u], 16 * i + 16)
                        pe.wait_ge(h_ready, done(i, u))
                        pe.wait_ge(y_ready, before(i, u))
                        for m in range(2):
                            last = nc.tensor.matmul(B[u][2][:, 0:D], hT[:, u, m, :], w2[:, u, m, :], start=(m == 0), stop=(m == 1))
                        last.then_inc(y_done, 1)

            @block.scalar
            def _(act):
                for sem in (xT_ready, th_ready, y_ready):
                    act.sem_inc(sem, 2)
                for u in range(2):
                    act.sem_inc(stored[u], 16)
                with act.Fori(0, EXPERTS // 2) as i:
                    for u in range(2):
                        act.wait_ge(x_turned, done(i, u))
                        act.wait_ge(up_done, before(i, u))
                        nc.scalar.activation(xT[:, u].rearrange("p c t -> p (c t)"), B[u][3][:, 0:KC * P], ACT.Copy).then_inc(xT_ready, 1)
                    for u in range(2):
                        act.wait_ge(up_done, done(i, u))
                        act.wait_ge(h1_ready, before(i, u))
                        nc.scalar.activation(th[:, u, :], B[u][0][:HC, 0:2 * P], ACT.Tanh, scale=0.5).then_inc(th_ready, 1)
                    for u in range(2):
                        act.wait_ge(y_done, done(i, u))
                        act.wait_ge(stored[u], 16 * i + 16)
                        nc.scalar.activation(y[:, u, :], B[u][2][:, 0:D], ACT.Copy).then_inc(y_ready, 1)
                    for u in range(2):
                        act.wait_ge(y_ready, done(i, u))
                        act.dma_start(ys[2 * i + u], y[:, u, :]).then_inc(stored[u], 16)
                for u in range(2):
                    act.wait_ge(stored[u], 16 * (EXPERTS // 2) + 16)

            @block.vector
            def _(dve):
                for sem in (h1_ready, h_ready):
                    dve.sem_inc(sem, 2)
                with dve.Fori(0, EXPERTS // 2) as i:
                    for u in range(2):
                        dve.wait_ge(th_ready, done(i, u))
                        nc.vector.scalar_tensor_tensor(h1[:, u, :], th[:, u, :], 1.0, B[u][0][:HC, 0:2 * P],
                                                       ALU.add, ALU.mult).then_inc(h1_ready, 1)
                    for u in range(2):
                        dve.wait_ge(h1_ready, done(i, u))
                        dve.wait_ge(y_done, before(i, u))
                        nc.vector.scalar_tensor_tensor(hT[:, u, :, :].rearrange("p m t -> p (m t)"), h1[:, u, :], 0.5,
                                                       B[u][1][:HC, 0:2 * P], ALU.mult, ALU.mult).then_inc(h_ready, 1)


def linear_attention(nc, NB, xz, slot_out, slot_ids, slot_weights, x_out, w, n_out=None):
    EPS = 1e-6
    with ExitStack() as ctx:
        s = Store(nc, ctx, "la")
        wqk = s.sb("wqk", [P, KC, 2 * D])
        wv = s.sb("wv", [P, KC, D])
        wo = s.sb("wo", [P, KC, D])
        bqk = s.sb("bqk", [T, 2 * D])
        bv = s.sb("bv", [T, D])
        bo = s.sb("bo", [T, D])
        ident = s.sb("ident", [P, P])
        ones = s.sb("ones", [T, T])
        block_mask = s.sb("block_mask", [P, P])
        ids = s.sb("ids", [T, 2, TOPK], U32)
        wts = s.sb("wts", [T, 2, TOPK])
        rows = s.sb("rows", [T, 2, TOPK, D])
        acc = s.sb("acc", [T, 2, 2, D])
        x_3 = s.sb("x_3", [T, 2, D])
        x_bo = s.sb("x_bo", [T, 2, D])
        xT = s.sb("xT", [P, 2, KC, T])
        qk = s.sb("qk", [T, 2, 2, D])
        qke = s.sb("qke", [T, 2, 2, D])
        t1 = s.sb("t1", [T, 2, 2, D])
        v = s.sb("v", [T, 2, D])
        flow = s.sb("flow", [T, 2, 2 * HEADS])
        kept = s.sb("kept", [T, 2, 2 * HEADS])
        comp = s.sb("comp", [T, 2, HEADS])
        ecs = s.sb("ecs", [T, 2, HEADS])
        alloc = s.sb("alloc", [T, 2, HEADS])
        qT = s.sb("qT", [P, 2, KC, T])
        kv = s.sb("kv", [P, 2, KC, P])
        y = s.sb("y", [T, 2, D])
        yT = s.sb("yT", [P, 2, KC, T])
        r = s.sb("r", [T, 2, D])
        x_o = s.sb("x_o", [T, 2, D])
        norm3 = Norm(s, nc, tag="3")
        norm = Norm(s, nc)
        B = [[s.ps(f"B{b}_{u}", [P, 512]) for b in range(4)] for u in range(2)]

        w_in, ones_set = s.sem("weights_loaded"), s.sem("ones_set")
        ids_loaded, wts_loaded, xz_loaded, gathered, stored = (s.sems(n) for n in (
            "ids_loaded", "wts_loaded", "xz_loaded", "gathered", "stored"))
        names = ["x3_ready", "x_turned", "xT_ready", "qkv_done", "biased", "th_ready", "qk_ready", "summed",
                 "flows_ready", "flowed", "kept_ready", "ecs_ready", "esummed", "v_ready", "kv_done", "kv_ready", "q_turned",
                 "qT_ready", "attended", "y_ready", "y_turned", "yT_ready", "o_done", "r_ready", "out_ready", "xbo_ready"]
        (x3_ready, x_turned, xT_ready, qkv_done, biased, th_ready, qk_ready, summed, flows_ready, flowed, kept_ready,
         ecs_ready, esummed, v_ready, kv_done, kv_ready, q_turned, qT_ready, attended, y_ready, y_turned, yT_ready, o_done,
         r_ready, out_ready, xbo_ready) = (s.sem(n) for n in names)
        gather_over, ids_seen = s.sem("gather_over"), s.sem("ids_seen")
        vlink = s.sem("dve_link")

        kp = "(k p) n -> p k n"
        loads = [(wqk[:], w["L1_wqkT"].rearrange(kp, p=P)), (wv[:], w["L1_wvT"].rearrange(kp, p=P)),
                 (wo[:], w["L1_woT"].rearrange(kp, p=P)), (bqk[:], w["L1_bqk"].to_broadcast([T, 2 * D])),
                 (bv[:], w["L1_bv"].to_broadcast([T, D])), (bo[:], w["L1_bo"].to_broadcast([T, D])),
                 (ident[:], w["ident"]), (block_mask[:], w["block_mask"])]
        W_ALL = 16 * len(loads)

        with nc.Block() as block:

            @block.sync
            def _(sp):
                for dst, src in loads:
                    sp.dma_start(dst, src).then_inc(w_in, 16)
                with sp.Fori(0, NB // 2) as i:
                    for u in range(2):
                        sp.wait_ge(gather_over, before(i, u))
                        sp.dma_start(ids[:, u, :], slot_ids[2 * i + u]).then_inc(ids_loaded[u], 16)
                        sp.wait_ge(x3_ready, before(i, u))
                        sp.dma_start(wts[:, u, :], slot_weights[2 * i + u]).then_inc(wts_loaded[u], 16)
                        sp.dma_start(acc[:, u, 0, :], xz[2 * i + u]).then_inc(xz_loaded[u], 16)

            @block.gpsimd
            def _(pool):
                pool.sem_inc(gather_over, 2)
                pool.sem_inc(xbo_ready, 2)
                nc.gpsimd.memset(ones[:], 1.0).then_inc(ones_set, 1)
                norm3.set_power(pool)
                norm.set_power(pool)
                pool.wait_ge(w_in, W_ALL)
                with pool.Fori(0, NB // 2) as i:
                    for u in range(2):
                        pool.wait_ge(ids_loaded[u], 16 * i + 16)
                        pool.wait_ge(x3_ready, before(i, u))
                        pool.sem_inc(ids_seen, 1)
                        for k in range(TOPK):
                            nc.gpsimd.indirect_dma_start(rows[:, u, k, :], None, slot_out,
                                                         bass.IndirectOffsetOnAxis(ids[:, u, k:k + 1], 0)).then_inc(gathered[u], 16)
                    for u in range(2):
                        pool.wait_ge(gathered[u], 16 * TOPK * i + 16 * TOPK)
                        pool.sem_inc(gather_over, 1)
                    norm3.raise_power(pool, i)
                    for u in range(2):
                        pool.wait_ge(x3_ready, done(i, u))
                        pool.wait_ge(r_ready, before(i, u))
                        nc.gpsimd.tensor_tensor(x_bo[:, u, :], x_3[:, u, :], bo[:], ALU.add).then_inc(xbo_ready, 1)
                    norm.raise_power(pool, i)

            @block.tensor
            def _(pe):
                for sem in (x_turned, qkv_done, summed, flowed, esummed, kv_done, q_turned, attended, y_turned, o_done):
                    pe.sem_inc(sem, 2)
                pe.wait_ge(w_in, W_ALL)
                pe.wait_ge(ones_set, 1)
                with pe.Fori(0, NB // 2) as i:
                    for u in range(2):
                        pe.wait_ge(x3_ready, done(i, u))
                        pe.wait_ge(yT_ready, before(i, u))
                        for c in range(KC):
                            last = nc.tensor.transpose(B[u][3][:, c * T:(c + 1) * T], x_3[:, u, c * P:(c + 1) * P], ident[:T, :T])
                        last.then_inc(x_turned, 1)
                    for u in range(2):
                        pe.wait_ge(xT_ready, done(i, u))
                        pe.wait_ge(r_ready, before(i, u))
                        for c in range(KC):
                            nc.tensor.matmul(B[u][0][:T, :], xT[:, u, c, :], wqk[:, c, :], start=(c == 0), stop=(c == KC - 1))
                        for c in range(KC):
                            last = nc.tensor.matmul(B[u][1][:T, 0:D], xT[:, u, c, :], wv[:, c, :], start=(c == 0), stop=(c == KC - 1))
                        last.then_inc(qkv_done, 1)
                    for u in range(2):
                        pe.wait_ge(qk_ready, done(i, u))
                        nc.tensor.matmul(B[u][2][:T, :], ones[:], qk[:, u].rearrange("p a d -> p (a d)"), start=True,
                                         stop=True).then_inc(summed, 1)
                    for u in range(2):
                        for c in range(KC):
                            last = nc.tensor.transpose(B[u][3][:, c * T:(c + 1) * T], qk[:, u, 0, c * P:(c + 1) * P], ident[:T, :T])
                        last.then_inc(q_turned, 1)
                    for u in range(2):
                        pe.wait_ge(flows_ready, done(i, u))
                        nc.tensor.matmul(B[u][1][:T, :], ones[:], t1[:, u].rearrange("p a d -> p (a d)"), start=True,
                                         stop=True).then_inc(flowed, 1)
                    for u in range(2):
                        pe.wait_ge(ecs_ready, done(i, u))
                        nc.tensor.matmul(B[u][2][:T, 0:HEADS], ones[:], ecs[:, u, :], start=True, stop=True).then_inc(esummed, 1)
                    for u in range(2):
                        pe.wait_ge(v_ready, done(i, u))
                        for c in range(KC):
                            last = nc.tensor.matmul(B[u][0][:, c * P:(c + 1) * P], qk[:, u, 1, c * P:(c + 1) * P],
                                                    v[:, u, c * P:(c + 1) * P], start=True, stop=True)
                        last.then_inc(kv_done, 1)
                    for u in range(2):
                        pe.wait_ge(kv_ready, done(i, u))
                        pe.wait_ge(qT_ready, done(i, u))
                        for c in range(KC):
                            last = nc.tensor.matmul(B[u][2][:T, c * P:(c + 1) * P], qT[:, u, c, :], kv[:, u, c, :], start=True, stop=True)
                        last.then_inc(attended, 1)
                    for u in range(2):
                        pe.wait_ge(y_ready, done(i, u))
                        for c in range(KC):
                            last = nc.tensor.transpose(B[u][3][:, c * T:(c + 1) * T], y[:, u, c * P:(c + 1) * P], ident[:T, :T])
                        last.then_inc(y_turned, 1)
                    for u in range(2):
                        pe.wait_ge(yT_ready, done(i, u))
                        for c in range(KC):
                            last = nc.tensor.matmul(B[u][1][:T, 0:D], yT[:, u, c, :], wo[:, c, :], start=(c == 0), stop=(c == KC - 1))
                        last.then_inc(o_done, 1)

            @block.scalar
            def _(act):
                for sem in (xT_ready, th_ready, qT_ready, ecs_ready, yT_ready):
                    act.sem_inc(sem, 2)
                for u in range(2):
                    act.sem_inc(stored[u], 16)
                with act.Fori(0, NB // 2) as i:
                    for u in range(2):
                        act.wait_ge(x_turned, done(i, u))
                        nc.scalar.activation(xT[:, u].rearrange("p c t -> p (c t)"), B[u][3][:, 0:KC * T], ACT.Copy).then_inc(xT_ready, 1)
                    for u in range(2):
                        act.wait_ge(biased, done(i, u))
                        nc.scalar.activation(t1[:, u].rearrange("p a d -> p (a d)"), qke[:, u].rearrange("p a d -> p (a d)"),
                                             ACT.Tanh, scale=0.5).then_inc(th_ready, 1)
                    for u in range(2):
                        act.wait_ge(q_turned, done(i, u))
                        nc.scalar.activation(qT[:, u].rearrange("p c t -> p (c t)"), B[u][3][:, 0:KC * T], ACT.Copy).then_inc(qT_ready, 1)
                    for u in range(2):
                        act.wait_ge(kept_ready, done(i, u))
                        nc.scalar.activation(alloc[:, u, :], kept[:, u, 0:HEADS], ACT.Tanh, scale=0.5)
                        nc.scalar.activation(ecs[:, u, :], kept[:, u, HEADS:2 * HEADS], ACT.Exp).then_inc(ecs_ready, 1)
                    for u in range(2):
                        act.wait_ge(y_turned, done(i, u))
                        nc.scalar.activation(yT[:, u].rearrange("p c t -> p (c t)"), B[u][3][:, 0:KC * T], ACT.Copy).then_inc(yT_ready, 1)
                    for u in range(2):
                        act.wait_ge(out_ready, done(i, u))
                        act.dma_start(x_out[2 * i + u], x_o[:, u, :]).then_inc(stored[u], 16)
                for u in range(2):
                    act.wait_ge(stored[u], 16 * (NB // 2) + 16)

            @block.vector
            def _(dve):
                for sem in (x3_ready, biased, qk_ready, flows_ready, kept_ready, v_ready, kv_ready, y_ready, r_ready, out_ready):
                    dve.sem_inc(sem, 2)
                dve.wait_ge(w_in, W_ALL)

                def heads(ap):
                    return ap.rearrange("p a (h d) -> p (a h) d", d=DH)

                with dve.Fori(0, NB // 2) as i:
                    links = Links(dve, vlink, i, 44)
                    for u in range(2):
                        dve.wait_ge(gather_over, done(i, u))
                        dve.wait_ge(wts_loaded[u], 16 * i + 16)
                        dve.wait_ge(xz_loaded[u], 16 * i + 16)
                    for k in range(TOPK):
                        for u in range(2):
                            add = nc.vector.scalar_tensor_tensor(acc[:, u, (k + 1) % 2, :], rows[:, u, k, :], wts[:, u, k:k + 1],
                                                                 acc[:, u, k % 2, :], ALU.mult, ALU.add)
                            links.add(add)
                        links.wait()
                    norm3.steps(dve, links, i, acc[:, :, 0, :], x_3, x3_ready)
                    for u in range(2):
                        dve.wait_ge(qkv_done, done(i, u))
                        nc.vector.tensor_tensor(v[:, u, :], B[u][1][:T, 0:D], bv[:], ALU.add)
                        nc.vector.tensor_tensor(qke[:, u].rearrange("p a d -> p (a d)"), B[u][0][:T, :], bqk[:], ALU.add).then_inc(biased, 1)
                    for u in range(2):
                        dve.wait_ge(th_ready, done(i, u))
                        nc.vector.tensor_scalar(qk[:, u].rearrange("p a d -> p (a d)"), t1[:, u].rearrange("p a d -> p (a d)"),
                                                0.5, 0.5, ALU.mult, ALU.add).then_inc(qk_ready, 1)
                    for u in range(2):
                        dve.wait_ge(qk_ready, done(i, u))
                        links.add(nc.vector.tensor_scalar(qke[:, u].rearrange("p a d -> p (a d)"), qk[:, u].rearrange("p a d -> p (a d)"),
                                                          EPS, None, ALU.add))
                    links.wait()

                    def against_sums(sums, signal):
                        for u in range(2):
                            dve.wait_ge(signal, done(i, u))
                            for a in range(2):
                                links.add(nc.vector.scalar_tensor_tensor(t1[:, u, a, :], sums[u][:T, (1 - a) * D:(2 - a) * D], EPS,
                                                                         qke[:, u, a, :], ALU.add, ALU.mult))
                        links.wait()

                    against_sums([B[0][2], B[1][2]], summed)
                    for u in range(2):
                        links.add(nc.vector.tensor_reduce(flow[:, u, :], heads(t1[:, u]), axis=AXIS_X, op=ALU.add))
                    links.wait()
                    for u in range(2):
                        links.add(nc.vector.reciprocal(flow[:, u, :], flow[:, u, :]))
                    links.wait()
                    for u in range(2):
                        nc.vector.tensor_tensor(heads(t1[:, u]), heads(qk[:, u]), flow[:, u, :].unsqueeze(2).to_broadcast([T, 2 * HEADS, DH]),
                                                ALU.mult).then_inc(flows_ready, 1)
                    against_sums([B[0][1], B[1][1]], flowed)
                    for u in range(2):
                        links.add(nc.vector.tensor_reduce(kept[:, u, :], heads(t1[:, u]), axis=AXIS_X, op=ALU.add))
                    links.wait()
                    for u in range(2):
                        nc.vector.tensor_scalar(kept[:, u, HEADS:2 * HEADS], kept[:, u, HEADS:2 * HEADS], -1.0, 1.0,
                                                ALU.max, ALU.min).then_inc(kept_ready, 1)
                    for u in range(2):
                        dve.wait_ge(esummed, done(i, u))
                        links.add(nc.vector.reciprocal(comp[:, u, :], B[u][2][:T, 0:HEADS]))
                        links.add(nc.vector.tensor_scalar(alloc[:, u, :], alloc[:, u, :], 0.5, 0.5, ALU.mult, ALU.add))
                    links.wait()
                    for u in range(2):
                        links.add(nc.vector.tensor_tensor(comp[:, u, :], comp[:, u, :], ecs[:, u, :], ALU.mult))
                        links.add(nc.vector.tensor_tensor(alloc[:, u, :], alloc[:, u, :], flow[:, u, 0:HEADS], ALU.mult))
                    links.wait()
                    for u in range(2):
                        vh = v[:, u, :].rearrange("p (h d) -> p h d", d=DH)
                        nc.vector.scalar_tensor_tensor(vh, vh, float(T), comp[:, u, :].unsqueeze(2).to_broadcast([T, HEADS, DH]),
                                                       ALU.mult, ALU.mult).then_inc(v_ready, 1)
                    for u in range(2):
                        dve.wait_ge(kv_done, done(i, u))
                        nc.vector.tensor_tensor(kv[:, u], B[u][0][:, 0:KC * P].rearrange("p (c n) -> p c n", n=P),
                                                block_mask[:].unsqueeze(1).to_broadcast([P, KC, P]), ALU.mult).then_inc(kv_ready, 1)
                    for u in range(2):
                        dve.wait_ge(attended, done(i, u))
                        nc.vector.tensor_tensor(y[:, u, :].rearrange("p (h d) -> p h d", d=DH),
                                                B[u][2][:T, 0:D].rearrange("p (h d) -> p h d", d=DH),
                                                alloc[:, u, :].unsqueeze(2).to_broadcast([T, HEADS, DH]), ALU.mult).then_inc(y_ready, 1)
                    for u in range(2):
                        dve.wait_ge(o_done, done(i, u))
                        dve.wait_ge(xbo_ready, done(i, u))
                        nc.vector.tensor_tensor(r[:, u, :], B[u][1][:T, 0:D], x_bo[:, u, :], ALU.add).then_inc(r_ready, 1)
                    dve.wait_ge(r_ready, done(i, 1))
                    for u in range(2):
                        dve.wait_ge(stored[u], 16 * i + 16)
                    norm.steps(dve, links, i, r, x_o, out_ready)
                    links.end()


def cross_attention(nc, NB, x_in, x_out, w, src_len):
    NCH = 3
    STEP = (src_len - 1) // NCH
    ROWS = STEP + 1
    assert STEP * NCH + 1 == src_len and ROWS <= P
    G = GROUPS
    with ExitStack() as ctx:
        s = Store(nc, ctx, "xa")
        wq = s.sb("wq", [P, 2, KC, D])
        wk = s.sb("wk", [P, 2, KC, D])
        wv = s.sb("wv", [P, KC, D])
        wo = s.sb("wo", [P, KC, D])
        wg = s.sb("wg", [P, KC, D])
        bo = s.sb("bo", [T, D])
        bg = s.sb("bg", [T, D])
        gamma = s.sb("gamma", [P, KC])
        beta = s.sb("beta", [P, KC])
        cosT = s.sb("cosT", [P, src_len])
        sinT = s.sb("sinT", [P, src_len])
        bias = s.sb("bias", [ROWS, NCH, T])
        head_mask = s.sb("head_mask", [P, 8])
        head_mask2 = s.sb("head_mask2", [P, 4])
        ident = s.sb("ident", [P, P])
        neg1 = s.sb("neg1", [T, ROWS], F32R)
        x_t = s.sb("x_t", [T, 2, D])
        x_res = s.sb("x_res", [T, 2, D])
        x_2 = s.sb("x_2", [T, 2, D])
        x_n = s.sb("x_n", [T, 2, D])
        xT = s.sb("xT", [P, 2, KC, T])
        c_t = s.sb("c_t", [ROWS, 2, NCH, D])
        c_n = s.sb("c_n", [ROWS, 2, NCH, D])
        cT = s.sb("cT", [P, 2, KC, src_len])
        k_c = s.sb("k_c", [P, 2, KC, src_len])
        k_s = s.sb("k_s", [P, 2, KC, src_len])
        kT = s.sb("kT", [P, 2, KC, src_len])
        q_c = s.sb("q_c", [P, 2, KC, T])
        q_s = s.sb("q_s", [P, 2, KC, T])
        q_bd = s.sb("q_bd", [P, 2, KC, 8, T])
        v1 = s.sb("v1", [ROWS, 2, NCH, G, P])
        mx = s.sb("mx", [ROWS, 2, GW])
        nmax = s.sb("nmax", [T, 2, HPG])
        dmax = s.sb("dmax", [T, 2, HPG, T], F32R)
        prob = s.sb("prob", [ROWS, 2, NCH, GW])
        own = s.sb("own", [P, 2, GW])
        nd = s.sb("nd", [P, 2, T])
        rec = s.sb("rec", [64, 2, T])
        yT = s.sb("yT", [P, 2, KC, T])
        att = s.sb("att", [T, 2, D])
        aT = s.sb("aT", [P, 2, KC, T])
        gl = s.sb("gl", [T, 2, D])
        dif = s.sb("dif", [T, 2, D])
        r = s.sb("r", [T, 2, D])
        x_o = s.sb("x_o", [T, 2, D])
        norm_q, norm_c, norm = Norm(s, nc, tag="q"), Norm(s, nc, ROWS, "c", lots=2 * NCH), Norm(s, nc)
        S = [s.ps(f"S{u}", [P, 3, 512]) for u in range(2)]
        W = [s.ps(f"W{u}", [P, 512]) for u in range(2)]

        w_in, const_ready = s.sem("weights_loaded"), s.sem("const_ready")
        x_loaded, res_loaded, c_loaded, stored = (s.sems(n) for n in ("x_loaded", "res_loaded", "c_loaded", "stored"))
        xn_ready, cn_ready = s.sem("xn_ready"), s.sem("cn_ready")
        x_turned, c_turned = s.sem("x_turned"), s.sem("c_turned")
        xT_ready, cT_ready = s.sem("xT_ready"), s.sem("cT_ready")
        k_done, v_done, q_done = s.sem("k_done"), s.sem("v_done"), s.sem("q_done")
        k_rot, q_rot = s.sem("k_rot"), s.sem("q_rot")
        k_ready, q_sum, qbd_ready = s.sem("k_ready"), s.sem("q_sum"), s.sem("qbd_ready")
        v_ready = s.sem("v_ready")
        scored, mx_turned, shifted, av_done = (s.sem(n) for n in ("scored", "mx_turned", "shifted", "av_done"))
        mx_ready, max_ready, less_ready, own_ready, yT_ready = (s.sem(n) for n in (
            "mx_ready", "max_ready", "less_ready", "own_ready", "yT_ready"))
        prob_ready = s.sem("prob_ready")
        o_done, a_turned, g_done = s.sem("o_done"), s.sem("a_turned"), s.sem("g_done")
        att_ready, gl_ready, r_ready, out_ready = (s.sem(n) for n in ("att_ready", "gl_ready", "r_ready", "out_ready"))
        aT_ready, th_ready = s.sem("aT_ready"), s.sem("th_ready")
        x2_ready = s.sem("x2_ready")
        vlink = s.sem("dve_link")

        kp = "(k p) n -> p k n"
        wqkv = w["L1x_wqkvT"].rearrange(kp, p=P)
        loads = [(wq[:, 0], wqkv[:, :, 0:D]), (wk[:, 0], wqkv[:, :, D:2 * D]), (wv[:], wqkv[:, :, 2 * D:3 * D]),
                 (wo[:], w["L1x_woT"].rearrange(kp, p=P)), (wg[:], w["L1x_wgT"].rearrange(kp, p=P)),
                 (bo[:], w["L1x_bo"].to_broadcast([T, D])), (bg[:], w["L1x_bg"].to_broadcast([T, D])),
                 (gamma[:], w["L1x_gamma"]), (beta[:], w["L1x_beta"]), (cosT[:], w["cos_xa"]), (sinT[:], w["sin_xa"]),
                 (bias[:], w["bias_xa"]), (head_mask[:], w["head_mask"]), (head_mask2[:], w["head_mask2"]), (ident[:], w["ident"])]
        W_ALL = 16 * len(loads)

        with nc.Block() as block:

            @block.sync
            def _(sp):
                for dst, src in loads:
                    sp.dma_start(dst, src).then_inc(w_in, 16)
                with sp.Fori(0, NB // 2) as i:
                    for u in range(2):
                        sp.wait_ge(xn_ready, before(i, u))
                        sp.dma_start(x_t[:, u, :], x_in[2 * i + u]).then_inc(x_loaded[u], 16)
                        sp.wait_ge(cn_ready, before(i, u, NCH - 1, NCH))
                        for c in range(NCH):
                            sp.dma_start(c_t[:, u, c, :], w["ctx"][2 * i + u, c * STEP:c * STEP + ROWS, :]).then_inc(c_loaded[u], 16)
                    for u in range(2):
                        sp.wait_ge(r_ready, before(i, u))
                        sp.dma_start(x_res[:, u, :], x_in[2 * i + u]).then_inc(res_loaded[u], 16)

            @block.tensor
            def _(pe):
                for sem, steps in ((x_turned, 1), (c_turned, 1), (k_done, 1), (v_done, 1), (q_done, 1), (scored, G),
                                   (mx_turned, G), (shifted, G), (av_done, G), (o_done, 1), (a_turned, 1), (g_done, 1)):
                    pe.sem_inc(sem, 2 * steps)
                pe.wait_ge(w_in, W_ALL)
                pe.wait_ge(const_ready, 1)
                with pe.Fori(0, NB // 2) as i:
                    for u in range(2):
                        pe.wait_ge(xn_ready, done(i, u))
                        pe.wait_ge(gl_ready, before(i, u))
                        for c in range(KC):
                            last = nc.tensor.transpose(W[u][:, c * T:(c + 1) * T], x_n[:, u, c * P:(c + 1) * P], ident[:T, :T])
                        last.then_inc(x_turned, 1)
                    for u in range(2):
                        pe.wait_ge(cn_ready, done(i, u, NCH - 1, NCH))
                        pe.wait_ge(less_ready, before(i, u, G - 1, G))
                        for c in range(KC):
                            for n in range(NCH):
                                last = nc.tensor.transpose(S[u][:, c, n * STEP:n * STEP + ROWS], c_n[:, u, n, c * P:(c + 1) * P],
                                                           ident[:ROWS, :ROWS])
                        last.then_inc(c_turned, 1)
                    for u in range(2):
                        pe.wait_ge(xT_ready, done(i, u))
                        pe.wait_ge(cT_ready, done(i, u))
                        for g in range(KC):
                            for turned in range(2):
                                k = 2 * g + turned
                                dst = W[u][:, 0:src_len] if k == 3 else S[u][:, k, 0:src_len]
                                for c in range(KC):
                                    last = nc.tensor.matmul(dst, wk[:, turned, c, g * P:(g + 1) * P], cT[:, u, c, :],
                                                            start=(c == 0), stop=(c == KC - 1))
                        last.then_inc(k_done, 1)
                    for u in range(2):
                        pe.wait_ge(k_rot, done(i, u))
                        for n in range(NCH):
                            for c in range(KC):
                                last = nc.tensor.matmul(S[u][:ROWS, n // 2, (n % 2) * D:(n % 2) * D + D],
                                                        cT[:, u, c, n * STEP:n * STEP + ROWS], wv[:, c, :],
                                                        start=(c == 0), stop=(c == KC - 1))
                        last.then_inc(v_done, 1)
                        for turned in range(2):
                            for g in range(KC):
                                col = (turned * KC + g) * T
                                for c in range(KC):
                                    last = nc.tensor.matmul(S[u][:, 2, col:col + T], wq[:, turned, c, g * P:(g + 1) * P],
                                                            xT[:, u, c, :], start=(c == 0), stop=(c == KC - 1))
                        last.then_inc(q_done, 1)

                    def attend(j):
                        for u in range(2):
                            pe.wait_ge(prob_ready, done(i, u, j, G))
                            pe.wait_ge(max_ready, done(i, u, j, G))
                            for n in range(NCH):
                                rows = ROWS if n == NCH - 1 else STEP
                                last = nc.tensor.matmul(W[u][:, 0:GW], v1[0:rows, u, n, j, :], prob[0:rows, u, n, :],
                                                        start=(n == 0), stop=(n == NCH - 1))
                            last.then_inc(av_done, 1)

                    for j in range(G):
                        for u in range(2):
                            if j == 0:
                                pe.wait_ge(v_ready, done(i, u))
                                pe.wait_ge(k_ready, done(i, u))
                                pe.wait_ge(qbd_ready, done(i, u))
                            else:
                                pe.wait_ge(less_ready, done(i, u, j - 1, G))
                            g, h0 = j // 2, 4 * (j % 2)
                            for n in range(NCH):
                                last = nc.tensor.matmul(S[u][:ROWS, n, 0:GW], kT[:, u, g, n * STEP:n * STEP + ROWS],
                                                        q_bd[:, u, g, h0:h0 + 4, :].rearrange("p h t -> p (h t)"),
                                                        start=True, stop=True)
                            last.then_inc(scored, 1)
                        if j:
                            attend(j - 1)
                        for u in range(2):
                            pe.wait_ge(mx_ready, done(i, u, j, G))
                            if j:
                                pe.wait_ge(own_ready, done(i, u, j - 1, G))
                            for h in range(HPG):
                                last = nc.tensor.transpose(W[u][:T, h * P:h * P + ROWS], mx[:, u, h * T:(h + 1) * T],
                                                           ident[:ROWS, :ROWS])
                            last.then_inc(mx_turned, 1)
                        for u in range(2):
                            pe.wait_ge(max_ready, done(i, u, j, G))
                            for n in range(NCH):
                                last = nc.tensor.matmul(S[u][:ROWS, n, 0:GW], neg1[:], dmax[:, u, :, :].rearrange("p h t -> p (h t)"),
                                                        start=False, stop=True, skip_group_check=True)
                            last.then_inc(shifted, 1)
                    attend(G - 1)
                    for u in range(2):
                        pe.wait_ge(yT_ready, done(i, u, G - 1, G))
                        for c in range(KC):
                            last = nc.tensor.matmul(W[u][:T, 0:D], yT[:, u, c, :], wo[:, c, :], start=(c == 0), stop=(c == KC - 1))
                        last.then_inc(o_done, 1)
                    for u in range(2):
                        pe.wait_ge(att_ready, done(i, u))
                        for c in range(KC):
                            last = nc.tensor.transpose(W[u][:, c * T:(c + 1) * T], att[:, u, c * P:(c + 1) * P], ident[:T, :T])
                        last.then_inc(a_turned, 1)
                    for u in range(2):
                        pe.wait_ge(aT_ready, done(i, u))
                        for c in range(KC):
                            last = nc.tensor.matmul(W[u][:T, 0:D], aT[:, u, c, :], wg[:, c, :], start=(c == 0), stop=(c == KC - 1))
                        last.then_inc(g_done, 1)

            @block.scalar
            def _(act):
                for sem, steps in ((xT_ready, 1), (cT_ready, 1), (v_ready, 1), (prob_ready, G), (aT_ready, 1), (th_ready, 1)):
                    act.sem_inc(sem, 2 * steps)
                for u in range(2):
                    act.sem_inc(stored[u], 16)
                act.wait_ge(w_in, W_ALL)
                with act.Fori(0, NB // 2) as i:
                    for u in range(2):
                        act.wait_ge(x_turned, done(i, u))
                        for c in range(KC):
                            last = nc.scalar.activation(xT[:, u, c, :], W[u][:, c * T:(c + 1) * T], ACT.Identity,
                                                        scale=gamma[:, c:c + 1], bias=beta[:, c:c + 1])
                        last.then_inc(xT_ready, 1)
                    for u in range(2):
                        act.wait_ge(c_turned, done(i, u))
                        for c in range(KC):
                            last = nc.scalar.activation(cT[:, u, c, :], S[u][:, c, 0:src_len], ACT.Identity,
                                                        scale=gamma[:, c:c + 1], bias=beta[:, c:c + 1])
                        last.then_inc(cT_ready, 1)
                    for u in range(2):
                        act.wait_ge(v_done, done(i, u))
                        act.wait_ge(av_done, before(i, u, G - 1, G))
                        nc.scalar.activation(v1[:, u, 0:2, :, 0:64],
                                             S[u][:ROWS, 0, :].rearrange("p (n g f) -> p n g f", n=2, f=64), ACT.Copy)
                        nc.scalar.activation(v1[:, u, 2, :, 0:64], S[u][:ROWS, 1, 0:D].rearrange("p (g f) -> p g f", f=64),
                                             ACT.Copy).then_inc(v_ready, 1)
                    for j in range(G):
                        for u in range(2):
                            act.wait_ge(less_ready, done(i, u, j, G))
                            nc.scalar.activation(prob[:, u, :, :].rearrange("p n t -> p (n t)"),
                                                 prob[:, u, :, :].rearrange("p n t -> p (n t)"), ACT.Exp,
                                                 scale=float(DH) ** -0.5).then_inc(prob_ready, 1)
                    for u in range(2):
                        act.wait_ge(a_turned, done(i, u))
                        nc.scalar.activation(aT[:, u].rearrange("p c t -> p (c t)"), W[u][:, 0:KC * T], ACT.Copy).then_inc(aT_ready, 1)
                    for u in range(2):
                        act.wait_ge(gl_ready, done(i, u))
                        nc.scalar.activation(gl[:, u, :], gl[:, u, :], ACT.Tanh, scale=0.5).then_inc(th_ready, 1)
                    for u in range(2):
                        act.wait_ge(out_ready, done(i, u))
                        act.dma_start(x_out[2 * i + u], x_o[:, u, :]).then_inc(stored[u], 16)
                for u in range(2):
                    act.wait_ge(stored[u], 16 * (NB // 2) + 16)

            @block.gpsimd
            def _(pool):
                for sem in (k_ready, q_sum, qbd_ready, x2_ready):
                    pool.sem_inc(sem, 2)
                norm_q.set_power(pool)
                norm_c.set_power(pool)
                norm.set_power(pool)
                pool.wait_ge(w_in, W_ALL)
                with pool.Fori(0, NB // 2) as i:
                    norm_q.raise_power(pool, i)
                    norm_c.raise_power(pool, i)
                    for u in range(2):
                        pool.wait_ge(k_rot, done(i, u))
                        pool.wait_ge(scored, before(i, u, G - 1, G))
                        nc.gpsimd.tensor_tensor(kT[:, u].rearrange("p c t -> p (c t)"), k_c[:, u].rearrange("p c t -> p (c t)"),
                                                k_s[:, u].rearrange("p c t -> p (c t)"), ALU.add).then_inc(k_ready, 1)
                    for u in range(2):
                        pool.wait_ge(q_rot, done(i, u))
                        nc.gpsimd.tensor_tensor(q_c[:, u].rearrange("p c t -> p (c t)"), q_c[:, u].rearrange("p c t -> p (c t)"),
                                                q_s[:, u].rearrange("p c t -> p (c t)"), ALU.add).then_inc(q_sum, 1)
                    for u in range(2):
                        pool.wait_ge(q_sum, done(i, u))
                        for g in range(KC):
                            last = nc.gpsimd.tensor_tensor(q_bd[:, u, g, :, :],
                                                           q_c[:, u, g, :].unsqueeze(1).to_broadcast([P, 8, T]),
                                                           head_mask[:].unsqueeze(2).to_broadcast([P, 8, T]), ALU.mult)
                        last.then_inc(qbd_ready, 1)
                    for u in range(2):
                        pool.wait_ge(res_loaded[u], 16 * i + 16)
                        nc.gpsimd.tensor_tensor(x_2[:, u, :], x_res[:, u, :], x_res[:, u, :], ALU.add).then_inc(x2_ready, 1)
                    norm.raise_power(pool, i)

            @block.vector
            def _(dve):
                nc.vector.memset(v1[:], 1.0)
                nc.vector.memset(neg1[:].bitcast(F32), -1.0)
                for sem, steps in ((xn_ready, 1), (cn_ready, NCH), (k_rot, 1), (q_rot, 1), (mx_ready, G), (max_ready, G),
                                   (less_ready, G), (own_ready, G), (yT_ready, G), (att_ready, 1), (gl_ready, 1),
                                   (r_ready, 1), (out_ready, 1)):
                    dve.sem_inc(sem, 2 * steps)
                dve.wait_ge(w_in, W_ALL)
                H2 = DH // 2
                for wm in (wq, wk):
                    for c in range(KC):
                        a = wm[:, 0, c, :].rearrange("p (h two d) -> p h two d", two=2, d=H2)
                        t = wm[:, 1, c, :].rearrange("p (h two d) -> p h two d", two=2, d=H2)
                        nc.vector.tensor_scalar(t[:, :, 0, :], a[:, :, 1, :], -1.0, None, ALU.mult)
                        last = nc.vector.tensor_copy(t[:, :, 1, :], a[:, :, 0, :])
                last.then_inc(const_ready, 1)
                with dve.Fori(0, NB // 2) as i:
                    links = Links(dve, vlink, i, 48)
                    for u in range(2):
                        dve.wait_ge(x_loaded[u], 16 * i + 16)
                    dve.wait_ge(x_turned, before(i, 1))
                    norm_q.steps(dve, links, i, x_t, x_n, xn_ready)
                    for u in range(2):
                        dve.wait_ge(c_loaded[u], 16 * NCH * i + 16 * NCH)
                    dve.wait_ge(c_turned, before(i, 1))
                    norm_c.steps_of(dve, links, i, [c_t[:, u, n, :] for n in range(NCH) for u in range(2)],
                                    [c_n[:, u, n, :] for n in range(NCH) for u in range(2)], cn_ready)
                    for u in range(2):
                        dve.wait_ge(k_done, done(i, u))
                        dve.wait_ge(k_ready, before(i, u))
                        for g in range(KC):
                            nc.vector.tensor_tensor(k_c[:, u, g, :], S[u][:, 2 * g, 0:src_len], cosT[:], ALU.mult)
                            turned = W[u][:, 0:src_len] if g else S[u][:, 1, 0:src_len]
                            last = nc.vector.tensor_tensor(k_s[:, u, g, :], turned, sinT[:], ALU.mult)
                        last.then_inc(k_rot, 1)
                    for u in range(2):
                        dve.wait_ge(q_done, done(i, u))
                        dve.wait_ge(qbd_ready, before(i, u))
                        src = S[u][:, 2, 0:4 * T].rearrange("p (r g t) -> p r g t", r=2, t=T)
                        nc.vector.tensor_tensor(q_c[:, u], src[:, 0], cosT[:, 0:T].unsqueeze(1).to_broadcast([P, KC, T]), ALU.mult)
                        nc.vector.tensor_tensor(q_s[:, u], src[:, 1], sinT[:, 0:T].unsqueeze(1).to_broadcast([P, KC, T]),
                                                ALU.mult).then_inc(q_rot, 1)

                    def normalise(j):
                        for u in range(2):
                            dve.wait_ge(av_done, done(i, u, j, G))
                            nc.vector.tensor_tensor(own[:, u, :].rearrange("p (h t) -> p h t", t=T),
                                                    W[u][:, 0:GW].rearrange("p (h t) -> p h t", t=T),
                                                    head_mask2[:].unsqueeze(2).to_broadcast([P, HPG, T]), ALU.mult)\
                                .then_inc(own_ready, 1)
                        for u in range(2):
                            dve.wait_ge(own_ready, done(i, u, j, G))
                            links.add(nc.vector.tensor_reduce(nd[:, u, :], own[:, u, :].rearrange("p (h t) -> p t h", t=T),
                                                              axis=AXIS_X, op=ALU.add))
                        links.wait()
                        for u in range(2):
                            links.add(nc.vector.reciprocal(rec[:, u, :], nd[64:128, u, :]))
                        links.wait()
                        o = 64 * (j % 2)
                        for u in range(2):
                            if j == 0:
                                dve.wait_ge(o_done, before(i, u))
                            nc.vector.tensor_tensor(yT[o:o + 64, u, j // 2, :], nd[0:64, u, :], rec[:, u, :],
                                                    ALU.mult).then_inc(yT_ready, 1)

                    for j in range(G):
                        for u in range(2):
                            dve.wait_ge(scored, done(i, u, j, G))
                            nc.vector.tensor_reduce(mx[:, u, :], S[u][:ROWS, :, 0:GW].rearrange("p n t -> p t n"),
                                                    axis=AXIS_X, op=ALU.max).then_inc(mx_ready, 1)
                        if j:
                            normalise(j - 1)
                        for u in range(2):
                            dve.wait_ge(mx_turned, done(i, u, j, G))
                            links.add(nc.vector.tensor_reduce(nmax[:, u, :], W[u][:T, :].rearrange("p (h t) -> p h t", t=P)[:, :, 0:ROWS],
                                                              axis=AXIS_X, op=ALU.max))
                        links.wait()
                        for u in range(2):
                            nc.vector.tensor_tensor(dmax[:, u, :, :], ident[:T, :T].unsqueeze(1).to_broadcast([T, HPG, T]),
                                                    nmax[:, u, :].unsqueeze(2).to_broadcast([T, HPG, T]),
                                                    ALU.mult).then_inc(max_ready, 1)
                        for u in range(2):
                            dve.wait_ge(shifted, done(i, u, j, G))
                            if j:
                                dve.wait_ge(av_done, done(i, u, j - 1, G))
                            for n in range(NCH):
                                last = nc.vector.tensor_tensor(prob[:, u, n, :].rearrange("p (h t) -> p h t", t=T),
                                                               S[u][:ROWS, n, 0:GW].rearrange("p (h t) -> p h t", t=T),
                                                               bias[:, n, :].unsqueeze(1).to_broadcast([ROWS, HPG, T]), ALU.add)
                            last.then_inc(less_ready, 1)
                    normalise(G - 1)
                    for u in range(2):
                        dve.wait_ge(o_done, done(i, u))
                        nc.vector.tensor_tensor(att[:, u, :], W[u][:T, 0:D], bo[:], ALU.add).then_inc(att_ready, 1)
                    for u in range(2):
                        dve.wait_ge(att_ready, done(i, u))
                        dve.wait_ge(res_loaded[u], 16 * i + 16)
                        links.add(nc.vector.tensor_tensor(dif[:, u, :], att[:, u, :], x_res[:, u, :], ALU.subtract))
                    for u in range(2):
                        dve.wait_ge(g_done, done(i, u))
                        nc.vector.tensor_tensor(gl[:, u, :], W[u][:T, 0:D], bg[:], ALU.add).then_inc(gl_ready, 1)
                    links.wait()
                    for u in range(2):
                        dve.wait_ge(th_ready, done(i, u))
                        links.add(nc.vector.scalar_tensor_tensor(dif[:, u, :], gl[:, u, :], 1.0, dif[:, u, :], ALU.add, ALU.mult))
                    links.wait()
                    for u in range(2):
                        dve.wait_ge(x2_ready, done(i, u))
                        nc.vector.scalar_tensor_tensor(r[:, u, :], dif[:, u, :], 0.5, x_2[:, u, :], ALU.mult, ALU.add).then_inc(r_ready, 1)
                    dve.wait_ge(r_ready, done(i, 1))
                    for u in range(2):
                        dve.wait_ge(stored[u], 16 * i + 16)
                    norm.steps(dve, links, i, r, x_o, out_ready)
                    links.end()


ROUND = 12582912.0


def bit_ffn(nc, NB, x_in, x_out, w):
    F = 1024
    FC = F // P
    EPS_N, EPS_Q = 1e-8, 1e-5
    with ExitStack() as ctx:
        s = Store(nc, ctx, "bf")
        w1f = s.sb("w1f", [P, KC, F])
        w2f = s.sb("w2f", [P, FC, D])
        w1t = s.sb("w1t", [P, KC, F], BF16)
        w2t = s.sb("w2t", [P, FC, D], BF16)
        wsum = s.sb("wsum", [P, 2])
        wmean = s.sb("wmean", [P, 2])
        wscale = s.sb("wscale", [P, 2])
        ones = s.sb("ones", [P, P])
        n1 = s.sb("n1", [T, D])
        n2 = s.sb("n2", [T, F])
        a_s = s.sb("a_s", [T, 2])
        ident = s.sb("ident", [P, P])
        identb = s.sb("identb", [P, P], BF16)
        x_t = s.sb("x_t", [T, 2, D])
        sq = s.sb("sq", [T, 2, F])
        ss = s.sb("ss", [T, 2, 2])
        ms = s.sb("ms", [T, 2, 2])
        rms = s.sb("rms", [T, 2, 2])
        power = s.sb("power", [T, 2])
        xn = s.sb("xn", [T, 2, D])
        amax = s.sb("amax", [T, 2, 2])
        ascale = s.sb("ascale", [T, 2, 2])
        back = s.sb("back", [T, 2, 2])
        xq = s.sb("xq", [T, 2, D])
        xi = s.sb("xi", [T, 2, D], BF16)
        xiT = s.sb("xiT", [P, 2, KC, T], BF16)
        h = s.sb("h", [T, 2, F])
        hn = s.sb("hn", [T, 2, F])
        hi = s.sb("hi", [T, 2, F], BF16)
        hiT = s.sb("hiT", [P, 2, FC, T], BF16)
        r = s.sb("r", [T, 2, D])
        x_o = s.sb("x_o", [T, 2, D])
        norm = Norm(s, nc)
        H = [s.ps(f"H{u}", [P, F]) for u in range(2)]
        TT = [s.ps(f"TT{u}", [P, FC, T], BF16) for u in range(2)]
        Y = [s.ps(f"Y{u}", [P, D]) for u in range(2)]

        w_in, summed_w, wsum_ready, ones_set, tern_ready, power_set = (s.sem(n) for n in (
            "weights_loaded", "weight_sums", "wsum_ready", "ones_set", "ternary_ready", "power_set"))
        x_loaded, stored = s.sems("x_loaded"), s.sems("stored")
        ss1_ready, h_relu, h_sq, ss2_ready = (s.sem(n) for n in ("ss1_ready", "h_relu", "h_sq", "ss2_ready"))
        ms1_ready, xi_ready, back1_ready, h_ready, ms2_ready, hi_ready, r_ready, out_ready = (s.sem(n) for n in (
            "ms1_ready", "xi_ready", "back1_ready", "h_ready", "ms2_ready", "hi_ready", "r_ready", "out_ready"))
        rms1_ready, rms2_ready = s.sem("rms1_ready"), s.sem("rms2_ready")
        x_turned, h_done, h_turned, y_done = (s.sem(n) for n in ("x_turned", "h_done", "h_turned", "y_done"))
        xiT_ready, hiT_ready = s.sem("xiT_ready"), s.sem("hiT_ready")
        vlink, alink = s.sem("dve_link"), s.sem("act_link")

        kp = "(k p) n -> p k n"
        loads = [(w1f[:], w["ff_w1T"].rearrange(kp, p=P)), (w2f[:], w["ff_w2T"].rearrange(kp, p=P)),
                 (n1[:], w["ff_n1"].to_broadcast([T, D])), (n2[:], w["ff_n2"].to_broadcast([T, F])),
                 (a_s[:, 0:1], w["ff_as"].to_broadcast([T, 1])), (a_s[:, 1:2], w["ff_ab"].to_broadcast([T, 1])),
                 (ident[:], w["ident"])]
        W_ALL = 16 * len(loads)

        with nc.Block() as block:

            @block.sync
            def _(sp):
                for dst, src in loads:
                    sp.dma_start(dst, src).then_inc(w_in, 16)
                with sp.Fori(0, NB // 2) as i:
                    for u in range(2):
                        sp.wait_ge(r_ready, before(i, u))
                        sp.dma_start(x_t[:, u, :], x_in[2 * i + u]).then_inc(x_loaded[u], 16)

            @block.gpsimd
            def _(pool):
                nc.gpsimd.memset(ones[:], 1.0).then_inc(ones_set, 1)
                nc.gpsimd.memset(power[:], -0.5).then_inc(power_set, 1)
                norm.set_power(pool)
                pool.wait_ge(power_set, 1)
                with pool.Fori(0, NB // 2) as i:
                    for k, (there, ready) in enumerate(((ms1_ready, rms1_ready), (ms2_ready, rms2_ready))):
                        pool.wait_ge(there, i + 1)
                        nc.gpsimd.tensor_tensor(rms[:, :, k], ms[:, :, k], power[:], ALU.pow).then_inc(ready, 1)
                    norm.raise_power(pool, i)

            @block.tensor
            def _(pe):
                for sem in (x_turned, h_done, h_turned, y_done):
                    pe.sem_inc(sem, 2)
                pe.wait_ge(ones_set, 1)
                pe.wait_ge(wsum_ready, 1)
                nc.tensor.matmul(Y[0][:, 0:2], ones[:], wsum[:], start=True, stop=True).then_inc(summed_w, 1)
                pe.wait_ge(tern_ready, 1)
                with pe.Fori(0, NB // 2) as i:
                    for u in range(2):
                        pe.wait_ge(xi_ready, done(i, u))
                        pe.wait_ge(hiT_ready, before(i, u))
                        for c in range(KC):
                            last = nc.tensor.transpose(TT[u][:, c, :], xi[:, u, c * P:(c + 1) * P], identb[:T, :T])
                        last.then_inc(x_turned, 1)
                    for u in range(2):
                        pe.wait_ge(xiT_ready, done(i, u))
                        pe.wait_ge(h_relu, before(i, u))
                        for half in range(F // 512):
                            for c in range(KC):
                                last = nc.tensor.matmul(H[u][:T, half * 512:(half + 1) * 512], xiT[:, u, c, :],
                                                        w1t[:, c, half * 512:(half + 1) * 512], start=(c == 0), stop=(c == KC - 1))
                        last.then_inc(h_done, 1)
                    for u in range(2):
                        pe.wait_ge(hi_ready, done(i, u))
                        for c in range(FC):
                            last = nc.tensor.transpose(TT[u][:, c, :], hi[:, u, c * P:(c + 1) * P], identb[:T, :T])
                        last.then_inc(h_turned, 1)
                    for u in range(2):
                        pe.wait_ge(hiT_ready, done(i, u))
                        pe.wait_ge(r_ready, before(i, u))
                        for c in range(FC):
                            last = nc.tensor.matmul(Y[u][:T, :], hiT[:, u, c, :], w2t[:, c, :], start=(c == 0), stop=(c == FC - 1))
                        last.then_inc(y_done, 1)

            @block.scalar
            def _(act):
                for sem in (ss1_ready, h_relu, h_sq, ss2_ready, xiT_ready, hiT_ready):
                    act.sem_inc(sem, 2)
                for u in range(2):
                    act.sem_inc(stored[u], 16)
                with act.Fori(0, NB // 2) as i:
                    for u in range(2):
                        act.wait_ge(x_loaded[u], 16 * i + 16)
                        nc.scalar.activation(sq[:, u, 0:D], x_t[:, u, :], ACT.Square, accum_out=ss[:, u, 0:1]).then_inc(ss1_ready, 1)
                    for u in range(2):
                        act.wait_ge(x_turned, done(i, u))
                        act.wait_ge(h_done, before(i, u))
                        nc.scalar.activation(xiT[:, u], TT[u][:, 0:KC, :], ACT.Copy).then_inc(xiT_ready, 1)
                    for u in range(2):
                        act.wait_ge(h_done, done(i, u))
                        act.wait_ge(back1_ready, done(i, u))
                        act.wait_ge(hi_ready, before(i, u))
                        nc.scalar.activation(h[:, u, :], H[u][:T, :], ACT.Relu, scale=back[:, u, 0:1]).then_inc(h_relu, 1)
                    for u in range(2):
                        act.wait_ge(h_relu, done(i, u))
                        nc.scalar.activation(h[:, u, :], h[:, u, :], ACT.Square).then_inc(h_sq, 1)
                    for u in range(2):
                        act.wait_ge(h_ready, done(i, u))
                        nc.scalar.activation(sq[:, u, :], h[:, u, :], ACT.Square, accum_out=ss[:, u, 1:2]).then_inc(ss2_ready, 1)
                    for u in range(2):
                        act.wait_ge(h_turned, done(i, u))
                        act.wait_ge(y_done, before(i, u))
                        nc.scalar.activation(hiT[:, u], TT[u][:, :, :], ACT.Copy).then_inc(hiT_ready, 1)
                    for u in range(2):
                        act.wait_ge(out_ready, done(i, u))
                        act.dma_start(x_out[2 * i + u], x_o[:, u, :]).then_inc(stored[u], 16)
                for u in range(2):
                    act.wait_ge(stored[u], 16 * (NB // 2) + 16)

            @block.vector
            def _(dve):
                for sem in (xi_ready, back1_ready, h_ready, hi_ready, r_ready, out_ready):
                    dve.sem_inc(sem, 2)
                dve.wait_ge(w_in, W_ALL)
                count = 0

                def step(*instructions):
                    nonlocal count
                    for ins in instructions:
                        ins.then_inc(alink, 1)
                        count += 1
                    dve.wait_ge(alink, count)

                step(nc.vector.tensor_copy(identb[:], ident[:]))
                for k, wf in ((0, w1f), (1, w2f)):
                    last = nc.vector.tensor_reduce(wsum[:, k:k + 1], wf[:], axis=mybir.AxisListType.XY, op=ALU.add,
                                                   apply_absolute_value=True)
                last.then_inc(wsum_ready, 1)
                dve.wait_ge(summed_w, 1)
                step(nc.vector.tensor_scalar(wmean[:], Y[0][:, 0:2], 1.0 / (D * F), EPS_Q, ALU.mult, ALU.max))
                step(nc.vector.reciprocal(wscale[:], wmean[:]))
                for k, wf, wt in ((0, w1f, w1t), (1, w2f, w2t)):
                    step(nc.vector.tensor_scalar(wf[:], wf[:], wscale[:, k:k + 1], ROUND, ALU.mult, ALU.add))
                    step(nc.vector.tensor_scalar(wf[:], wf[:], ROUND, 1.0, ALU.subtract, ALU.min))
                    last = nc.vector.tensor_scalar(wt[:], wf[:], -1.0, None, ALU.max)
                last.then_inc(tern_ready, 1)

                with dve.Fori(0, NB // 2) as i:
                    links = Links(dve, vlink, i, 26)

                    def quantise(src, dst, k, scratch, ready):
                        for u in range(2):
                            links.add(nc.vector.tensor_reduce(amax[:, u, k:k + 1], src[:, u, :], axis=AXIS_X, op=ALU.max,
                                                              apply_absolute_value=True))
                        links.wait()
                        for u in range(2):
                            links.add(nc.vector.tensor_scalar(back[:, u, k:k + 1], amax[:, u, k:k + 1], EPS_Q, 1.0 / 127.0, ALU.max, ALU.mult))
                        links.wait()
                        for u in range(2):
                            links.add(nc.vector.reciprocal(ascale[:, u, k:k + 1], back[:, u, k:k + 1]))
                        links.wait()
                        for u in range(2):
                            links.add(nc.vector.tensor_scalar(scratch[:, u, :], src[:, u, :], ascale[:, u, k:k + 1], ROUND, ALU.mult, ALU.add))
                            if k == 0:
                                nc.vector.tensor_scalar(back[:, u, k:k + 1], back[:, u, k:k + 1], wmean[:T, k:k + 1], None,
                                                        ALU.mult).then_inc(back1_ready, 1)
                            else:
                                links.add(nc.vector.tensor_scalar(back[:, u, k:k + 1], back[:, u, k:k + 1], wmean[:T, k:k + 1], None, ALU.mult))
                        links.wait()
                        for u in range(2):
                            nc.vector.tensor_scalar(dst[:, u, :], scratch[:, u, :], ROUND, 127.0, ALU.subtract, ALU.min).then_inc(ready, 1)

                    dve.wait_ge(ss1_ready, done(i, 1))
                    nc.vector.tensor_scalar(ms[:, :, 0], ss[:, :, 0], 1.0 / D, EPS_N, ALU.mult, ALU.add).then_inc(ms1_ready, 1)
                    dve.wait_ge(rms1_ready, i + 1)
                    for u in range(2):
                        links.add(nc.vector.scalar_tensor_tensor(xn[:, u, :], x_t[:, u, :], rms[:, u, 0:1], n1[:], ALU.mult, ALU.mult))
                    links.wait()
                    dve.wait_ge(x_turned, before(i, 1))
                    dve.wait_ge(h_relu, before(i, 1))
                    quantise(xn, xi, 0, xq, xi_ready)
                    for u in range(2):
                        dve.wait_ge(h_sq, done(i, u))
                        nc.vector.tensor_scalar(h[:, u, :], h[:, u, :], a_s[:, 0:1], a_s[:, 1:2], ALU.mult, ALU.add).then_inc(h_ready, 1)
                    dve.wait_ge(ss2_ready, done(i, 1))
                    nc.vector.tensor_scalar(ms[:, :, 1], ss[:, :, 1], 1.0 / F, EPS_N, ALU.mult, ALU.add).then_inc(ms2_ready, 1)
                    dve.wait_ge(rms2_ready, i + 1)
                    for u in range(2):
                        links.add(nc.vector.scalar_tensor_tensor(hn[:, u, :], h[:, u, :], rms[:, u, 1:2], n2[:], ALU.mult, ALU.mult))
                    links.wait()
                    dve.wait_ge(h_turned, before(i, 1))
                    quantise(hn, hi, 1, hn, hi_ready)
                    for u in range(2):
                        dve.wait_ge(y_done, done(i, u))
                        nc.vector.scalar_tensor_tensor(r[:, u, :], Y[u][:T, :], back[:, u, 1:2], x_t[:, u, :], ALU.mult, ALU.add).then_inc(r_ready, 1)
                    dve.wait_ge(r_ready, done(i, 1))
                    for u in range(2):
                        dve.wait_ge(stored[u], 16 * i + 16)
                    norm.steps(dve, links, i, r, x_o, out_ready)
                    links.end()


def decoder(nc, x, out, w):
    NB = x.shape[0]
    src_len = w["ctx"].shape[1]

    def scratch(name, shape, dt=F32):
        return nc.dram_tensor(name, shape, dt, kind="Internal").ap()

    x1, x2, xz, x4, x5 = (scratch(n, [NB, T, D]) for n in ("x1", "x2", "x_plus_shared", "x4", "x5"))
    slot_rows = scratch("slot_rows", [SLOTS, D])
    slot_out = scratch("slot_out", [SLOTS, D])
    slot_ids = scratch("slot_ids", [NB, T, TOPK], U32)
    slot_weights = scratch("slot_weights", [NB, T, TOPK])
    self_attention(nc, NB, x, x1, w)
    cross_attention_strided(nc, NB, x1, x2, w, src_len)
    route(nc, NB, x2, w, slot_rows, xz, slot_ids, slot_weights)
    experts(nc, w, slot_rows, slot_out)
    linear_attention(nc, NB, xz, slot_out, slot_ids, slot_weights, x4, w)
    cross_attention(nc, NB, x4, x5, w, src_len)
    bit_ffn(nc, NB, x5, out, w)


def rope_tables(t, dim, theta):
    inv = (1.0 / theta ** (np.arange(0, dim, 2, dtype=np.float32) / np.float32(dim))).astype(np.float32)
    f = np.arange(t, dtype=np.float32)[:, None] * inv[None, :]
    e = np.concatenate((f, f), -1)
    return np.cos(e).astype(np.float32), np.sin(e).astype(np.float32)


def resize_matrix(n, m):
    inv = np.float32(n / m)
    k = max(float(inv), 1.0)
    f = (np.arange(m, dtype=np.float32) + np.float32(0.5)) * inv - np.float32(0.5)
    d = np.abs(f[None, :] - np.arange(n, dtype=np.float32)[:, None]) / np.float32(k)
    wt = np.maximum(np.float32(0), np.float32(1) - d)
    return (wt / wt.sum(0, keepdims=True)).astype(np.float32)


def position_bias(lq, lkv, length=128):
    pos = np.arange(length, dtype=np.float32)
    dist = np.abs(pos[None, :] - pos[:, None])
    bias = (np.exp(-dist * np.float32(0.1)) - dist * np.float32(0.05)).astype(np.float64)
    return (resize_matrix(length, lq).T.astype(np.float64) @ bias @ resize_matrix(length, lkv).astype(np.float64)).astype(np.float32)


def shape_constants(src_len):
    c = {}
    p = np.arange(P)
    t = np.arange(T)
    cos, sin = rope_tables(T, DH // 2, 10000.0)
    c["cos_sa"] = np.ones((P, T), np.float32)
    c["sin_sa"] = np.zeros((P, T), np.float32)
    for h in range(P // DH):
        c["cos_sa"][h * DH + DH // 2:(h + 1) * DH] = cos.T
        c["sin_sa"][h * DH + DH // 2:(h + 1) * DH] = sin.T
    cos, sin = rope_tables(src_len, DH, 10000.0)
    c["cos_xa"] = np.tile(cos.T, (P // DH, 1))
    c["sin_xa"] = np.tile(sin.T, (P // DH, 1))
    bias = position_bias(T, src_len) * np.float32(DH ** 0.5)
    step = (src_len - 1) // 3
    c["bias_xa"] = np.stack([bias[:, step * n:step * n + step + 1].T for n in range(3)], 1)
    c["head_mask"] = (p[:, None] // DH == np.arange(8)[None]).astype(np.float32)
    c["head_mask2"] = ((p[:, None] % 64) // DH == np.arange(4)[None]).astype(np.float32)
    c["head_mask4"] = (p[:, None] // 32 == np.arange(4)[None]).astype(np.float32)
    c["block_mask"] = (p[:, None] // DH == p[None] // DH).astype(np.float32)
    c["ident"] = np.eye(P, dtype=np.float32)
    c["causal"] = np.where(t[None, :] >= t[:, None], 0, NEG).astype(np.float32)
    c["earlier"] = (t[:, None] < t[None]).astype(np.float32)
    c["expert_no"] = np.tile(np.arange(EXPERTS, dtype=np.float32), (T, 1))
    c["first_slot"] = np.tile(np.arange(0, SLOTS, CAP, dtype=np.float32), (T, 1))
    keys = -(-src_len // 8)
    c["v_ones"] = np.zeros((P, 4, 96), np.float32)
    for h in range(8):
        row = 64 * (h % 2)
        c["v_ones"][row:row + len(range(h, src_len, 8)), h // 2, 33 * (h % 2) + 32] = 1
    assert keys <= 64
    return c


def layouts(x):
    o = {}
    for k in ("Wq_down", "Wk_down", "Wv_down"):
        o["L0_attn_" + k] = x["L0_attn_" + k].T
    for k in ("Wq_up_c", "Wq_up_e", "Wk_up_c", "Wk_up_e", "Wv_up", "Wc"):
        o["L0_attn_" + k] = x["L0_attn_" + k]
    for k in ("Wq", "Wk", "Wv", "Wo"):
        o["L0_xattn_" + k] = x["L0_xattn_" + k]
    for k in ("bq", "bk", "bv"):
        o["L0_xattn_" + k] = x["L0_xattn_" + k].reshape(KC, P).T
    o["L0_xattn_bo"] = x["L0_xattn_bo"].reshape(1, D)
    ctx = x["ctx_1024"]
    n, src_len, _ = ctx.shape
    strided = np.zeros((n, 8, 64, D), ctx.dtype)
    for h in range(8):
        strided[:, h, :len(range(h, src_len, 8))] = ctx[:, h::8]
    o["ctxT"] = strided.reshape(n, 512, KC, P).transpose(0, 3, 2, 1)
    o["ctx"] = ctx
    o["gate_wT"], o["gate_b"] = x["L0_ffn_gate_w"].T, x["L0_ffn_gate_b"].reshape(1, EXPERTS)
    o["ws1T"], o["ws2T"], o["ws3T"] = x["L0_ffn_ws1"].T, x["L0_ffn_ws2"].T, x["L0_ffn_ws3"].T
    for k in ("w1", "w2", "w3"):
        o[k + "T"] = x["L0_ffn_" + k].transpose(0, 2, 1)
    o["L1_wqkT"] = np.concatenate([x["L1_attn_Wq"].T, x["L1_attn_Wk"].T], 1)
    o["L1_wvT"], o["L1_woT"] = x["L1_attn_Wv"].T, x["L1_attn_Wo"].T
    o["L1_bqk"] = np.concatenate([x["L1_attn_bq"], x["L1_attn_bk"]]).reshape(1, 2 * D)
    o["L1_bv"], o["L1_bo"] = x["L1_attn_bv"].reshape(1, D), x["L1_attn_bo"].reshape(1, D)
    o["L1x_wqkvT"], o["L1x_woT"], o["L1x_wgT"] = x["L1_xattn_Wqkv"].T, x["L1_xattn_Wout"].T, x["L1_xattn_Wgate"].T
    o["L1x_bo"], o["L1x_bg"] = x["L1_xattn_b_out"].reshape(1, D), x["L1_xattn_b_gate"].reshape(1, D)
    o["L1x_gamma"], o["L1x_beta"] = x["L1_xattn_gamma"].reshape(KC, P).T, x["L1_xattn_beta"].reshape(KC, P).T
    o["ff_w1T"], o["ff_w2T"] = x["L1_ffn_w1"].T, x["L1_ffn_w2"].T
    o["ff_n1"], o["ff_n2"] = x["L1_ffn_norm1_w"].reshape(1, -1), x["L1_ffn_norm2_w"].reshape(1, -1)
    o["ff_as"], o["ff_ab"] = x["L1_ffn_act_scale"].reshape(1, 1), x["L1_ffn_act_bias"].reshape(1, 1)
    return o


def kernel(**inputs):
    import concourse.bacc as _bacc
    from concourse.bass_utils import run_bass_kernel_spmd as _run

    x = {k: np.asarray(v) for k, v in inputs.items()}
    arrays = {"x_tokens": x["x"], **layouts(x), **shape_constants(x["ctx_1024"].shape[1])}
    arrays = {f"in_{k}": np.ascontiguousarray(v) for k, v in arrays.items()}
    nc = _bacc.Bacc("TRN2", target_bir_lowering=False, num_devices=1)
    w = {k[3:]: nc.dram_tensor(k, v.shape, mybir.dt.from_np(v.dtype), kind="ExternalInput").ap() for k, v in arrays.items()}
    out = nc.dram_tensor("out_0", list(x["x"].shape), F32, kind="ExternalOutput").ap()
    decoder(nc, w["x_tokens"], out, w)
    r = _run(nc, [arrays], core_ids=[0])
    return r.results[0]["out_0"]
```

```python
from contextlib import ExitStack

import numpy as np

import concourse.bass as bass
from concourse import mybir

F32 = mybir.dt.float32
F32R = mybir.dt.float32r
BF16 = mybir.dt.bfloat16
U32 = mybir.dt.uint32
ALU = mybir.AluOpType
ACT = mybir.ActivationFunctionType
AXIS_X = mybir.AxisListType.X

T = 100
D = 256
P = 128
KC = D // P
HEADS = 16
DH = D // HEADS
GROUPS = 4
HPG = HEADS // GROUPS
GW = HPG * T
LN_EPS = 1e-5
NEG = -1e30


def counts(U):

    def done(i, u, j=0, steps=1):
        return i * (U * steps) + (U * steps + U * j + u + 1)

    def before(i, u, j=0, steps=1):
        return i * (U * steps) + (U * j + u + 1)

    return done, before


class Links:

    def __init__(self, eng, sem, i, per_iter):
        self.eng, self.sem, self.i, self.per_iter, self.k = eng, sem, i, per_iter, 0

    def add(self, ins):
        self.k += 1
        ins.then_inc(self.sem, 1)

    def wait(self, back=0):
        self.eng.wait_ge(self.sem, self.i * self.per_iter + (self.k - back))

    def end(self):
        assert self.k == self.per_iter, f"links in one iteration: {self.k}"


class Store:

    def __init__(self, nc, ctx, stage, U):
        self.U = U
        self.nc, self.ctx, self.stage = nc, ctx, stage
        self.semaphores = []
        ctx.callback(self.end)

    def sb(self, name, shape, dt=F32):
        return self.ctx.enter_context(self.nc.sbuf_tensor(f"{self.stage}_{name}", shape, dt))

    def ps(self, name, shape, dt=F32):
        return self.ctx.enter_context(self.nc.psum_tensor(f"{self.stage}_{name}", shape, dt))

    def sem(self, name):
        self.semaphores.append(self.nc.alloc_semaphore(f"{self.stage}_{name}"))
        return self.semaphores[-1]

    def end(self):
        self.nc.clear_and_free_semaphores(self.semaphores)
        self.nc.all_engine_barrier()

    def sems(self, name):
        return [self.sem(f"{name}{u}") for u in range(self.U)]


class Norm:

    def __init__(self, s, nc, rows=T, tag="", lots=None):
        lots = lots or s.U
        self.U = s.U
        self.nc, self.rows = nc, rows
        tag = "ln" + tag + "_"
        self.stats = s.sb(tag + "stats", [rows, lots, 6])
        self.mv = s.sb(tag + "mv", [rows, lots, 2])
        self.spare = s.sb(tag + "spare", [rows, 1])
        self.var = s.sb(tag + "var", [rows, lots])
        self.rstd = s.sb(tag + "rstd", [rows, lots])
        self.power = s.sb(tag + "power", [rows, lots])
        self.var_ready = s.sem(tag + "var_ready")
        self.rstd_ready = s.sem(tag + "rstd_ready")
        self.power_set = s.sem(tag + "power_set")

    def set_power(self, pool):
        self.nc.gpsimd.memset(self.power[:], -0.5).then_inc(self.power_set, 1)
        pool.wait_ge(self.power_set, 1)

    def raise_power(self, pool, i):
        pool.wait_ge(self.var_ready, i + 1)
        self.nc.gpsimd.tensor_tensor(self.rstd[:], self.var[:], self.power[:], ALU.pow).then_inc(self.rstd_ready, 1)

    def steps_of(self, dve, links, i, sources, outs, out_ready):
        nc, mv = self.nc, self.mv
        for n, src in enumerate(sources):
            links.add(nc.vector.bn_stats(self.stats[:, n, :], src))
        links.wait()
        nc.vector.memset(self.spare[:], 0.0)
        for n in range(len(sources)):
            links.add(nc.vector.bn_aggr(mv[:, n, :], self.stats[:, n, :]))
        links.wait()
        nc.vector.tensor_scalar(self.var[:], mv[:, :, 1], LN_EPS, None, ALU.add).then_inc(self.var_ready, 1)
        dve.wait_ge(self.rstd_ready, i + 1)
        for n, (src, out) in enumerate(zip(sources, outs)):
            nc.vector.tensor_scalar(out, src, mv[:, n, 0:1], self.rstd[:, n:n + 1],
                                    ALU.subtract, ALU.mult).then_inc(out_ready, 1)

    def steps(self, dve, links, i, src, out, out_ready):
        self.steps_of(dve, links, i, [src[:, u, :] for u in range(self.U)], [out[:, u, :] for u in range(self.U)], out_ready)


def self_attention(nc, NB, x_in, x_out, w):
    with ExitStack() as ctx:
        U = 2
        done, before = counts(U)
        s = Store(nc, ctx, "sa", U)
        down = s.sb("down", [64, 3, HEADS, D])
        up = s.sb("up", [64, 3, 32])
        wq = s.sb("wq", [P, 2, KC, D])
        wk = s.sb("wk", [P, 2, KC, D])
        wv = s.sb("wv", [P, KC, D])
        wc = s.sb("wc", [P, KC, D])
        cosT = s.sb("cosT", [P, T])
        sinT = s.sb("sinT", [P, T])
        head_mask = s.sb("head_mask", [P, 8])
        head_mask2 = s.sb("head_mask2", [P, 4])
        ident = s.sb("ident", [P, P])
        identb = s.sb("identb", [P, P], BF16)
        causalf = s.sb("causalf", [T, T])
        causal = s.sb("causal", [T, HPG, T], BF16)
        neg1 = s.sb("neg1", [T, T], F32R)
        x_t = s.sb("x_t", [T, 2, D])
        x_res = s.sb("x_res", [T, 2, D])
        xT = s.sb("xT", [P, 2, KC, T])
        qk_c = s.sb("qk_c", [P, 2, 2, KC, T])
        qk_s = s.sb("qk_s", [P, 2, 2, KC, T])
        qkT = s.sb("qkT", [P, 2, 2, KC, T])
        q_bd = s.sb("q_bd", [P, 2, KC, 8, T])
        v1 = s.sb("v1", [T, 2, GROUPS, P])
        mx = s.sb("mx", [T, 2, GW])
        nmax = s.sb("nmax", [T, 2, HPG])
        dmax = s.sb("dmax", [T, 2, HPG, T], F32R)
        prob = s.sb("prob", [T, 2, GW])
        own = s.sb("own", [P, 2, GW])
        nd = s.sb("nd", [P, 2, T])
        rec = s.sb("rec", [64, 2, T])
        yT = s.sb("yT", [P, 2, KC, T])
        r = s.sb("r", [T, 2, D])
        norm = Norm(s, nc)
        x_o = s.sb("x_o", [T, 2, D])
        S = [s.ps(f"S{u}", [P, 3, 512]) for u in range(U)]
        W = [s.ps(f"W{u}", [P, 512]) for u in range(U)]

        w_in = s.sem("weights_loaded")
        up_ready = s.sem("up_ready")
        fused = s.sem("fused_in_psum")
        fused_sb = s.sem("fused_in_sbuf")
        const_ready = s.sem("const_ready")
        x_loaded = s.sems("x_loaded")
        res_loaded = s.sems("res_loaded")
        stored = s.sems("stored")
        x_turned = s.sem("x_turned")
        xT_ready = s.sem("xT_ready")
        qkv_done = s.sem("qkv_done")
        v_ready = s.sem("v_ready")
        qk_rot = s.sem("qk_rot")
        qk_ready = s.sem("qk_ready")
        qbd_ready = s.sem("qbd_ready")
        scored = s.sem("scored")
        mx_copied = s.sem("mx_copied")
        mx_turned = s.sem("mx_turned")
        max_ready = s.sem("max_ready")
        shifted = s.sem("shifted")
        prob_ready = s.sem("prob_ready")
        av_done = s.sem("av_done")
        own_ready = s.sem("own_ready")
        yT_ready = s.sem("yT_ready")
        y_done = s.sem("y_done")
        r_ready = s.sem("r_ready")
        out_ready = s.sem("out_ready")
        vlink = s.sem("dve_link")
        alink = s.sem("act_link")
        plink = s.sem("pool_link")
        G = GROUPS

        with nc.Block() as block:

            @block.sync
            def _(sp):
                for k, name in enumerate(("L0_attn_Wq_down", "L0_attn_Wk_down", "L0_attn_Wv_down")):
                    sp.dma_start(down[:, k, :, :], w[name].rearrange("(h l) c -> l h c", l=64)).then_inc(w_in, 16)
                for k, (c_, e_) in enumerate((("Wq_up_c", "Wq_up_e"), ("Wk_up_c", "Wk_up_e"))):
                    sp.dma_start(up[:, k, 0:8], w["L0_attn_" + c_]).then_inc(w_in, 16)
                    sp.dma_start(up[:, k, 8:16], w["L0_attn_" + e_]).then_inc(w_in, 16)
                sp.dma_start(up[:, 2, 0:16], w["L0_attn_Wv_up"]).then_inc(w_in, 16)
                sp.dma_start(wc[:], w["L0_attn_Wc"].rearrange("(k p) n -> p k n", p=P)).then_inc(w_in, 16)
                sp.dma_start(cosT[:], w["cos_sa"]).then_inc(w_in, 16)
                sp.dma_start(sinT[:], w["sin_sa"]).then_inc(w_in, 16)
                sp.dma_start(head_mask[:], w["head_mask"]).then_inc(w_in, 16)
                sp.dma_start(head_mask2[:], w["head_mask2"]).then_inc(w_in, 16)
                sp.dma_start(ident[:], w["ident"]).then_inc(w_in, 16)
                sp.dma_start(causalf[:], w["causal"]).then_inc(w_in, 16)
                with sp.Fori(0, NB // U) as i:
                    for u in range(U):
                        sp.wait_ge(x_turned, before(i, u))
                        sp.dma_start(x_t[:, u, :], x_in[U * i + u]).then_inc(x_loaded[u], 16)
                    for u in range(U):
                        sp.wait_ge(r_ready, before(i, u))
                        sp.dma_start(x_res[:, u, :], x_in[U * i + u]).then_inc(res_loaded[u], 16)

            W_ALL = 16 * 15

            @block.tensor
            def _(pe):
                for sem, steps in ((x_turned, 1), (qkv_done, 1), (scored, G), (mx_turned, G), (shifted, G),
                                   (av_done, G), (y_done, 1)):
                    pe.sem_inc(sem, U * steps)
                pe.wait_ge(w_in, W_ALL)
                pe.wait_ge(up_ready, 1)
                for k in range(3):
                    n = 32 if k < 2 else 16
                    if k:
                        pe.wait_ge(fused_sb, k)
                    for c in range(KC):
                        for h in range(HEADS):
                            last = nc.tensor.matmul(S[0][:, c, h * n:(h + 1) * n], down[:, k, h, c * P:(c + 1) * P],
                                                    up[:, k, 0:n], start=True, stop=True)
                    last.then_inc(fused, 1)
                pe.wait_ge(fused_sb, 3)
                pe.wait_ge(const_ready, 1)
                with pe.Fori(0, NB // U) as i:
                    for u in range(U):
                        pe.wait_ge(x_loaded[u], 16 * i + 16)
                        pe.wait_ge(r_ready, before(i, u))
                        for c in range(KC):
                            last = nc.tensor.transpose(W[u][:, c * T:(c + 1) * T], x_t[:, u, c * P:(c + 1) * P],
                                                       ident[:T, :T])
                        last.then_inc(x_turned, 1)
                    for u in range(U):
                        pe.wait_ge(xT_ready, done(i, u))
                        pe.wait_ge(prob_ready, before(i, u, G - 1, G))
                        for k, wm in ((0, wq), (1, wk)):
                            for turned in range(2):
                                for g in range(KC):
                                    col = (turned * KC + g) * T
                                    for c in range(KC):
                                        nc.tensor.matmul(S[u][:, k, col:col + T], wm[:, turned, c, g * P:(g + 1) * P],
                                                         xT[:, u, c, :], start=(c == 0), stop=(c == KC - 1))
                        for c in range(KC):
                            last = nc.tensor.matmul(S[u][:T, 2, 0:D], xT[:, u, c, :], wv[:, c, :],
                                                    start=(c == 0), stop=(c == KC - 1))
                        last.then_inc(qkv_done, 1)

                    def attend(j):
                        for u in range(U):
                            pe.wait_ge(prob_ready, done(i, u, j, G))
                            pe.wait_ge(max_ready, done(i, u, j, G))
                            nc.tensor.matmul(W[u][:, 0:GW], v1[:, u, j, :], prob[:, u, :],
                                             start=True, stop=True).then_inc(av_done, 1)

                    for j in range(G):
                        bank = j % 3
                        for u in range(U):
                            if j == 0:
                                pe.wait_ge(qk_rot, done(i, u))
                                pe.wait_ge(v_ready, done(i, u))
                                pe.wait_ge(qbd_ready, done(i, u))
                            g, h0 = j // 2, 4 * (j % 2)
                            nc.tensor.matmul(S[u][:T, bank, 0:GW], qkT[:, u, 1, g, :],
                                             q_bd[:, u, g, h0:h0 + 4, :].rearrange("p h t -> p (h t)"),
                                             start=True, stop=False)
                            nc.tensor.matmul(S[u][:T, bank, 0:GW], identb[:T, :T],
                                             causal[:].rearrange("p h t -> p (h t)"), start=False, stop=True).then_inc(scored, 1)
                        if j:
                            attend(j - 1)
                        for u in range(U):
                            pe.wait_ge(mx_copied, done(i, u, j, G))
                            if j:
                                pe.wait_ge(own_ready, done(i, u, j - 1, G))
                            for h in range(HPG):
                                last = nc.tensor.transpose(W[u][:T, h * P:h * P + T], mx[:, u, h * T:(h + 1) * T],
                                                           ident[:T, :T])
                            last.then_inc(mx_turned, 1)
                        for u in range(U):
                            pe.wait_ge(max_ready, done(i, u, j, G))
                            nc.tensor.matmul(S[u][:T, bank, 0:GW], neg1[:], dmax[:, u, :, :].rearrange("p h t -> p (h t)"),
                                             start=False, stop=True, skip_group_check=True).then_inc(shifted, 1)
                    attend(G - 1)
                    for u in range(U):
                        pe.wait_ge(yT_ready, done(i, u, G - 1, G))
                        for c in range(KC):
                            last = nc.tensor.matmul(W[u][:T, 0:D], yT[:, u, c, :], wc[:, c, :],
                                                    start=(c == 0), stop=(c == KC - 1))
                        last.then_inc(y_done, 1)

            @block.scalar
            def _(act):
                act.sem_inc(xT_ready, U)
                act.sem_inc(v_ready, U)
                act.sem_inc(mx_copied, 2 * G)
                act.sem_inc(prob_ready, 2 * G)
                for u in range(U):
                    act.sem_inc(stored[u], 16)
                for k in range(3):
                    act.wait_ge(fused, k + 1)
                    for c in range(KC):
                        if k < 2:
                            src = S[0][:, c, :].rearrange("p (h n) -> p h n", n=32)
                            dst = (wq, wk)[k]
                            for t in range(2):
                                last = nc.scalar.activation(dst[:, t, c, :].rearrange("p (h n) -> p h n", n=16),
                                                            src[:, :, 16 * t:16 * t + 16], ACT.Copy)
                        else:
                            last = nc.scalar.activation(wv[:, c, :], S[0][:, c, 0:D], ACT.Copy)
                    last.then_inc(fused_sb, 1)
                with act.Fori(0, NB // U) as i:
                    for u in range(U):
                        act.wait_ge(x_turned, done(i, u))
                        act.wait_ge(qkv_done, before(i, u))
                        nc.scalar.activation(xT[:, u, :, :].rearrange("p c t -> p (c t)"), W[u][:, 0:KC * T],
                                             ACT.Copy).then_inc(xT_ready, 1)
                    for u in range(U):
                        act.wait_ge(qkv_done, done(i, u))
                        act.wait_ge(av_done, before(i, u, G - 1, G))
                        nc.scalar.activation(v1[:, u, :, 0:64], S[u][:T, 2, 0:D].rearrange("p (g n) -> p g n", n=64),
                                             ACT.Copy).then_inc(v_ready, 1)
                    for j in range(G):
                        bank = j % 3
                        for u in range(U):
                            act.wait_ge(scored, done(i, u, j, G))
                            nc.scalar.activation(mx[:, u, :], S[u][:T, bank, 0:GW], ACT.Copy).then_inc(mx_copied, 1)
                        for u in range(U):
                            act.wait_ge(shifted, done(i, u, j, G))
                            if j:
                                act.wait_ge(av_done, done(i, u, j - 1, G))
                            nc.scalar.activation(prob[:, u, :], S[u][:T, bank, 0:GW], ACT.Exp,
                                                 scale=float(DH) ** -0.5).then_inc(prob_ready, 1)
                    for u in range(U):
                        act.wait_ge(out_ready, done(i, u))
                        act.dma_start(x_out[U * i + u], x_o[:, u, :]).then_inc(stored[u], 16)
                for u in range(U):
                    act.wait_ge(stored[u], 16 * (NB // U) + 16)

            @block.gpsimd
            def _(pool):
                pool.sem_inc(qk_ready, U)
                pool.sem_inc(qbd_ready, U)
                norm.set_power(pool)
                with pool.Fori(0, NB // U) as i:
                    for u in range(U):
                        pool.wait_ge(qk_rot, done(i, u))
                        pool.wait_ge(scored, before(i, u, G - 1, G))
                        nc.gpsimd.tensor_tensor(qkT[:, u, :, :, :].rearrange("p a c t -> p (a c t)"),
                                                qk_c[:, u, :, :, :].rearrange("p a c t -> p (a c t)"),
                                                qk_s[:, u, :, :, :].rearrange("p a c t -> p (a c t)"),
                                                ALU.add).then_inc(qk_ready, 1)
                    for u in range(U):
                        pool.wait_ge(qk_ready, done(i, u))
                        pool.wait_ge(scored, before(i, u, G - 1, G))
                        for g in range(KC):
                            last = nc.gpsimd.tensor_tensor(q_bd[:, u, g, :, :],
                                                           qkT[:, u, 0, g, :].unsqueeze(1).to_broadcast([P, 8, T]),
                                                           head_mask[:].unsqueeze(2).to_broadcast([P, 8, T]), ALU.mult)
                        last.then_inc(qbd_ready, 1)
                    norm.raise_power(pool, i)

            @block.vector
            def _(dve):
                nc.vector.memset(v1[:], 1.0)
                nc.vector.memset(neg1[:].bitcast(F32), -1.0)
                for sem, steps in ((qk_rot, 1), (max_ready, G), (own_ready, G), (yT_ready, G), (r_ready, 1),
                                   (out_ready, 1)):
                    dve.sem_inc(sem, U * steps)
                dve.wait_ge(w_in, W_ALL)
                nc.vector.memset(up[:, 0:2, 16:24], 0.0)
                for k in range(2):
                    e = up[:, k, 8:16].rearrange("p (n two) -> p n two", two=2)
                    t = up[:, k, 24:32].rearrange("p (n two) -> p n two", two=2)
                    nc.vector.tensor_scalar(t[:, :, 0], e[:, :, 1], -1.0, None, ALU.mult)
                    last = nc.vector.tensor_copy(t[:, :, 1], e[:, :, 0])
                last.then_inc(up_ready, 1)
                nc.vector.tensor_copy(identb[:], ident[:])
                nc.vector.tensor_copy(causal[:], causalf[:].unsqueeze(1).to_broadcast([T, HPG, T])).then_inc(const_ready, 1)
                with dve.Fori(0, NB // U) as i:
                    links = Links(dve, vlink, i, 2 * 3 * G + 2 * 2)
                    for u in range(U):
                        dve.wait_ge(qkv_done, done(i, u))
                        dve.wait_ge(qk_ready, before(i, u))
                        for k in range(2):
                            src = S[u][:, k, 0:4 * T].rearrange("p (r g t) -> p r g t", r=2, t=T)
                            nc.vector.tensor_tensor(qk_c[:, u, k, :, :], src[:, 0], cosT[:].unsqueeze(1).to_broadcast([P, KC, T]), ALU.mult)
                            last = nc.vector.tensor_tensor(qk_s[:, u, k, :, :], src[:, 1], sinT[:].unsqueeze(1).to_broadcast([P, KC, T]), ALU.mult)
                        last.then_inc(qk_rot, 1)

                    def normalise(j):
                        for u in range(U):
                            dve.wait_ge(av_done, done(i, u, j, G))
                            nc.vector.tensor_tensor(own[:, u, :].rearrange("p (h t) -> p h t", t=T),
                                                    W[u][:, 0:GW].rearrange("p (h t) -> p h t", t=T),
                                                    head_mask2[:].unsqueeze(2).to_broadcast([P, HPG, T]), ALU.mult)\
                                .then_inc(own_ready, 1)
                        for u in range(U):
                            dve.wait_ge(own_ready, done(i, u, j, G))
                            links.add(nc.vector.tensor_reduce(nd[:, u, :], own[:, u, :].rearrange("p (h t) -> p t h", t=T),
                                                              axis=AXIS_X, op=ALU.add))
                        links.wait()
                        for u in range(U):
                            links.add(nc.vector.reciprocal(rec[:, u, :], nd[64:128, u, :]))
                        links.wait()
                        o = 64 * (j % 2)
                        for u in range(U):
                            if j == 0:
                                dve.wait_ge(y_done, before(i, u))
                            nc.vector.tensor_tensor(yT[o:o + 64, u, j // 2, :], nd[0:64, u, :], rec[:, u, :],
                                                    ALU.mult).then_inc(yT_ready, 1)

                    for j in range(G):
                        if j:
                            normalise(j - 1)
                        for u in range(U):
                            dve.wait_ge(mx_turned, done(i, u, j, G))
                            links.add(nc.vector.tensor_reduce(nmax[:, u, :], W[u][:T, :].rearrange("p (h t) -> p h t", t=P)[:, :, 0:T],
                                                              axis=AXIS_X, op=ALU.max))
                        links.wait()
                        for u in range(U):
                            if j:
                                dve.wait_ge(shifted, done(i, u, j - 1, G))
                            nc.vector.tensor_tensor(dmax[:, u, :, :], ident[:T, :T].unsqueeze(1).to_broadcast([T, HPG, T]),
                                                    nmax[:, u, :].unsqueeze(2).to_broadcast([T, HPG, T]),
                                                    ALU.mult).then_inc(max_ready, 1)
                    normalise(G - 1)
                    for u in range(U):
                        dve.wait_ge(y_done, done(i, u))
                        dve.wait_ge(res_loaded[u], 16 * i + 16)
                        nc.vector.tensor_tensor(r[:, u, :], W[u][:T, 0:D], x_res[:, u, :], ALU.add).then_inc(r_ready, 1)
                    dve.wait_ge(r_ready, done(i, U - 1))
                    for u in range(U):
                        dve.wait_ge(stored[u], 16 * i + 16)
                    norm.steps(dve, links, i, r, x_o, out_ready)
                    links.end()
def cross_attention_strided(nc, NB, x_in, x_out, w, src_len):
    NH = 8
    HD = D // NH
    KPH = -(-src_len // NH)
    KFULL = src_len - (KPH - 1) * NH
    assert KFULL == 1
    SLOT = 64
    PAIRS = NH // 2
    VW = 96
    with ExitStack() as ctx:
        U = 4
        done, before = counts(U)
        s = Store(nc, ctx, "xs", U)
        wq = s.sb("wq", [P, KC, D])
        wk = s.sb("wk", [P, KC, D])
        wv = s.sb("wv", [P, KC, D + 64])
        wo = s.sb("wo", [P, KC, D])
        bq = s.sb("bq", [P, KC])
        bk = s.sb("bk", [P, KC])
        bv = s.sb("bv", [P, KC])
        bo = s.sb("bo", [T, D])
        ident = s.sb("ident", [P, P])
        head_mask = s.sb("head_mask", [P, 4])
        x_t = s.sb("x_t", [T, U, D])
        x_res = s.sb("x_res", [T, U, D])
        x_bo = s.sb("x_bo", [T, U, D])
        xT = s.sb("xT", [P, U, KC, T])
        ctxT = s.sb("ctxT", [P, U, KC, NH, SLOT])
        qT = s.sb("qT", [P, U, KC, T])
        q_bd = s.sb("q_bd", [P, U, KC, 4, T])
        kT = s.sb("kT", [P, U, KC, NH, KPH])
        v_bd = s.sb("v_bd", [P, U, PAIRS, VW])
        smax = s.sb("smax", [T, U, NH])
        prob = s.sb("prob", [T, U, NH, SLOT])
        pT = s.sb("pT", [P, U, PAIRS, T])
        rec = s.sb("rec", [T, U, NH])
        y = s.sb("y", [T, U, D])
        yT = s.sb("yT", [P, U, KC, T])
        r = s.sb("r", [T, U, D])
        x_o = s.sb("x_o", [T, U, D])
        norm = Norm(s, nc)
        B = [[s.ps(f"B{b}_{u}", [P, 512]) for b in range(2)] for u in range(U)]

        w_in = s.sem("weights_loaded")
        const_ready = s.sem("const_ready")
        x_loaded, res_loaded, ctx_loaded, stored = s.sems("x_loaded"), s.sems("res_loaded"), s.sems("ctx_loaded"), s.sems("stored")
        x_turned, xT_ready = s.sem("x_turned"), s.sem("xT_ready")
        k_done, q_done, v_done = s.sem("k_done"), s.sem("q_done"), s.sem("v_done")
        q_ready, k_ready, v_ready = s.sem("q_ready"), s.sem("k_ready"), s.sem("v_ready")
        qbd_ready = s.sem("qbd_ready")
        xbo_ready = s.sem("xbo_ready")
        scored = s.sem("scored")
        less_ready = s.sem("less_ready")
        prob_ready = s.sem("prob_ready")
        p_turned, pT_ready = s.sem("p_turned"), s.sem("pT_ready")
        av_done = s.sem("av_done")
        y_ready = s.sem("y_ready")
        y_turned, yT_ready = s.sem("y_turned"), s.sem("yT_ready")
        o_done, r_ready, out_ready = s.sem("o_done"), s.sem("r_ready"), s.sem("out_ready")
        vlink = s.sem("dve_link")

        loads = [(wq[:], w["L0_xattn_Wq"].rearrange("(k p) n -> p k n", p=P)),
                 (wk[:], w["L0_xattn_Wk"].rearrange("(k p) n -> p k n", p=P)),
                 (wv[:, :, 0:D], w["L0_xattn_Wv"].rearrange("(k p) n -> p k n", p=P)),
                 (wo[:], w["L0_xattn_Wo"].rearrange("(k p) n -> p k n", p=P)),
                 (bq[:], w["L0_xattn_bq"]), (bk[:], w["L0_xattn_bk"]), (bv[:], w["L0_xattn_bv"]),
                 (bo[:], w["L0_xattn_bo"].to_broadcast([T, D])),
                 (ident[:], w["ident"]), (head_mask[:], w["head_mask4"]),
                 *[(v_bd[:, u], w["v_ones"]) for u in range(U)]]
        W_ALL = 16 * len(loads)
        SC = float(1.0 / np.sqrt(np.float32(HD)))

        with nc.Block() as block:

            @block.sync
            def _(sp):
                for dst, src in loads:
                    sp.dma_start(dst, src).then_inc(w_in, 16)
                with sp.Fori(0, NB // U) as i:
                    for u in range(U):
                        sp.wait_ge(x_turned, before(i, u))
                        sp.dma_start(x_t[:, u, :], x_in[U * i + u]).then_inc(x_loaded[u], 16)
                        sp.wait_ge(v_done, before(i, u))
                        sp.dma_start(ctxT[:, u].rearrange("p k h s -> p k (h s)"), w["ctxT"][U * i + u]).then_inc(ctx_loaded[u], 16)
                    for u in range(U):
                        sp.wait_ge(xbo_ready, before(i, u))
                        sp.dma_start(x_res[:, u, :], x_in[U * i + u]).then_inc(res_loaded[u], 16)

            @block.tensor
            def _(pe):
                for sem in (x_turned, k_done, q_done, v_done, scored, p_turned, av_done, y_turned, o_done):
                    pe.sem_inc(sem, U)
                pe.wait_ge(w_in, W_ALL)
                pe.wait_ge(const_ready, 1)
                with pe.Fori(0, NB // U) as i:
                    for u in range(U):
                        pe.wait_ge(x_loaded[u], 16 * i + 16)
                        pe.wait_ge(r_ready, before(i, u))
                        for c in range(KC):
                            last = nc.tensor.transpose(B[u][1][:, c * T:(c + 1) * T], x_t[:, u, c * P:(c + 1) * P], ident[:T, :T])
                        last.then_inc(x_turned, 1)
                    for u in range(U):
                        pe.wait_ge(ctx_loaded[u], 16 * i + 16)
                        pe.wait_ge(xT_ready, done(i, u))
                        for g in range(KC):
                            for c in range(KC):
                                last = nc.tensor.matmul(B[u][g][:, 0:NH * KPH], wk[:, c, g * P:(g + 1) * P],
                                                        ctxT[:, u, c, :, 0:KPH], start=(c == 0), stop=(c == KC - 1))
                        last.then_inc(k_done, 1)
                    for u in range(U):
                        pe.wait_ge(k_ready, done(i, u))
                        for g in range(KC):
                            for c in range(KC):
                                last = nc.tensor.matmul(B[u][1][:, g * T:(g + 1) * T], wq[:, c, g * P:(g + 1) * P],
                                                        xT[:, u, c, :], start=(c == 0), stop=(c == KC - 1))
                        last.then_inc(q_done, 1)
                        for p in range(PAIRS):
                            for c in range(KC):
                                last = nc.tensor.matmul(B[u][0][:, p * P:(p + 1) * P],
                                                        ctxT[:, u, c, 2 * p:2 * p + 2, :].rearrange("p h s -> p (h s)"),
                                                        wv[:, c, 64 * p:64 * p + P], start=(c == 0), stop=(c == KC - 1))
                        last.then_inc(v_done, 1)
                    for u in range(U):
                        pe.wait_ge(qbd_ready, done(i, u))
                        for h in range(NH):
                            last = nc.tensor.matmul(B[u][1][:T, h * KPH:(h + 1) * KPH], q_bd[:, u, h // 4, h % 4, :],
                                                    kT[:, u, h // 4, h, :], start=True, stop=True)
                        last.then_inc(scored, 1)
                    for u in range(U):
                        pe.wait_ge(prob_ready, done(i, u))
                        pe.wait_ge(v_ready, done(i, u))
                        for p in range(PAIRS):
                            last = nc.tensor.transpose(B[u][0][:, p * T:(p + 1) * T],
                                                       prob[:, u, 2 * p:2 * p + 2, :].rearrange("p h s -> p (h s)"), ident[:T, :T])
                        last.then_inc(p_turned, 1)
                    for u in range(U):
                        pe.wait_ge(pT_ready, done(i, u))
                        for p in range(PAIRS):
                            last = nc.tensor.matmul(B[u][1][:T, p * VW:(p + 1) * VW], pT[:, u, p, :], v_bd[:, u, p, :],
                                                    start=True, stop=True)
                        last.then_inc(av_done, 1)
                    for u in range(U):
                        pe.wait_ge(y_ready, done(i, u))
                        for c in range(KC):
                            last = nc.tensor.transpose(B[u][0][:, c * T:(c + 1) * T], y[:, u, c * P:(c + 1) * P], ident[:T, :T])
                        last.then_inc(y_turned, 1)
                    for u in range(U):
                        pe.wait_ge(yT_ready, done(i, u))
                        for c in range(KC):
                            last = nc.tensor.matmul(B[u][1][:T, 0:D], yT[:, u, c, :], wo[:, c, :],
                                                    start=(c == 0), stop=(c == KC - 1))
                        last.then_inc(o_done, 1)

            @block.scalar
            def _(act):
                for sem in (xT_ready, q_ready, k_ready, v_ready, prob_ready, pT_ready, yT_ready):
                    act.sem_inc(sem, U)
                for u in range(U):
                    act.sem_inc(stored[u], 16)
                act.wait_ge(w_in, W_ALL)
                with act.Fori(0, NB // U) as i:
                    for u in range(U):
                        act.wait_ge(x_turned, done(i, u))
                        nc.scalar.activation(xT[:, u, :, :].rearrange("p c t -> p (c t)"), B[u][1][:, 0:KC * T],
                                             ACT.Copy).then_inc(xT_ready, 1)
                    for u in range(U):
                        act.wait_ge(k_done, done(i, u))
                        for g in range(KC):
                            last = nc.scalar.activation(kT[:, u, g, :, :].rearrange("p h s -> p (h s)"), B[u][g][:, 0:NH * KPH],
                                                        ACT.Identity, bias=bk[:, g:g + 1])
                        last.then_inc(k_ready, 1)
                    for u in range(U):
                        act.wait_ge(q_done, done(i, u))
                        act.wait_ge(qbd_ready, before(i, u))
                        for g in range(KC):
                            last = nc.scalar.activation(qT[:, u, g, :], B[u][1][:, g * T:(g + 1) * T], ACT.Identity, bias=bq[:, g:g + 1])
                        last.then_inc(q_ready, 1)
                        act.wait_ge(v_done, done(i, u))
                        v = B[u][0][:, :].rearrange("p (n f) -> p n f", f=P)
                        nc.scalar.activation(v_bd[0:KPH, u, :, 0:HD], v[0:KPH, :, 0:HD], ACT.Copy)
                        nc.scalar.activation(v_bd[SLOT:SLOT + KPH, u, :, HD + 1:2 * HD + 1], v[SLOT:SLOT + KPH, :, HD:2 * HD],
                                             ACT.Copy).then_inc(v_ready, 1)
                    for u in range(U):
                        act.wait_ge(less_ready, done(i, u))
                        nc.scalar.activation(prob[:, u, :, 0:KPH - 1], prob[:, u, :, 0:KPH - 1], ACT.Exp, scale=SC)
                        nc.scalar.activation(prob[:, u, 0, KPH - 1:KPH], prob[:, u, 0, KPH - 1:KPH], ACT.Exp,
                                             scale=SC).then_inc(prob_ready, 1)
                    for u in range(U):
                        act.wait_ge(p_turned, done(i, u))
                        nc.scalar.activation(pT[:, u, :, :].rearrange("p n t -> p (n t)"), B[u][0][:, 0:PAIRS * T],
                                             ACT.Copy).then_inc(pT_ready, 1)
                    for u in range(U):
                        act.wait_ge(y_turned, done(i, u))
                        for g in range(KC):
                            last = nc.scalar.activation(yT[:, u, g, :], B[u][0][:, g * T:(g + 1) * T], ACT.Identity, bias=bv[:, g:g + 1])
                        last.then_inc(yT_ready, 1)
                    for u in range(U):
                        act.wait_ge(out_ready, done(i, u))
                        act.dma_start(x_out[U * i + u], x_o[:, u, :]).then_inc(stored[u], 16)
                for u in range(U):
                    act.wait_ge(stored[u], 16 * (NB // U) + 16)

            @block.gpsimd
            def _(pool):
                nc.gpsimd.memset(wv[:, :, D:D + 64], 0.0)
                nc.gpsimd.memset(prob[:], 0.0).then_inc(const_ready, 1)
                pool.sem_inc(qbd_ready, U)
                pool.sem_inc(xbo_ready, U)
                norm.set_power(pool)
                pool.wait_ge(w_in, W_ALL)
                with pool.Fori(0, NB // U) as i:
                    for u in range(U):
                        pool.wait_ge(q_ready, done(i, u))
                        pool.wait_ge(scored, before(i, u))
                        for g in range(KC):
                            last = nc.gpsimd.tensor_tensor(q_bd[:, u, g, :, :],
                                                           qT[:, u, g, :].unsqueeze(1).to_broadcast([P, 4, T]),
                                                           head_mask[:].unsqueeze(2).to_broadcast([P, 4, T]), ALU.mult)
                        last.then_inc(qbd_ready, 1)
                    for u in range(U):
                        pool.wait_ge(res_loaded[u], 16 * i + 16)
                        pool.wait_ge(r_ready, before(i, u))
                        nc.gpsimd.tensor_tensor(x_bo[:, u, :], x_res[:, u, :], bo[:], ALU.add).then_inc(xbo_ready, 1)
                    norm.raise_power(pool, i)

            @block.vector
            def _(dve):
                for sem in (less_ready, y_ready, r_ready, out_ready):
                    dve.sem_inc(sem, U)
                dve.wait_ge(const_ready, 1)
                with dve.Fori(0, NB // U) as i:
                    links = Links(dve, vlink, i, 20)
                    for u in range(U):
                        dve.wait_ge(scored, done(i, u))
                        sc = B[u][1][:T, 0:NH * KPH].rearrange("p (h s) -> p h s", s=KPH)
                        links.add(nc.vector.tensor_reduce(smax[:, u, :], sc[:, :, 0:KPH - 1], axis=AXIS_X, op=ALU.max))
                    links.wait()
                    for u in range(U):
                        links.add(nc.vector.tensor_tensor(smax[:, u, 0:1], smax[:, u, 0:1], B[u][1][:T, KPH - 1:KPH], ALU.max))
                    links.wait()
                    for u in range(U):
                        sc = B[u][1][:T, 0:NH * KPH].rearrange("p (h s) -> p h s", s=KPH)
                        dve.wait_ge(p_turned, before(i, u))
                        nc.vector.tensor_tensor(prob[:, u, :, 0:KPH - 1], sc[:, :, 0:KPH - 1],
                                                smax[:, u, :].unsqueeze(2).to_broadcast([T, NH, KPH - 1]), ALU.subtract)
                        nc.vector.tensor_tensor(prob[:, u, 0, KPH - 1:KPH], sc[:, 0, KPH - 1:KPH], smax[:, u, 0:1],
                                                ALU.subtract).then_inc(less_ready, 1)
                    for u in range(U):
                        dve.wait_ge(av_done, done(i, u))
                        av = B[u][1][:T, 0:PAIRS * VW].rearrange("p (n c) -> p n c", c=VW)[:, :, 0:2 * (HD + 1)]\
                            .rearrange("p n (two c) -> p n two c", c=HD + 1)
                        links.add(nc.vector.reciprocal(rec[:, u, :].rearrange("p (n two) -> p n two", two=2), av[:, :, :, HD]))
                    links.wait()
                    for u in range(U):
                        av = B[u][1][:T, 0:PAIRS * VW].rearrange("p (n c) -> p n c", c=VW)[:, :, 0:2 * (HD + 1)]\
                            .rearrange("p n (two c) -> p n two c", c=HD + 1)
                        dve.wait_ge(y_turned, before(i, u))
                        nc.vector.tensor_tensor(y[:, u, :].rearrange("p (n two c) -> p n two c", two=2, c=HD), av[:, :, :, 0:HD],
                                                rec[:, u, :].rearrange("p (n two) -> p n two", two=2).unsqueeze(3).to_broadcast([T, PAIRS, 2, HD]),
                                                ALU.mult).then_inc(y_ready, 1)
                    for u in range(U):
                        dve.wait_ge(o_done, done(i, u))
                        dve.wait_ge(xbo_ready, done(i, u))
                        nc.vector.tensor_tensor(r[:, u, :], B[u][1][:T, 0:D], x_bo[:, u, :], ALU.add).then_inc(r_ready, 1)
                    dve.wait_ge(r_ready, done(i, U - 1))
                    for u in range(U):
                        dve.wait_ge(stored[u], 16 * i + 16)
                    norm.steps(dve, links, i, r, x_o, out_ready)
                    links.end()


EXPERTS = 64
TOPK = 6
CAP = 128
SLOTS = EXPERTS * CAP
FE = 176
FS = 352
HC = 88
FAR = 65536.0


def route(nc, NB, x_in, w, slot_rows, xz, slot_ids, slot_weights):
    with ExitStack() as ctx:
        U = 4
        done, before = counts(U)
        s = Store(nc, ctx, "rt", U)
        gate = s.sb("gate", [P, KC, EXPERTS])
        gate_b = s.sb("gate_b", [T, EXPERTS])
        ws1 = s.sb("ws1", [P, KC, FS])
        ws3 = s.sb("ws3", [P, KC, FS])
        ws2 = s.sb("ws2", [HC, FS // HC, D])
        ident = s.sb("ident", [P, P])
        earlier = s.sb("earlier", [T, T])
        ones = s.sb("ones", [T, T])
        expert_no = s.sb("expert_no", [T, EXPERTS])
        first_slot = s.sb("first_slot", [T, EXPERTS])
        x_t = s.sb("x_t", [T, U, D])
        xT = s.sb("xT", [P, U, KC, T])
        nmax = s.sb("nmax", [T, U])
        spare = s.sb("spare", [T, 1])
        esum = s.sb("esum", [T, U])
        rec = s.sb("rec", [T, U])
        e = s.sb("e", [T, U, EXPERTS])
        probs = s.sb("probs", [T, U, EXPERTS])
        biased = s.sb("biased", [T, U, EXPERTS])
        top = s.sb("top", [T, U, 8])
        top_i = s.sb("top_i", [T, U, 8], U32)
        top_f = s.sb("top_f", [T, U, TOPK])
        hot = s.sb("hot", [T, U, TOPK, EXPERTS])
        chosen = s.sb("chosen", [T, U, EXPERTS])
        sofar = s.sb("sofar", [T, U, EXPERTS])
        over = s.sb("over", [T, U, EXPERTS])
        slot_e = s.sb("slot_e", [T, U, EXPERTS])
        picked = s.sb("picked", [T, U, 2, TOPK, EXPERTS])
        slot_w = s.sb("slot_w", [T, U, 2, TOPK])
        slot_u = s.sb("slot_u", [T, U, TOPK], U32)
        gat_u = s.sb("gat_u", [T, U, TOPK], U32)
        w_keep = s.sb("w_keep", [T, U, TOPK])
        th = s.sb("th", [HC, U, 4 * T])
        h1 = s.sb("h1", [HC, U, 4 * T])
        hT = s.sb("hT", [HC, U, 4, T])
        x_z = s.sb("x_z", [T, U, D])
        zero = s.sb("zero", [P, 8, D])
        B = [[s.ps(f"B{b}_{u}", [P, 512]) for b in range(2)] for u in range(U)]

        w_in = s.sem("weights_loaded")
        scatter_over, routes_seen = s.sem("scatter_over"), s.sem("routes_seen")
        zero_set = s.sem("zero_set")
        zeroed = s.sem("slots_zeroed")
        ones_set = s.sem("ones_set")
        x_loaded, scattered, kept, z_stored = s.sems("x_loaded"), s.sems("scattered"), s.sems("routes_kept"), s.sems("z_stored")
        x_turned, xT_ready = s.sem("x_turned"), s.sem("xT_ready")
        gated, up_done, ranked, z_done = s.sem("gated"), s.sem("up_done"), s.sem("ranked"), s.sem("z_done")
        nmax_ready, chosen_ready, h_ready, routes_ready = s.sem("nmax_ready"), s.sem("chosen_ready"), s.sem("h_ready"), s.sem("routes_ready")
        gate_read = s.sem("gate_read")
        slots_known = s.sem("slots_known")
        th_ready = s.sem("th_ready")
        xz_ready = s.sem("xz_ready")
        vlink = s.sem("dve_link")

        loads = [(gate[:], w["gate_wT"].rearrange("(k p) n -> p k n", p=P)),
                 (gate_b[:], w["gate_b"].to_broadcast([T, EXPERTS])),
                 (ws1[:], w["ws1T"].rearrange("(k p) n -> p k n", p=P)),
                 (ws3[:], w["ws3T"].rearrange("(k p) n -> p k n", p=P)),
                 (ws2[:], w["ws2T"].rearrange("(k p) n -> p k n", p=HC)),
                 (ident[:], w["ident"]), (earlier[:], w["earlier"]),
                 (expert_no[:], w["expert_no"]), (first_slot[:], w["first_slot"])]
        W_ALL = 16 * len(loads)

        with nc.Block() as block:

            @block.sync
            def _(sp):
                for dst, src in loads:
                    sp.dma_start(dst, src).then_inc(w_in, 16)
                sp.wait_ge(zero_set, 1)
                z = slot_rows.rearrange("(n p r) d -> n p r d", p=P, r=8)
                for n in range(SLOTS // (P * 8)):
                    sp.dma_start(z[n], zero[:]).then_inc(zeroed, 16)
                with sp.Fori(0, NB // U) as i:
                    for u in range(U):
                        sp.wait_ge(xz_ready, before(i, u))
                        sp.wait_ge(scatter_over, before(i, u))
                        sp.dma_start(x_t[:, u, :], x_in[U * i + u]).then_inc(x_loaded[u], 16)

            @block.tensor
            def _(pe):
                for sem in (x_turned, gated, up_done, ranked, z_done):
                    pe.sem_inc(sem, U)
                pe.wait_ge(w_in, W_ALL)
                pe.wait_ge(ones_set, 1)
                with pe.Fori(0, NB // U) as i:
                    for u in range(U):
                        pe.wait_ge(x_loaded[u], 16 * i + 16)
                        pe.wait_ge(slots_known, before(i, u))
                        for c in range(KC):
                            last = nc.tensor.transpose(B[u][1][:, c * T:(c + 1) * T], x_t[:, u, c * P:(c + 1) * P], ident[:T, :T])
                        last.then_inc(x_turned, 1)
                    for u in range(U):
                        pe.wait_ge(xT_ready, done(i, u))
                        pe.wait_ge(xz_ready, before(i, u))
                        for c in range(KC):
                            last = nc.tensor.matmul(B[u][0][:T, 0:EXPERTS], xT[:, u, c, :], gate[:, c, :],
                                                    start=(c == 0), stop=(c == KC - 1))
                        last.then_inc(gated, 1)
                    for u in range(U):
                        pe.wait_ge(gate_read, done(i, u))
                        for b, ws in ((0, ws1), (1, ws3)):
                            for m in range(FS // HC):
                                for c in range(KC):
                                    last = nc.tensor.matmul(B[u][b][:HC, m * T:(m + 1) * T], ws[:, c, m * HC:(m + 1) * HC],
                                                            xT[:, u, c, :], start=(c == 0), stop=(c == KC - 1))
                        last.then_inc(up_done, 1)
                    for u in range(U):
                        pe.wait_ge(h_ready, done(i, u))
                        pe.wait_ge(chosen_ready, done(i, u))
                        nc.tensor.matmul(B[u][1][:T, 0:EXPERTS], earlier[:], chosen[:, u, :], start=True, stop=False)
                        nc.tensor.matmul(B[u][1][:T, 0:EXPERTS], ones[:], sofar[:, u, :], start=False,
                                         stop=True).then_inc(ranked, 1)
                        for m in range(FS // HC):
                            last = nc.tensor.matmul(B[u][0][:T, 0:D], hT[:, u, m, :], ws2[:, m, :], start=(m == 0),
                                                    stop=(m == FS // HC - 1))
                        last.then_inc(z_done, 1)

            @block.scalar
            def _(act):
                for sem in (xT_ready, gate_read, th_ready):
                    act.sem_inc(sem, U)
                for u in range(U):
                    act.sem_inc(z_stored[u], 16)
                    act.sem_inc(kept[u], 32)
                with act.Fori(0, NB // U) as i:
                    for u in range(U):
                        act.wait_ge(x_turned, done(i, u))
                        act.wait_ge(up_done, before(i, u))
                        nc.scalar.activation(xT[:, u, :, :].rearrange("p c t -> p (c t)"), B[u][1][:, 0:KC * T],
                                             ACT.Copy).then_inc(xT_ready, 1)
                    for u in range(U):
                        act.wait_ge(nmax_ready, done(i, u))
                        nc.scalar.activation(e[:, u, :], B[u][0][:T, 0:EXPERTS], ACT.Exp, bias=nmax[:, u:u + 1],
                                             accum_out=esum[:, u:u + 1]).then_inc(gate_read, 1)
                    for u in range(U):
                        act.wait_ge(up_done, done(i, u))
                        act.wait_ge(h_ready, before(i, u))
                        nc.scalar.activation(th[:, u, :], B[u][0][:HC, 0:4 * T], ACT.Tanh, scale=0.5).then_inc(th_ready, 1)
                    for u in range(U):
                        act.wait_ge(routes_ready, done(i, u))
                        act.dma_start(slot_ids[U * i + u], gat_u[:, u, :]).then_inc(kept[u], 16)
                        act.dma_start(slot_weights[U * i + u], w_keep[:, u, :]).then_inc(kept[u], 16)
                    for u in range(U):
                        act.wait_ge(xz_ready, done(i, u))
                        act.dma_start(xz[U * i + u], x_z[:, u, :]).then_inc(z_stored[u], 16)
                for u in range(U):
                    act.wait_ge(z_stored[u], 16 * (NB // U) + 16)
                    act.wait_ge(kept[u], 32 * (NB // U) + 32)

            @block.gpsimd
            def _(pool):
                pool.sem_inc(scatter_over, U)
                nc.gpsimd.memset(ones[:], 1.0).then_inc(ones_set, 1)
                nc.gpsimd.memset(zero[:], 0.0).then_inc(zero_set, 1)
                pool.wait_ge(zeroed, 16 * (SLOTS // (P * 8)))
                with pool.Fori(0, NB // U) as i:
                    for u in range(U):
                        pool.wait_ge(routes_ready, done(i, u))
                        pool.sem_inc(routes_seen, 1)
                        for k in range(TOPK):
                            nc.gpsimd.indirect_dma_start(slot_rows, bass.IndirectOffsetOnAxis(slot_u[:, u, k:k + 1], 0),
                                                         x_t[:, u, :], None, bounds_check=SLOTS - 1,
                                                         oob_is_err=False).then_inc(scattered[u], 16)
                    for u in range(U):
                        pool.wait_ge(scattered[u], 16 * TOPK * i + 16 * TOPK)
                        pool.sem_inc(scatter_over, 1)

            @block.vector
            def _(dve):
                for sem in (nmax_ready, chosen_ready, slots_known, h_ready, routes_ready, xz_ready):
                    dve.sem_inc(sem, U)
                nc.vector.memset(sofar[:], 0.0)
                dve.wait_ge(w_in, W_ALL)
                with dve.Fori(0, NB // U) as i:
                    links = Links(dve, vlink, i, 56)
                    for u in range(U):
                        dve.wait_ge(gated, done(i, u))
                        nc.vector.tensor_reduce(nmax[:, u:u + 1], B[u][0][:T, 0:EXPERTS], axis=AXIS_X, op=ALU.max,
                                                negate=True).then_inc(nmax_ready, 1)
                    for u in range(U):
                        dve.wait_ge(gate_read, done(i, u))
                        links.add(nc.vector.reciprocal(rec[:, u:u + 1], esum[:, u:u + 1]))
                    links.wait()
                    for u in range(U):
                        links.add(nc.vector.tensor_scalar(probs[:, u, :], e[:, u, :], rec[:, u:u + 1], None, ALU.mult))
                    links.wait()
                    for u in range(U):
                        links.add(nc.vector.tensor_tensor(biased[:, u, :], probs[:, u, :], gate_b[:], ALU.add))
                    links.wait()
                    nc.vector.memset(spare[:], 0.0)
                    for u in range(U):
                        links.add(nc.vector.max(top[:, u, :], biased[:, u, :]))
                    links.wait()
                    nc.vector.memset(spare[:], 0.0)
                    for u in range(U):
                        links.add(nc.vector.max_index(top_i[:, u, :], top[:, u, :], biased[:, u, :]))
                    links.wait()
                    for u in range(U):
                        links.add(nc.vector.tensor_copy(top_f[:, u, :], top_i[:, u, 0:TOPK]))
                    links.wait()
                    for u in range(U):
                        links.add(nc.vector.tensor_tensor(hot[:, u, :, :], expert_no[:].unsqueeze(1).to_broadcast([T, TOPK, EXPERTS]),
                                                          top_f[:, u, :].unsqueeze(2).to_broadcast([T, TOPK, EXPERTS]), ALU.is_equal))
                    links.wait()
                    dve.wait_ge(ranked, before(i, U - 1))
                    for u in range(U):
                        nc.vector.tensor_reduce(chosen[:, u, :], hot[:, u, :, :].rearrange("p k e -> p e k"), axis=AXIS_X,
                                                op=ALU.add).then_inc(chosen_ready, 1)
                    for u in range(U - 1):
                        dve.wait_ge(chosen_ready, done(i, u))
                        links.add(nc.vector.tensor_tensor(sofar[:, u + 1, :], sofar[:, u, :], chosen[:, u, :], ALU.add))
                        links.wait()
                    for u in range(U):
                        dve.wait_ge(th_ready, done(i, u))
                        links.add(nc.vector.scalar_tensor_tensor(h1[:, u, :], th[:, u, :], 1.0, B[u][0][:HC, 0:4 * T],
                                                                 ALU.add, ALU.mult))
                    links.wait()
                    for u in range(U):
                        dve.wait_ge(z_done, before(i, u))
                        nc.vector.scalar_tensor_tensor(hT[:, u, :, :].rearrange("p m t -> p (m t)"), h1[:, u, :], 0.5,
                                                       B[u][1][:HC, 0:4 * T], ALU.mult, ALU.mult).then_inc(h_ready, 1)
                    for u in range(U):
                        dve.wait_ge(ranked, done(i, u))
                        rank = B[u][1][:T, 0:EXPERTS]
                        links.add(nc.vector.tensor_scalar(over[:, u, :], rank, float(CAP), FAR, ALU.is_ge, ALU.mult))
                        nc.vector.tensor_tensor(slot_e[:, u, :], rank, first_slot[:], ALU.add).then_inc(slots_known, 1)
                    links.add(nc.vector.tensor_tensor(sofar[:, 0, :], sofar[:, U - 1, :], chosen[:, U - 1, :], ALU.add))
                    links.wait()
                    for u in range(U):
                        dve.wait_ge(slots_known, done(i, u))
                        links.add(nc.vector.tensor_tensor(slot_e[:, u, :], slot_e[:, u, :], over[:, u, :], ALU.add))
                    links.wait()
                    for u in range(U):
                        for k, what in ((0, slot_e), (1, probs)):
                            links.add(nc.vector.tensor_tensor(picked[:, u, k, :, :], hot[:, u, :, :],
                                                              what[:, u, :].unsqueeze(1).to_broadcast([T, TOPK, EXPERTS]), ALU.mult))
                    links.wait()
                    for u in range(U):
                        links.add(nc.vector.tensor_reduce(slot_w[:, u, :, :], picked[:, u, :, :, :], axis=AXIS_X, op=ALU.add))
                    links.wait()
                    for u in range(U):
                        dve.wait_ge(scatter_over, before(i, u))
                        dve.wait_ge(kept[u], 32 * i + 32)
                        nc.vector.tensor_copy(slot_u[:, u, :], slot_w[:, u, 0, :])
                        nc.vector.tensor_scalar(gat_u[:, u, :], slot_w[:, u, 0, :], float(SLOTS - 1), None, ALU.min)
                        nc.vector.scalar_tensor_tensor(w_keep[:, u, :], slot_w[:, u, 0, :], float(SLOTS), slot_w[:, u, 1, :],
                                                       ALU.is_lt, ALU.mult).then_inc(routes_ready, 1)
                    for u in range(U):
                        dve.wait_ge(z_done, done(i, u))
                        dve.wait_ge(z_stored[u], 16 * i + 16)
                        nc.vector.tensor_tensor(x_z[:, u, :], B[u][0][:T, 0:D], x_t[:, u, :], ALU.add).then_inc(xz_ready, 1)
                    links.end()


def experts(nc, w, slot_rows, slot_out):
    with ExitStack() as ctx:
        U = 4
        done, before = counts(U)
        s = Store(nc, ctx, "ex", U)
        ident = s.sb("ident", [P, P])
        w1 = s.sb("w1", [P, U, KC, FE])
        w3 = s.sb("w3", [P, U, KC, FE])
        w2 = s.sb("w2", [HC, U, 2, D])
        x_t = s.sb("x_t", [P, U, D])
        xT = s.sb("xT", [P, U, KC, P])
        th = s.sb("th", [HC, U, 2 * P])
        h1 = s.sb("h1", [HC, U, 2 * P])
        hT = s.sb("hT", [HC, U, 2, P])
        y = s.sb("y", [P, U, D])
        B = [[s.ps(f"B{b}_{u}", [P, 512]) for b in range(2)] for u in range(U)]

        ident_in = s.sem("ident_loaded")
        up_loaded, down_loaded, x_loaded, stored = s.sems("up_loaded"), s.sems("down_loaded"), s.sems("x_loaded"), s.sems("stored")
        x_turned, xT_ready, up_done, y_done = s.sem("x_turned"), s.sem("xT_ready"), s.sem("up_done"), s.sem("y_done")
        th_ready, h1_ready, h_ready, y_ready = s.sem("th_ready"), s.sem("h1_ready"), s.sem("h_ready"), s.sem("y_ready")
        xs = slot_rows.rearrange("(e p) d -> e p d", p=P)
        ys = slot_out.rearrange("(e p) d -> e p d", p=P)

        with nc.Block() as block:

            @block.sync
            def _(sp):
                sp.dma_start(ident[:], w["ident"]).then_inc(ident_in, 16)
                with sp.Fori(0, EXPERTS // U) as i:
                    for u in range(U):
                        sp.wait_ge(x_turned, before(i, u))
                        sp.dma_start(x_t[:, u, :], xs[U * i + u]).then_inc(x_loaded[u], 16)
                        sp.wait_ge(up_done, before(i, u))
                        sp.dma_start(w1[:, u], w["w1T"][U * i + u].rearrange("(k p) n -> p k n", p=P)).then_inc(up_loaded[u], 16)
                        sp.dma_start(w3[:, u], w["w3T"][U * i + u].rearrange("(k p) n -> p k n", p=P)).then_inc(up_loaded[u], 16)
                        sp.wait_ge(y_done, before(i, u))
                        sp.dma_start(w2[:, u], w["w2T"][U * i + u].rearrange("(k p) n -> p k n", p=HC)).then_inc(down_loaded[u], 16)

            @block.tensor
            def _(pe):
                for sem in (x_turned, up_done, y_done):
                    pe.sem_inc(sem, U)
                pe.wait_ge(ident_in, 16)
                with pe.Fori(0, EXPERTS // U) as i:
                    for u in range(U):
                        pe.wait_ge(x_loaded[u], 16 * i + 16)
                        pe.wait_ge(y_ready, before(i, u))
                        for c in range(KC):
                            last = nc.tensor.transpose(B[u][1][:, c * P:(c + 1) * P], x_t[:, u, c * P:(c + 1) * P], ident[:])
                        last.then_inc(x_turned, 1)
                    for u in range(U):
                        pe.wait_ge(up_loaded[u], 32 * i + 32)
                        pe.wait_ge(xT_ready, done(i, u))
                        pe.wait_ge(h_ready, before(i, u))
                        for b, wu in ((0, w1), (2, w3)):
                            for m in range(2):
                                for c in range(KC):
                                    last = nc.tensor.matmul(B[u][0][:HC, (b + m) * P:(b + m + 1) * P], wu[:, u, c, m * HC:(m + 1) * HC],
                                                            xT[:, u, c, :], start=(c == 0), stop=(c == KC - 1))
                        last.then_inc(up_done, 1)
                    for u in range(U):
                        pe.wait_ge(down_loaded[u], 16 * i + 16)
                        pe.wait_ge(h_ready, done(i, u))
                        for m in range(2):
                            last = nc.tensor.matmul(B[u][1][:, 0:D], hT[:, u, m, :], w2[:, u, m, :], start=(m == 0), stop=(m == 1))
                        last.then_inc(y_done, 1)

            @block.scalar
            def _(act):
                for sem in (xT_ready, th_ready, y_ready):
                    act.sem_inc(sem, U)
                for u in range(U):
                    act.sem_inc(stored[u], 16)
                with act.Fori(0, EXPERTS // U) as i:
                    for u in range(U):
                        act.wait_ge(x_turned, done(i, u))
                        act.wait_ge(up_done, before(i, u))
                        nc.scalar.activation(xT[:, u].rearrange("p c t -> p (c t)"), B[u][1][:, 0:KC * P], ACT.Copy).then_inc(xT_ready, 1)
                    for u in range(U):
                        act.wait_ge(up_done, done(i, u))
                        act.wait_ge(h1_ready, before(i, u))
                        nc.scalar.activation(th[:, u, :], B[u][0][:HC, 0:2 * P], ACT.Tanh, scale=0.5).then_inc(th_ready, 1)
                    for u in range(U):
                        act.wait_ge(y_done, done(i, u))
                        act.wait_ge(stored[u], 16 * i + 16)
                        nc.scalar.activation(y[:, u, :], B[u][1][:, 0:D], ACT.Copy).then_inc(y_ready, 1)
                    for u in range(U):
                        act.wait_ge(y_ready, done(i, u))
                        act.dma_start(ys[U * i + u], y[:, u, :]).then_inc(stored[u], 16)
                for u in range(U):
                    act.wait_ge(stored[u], 16 * (EXPERTS // U) + 16)

            @block.vector
            def _(dve):
                for sem in (h1_ready, h_ready):
                    dve.sem_inc(sem, U)
                with dve.Fori(0, EXPERTS // U) as i:
                    for u in range(U):
                        dve.wait_ge(th_ready, done(i, u))
                        nc.vector.scalar_tensor_tensor(h1[:, u, :], th[:, u, :], 1.0, B[u][0][:HC, 0:2 * P],
                                                       ALU.add, ALU.mult).then_inc(h1_ready, 1)
                    for u in range(U):
                        dve.wait_ge(h1_ready, done(i, u))
                        dve.wait_ge(y_done, before(i, u))
                        nc.vector.scalar_tensor_tensor(hT[:, u, :, :].rearrange("p m t -> p (m t)"), h1[:, u, :], 0.5,
                                                       B[u][0][:HC, 2 * P:4 * P], ALU.mult, ALU.mult).then_inc(h_ready, 1)


def linear_attention(nc, NB, xz, slot_out, slot_ids, slot_weights, x_out, w, n_out=None):
    EPS = 1e-6
    with ExitStack() as ctx:
        U = 4
        done, before = counts(U)
        s = Store(nc, ctx, "la", U)
        wqk = s.sb("wqk", [P, KC, 2 * D])
        wv = s.sb("wv", [P, KC, D])
        wo = s.sb("wo", [P, KC, D])
        bqk = s.sb("bqk", [T, 2 * D])
        bv = s.sb("bv", [T, D])
        bo = s.sb("bo", [T, D])
        ident = s.sb("ident", [P, P])
        ones = s.sb("ones", [T, T])
        block_mask = s.sb("block_mask", [P, P])
        ids = s.sb("ids", [T, U, TOPK], U32)
        wts = s.sb("wts", [T, U, TOPK])
        rows = s.sb("rows", [T, U, TOPK, D])
        acc = s.sb("acc", [T, U, 2, D])
        x_3 = s.sb("x_3", [T, U, D])
        x_bo = s.sb("x_bo", [T, U, D])
        xT = s.sb("xT", [P, U, KC, T])
        qk = s.sb("qk", [T, U, 2, D])
        qke = s.sb("qke", [T, U, 2, D])
        t1 = s.sb("t1", [T, U, 2, D])
        v = s.sb("v", [T, U, D])
        flow = s.sb("flow", [T, U, 2 * HEADS])
        kept = s.sb("kept", [T, U, 2 * HEADS])
        comp = s.sb("comp", [T, U, HEADS])
        ecs = s.sb("ecs", [T, U, HEADS])
        alloc = s.sb("alloc", [T, U, HEADS])
        qT = s.sb("qT", [P, U, KC, T])
        kv = s.sb("kv", [P, U, KC, P])
        y = s.sb("y", [T, U, D])
        yT = s.sb("yT", [P, U, KC, T])
        r = s.sb("r", [T, U, D])
        x_o = s.sb("x_o", [T, U, D])
        norm3 = Norm(s, nc, tag="3")
        norm = Norm(s, nc)
        B = [[s.ps(f"B{b}_{u}", [P, 512]) for b in range(2)] for u in range(U)]

        w_in, ones_set = s.sem("weights_loaded"), s.sem("ones_set")
        ids_loaded, wts_loaded, xz_loaded, gathered, stored = (s.sems(n) for n in (
            "ids_loaded", "wts_loaded", "xz_loaded", "gathered", "stored"))
        names = ["x3_ready", "x_turned", "xT_ready", "qkv_done", "biased", "th_ready", "qk_ready", "summed",
                 "flows_ready", "flowed", "kept_ready", "ecs_ready", "esummed", "v_ready", "kv_done", "kv_ready", "q_turned",
                 "qT_ready", "attended", "y_ready", "y_turned", "yT_ready", "o_done", "r_ready", "out_ready", "xbo_ready"]
        (x3_ready, x_turned, xT_ready, qkv_done, biased, th_ready, qk_ready, summed, flows_ready, flowed, kept_ready,
         ecs_ready, esummed, v_ready, kv_done, kv_ready, q_turned, qT_ready, attended, y_ready, y_turned, yT_ready, o_done,
         r_ready, out_ready, xbo_ready) = (s.sem(n) for n in names)
        gather_over, ids_seen = s.sem("gather_over"), s.sem("ids_seen")
        vlink = s.sem("dve_link")

        kp = "(k p) n -> p k n"
        loads = [(wqk[:], w["L1_wqkT"].rearrange(kp, p=P)), (wv[:], w["L1_wvT"].rearrange(kp, p=P)),
                 (wo[:], w["L1_woT"].rearrange(kp, p=P)), (bqk[:], w["L1_bqk"].to_broadcast([T, 2 * D])),
                 (bv[:], w["L1_bv"].to_broadcast([T, D])), (bo[:], w["L1_bo"].to_broadcast([T, D])),
                 (ident[:], w["ident"]), (block_mask[:], w["block_mask"])]
        W_ALL = 16 * len(loads)

        with nc.Block() as block:

            @block.sync
            def _(sp):
                for dst, src in loads:
                    sp.dma_start(dst, src).then_inc(w_in, 16)
                with sp.Fori(0, NB // U) as i:
                    for u in range(U):
                        sp.wait_ge(gather_over, before(i, u))
                        sp.dma_start(ids[:, u, :], slot_ids[U * i + u]).then_inc(ids_loaded[u], 16)
                        sp.wait_ge(x3_ready, before(i, u))
                        sp.dma_start(wts[:, u, :], slot_weights[U * i + u]).then_inc(wts_loaded[u], 16)
                        sp.dma_start(acc[:, u, 0, :], xz[U * i + u]).then_inc(xz_loaded[u], 16)

            @block.gpsimd
            def _(pool):
                pool.sem_inc(gather_over, U)
                pool.sem_inc(xbo_ready, U)
                nc.gpsimd.memset(ones[:], 1.0).then_inc(ones_set, 1)
                norm3.set_power(pool)
                norm.set_power(pool)
                pool.wait_ge(w_in, W_ALL)
                with pool.Fori(0, NB // U) as i:
                    for u in range(U):
                        pool.wait_ge(ids_loaded[u], 16 * i + 16)
                        pool.wait_ge(x3_ready, before(i, u))
                        pool.sem_inc(ids_seen, 1)
                        for k in range(TOPK):
                            nc.gpsimd.indirect_dma_start(rows[:, u, k, :], None, slot_out,
                                                         bass.IndirectOffsetOnAxis(ids[:, u, k:k + 1], 0)).then_inc(gathered[u], 16)
                    for u in range(U):
                        pool.wait_ge(gathered[u], 16 * TOPK * i + 16 * TOPK)
                        pool.sem_inc(gather_over, 1)
                    norm3.raise_power(pool, i)
                    for u in range(U):
                        pool.wait_ge(x3_ready, done(i, u))
                        pool.wait_ge(r_ready, before(i, u))
                        nc.gpsimd.tensor_tensor(x_bo[:, u, :], x_3[:, u, :], bo[:], ALU.add).then_inc(xbo_ready, 1)
                    norm.raise_power(pool, i)

            @block.tensor
            def _(pe):
                for sem in (x_turned, qkv_done, summed, flowed, esummed, kv_done, q_turned, attended, y_turned, o_done):
                    pe.sem_inc(sem, U)
                pe.wait_ge(w_in, W_ALL)
                pe.wait_ge(ones_set, 1)
                with pe.Fori(0, NB // U) as i:
                    for u in range(U):
                        pe.wait_ge(x3_ready, done(i, u))
                        pe.wait_ge(r_ready, before(i, u))
                        for c in range(KC):
                            last = nc.tensor.transpose(B[u][1][:, c * T:(c + 1) * T], x_3[:, u, c * P:(c + 1) * P], ident[:T, :T])
                        last.then_inc(x_turned, 1)
                    for u in range(U):
                        pe.wait_ge(xT_ready, done(i, u))
                        for c in range(KC):
                            nc.tensor.matmul(B[u][0][:T, :], xT[:, u, c, :], wqk[:, c, :], start=(c == 0), stop=(c == KC - 1))
                        for c in range(KC):
                            last = nc.tensor.matmul(B[u][1][:T, 0:D], xT[:, u, c, :], wv[:, c, :], start=(c == 0), stop=(c == KC - 1))
                        last.then_inc(qkv_done, 1)
                    for u in range(U):
                        pe.wait_ge(qk_ready, done(i, u))
                        nc.tensor.matmul(B[u][0][:T, :], ones[:], qk[:, u].rearrange("p a d -> p (a d)"), start=True,
                                         stop=True).then_inc(summed, 1)
                    for u in range(U):
                        for c in range(KC):
                            last = nc.tensor.transpose(B[u][1][:, c * T:(c + 1) * T], qk[:, u, 0, c * P:(c + 1) * P], ident[:T, :T])
                        last.then_inc(q_turned, 1)
                    for u in range(U):
                        pe.wait_ge(flows_ready, done(i, u))
                        nc.tensor.matmul(B[u][0][:T, :], ones[:], t1[:, u].rearrange("p a d -> p (a d)"), start=True,
                                         stop=True).then_inc(flowed, 1)
                    for u in range(U):
                        pe.wait_ge(ecs_ready, done(i, u))
                        pe.wait_ge(qT_ready, done(i, u))
                        nc.tensor.matmul(B[u][1][:T, 0:HEADS], ones[:], ecs[:, u, :], start=True, stop=True).then_inc(esummed, 1)
                    for u in range(U):
                        pe.wait_ge(v_ready, done(i, u))
                        for c in range(KC):
                            last = nc.tensor.matmul(B[u][0][:, c * P:(c + 1) * P], qk[:, u, 1, c * P:(c + 1) * P],
                                                    v[:, u, c * P:(c + 1) * P], start=True, stop=True)
                        last.then_inc(kv_done, 1)
                    for u in range(U):
                        pe.wait_ge(kv_ready, done(i, u))
                        for c in range(KC):
                            last = nc.tensor.matmul(B[u][1][:T, c * P:(c + 1) * P], qT[:, u, c, :], kv[:, u, c, :], start=True, stop=True)
                        last.then_inc(attended, 1)
                    for u in range(U):
                        pe.wait_ge(y_ready, done(i, u))
                        for c in range(KC):
                            last = nc.tensor.transpose(B[u][0][:, c * T:(c + 1) * T], y[:, u, c * P:(c + 1) * P], ident[:T, :T])
                        last.then_inc(y_turned, 1)
                    for u in range(U):
                        pe.wait_ge(yT_ready, done(i, u))
                        for c in range(KC):
                            last = nc.tensor.matmul(B[u][1][:T, 0:D], yT[:, u, c, :], wo[:, c, :], start=(c == 0), stop=(c == KC - 1))
                        last.then_inc(o_done, 1)

            @block.scalar
            def _(act):
                for sem in (xT_ready, th_ready, qT_ready, ecs_ready, yT_ready):
                    act.sem_inc(sem, U)
                for u in range(U):
                    act.sem_inc(stored[u], 16)
                with act.Fori(0, NB // U) as i:
                    for u in range(U):
                        act.wait_ge(x_turned, done(i, u))
                        nc.scalar.activation(xT[:, u].rearrange("p c t -> p (c t)"), B[u][1][:, 0:KC * T], ACT.Copy).then_inc(xT_ready, 1)
                    for u in range(U):
                        act.wait_ge(biased, done(i, u))
                        nc.scalar.activation(t1[:, u].rearrange("p a d -> p (a d)"), qke[:, u].rearrange("p a d -> p (a d)"),
                                             ACT.Tanh, scale=0.5).then_inc(th_ready, 1)
                    for u in range(U):
                        act.wait_ge(q_turned, done(i, u))
                        nc.scalar.activation(qT[:, u].rearrange("p c t -> p (c t)"), B[u][1][:, 0:KC * T], ACT.Copy).then_inc(qT_ready, 1)
                    for u in range(U):
                        act.wait_ge(kept_ready, done(i, u))
                        nc.scalar.activation(alloc[:, u, :], kept[:, u, 0:HEADS], ACT.Tanh, scale=0.5)
                        nc.scalar.activation(ecs[:, u, :], kept[:, u, HEADS:2 * HEADS], ACT.Exp).then_inc(ecs_ready, 1)
                    for u in range(U):
                        act.wait_ge(y_turned, done(i, u))
                        nc.scalar.activation(yT[:, u].rearrange("p c t -> p (c t)"), B[u][0][:, 0:KC * T], ACT.Copy).then_inc(yT_ready, 1)
                    for u in range(U):
                        act.wait_ge(out_ready, done(i, u))
                        act.dma_start(x_out[U * i + u], x_o[:, u, :]).then_inc(stored[u], 16)
                for u in range(U):
                    act.wait_ge(stored[u], 16 * (NB // U) + 16)

            @block.vector
            def _(dve):
                for sem in (x3_ready, biased, qk_ready, flows_ready, kept_ready, v_ready, kv_ready, y_ready, r_ready, out_ready):
                    dve.sem_inc(sem, U)
                dve.wait_ge(w_in, W_ALL)

                def heads(ap):
                    return ap.rearrange("p a (h d) -> p (a h) d", d=DH)

                with dve.Fori(0, NB // U) as i:
                    links = Links(dve, vlink, i, 88)
                    for u in range(U):
                        dve.wait_ge(gather_over, done(i, u))
                        dve.wait_ge(wts_loaded[u], 16 * i + 16)
                        dve.wait_ge(xz_loaded[u], 16 * i + 16)
                    for k in range(TOPK):
                        for u in range(U):
                            add = nc.vector.scalar_tensor_tensor(acc[:, u, (k + 1) % 2, :], rows[:, u, k, :], wts[:, u, k:k + 1],
                                                                 acc[:, u, k % 2, :], ALU.mult, ALU.add)
                            links.add(add)
                        links.wait()
                    norm3.steps(dve, links, i, acc[:, :, 0, :], x_3, x3_ready)
                    for u in range(U):
                        dve.wait_ge(qkv_done, done(i, u))
                        nc.vector.tensor_tensor(v[:, u, :], B[u][1][:T, 0:D], bv[:], ALU.add)
                        nc.vector.tensor_tensor(qke[:, u].rearrange("p a d -> p (a d)"), B[u][0][:T, :], bqk[:], ALU.add).then_inc(biased, 1)
                    for u in range(U):
                        dve.wait_ge(th_ready, done(i, u))
                        nc.vector.tensor_scalar(qk[:, u].rearrange("p a d -> p (a d)"), t1[:, u].rearrange("p a d -> p (a d)"),
                                                0.5, 0.5, ALU.mult, ALU.add).then_inc(qk_ready, 1)
                    for u in range(U):
                        dve.wait_ge(qk_ready, done(i, u))
                        links.add(nc.vector.tensor_scalar(qke[:, u].rearrange("p a d -> p (a d)"), qk[:, u].rearrange("p a d -> p (a d)"),
                                                          EPS, None, ALU.add))
                    links.wait()

                    def against_sums(sums, signal):
                        for u in range(U):
                            dve.wait_ge(signal, done(i, u))
                            for a in range(2):
                                links.add(nc.vector.scalar_tensor_tensor(t1[:, u, a, :], sums[u][:T, (1 - a) * D:(2 - a) * D], EPS,
                                                                         qke[:, u, a, :], ALU.add, ALU.mult))
                        links.wait()

                    against_sums([B[u][0] for u in range(U)], summed)
                    for u in range(U):
                        links.add(nc.vector.tensor_reduce(flow[:, u, :], heads(t1[:, u]), axis=AXIS_X, op=ALU.add))
                    links.wait()
                    for u in range(U):
                        links.add(nc.vector.reciprocal(flow[:, u, :], flow[:, u, :]))
                    links.wait()
                    for u in range(U):
                        nc.vector.tensor_tensor(heads(t1[:, u]), heads(qk[:, u]), flow[:, u, :].unsqueeze(2).to_broadcast([T, 2 * HEADS, DH]),
                                                ALU.mult).then_inc(flows_ready, 1)
                    against_sums([B[u][0] for u in range(U)], flowed)
                    for u in range(U):
                        links.add(nc.vector.tensor_reduce(kept[:, u, :], heads(t1[:, u]), axis=AXIS_X, op=ALU.add))
                    links.wait()
                    for u in range(U):
                        nc.vector.tensor_scalar(kept[:, u, HEADS:2 * HEADS], kept[:, u, HEADS:2 * HEADS], -1.0, 1.0,
                                                ALU.max, ALU.min).then_inc(kept_ready, 1)
                    for u in range(U):
                        dve.wait_ge(esummed, done(i, u))
                        links.add(nc.vector.reciprocal(comp[:, u, :], B[u][1][:T, 0:HEADS]))
                        links.add(nc.vector.tensor_scalar(alloc[:, u, :], alloc[:, u, :], 0.5, 0.5, ALU.mult, ALU.add))
                    links.wait()
                    for u in range(U):
                        links.add(nc.vector.tensor_tensor(comp[:, u, :], comp[:, u, :], ecs[:, u, :], ALU.mult))
                        links.add(nc.vector.tensor_tensor(alloc[:, u, :], alloc[:, u, :], flow[:, u, 0:HEADS], ALU.mult))
                    links.wait()
                    for u in range(U):
                        vh = v[:, u, :].rearrange("p (h d) -> p h d", d=DH)
                        nc.vector.scalar_tensor_tensor(vh, vh, float(T), comp[:, u, :].unsqueeze(2).to_broadcast([T, HEADS, DH]),
                                                       ALU.mult, ALU.mult).then_inc(v_ready, 1)
                    for u in range(U):
                        dve.wait_ge(kv_done, done(i, u))
                        nc.vector.tensor_tensor(kv[:, u], B[u][0][:, 0:KC * P].rearrange("p (c n) -> p c n", n=P),
                                                block_mask[:].unsqueeze(1).to_broadcast([P, KC, P]), ALU.mult).then_inc(kv_ready, 1)
                    for u in range(U):
                        dve.wait_ge(attended, done(i, u))
                        nc.vector.tensor_tensor(y[:, u, :].rearrange("p (h d) -> p h d", d=DH),
                                                B[u][1][:T, 0:D].rearrange("p (h d) -> p h d", d=DH),
                                                alloc[:, u, :].unsqueeze(2).to_broadcast([T, HEADS, DH]), ALU.mult).then_inc(y_ready, 1)
                    for u in range(U):
                        dve.wait_ge(o_done, done(i, u))
                        dve.wait_ge(xbo_ready, done(i, u))
                        nc.vector.tensor_tensor(r[:, u, :], B[u][1][:T, 0:D], x_bo[:, u, :], ALU.add).then_inc(r_ready, 1)
                    dve.wait_ge(r_ready, done(i, U - 1))
                    for u in range(U):
                        dve.wait_ge(stored[u], 16 * i + 16)
                    norm.steps(dve, links, i, r, x_o, out_ready)
                    links.end()


def cross_attention(nc, NB, x_in, x_out, w, src_len):
    NCH = 3
    STEP = (src_len - 1) // NCH
    ROWS = STEP + 1
    assert STEP * NCH + 1 == src_len and ROWS <= P
    G = GROUPS
    with ExitStack() as ctx:
        U = 2
        done, before = counts(U)
        s = Store(nc, ctx, "xa", U)
        wq = s.sb("wq", [P, 2, KC, D])
        wk = s.sb("wk", [P, 2, KC, D])
        wv = s.sb("wv", [P, KC, D])
        wo = s.sb("wo", [P, KC, D])
        wg = s.sb("wg", [P, KC, D])
        bo = s.sb("bo", [T, D])
        bg = s.sb("bg", [T, D])
        gamma = s.sb("gamma", [P, KC])
        beta = s.sb("beta", [P, KC])
        cosT = s.sb("cosT", [P, src_len])
        sinT = s.sb("sinT", [P, src_len])
        bias = s.sb("bias", [ROWS, NCH, T])
        head_mask = s.sb("head_mask", [P, 8])
        head_mask2 = s.sb("head_mask2", [P, 4])
        ident = s.sb("ident", [P, P])
        neg1 = s.sb("neg1", [T, ROWS], F32R)
        x_t = s.sb("x_t", [T, U, D])
        x_res = s.sb("x_res", [T, U, D])
        x_2 = s.sb("x_2", [T, U, D])
        x_n = s.sb("x_n", [T, U, D])
        xT = s.sb("xT", [P, KC, U, T])
        c_t = s.sb("c_t", [ROWS, U, NCH, D])
        c_n = s.sb("c_n", [ROWS, U, NCH, D])
        cT = s.sb("cT", [P, U, KC, src_len])
        k_c = s.sb("k_c", [P, U, KC, src_len])
        k_s = s.sb("k_s", [P, U, KC, src_len])
        kT = s.sb("kT", [P, U, KC, src_len])
        q_c = s.sb("q_c", [P, KC, U, T])
        q_s = s.sb("q_s", [P, KC, U, T])
        q_bd = s.sb("q_bd", [P, U, KC, 8, T])
        v1 = s.sb("v1", [ROWS, U, NCH, G, P])
        mx = s.sb("mx", [ROWS, U, GW])
        nmax = s.sb("nmax", [T, U, HPG])
        dmax = s.sb("dmax", [T, U, HPG, T], F32R)
        prob = s.sb("prob", [ROWS, U, NCH, GW])
        own = s.sb("own", [P, U, GW])
        nd = s.sb("nd", [P, U, T])
        rec = s.sb("rec", [64, U, T])
        yT = s.sb("yT", [P, U, KC, T])
        att = s.sb("att", [T, U, D])
        aT = s.sb("aT", [P, U, KC, T])
        gl = s.sb("gl", [T, U, D])
        dif = s.sb("dif", [T, U, D])
        r = s.sb("r", [T, U, D])
        x_o = s.sb("x_o", [T, U, D])
        norm_q, norm_c, norm = Norm(s, nc, tag="q"), Norm(s, nc, ROWS, "c", lots=U * NCH), Norm(s, nc)
        S = [s.ps(f"S{u}", [P, 3, 512]) for u in range(U)]
        W = [s.ps(f"W{u}", [P, 512]) for u in range(U)]

        w_in, const_ready = s.sem("weights_loaded"), s.sem("const_ready")
        x_loaded, res_loaded, c_loaded, stored = (s.sems(n) for n in ("x_loaded", "res_loaded", "c_loaded", "stored"))
        xn_ready, cn_ready = s.sem("xn_ready"), s.sem("cn_ready")
        turned = s.sem("turned")
        xT_ready, cT_ready = s.sem("xT_ready"), s.sem("cT_ready")
        k_done, v_done = s.sem("k_done"), s.sem("v_done")
        q_done = s.sem("q_done")
        k_rot = s.sem("k_rot")
        q_rot = s.sem("q_rot")
        k_ready, qbd_ready = s.sem("k_ready"), s.sem("qbd_ready")
        q_sum = s.sem("q_sum")
        v_ready = s.sem("v_ready")
        scored, mx_turned, av_done = (s.sem(n) for n in ("scored", "mx_turned", "av_done"))
        shifted = s.sem("shifted")
        mx_ready, max_ready, nd_ready, yT_ready = (s.sem(n) for n in ("mx_ready", "max_ready", "nd_ready", "yT_ready"))
        less_ready = s.sem("less_ready")
        own_ready = s.sem("own_ready")
        prob_ready = s.sem("prob_ready")
        o_done, a_turned, g_done = s.sem("o_done"), s.sem("a_turned"), s.sem("g_done")
        att_ready, gl_ready, r_ready, out_ready = (s.sem(n) for n in ("att_ready", "gl_ready", "r_ready", "out_ready"))
        aT_ready, th_ready = s.sem("aT_ready"), s.sem("th_ready")
        x2_ready = s.sem("x2_ready")
        vlink = s.sem("dve_link")
        vlink_norm = s.sem("dve_link_norm")

        kp = "(k p) n -> p k n"
        wqkv = w["L1x_wqkvT"].rearrange(kp, p=P)
        loads = [(wq[:, 0], wqkv[:, :, 0:D]), (wk[:, 0], wqkv[:, :, D:2 * D]), (wv[:], wqkv[:, :, 2 * D:3 * D]),
                 (wo[:], w["L1x_woT"].rearrange(kp, p=P)), (wg[:], w["L1x_wgT"].rearrange(kp, p=P)),
                 (bo[:], w["L1x_bo"].to_broadcast([T, D])), (bg[:], w["L1x_bg"].to_broadcast([T, D])),
                 (gamma[:], w["L1x_gamma"]), (beta[:], w["L1x_beta"]), (cosT[:], w["cos_xa"]), (sinT[:], w["sin_xa"]),
                 (bias[:], w["bias_xa"]), (head_mask[:], w["head_mask"]), (head_mask2[:], w["head_mask2"]), (ident[:], w["ident"])]
        W_ALL = 16 * len(loads)
        N = NB // U
        assert N >= 3

        def part(i, u, j, n):
            return (done(i, u, j, G) - 1) * NCH + n + 1

        def pipelined(eng, body):
            with eng.Fori(0, N - 2) as i:
                body(i, 2)
            body(N - 2, 1)
            body(N - 1, 0)

        slots = [(j, u) for j in range(G) for u in range(U)]

        def slot_before(j, u):
            return (j, 0) if u else (j - 1, 1)

        with nc.Block() as block:

            @block.sync
            def _(sp):
                for dst, src in loads:
                    sp.dma_start(dst, src).then_inc(w_in, 16)

                def rows(i):
                    for u in range(U):
                        sp.wait_ge(xn_ready, before(i, u))
                        sp.dma_start(x_t[:, u, :], x_in[U * i + u]).then_inc(x_loaded[u], 16)
                        sp.wait_ge(cn_ready, before(i, u, NCH - 1, NCH))
                        for c in range(NCH):
                            sp.dma_start(c_t[:, u, c, :], w["ctx"][U * i + u, c * STEP:c * STEP + ROWS, :]).then_inc(c_loaded[u], 16)

                rows(0)
                rows(1)

                def body(i, coming):
                    for u in range(U):
                        sp.wait_ge(r_ready, before(i, u))
                        sp.dma_start(x_res[:, u, :], x_in[U * i + u]).then_inc(res_loaded[u], 16)
                    if coming == 2:
                        rows(i + 2)

                pipelined(sp, body)

            @block.tensor
            def _(pe):
                for sem, steps in ((turned, 1), (k_done, KC), (v_done, 1), (scored, G), (mx_turned, G), (shifted, G * NCH),
                                   (av_done, G), (o_done, 1), (a_turned, 1), (g_done, 1)):
                    pe.sem_inc(sem, U * steps)
                pe.wait_ge(w_in, W_ALL)
                pe.wait_ge(const_ready, 1)

                def turn(i, u):
                    pe.wait_ge(xn_ready, done(i, u))
                    pe.wait_ge(cn_ready, done(i, u, NCH - 1, NCH))
                    pe.wait_ge(less_ready, before(i, u, G - 1, G) * NCH)
                    for c in range(KC):
                        nc.tensor.transpose(S[u][:, 2, c * T:(c + 1) * T], x_n[:, u, c * P:(c + 1) * P], ident[:T, :T])
                    for c in range(KC):
                        for n in range(NCH):
                            last = nc.tensor.transpose(S[u][:, c, n * STEP:n * STEP + ROWS], c_n[:, u, n, c * P:(c + 1) * P],
                                                       ident[:ROWS, :ROWS])
                    last.then_inc(turned, 1)

                def keys(i, u, banks, signals):
                    for k in banks:
                        for c in range(KC):
                            last = nc.tensor.matmul(S[u][:, k % 3, 0:src_len], wk[:, k % 2, c, (k // 2) * P:(k // 2 + 1) * P],
                                                    cT[:, u, c, :], start=(c == 0), stop=(c == KC - 1))
                        if k in signals:
                            last.then_inc(k_done, 1)

                def queries(i):
                    for u in range(U):
                        pe.wait_ge(k_rot, done(i, u, 1, KC))
                        pe.wait_ge(xT_ready, done(i, u))
                    for turned_ in range(2):
                        for g in range(KC):
                            for c in range(KC):
                                last = nc.tensor.matmul(S[turned_][:, 2, g * U * T:(g + 1) * U * T],
                                                        wq[:, turned_, c, g * P:(g + 1) * P],
                                                        xT[:, c, :, :].rearrange("p u t -> p (u t)"),
                                                        start=(c == 0), stop=(c == KC - 1))
                    last.then_inc(q_done, 1)

                def values(i, u):
                    for n in range(NCH):
                        for c in range(KC):
                            last = nc.tensor.matmul(S[u][:ROWS, n // 2, (n % 2) * D:(n % 2) * D + D],
                                                    cT[:, u, c, n * STEP:n * STEP + ROWS], wv[:, c, :],
                                                    start=(c == 0), stop=(c == KC - 1))
                    last.then_inc(v_done, 1)

                def ahead(i):
                    for u in range(U):
                        turn(i, u)
                    for u in range(U):
                        pe.wait_ge(xT_ready, done(i, u))
                        pe.wait_ge(cT_ready, done(i, u))
                        keys(i, u, (0, 1, 2), (1,))
                    for u in range(U):
                        pe.wait_ge(k_rot, done(i, u, 0, KC))
                        keys(i, u, (3,), (3,))

                def score(i, j, u):
                    if j == 0:
                        pe.wait_ge(v_ready, done(i, u))
                        pe.wait_ge(q_rot, i + 1)
                    else:
                        pe.wait_ge(less_ready, part(i, u, j - 1, NCH - 1))
                    g, h0 = j // 2, 4 * (j % 2)
                    if h0 == 0:
                        pe.wait_ge(k_ready, done(i, u, g, KC))
                        pe.wait_ge(qbd_ready, done(i, u, g, KC))
                    for n in range(NCH):
                        last = nc.tensor.matmul(S[u][:ROWS, n, 0:GW], kT[:, u, g, n * STEP:n * STEP + ROWS],
                                                q_bd[:, u, g, h0:h0 + 4, :].rearrange("p h t -> p (h t)"),
                                                start=True, stop=True)
                    last.then_inc(scored, 1)

                def attend(i, j, u, chunks):
                    for n in chunks:
                        pe.wait_ge(prob_ready, part(i, u, j, n))
                        rows = ROWS if n == NCH - 1 else STEP
                        last = nc.tensor.matmul(W[u][:, 0:GW], v1[0:rows, u, n, j, :], prob[0:rows, u, n, :],
                                                start=(n == 0), stop=(n == NCH - 1))
                    if n == NCH - 1:
                        last.then_inc(av_done, 1)

                def turn_maxima(i, j, u):
                    pe.wait_ge(mx_ready, done(i, u, j, G))
                    if j:
                        pe.wait_ge(own_ready, done(i, u, j - 1, G))
                    else:
                        pe.wait_ge(gl_ready, before(i, u))
                    for h in range(HPG):
                        last = nc.tensor.transpose(W[u][:T, h * P:h * P + ROWS], mx[:, u, h * T:(h + 1) * T],
                                                   ident[:ROWS, :ROWS])
                    last.then_inc(mx_turned, 1)

                def shift(i, j, u):
                    pe.wait_ge(max_ready, done(i, u, j, G))
                    for n in range(NCH):
                        nc.tensor.matmul(S[u][:ROWS, n, 0:GW], neg1[:], dmax[:, u, :, :].rearrange("p h t -> p (h t)"),
                                         start=False, stop=True, skip_group_check=True).then_inc(shifted, 1)

                def project(i, u):
                    pe.wait_ge(yT_ready, done(i, u, G - 1, G))
                    for c in range(KC):
                        last = nc.tensor.matmul(W[u][:T, 0:D], yT[:, u, c, :], wo[:, c, :], start=(c == 0), stop=(c == KC - 1))
                    last.then_inc(o_done, 1)

                def turn_attended(i, u):
                    pe.wait_ge(att_ready, done(i, u))
                    for c in range(KC):
                        last = nc.tensor.transpose(W[u][:, c * T:(c + 1) * T], att[:, u, c * P:(c + 1) * P], ident[:T, :T])
                    last.then_inc(a_turned, 1)

                def gate(i, u):
                    pe.wait_ge(aT_ready, done(i, u))
                    for c in range(KC):
                        last = nc.tensor.matmul(W[u][:T, 0:D], aT[:, u, c, :], wg[:, c, :], start=(c == 0), stop=(c == KC - 1))
                    last.then_inc(g_done, 1)

                def body(i, coming):
                    queries(i)
                    for u in range(U):
                        values(i, u)
                    for j, u in slots:
                        score(i, j, u)
                        jb, ub = slot_before(j, u)
                        if jb >= 0:
                            attend(i, jb, ub, range(NCH - 1))
                        turn_maxima(i, j, u)
                        if jb >= 0:
                            attend(i, jb, ub, (NCH - 1,))
                        shift(i, j, u)
                    if coming:
                        turn(i + 1, 0)
                    attend(i, G - 1, 1, range(NCH))
                    if coming:
                        turn(i + 1, 1)
                    for u in range(U):
                        if coming:
                            pe.wait_ge(xT_ready, done(i + 1, u))
                            pe.wait_ge(cT_ready, done(i + 1, u))
                            keys(i + 1, u, (0, 1, 2), (1,))
                        project(i, u)
                    for u in range(U):
                        if coming:
                            pe.wait_ge(k_rot, done(i + 1, u, 0, KC))
                            keys(i + 1, u, (3,), (3,))
                        turn_attended(i, u)
                    for u in range(U):
                        gate(i, u)

                ahead(0)
                pipelined(pe, body)

            @block.scalar
            def _(act):
                for sem, steps in ((xT_ready, 1), (cT_ready, 1), (v_ready, 1), (prob_ready, G * NCH), (own_ready, G),
                                   (aT_ready, 1), (th_ready, 1)):
                    act.sem_inc(sem, U * steps)
                for u in range(U):
                    act.sem_inc(stored[u], 16)
                act.wait_ge(w_in, W_ALL)

                def ahead(i):
                    for u in range(U):
                        act.wait_ge(turned, done(i, u))
                        for c in range(KC):
                            last = nc.scalar.activation(xT[:, c, u, :], S[u][:, 2, c * T:(c + 1) * T], ACT.Identity,
                                                        scale=gamma[:, c:c + 1], bias=beta[:, c:c + 1])
                        last.then_inc(xT_ready, 1)
                        for c in range(KC):
                            last = nc.scalar.activation(cT[:, u, c, :], S[u][:, c, 0:src_len], ACT.Identity,
                                                        scale=gamma[:, c:c + 1], bias=beta[:, c:c + 1])
                        last.then_inc(cT_ready, 1)

                def pick_own(i, j, u):
                    act.wait_ge(av_done, done(i, u, j, G))
                    if j:
                        act.wait_ge(nd_ready, done(i, u, j - 1, G))
                    else:
                        act.wait_ge(nd_ready, before(i, u, G - 1, G))
                    for h in range(HPG):
                        last = nc.scalar.activation(own[:, u, h * T:(h + 1) * T], W[u][:, h * T:(h + 1) * T], ACT.Copy,
                                                    scale=head_mask2[:, h:h + 1])
                    last.then_inc(own_ready, 1)

                def body(i, coming):
                    for u in range(U):
                        act.wait_ge(v_done, done(i, u))
                        act.wait_ge(av_done, before(i, u, G - 1, G))
                        nc.scalar.activation(v1[:, u, 0:2, :, 0:64],
                                             S[u][:ROWS, 0, :].rearrange("p (n g f) -> p n g f", n=2, f=64), ACT.Copy)
                        nc.scalar.activation(v1[:, u, 2, :, 0:64], S[u][:ROWS, 1, 0:D].rearrange("p (g f) -> p g f", f=64),
                                             ACT.Copy).then_inc(v_ready, 1)
                    for j, u in slots:
                        jb, ub = slot_before(j, u)
                        if jb >= 0:
                            pick_own(i, jb, ub)
                        for n in range(NCH):
                            act.wait_ge(less_ready, part(i, u, j, n))
                            nc.scalar.activation(prob[:, u, n, :], prob[:, u, n, :], ACT.Exp,
                                                 scale=float(DH) ** -0.5).then_inc(prob_ready, 1)
                    pick_own(i, G - 1, 1)
                    if coming:
                        ahead(i + 1)
                    for u in range(U):
                        act.wait_ge(a_turned, done(i, u))
                        nc.scalar.activation(aT[:, u].rearrange("p c t -> p (c t)"), W[u][:, 0:KC * T], ACT.Copy).then_inc(aT_ready, 1)
                    for u in range(U):
                        act.wait_ge(gl_ready, done(i, u))
                        nc.scalar.activation(gl[:, u, :], gl[:, u, :], ACT.Tanh, scale=0.5).then_inc(th_ready, 1)
                    for u in range(U):
                        act.wait_ge(out_ready, done(i, u))
                        act.dma_start(x_out[U * i + u], x_o[:, u, :]).then_inc(stored[u], 16)

                ahead(0)
                pipelined(act, body)
                for u in range(U):
                    act.wait_ge(stored[u], 16 * N + 16)

            @block.gpsimd
            def _(pool):
                for sem, steps in ((k_ready, KC), (qbd_ready, KC), (x2_ready, 1)):
                    pool.sem_inc(sem, U * steps)
                norm_q.set_power(pool)
                norm_c.set_power(pool)
                norm.set_power(pool)
                pool.wait_ge(w_in, W_ALL)

                def norms_ahead(i):
                    norm_q.raise_power(pool, i)
                    norm_c.raise_power(pool, i)

                def keys_ahead(i):
                    for g in range(KC):
                        for u in range(U):
                            pool.wait_ge(k_rot, done(i, u, g, KC))
                            pool.wait_ge(scored, before(i, u, G - 1, G))
                            nc.gpsimd.tensor_tensor(kT[:, u, g, :], k_c[:, u, g, :], k_s[:, u, g, :], ALU.add).then_inc(k_ready, 1)

                def spread(i, g, u):
                    pool.wait_ge(scored, before(i, u, G - 1, G))
                    nc.gpsimd.tensor_tensor(q_bd[:, u, g, :, :],
                                            q_c[:, g, u, :].unsqueeze(1).to_broadcast([P, 8, T]),
                                            head_mask[:].unsqueeze(2).to_broadcast([P, 8, T]), ALU.mult).then_inc(qbd_ready, 1)

                def ahead(i):
                    norms_ahead(i)
                    keys_ahead(i)

                def body(i, coming):
                    pool.wait_ge(q_rot, i + 1)
                    for g in range(KC):
                        nc.gpsimd.tensor_tensor(q_c[:, g, :, :].rearrange("p u t -> p (u t)"),
                                                q_c[:, g, :, :].rearrange("p u t -> p (u t)"),
                                                q_s[:, g, :, :].rearrange("p u t -> p (u t)"), ALU.add).then_inc(q_sum, 1)
                    pool.wait_ge(q_sum, KC * i + KC)
                    for u in range(U):
                        spread(i, 0, u)
                    for u in range(U):
                        spread(i, 1, u)
                    if coming == 2:
                        norms_ahead(i + 2)
                    if coming:
                        keys_ahead(i + 1)
                    for u in range(U):
                        pool.wait_ge(res_loaded[u], 16 * i + 16)
                        nc.gpsimd.tensor_tensor(x_2[:, u, :], x_res[:, u, :], x_res[:, u, :], ALU.add).then_inc(x2_ready, 1)
                    norm.raise_power(pool, i)

                ahead(0)
                norms_ahead(1)
                pipelined(pool, body)

            @block.vector
            def _(dve):
                nc.vector.memset(v1[:], 1.0)
                nc.vector.memset(neg1[:].bitcast(F32), -1.0)
                for sem, steps in ((xn_ready, 1), (cn_ready, NCH), (k_rot, KC), (mx_ready, G), (max_ready, G),
                                   (less_ready, G * NCH), (nd_ready, G), (yT_ready, G), (att_ready, 1), (gl_ready, 1),
                                   (r_ready, 1), (out_ready, 1)):
                    dve.sem_inc(sem, U * steps)
                dve.wait_ge(w_in, W_ALL)
                H2 = DH // 2
                for wm in (wq, wk):
                    for c in range(KC):
                        a = wm[:, 0, c, :].rearrange("p (h two d) -> p h two d", two=2, d=H2)
                        t = wm[:, 1, c, :].rearrange("p (h two d) -> p h two d", two=2, d=H2)
                        nc.vector.tensor_scalar(t[:, :, 0, :], a[:, :, 1, :], -1.0, None, ALU.mult)
                        last = nc.vector.tensor_copy(t[:, :, 1, :], a[:, :, 0, :])
                last.then_inc(const_ready, 1)

                def norms_ahead(i):
                    links = Links(dve, vlink_norm, i, 2 * (U + U * NCH))
                    for u in range(U):
                        dve.wait_ge(x_loaded[u], 16 * i + 16)
                    dve.wait_ge(turned, before(i, U - 1))
                    norm_q.steps(dve, links, i, x_t, x_n, xn_ready)
                    for u in range(U):
                        dve.wait_ge(c_loaded[u], 16 * NCH * i + 16 * NCH)
                    norm_c.steps_of(dve, links, i, [c_t[:, u, n, :] for n in range(NCH) for u in range(U)],
                                    [c_n[:, u, n, :] for n in range(NCH) for u in range(U)], cn_ready)
                    links.end()

                def rotate_keys(i, g, u):
                    dve.wait_ge(k_done, done(i, u, g, KC))
                    dve.wait_ge(k_ready, before(i, u, g, KC))
                    plain, turned_ = (2, 0) if g else (0, 1)
                    nc.vector.tensor_tensor(k_c[:, u, g, :], S[u][:, plain, 0:src_len], cosT[:], ALU.mult)
                    nc.vector.tensor_tensor(k_s[:, u, g, :], S[u][:, turned_, 0:src_len], sinT[:], ALU.mult).then_inc(k_rot, 1)

                def rotate_queries(i):
                    dve.wait_ge(q_done, i + 1)
                    for u in range(U):
                        dve.wait_ge(qbd_ready, before(i, u, KC - 1, KC))
                    for k, (dst, table) in enumerate(((q_c, cosT), (q_s, sinT))):
                        last = nc.vector.tensor_tensor(dst[:].rearrange("p g u t -> p (g u) t"),
                                                       S[k][:, 2, 0:KC * U * T].rearrange("p (a t) -> p a t", t=T),
                                                       table[:, 0:T].unsqueeze(1).to_broadcast([P, KC * U, T]), ALU.mult)
                    last.then_inc(q_rot, 1)

                def ahead(i):
                    norms_ahead(i)
                    for g in range(KC):
                        for u in range(U):
                            rotate_keys(i, g, u)

                def maxima(i, j, u):
                    dve.wait_ge(scored, done(i, u, j, G))
                    nc.vector.tensor_reduce(mx[:, u, :], S[u][:ROWS, :, 0:GW].rearrange("p n t -> p t n"),
                                            axis=AXIS_X, op=ALU.max).then_inc(mx_ready, 1)

                def spread_maxima(i, j, u, links):
                    dve.wait_ge(mx_turned, done(i, u, j, G))
                    links.add(nc.vector.tensor_reduce(nmax[:, u, :], W[u][:T, :].rearrange("p (h t) -> p h t", t=P)[:, :, 0:ROWS],
                                                      axis=AXIS_X, op=ALU.max))
                    links.wait()
                    nc.vector.tensor_tensor(dmax[:, u, :, :], ident[:T, :T].unsqueeze(1).to_broadcast([T, HPG, T]),
                                            nmax[:, u, :].unsqueeze(2).to_broadcast([T, HPG, T]),
                                            ALU.mult).then_inc(max_ready, 1)

                def add_bias(i, j, u):
                    if j:
                        dve.wait_ge(av_done, done(i, u, j - 1, G))
                    for n in range(NCH):
                        dve.wait_ge(shifted, part(i, u, j, n))
                        nc.vector.tensor_tensor(prob[:, u, n, :].rearrange("p (h t) -> p h t", t=T),
                                                S[u][:ROWS, n, 0:GW].rearrange("p (h t) -> p h t", t=T),
                                                bias[:, n, :].unsqueeze(1).to_broadcast([ROWS, HPG, T]),
                                                ALU.add).then_inc(less_ready, 1)

                def gather_own(i, j, u):
                    dve.wait_ge(own_ready, done(i, u, j, G))
                    nc.vector.tensor_reduce(nd[:, u, :], own[:, u, :].rearrange("p (h t) -> p t h", t=T),
                                            axis=AXIS_X, op=ALU.add).then_inc(nd_ready, 1)

                def invert(i, j, u, half, links):
                    cols = slice(half * (T // 2), (half + 1) * (T // 2))
                    dve.wait_ge(nd_ready, done(i, u, j, G))
                    links.add(nc.vector.reciprocal(rec[:, u, cols], nd[64:128, u, cols]))

                def normalise(i, j, u, links):
                    links.wait()
                    if j == 0:
                        dve.wait_ge(o_done, before(i, u))
                    o = 64 * (j % 2)
                    nc.vector.tensor_tensor(yT[o:o + 64, u, j // 2, :], nd[0:64, u, :], rec[:, u, :],
                                            ALU.mult).then_inc(yT_ready, 1)

                def body(i, coming):
                    links = Links(dve, vlink, i, 32)
                    rotate_queries(i)
                    for j, u in slots:
                        jb, ub = slot_before(j, u)
                        jbb, ubb = slot_before(jb, ub)
                        maxima(i, j, u)
                        if jbb >= 0:
                            invert(i, jbb, ubb, 0, links)
                        spread_maxima(i, j, u, links)
                        if jbb >= 0:
                            invert(i, jbb, ubb, 1, links)
                        add_bias(i, j, u)
                        if jbb >= 0:
                            normalise(i, jbb, ubb, links)
                        if jb >= 0:
                            gather_own(i, jb, ub)
                    invert(i, G - 1, 0, 0, links)
                    invert(i, G - 1, 0, 1, links)
                    normalise(i, G - 1, 0, links)
                    gather_own(i, G - 1, 1)
                    invert(i, G - 1, 1, 0, links)
                    invert(i, G - 1, 1, 1, links)
                    normalise(i, G - 1, 1, links)
                    if coming == 2:
                        norms_ahead(i + 2)
                    for u in range(U):
                        if coming:
                            rotate_keys(i + 1, 0, u)
                        dve.wait_ge(o_done, done(i, u))
                        nc.vector.tensor_tensor(att[:, u, :], W[u][:T, 0:D], bo[:], ALU.add).then_inc(att_ready, 1)
                    for u in range(U):
                        if coming:
                            rotate_keys(i + 1, 1, u)
                        dve.wait_ge(att_ready, done(i, u))
                        dve.wait_ge(res_loaded[u], 16 * i + 16)
                        links.add(nc.vector.tensor_tensor(dif[:, u, :], att[:, u, :], x_res[:, u, :], ALU.subtract))
                    for u in range(U):
                        dve.wait_ge(g_done, done(i, u))
                        nc.vector.tensor_tensor(gl[:, u, :], W[u][:T, 0:D], bg[:], ALU.add).then_inc(gl_ready, 1)
                    links.wait()
                    for u in range(U):
                        dve.wait_ge(th_ready, done(i, u))
                        links.add(nc.vector.scalar_tensor_tensor(dif[:, u, :], gl[:, u, :], 1.0, dif[:, u, :], ALU.add, ALU.mult))
                    links.wait()
                    for u in range(U):
                        dve.wait_ge(x2_ready, done(i, u))
                        nc.vector.scalar_tensor_tensor(r[:, u, :], dif[:, u, :], 0.5, x_2[:, u, :], ALU.mult, ALU.add).then_inc(r_ready, 1)
                    dve.wait_ge(r_ready, done(i, U - 1))
                    for u in range(U):
                        dve.wait_ge(stored[u], 16 * i + 16)
                    norm.steps(dve, links, i, r, x_o, out_ready)
                    links.end()

                ahead(0)
                norms_ahead(1)
                pipelined(dve, body)


ROUND = 12582912.0


def bit_ffn(nc, NB, x_in, x_out, w):
    F = 1024
    FC = F // P
    EPS_N, EPS_Q = 1e-8, 1e-5
    with ExitStack() as ctx:
        U = 4
        done, before = counts(U)
        s = Store(nc, ctx, "bf", U)
        w1f = s.sb("w1f", [P, KC, F])
        w2f = s.sb("w2f", [P, FC, D])
        w1t = s.sb("w1t", [P, KC, F], BF16)
        w2t = s.sb("w2t", [P, FC, D], BF16)
        wsum = s.sb("wsum", [P, 2])
        wmean = s.sb("wmean", [P, 2])
        wscale = s.sb("wscale", [P, 2])
        ones = s.sb("ones", [P, P])
        n1 = s.sb("n1", [T, D])
        n2 = s.sb("n2", [T, F])
        a_s = s.sb("a_s", [T, 2])
        ident = s.sb("ident", [P, P])
        identb = s.sb("identb", [P, P], BF16)
        x_t = s.sb("x_t", [T, U, D])
        sq = s.sb("sq", [T, U, F])
        ss = s.sb("ss", [T, U, 2])
        ms = s.sb("ms", [T, U, 2])
        rms = s.sb("rms", [T, U, 2])
        power = s.sb("power", [T, U])
        xn = s.sb("xn", [T, U, D])
        amax = s.sb("amax", [T, U, 2])
        ascale = s.sb("ascale", [T, U, 2])
        back = s.sb("back", [T, U, 2])
        xq = s.sb("xq", [T, U, D])
        xi = s.sb("xi", [T, U, D], BF16)
        xiT = s.sb("xiT", [P, U, KC, T], BF16)
        h = s.sb("h", [T, U, F])
        hn = s.sb("hn", [T, U, F])
        hi = s.sb("hi", [T, U, F], BF16)
        hiT = s.sb("hiT", [P, U, FC, T], BF16)
        r = s.sb("r", [T, U, D])
        x_o = s.sb("x_o", [T, U, D])
        norm = Norm(s, nc)
        H = [s.ps(f"H{u}", [P, F]) for u in range(U)]
        TT = [H[u][:, 0:FC * T // 2].bitcast(BF16).rearrange("p (c t) -> p c t", t=T) for u in range(U)]
        Y = [H[u][:, 512:512 + D] for u in range(U)]

        w_in, summed_w, wsum_ready, ones_set, tern_ready, power_set = (s.sem(n) for n in (
            "weights_loaded", "weight_sums", "wsum_ready", "ones_set", "ternary_ready", "power_set"))
        x_loaded, stored = s.sems("x_loaded"), s.sems("stored")
        ss1_ready, h_relu, h_sq, ss2_ready = (s.sem(n) for n in ("ss1_ready", "h_relu", "h_sq", "ss2_ready"))
        ms1_ready, xi_ready, back1_ready, h_ready, ms2_ready, hi_ready, r_ready, out_ready = (s.sem(n) for n in (
            "ms1_ready", "xi_ready", "back1_ready", "h_ready", "ms2_ready", "hi_ready", "r_ready", "out_ready"))
        rms1_ready, rms2_ready = s.sem("rms1_ready"), s.sem("rms2_ready")
        x_turned, h_done, h_turned, y_done = (s.sem(n) for n in ("x_turned", "h_done", "h_turned", "y_done"))
        xiT_ready, hiT_ready = s.sem("xiT_ready"), s.sem("hiT_ready")
        vlink, alink = s.sem("dve_link"), s.sem("act_link")

        kp = "(k p) n -> p k n"
        loads = [(w1f[:], w["ff_w1T"].rearrange(kp, p=P)), (w2f[:], w["ff_w2T"].rearrange(kp, p=P)),
                 (n1[:], w["ff_n1"].to_broadcast([T, D])), (n2[:], w["ff_n2"].to_broadcast([T, F])),
                 (a_s[:, 0:1], w["ff_as"].to_broadcast([T, 1])), (a_s[:, 1:2], w["ff_ab"].to_broadcast([T, 1])),
                 (ident[:], w["ident"])]
        W_ALL = 16 * len(loads)

        with nc.Block() as block:

            @block.sync
            def _(sp):
                for dst, src in loads:
                    sp.dma_start(dst, src).then_inc(w_in, 16)
                with sp.Fori(0, NB // U) as i:
                    for u in range(U):
                        sp.wait_ge(r_ready, before(i, u))
                        sp.dma_start(x_t[:, u, :], x_in[U * i + u]).then_inc(x_loaded[u], 16)

            @block.gpsimd
            def _(pool):
                nc.gpsimd.memset(ones[:], 1.0).then_inc(ones_set, 1)
                nc.gpsimd.memset(power[:], -0.5).then_inc(power_set, 1)
                norm.set_power(pool)
                pool.wait_ge(power_set, 1)
                with pool.Fori(0, NB // U) as i:
                    for k, (there, ready) in enumerate(((ms1_ready, rms1_ready), (ms2_ready, rms2_ready))):
                        pool.wait_ge(there, i + 1)
                        nc.gpsimd.tensor_tensor(rms[:, :, k], ms[:, :, k], power[:], ALU.pow).then_inc(ready, 1)
                    norm.raise_power(pool, i)

            @block.tensor
            def _(pe):
                for sem in (x_turned, h_done, h_turned, y_done):
                    pe.sem_inc(sem, U)
                pe.wait_ge(ones_set, 1)
                pe.wait_ge(wsum_ready, 1)
                nc.tensor.matmul(Y[0][:, 0:2], ones[:], wsum[:], start=True, stop=True).then_inc(summed_w, 1)
                pe.wait_ge(tern_ready, 1)
                with pe.Fori(0, NB // U) as i:
                    for u in range(U):
                        pe.wait_ge(xi_ready, done(i, u))
                        pe.wait_ge(r_ready, before(i, u))
                        for c in range(KC):
                            last = nc.tensor.transpose(TT[u][:, c, :], xi[:, u, c * P:(c + 1) * P], identb[:T, :T])
                        last.then_inc(x_turned, 1)
                    for u in range(U):
                        pe.wait_ge(xiT_ready, done(i, u))
                        for half in range(F // 512):
                            for c in range(KC):
                                last = nc.tensor.matmul(H[u][:T, half * 512:(half + 1) * 512], xiT[:, u, c, :],
                                                        w1t[:, c, half * 512:(half + 1) * 512], start=(c == 0), stop=(c == KC - 1))
                        last.then_inc(h_done, 1)
                    for u in range(U):
                        pe.wait_ge(hi_ready, done(i, u))
                        for c in range(FC):
                            last = nc.tensor.transpose(TT[u][:, c, :], hi[:, u, c * P:(c + 1) * P], identb[:T, :T])
                        last.then_inc(h_turned, 1)
                    for u in range(U):
                        pe.wait_ge(hiT_ready, done(i, u))
                        for c in range(FC):
                            last = nc.tensor.matmul(Y[u][:T, :], hiT[:, u, c, :], w2t[:, c, :], start=(c == 0), stop=(c == FC - 1))
                        last.then_inc(y_done, 1)

            @block.scalar
            def _(act):
                for sem in (ss1_ready, h_relu, h_sq, ss2_ready, xiT_ready, hiT_ready):
                    act.sem_inc(sem, U)
                for u in range(U):
                    act.sem_inc(stored[u], 16)
                with act.Fori(0, NB // U) as i:
                    for u in range(U):
                        act.wait_ge(x_loaded[u], 16 * i + 16)
                        nc.scalar.activation(sq[:, u, 0:D], x_t[:, u, :], ACT.Square, accum_out=ss[:, u, 0:1]).then_inc(ss1_ready, 1)
                    for u in range(U):
                        act.wait_ge(x_turned, done(i, u))
                        act.wait_ge(h_done, before(i, u))
                        nc.scalar.activation(xiT[:, u], TT[u][:, 0:KC, :], ACT.Copy).then_inc(xiT_ready, 1)
                    for u in range(U):
                        act.wait_ge(h_done, done(i, u))
                        act.wait_ge(back1_ready, done(i, u))
                        act.wait_ge(hi_ready, before(i, u))
                        nc.scalar.activation(h[:, u, :], H[u][:T, :], ACT.Relu, scale=back[:, u, 0:1]).then_inc(h_relu, 1)
                    for u in range(U):
                        act.wait_ge(h_relu, done(i, u))
                        nc.scalar.activation(h[:, u, :], h[:, u, :], ACT.Square).then_inc(h_sq, 1)
                    for u in range(U):
                        act.wait_ge(h_ready, done(i, u))
                        nc.scalar.activation(sq[:, u, :], h[:, u, :], ACT.Square, accum_out=ss[:, u, 1:2]).then_inc(ss2_ready, 1)
                    for u in range(U):
                        act.wait_ge(h_turned, done(i, u))
                        act.wait_ge(y_done, before(i, u))
                        nc.scalar.activation(hiT[:, u], TT[u][:, :, :], ACT.Copy).then_inc(hiT_ready, 1)
                    for u in range(U):
                        act.wait_ge(out_ready, done(i, u))
                        act.dma_start(x_out[U * i + u], x_o[:, u, :]).then_inc(stored[u], 16)
                for u in range(U):
                    act.wait_ge(stored[u], 16 * (NB // U) + 16)

            @block.vector
            def _(dve):
                for sem in (xi_ready, back1_ready, h_ready, hi_ready, r_ready, out_ready):
                    dve.sem_inc(sem, U)
                dve.wait_ge(w_in, W_ALL)
                count = 0

                def step(*instructions):
                    nonlocal count
                    for ins in instructions:
                        ins.then_inc(alink, 1)
                        count += 1
                    dve.wait_ge(alink, count)

                step(nc.vector.tensor_copy(identb[:], ident[:]))
                for k, wf in ((0, w1f), (1, w2f)):
                    last = nc.vector.tensor_reduce(wsum[:, k:k + 1], wf[:], axis=mybir.AxisListType.XY, op=ALU.add,
                                                   apply_absolute_value=True)
                last.then_inc(wsum_ready, 1)
                dve.wait_ge(summed_w, 1)
                step(nc.vector.tensor_scalar(wmean[:], Y[0][:, 0:2], 1.0 / (D * F), EPS_Q, ALU.mult, ALU.max))
                step(nc.vector.reciprocal(wscale[:], wmean[:]))
                for k, wf, wt in ((0, w1f, w1t), (1, w2f, w2t)):
                    step(nc.vector.tensor_scalar(wf[:], wf[:], wscale[:, k:k + 1], ROUND, ALU.mult, ALU.add))
                    step(nc.vector.tensor_scalar(wf[:], wf[:], ROUND, 1.0, ALU.subtract, ALU.min))
                    last = nc.vector.tensor_scalar(wt[:], wf[:], -1.0, None, ALU.max)
                last.then_inc(tern_ready, 1)

                with dve.Fori(0, NB // U) as i:
                    links = Links(dve, vlink, i, 52)

                    def quantise(src, dst, k, scratch, ready):
                        for u in range(U):
                            links.add(nc.vector.tensor_reduce(amax[:, u, k:k + 1], src[:, u, :], axis=AXIS_X, op=ALU.max,
                                                              apply_absolute_value=True))
                        links.wait()
                        for u in range(U):
                            links.add(nc.vector.tensor_scalar(back[:, u, k:k + 1], amax[:, u, k:k + 1], EPS_Q, 1.0 / 127.0, ALU.max, ALU.mult))
                        links.wait()
                        for u in range(U):
                            links.add(nc.vector.reciprocal(ascale[:, u, k:k + 1], back[:, u, k:k + 1]))
                        links.wait()
                        for u in range(U):
                            links.add(nc.vector.tensor_scalar(scratch[:, u, :], src[:, u, :], ascale[:, u, k:k + 1], ROUND, ALU.mult, ALU.add))
                            if k == 0:
                                nc.vector.tensor_scalar(back[:, u, k:k + 1], back[:, u, k:k + 1], wmean[:T, k:k + 1], None,
                                                        ALU.mult).then_inc(back1_ready, 1)
                            else:
                                links.add(nc.vector.tensor_scalar(back[:, u, k:k + 1], back[:, u, k:k + 1], wmean[:T, k:k + 1], None, ALU.mult))
                        links.wait()
                        for u in range(U):
                            nc.vector.tensor_scalar(dst[:, u, :], scratch[:, u, :], ROUND, 127.0, ALU.subtract, ALU.min).then_inc(ready, 1)

                    dve.wait_ge(ss1_ready, done(i, U - 1))
                    nc.vector.tensor_scalar(ms[:, :, 0], ss[:, :, 0], 1.0 / D, EPS_N, ALU.mult, ALU.add).then_inc(ms1_ready, 1)
                    dve.wait_ge(rms1_ready, i + 1)
                    for u in range(U):
                        links.add(nc.vector.scalar_tensor_tensor(xn[:, u, :], x_t[:, u, :], rms[:, u, 0:1], n1[:], ALU.mult, ALU.mult))
                    links.wait()
                    dve.wait_ge(x_turned, before(i, U - 1))
                    dve.wait_ge(h_relu, before(i, U - 1))
                    quantise(xn, xi, 0, xq, xi_ready)
                    for u in range(U):
                        dve.wait_ge(h_sq, done(i, u))
                        nc.vector.tensor_scalar(h[:, u, :], h[:, u, :], a_s[:, 0:1], a_s[:, 1:2], ALU.mult, ALU.add).then_inc(h_ready, 1)
                    dve.wait_ge(ss2_ready, done(i, U - 1))
                    nc.vector.tensor_scalar(ms[:, :, 1], ss[:, :, 1], 1.0 / F, EPS_N, ALU.mult, ALU.add).then_inc(ms2_ready, 1)
                    dve.wait_ge(rms2_ready, i + 1)
                    for u in range(U):
                        links.add(nc.vector.scalar_tensor_tensor(hn[:, u, :], h[:, u, :], rms[:, u, 1:2], n2[:], ALU.mult, ALU.mult))
                    links.wait()
                    dve.wait_ge(h_turned, before(i, U - 1))
                    quantise(hn, hi, 1, hn, hi_ready)
                    for u in range(U):
                        dve.wait_ge(y_done, done(i, u))
                        nc.vector.scalar_tensor_tensor(r[:, u, :], Y[u][:T, :], back[:, u, 1:2], x_t[:, u, :], ALU.mult, ALU.add).then_inc(r_ready, 1)
                    dve.wait_ge(r_ready, done(i, U - 1))
                    for u in range(U):
                        dve.wait_ge(stored[u], 16 * i + 16)
                    norm.steps(dve, links, i, r, x_o, out_ready)
                    links.end()


def decoder(nc, x, out, w):
    NB = x.shape[0]
    src_len = w["ctx"].shape[1]

    def scratch(name, shape, dt=F32):
        return nc.dram_tensor(name, shape, dt, kind="Internal").ap()

    x1, x2, xz, x4, x5 = (scratch(n, [NB, T, D]) for n in ("x1", "x2", "x_plus_shared", "x4", "x5"))
    slot_rows = scratch("slot_rows", [SLOTS, D])
    slot_out = scratch("slot_out", [SLOTS, D])
    slot_ids = scratch("slot_ids", [NB, T, TOPK], U32)
    slot_weights = scratch("slot_weights", [NB, T, TOPK])
    self_attention(nc, NB, x, x1, w)
    cross_attention_strided(nc, NB, x1, x2, w, src_len)
    route(nc, NB, x2, w, slot_rows, xz, slot_ids, slot_weights)
    experts(nc, w, slot_rows, slot_out)
    linear_attention(nc, NB, xz, slot_out, slot_ids, slot_weights, x4, w)
    cross_attention(nc, NB, x4, x5, w, src_len)
    bit_ffn(nc, NB, x5, out, w)


def rope_tables(t, dim, theta):
    inv = (1.0 / theta ** (np.arange(0, dim, 2, dtype=np.float32) / np.float32(dim))).astype(np.float32)
    f = np.arange(t, dtype=np.float32)[:, None] * inv[None, :]
    e = np.concatenate((f, f), -1)
    return np.cos(e).astype(np.float32), np.sin(e).astype(np.float32)


def resize_matrix(n, m):
    inv = np.float32(n / m)
    k = max(float(inv), 1.0)
    f = (np.arange(m, dtype=np.float32) + np.float32(0.5)) * inv - np.float32(0.5)
    d = np.abs(f[None, :] - np.arange(n, dtype=np.float32)[:, None]) / np.float32(k)
    wt = np.maximum(np.float32(0), np.float32(1) - d)
    return (wt / wt.sum(0, keepdims=True)).astype(np.float32)


def position_bias(lq, lkv, length=128):
    pos = np.arange(length, dtype=np.float32)
    dist = np.abs(pos[None, :] - pos[:, None])
    bias = (np.exp(-dist * np.float32(0.1)) - dist * np.float32(0.05)).astype(np.float64)
    return (resize_matrix(length, lq).T.astype(np.float64) @ bias @ resize_matrix(length, lkv).astype(np.float64)).astype(np.float32)


def shape_constants(src_len):
    c = {}
    p = np.arange(P)
    t = np.arange(T)
    cos, sin = rope_tables(T, DH // 2, 10000.0)
    c["cos_sa"] = np.ones((P, T), np.float32)
    c["sin_sa"] = np.zeros((P, T), np.float32)
    for h in range(P // DH):
        c["cos_sa"][h * DH + DH // 2:(h + 1) * DH] = cos.T
        c["sin_sa"][h * DH + DH // 2:(h + 1) * DH] = sin.T
    cos, sin = rope_tables(src_len, DH, 10000.0)
    c["cos_xa"] = np.tile(cos.T, (P // DH, 1))
    c["sin_xa"] = np.tile(sin.T, (P // DH, 1))
    bias = position_bias(T, src_len) * np.float32(DH ** 0.5)
    step = (src_len - 1) // 3
    c["bias_xa"] = np.stack([bias[:, step * n:step * n + step + 1].T for n in range(3)], 1)
    c["head_mask"] = (p[:, None] // DH == np.arange(8)[None]).astype(np.float32)
    c["head_mask2"] = ((p[:, None] % 64) // DH == np.arange(4)[None]).astype(np.float32)
    c["head_mask4"] = (p[:, None] // 32 == np.arange(4)[None]).astype(np.float32)
    c["block_mask"] = (p[:, None] // DH == p[None] // DH).astype(np.float32)
    c["ident"] = np.eye(P, dtype=np.float32)
    c["causal"] = np.where(t[None, :] >= t[:, None], 0, NEG).astype(np.float32)
    c["earlier"] = (t[:, None] < t[None]).astype(np.float32)
    c["expert_no"] = np.tile(np.arange(EXPERTS, dtype=np.float32), (T, 1))
    c["first_slot"] = np.tile(np.arange(0, SLOTS, CAP, dtype=np.float32), (T, 1))
    keys = -(-src_len // 8)
    c["v_ones"] = np.zeros((P, 4, 96), np.float32)
    for h in range(8):
        row = 64 * (h % 2)
        c["v_ones"][row:row + len(range(h, src_len, 8)), h // 2, 33 * (h % 2) + 32] = 1
    assert keys <= 64
    return c


def layouts(x):
    o = {}
    for k in ("Wq_down", "Wk_down", "Wv_down"):
        o["L0_attn_" + k] = x["L0_attn_" + k].T
    for k in ("Wq_up_c", "Wq_up_e", "Wk_up_c", "Wk_up_e", "Wv_up", "Wc"):
        o["L0_attn_" + k] = x["L0_attn_" + k]
    for k in ("Wq", "Wk", "Wv", "Wo"):
        o["L0_xattn_" + k] = x["L0_xattn_" + k]
    for k in ("bq", "bk", "bv"):
        o["L0_xattn_" + k] = x["L0_xattn_" + k].reshape(KC, P).T
    o["L0_xattn_bo"] = x["L0_xattn_bo"].reshape(1, D)
    ctx = x["ctx_1024"]
    n, src_len, _ = ctx.shape
    strided = np.zeros((n, 8, 64, D), ctx.dtype)
    for h in range(8):
        strided[:, h, :len(range(h, src_len, 8))] = ctx[:, h::8]
    o["ctxT"] = strided.reshape(n, 512, KC, P).transpose(0, 3, 2, 1)
    o["ctx"] = ctx
    o["gate_wT"], o["gate_b"] = x["L0_ffn_gate_w"].T, x["L0_ffn_gate_b"].reshape(1, EXPERTS)
    o["ws1T"], o["ws2T"], o["ws3T"] = x["L0_ffn_ws1"].T, x["L0_ffn_ws2"].T, x["L0_ffn_ws3"].T
    for k in ("w1", "w2", "w3"):
        o[k + "T"] = x["L0_ffn_" + k].transpose(0, 2, 1)
    o["L1_wqkT"] = np.concatenate([x["L1_attn_Wq"].T, x["L1_attn_Wk"].T], 1)
    o["L1_wvT"], o["L1_woT"] = x["L1_attn_Wv"].T, x["L1_attn_Wo"].T
    o["L1_bqk"] = np.concatenate([x["L1_attn_bq"], x["L1_attn_bk"]]).reshape(1, 2 * D)
    o["L1_bv"], o["L1_bo"] = x["L1_attn_bv"].reshape(1, D), x["L1_attn_bo"].reshape(1, D)
    o["L1x_wqkvT"], o["L1x_woT"], o["L1x_wgT"] = x["L1_xattn_Wqkv"].T, x["L1_xattn_Wout"].T, x["L1_xattn_Wgate"].T
    o["L1x_bo"], o["L1x_bg"] = x["L1_xattn_b_out"].reshape(1, D), x["L1_xattn_b_gate"].reshape(1, D)
    o["L1x_gamma"], o["L1x_beta"] = x["L1_xattn_gamma"].reshape(KC, P).T, x["L1_xattn_beta"].reshape(KC, P).T
    o["ff_w1T"], o["ff_w2T"] = x["L1_ffn_w1"].T, x["L1_ffn_w2"].T
    o["ff_n1"], o["ff_n2"] = x["L1_ffn_norm1_w"].reshape(1, -1), x["L1_ffn_norm2_w"].reshape(1, -1)
    o["ff_as"], o["ff_ab"] = x["L1_ffn_act_scale"].reshape(1, 1), x["L1_ffn_act_bias"].reshape(1, 1)
    return o


def kernel(**inputs):
    import concourse.bacc as _bacc
    from concourse.bass_utils import run_bass_kernel_spmd as _run

    x = {k: np.asarray(v) for k, v in inputs.items()}
    arrays = {"x_tokens": x["x"], **layouts(x), **shape_constants(x["ctx_1024"].shape[1])}
    arrays = {f"in_{k}": np.ascontiguousarray(v) for k, v in arrays.items()}
    nc = _bacc.Bacc("TRN2", target_bir_lowering=False, num_devices=1)
    w = {k[3:]: nc.dram_tensor(k, v.shape, mybir.dt.from_np(v.dtype), kind="ExternalInput").ap() for k, v in arrays.items()}
    out = nc.dram_tensor("out_0", list(x["x"].shape), F32, kind="ExternalOutput").ap()
    decoder(nc, w["x_tokens"], out, w)
    r = _run(nc, [arrays], core_ids=[0])
    return r.results[0]["out_0"]
```

```python
from contextlib import ExitStack

import numpy as np

import concourse.bass as bass
from concourse import mybir

F32 = mybir.dt.float32
F32R = mybir.dt.float32r
BF16 = mybir.dt.bfloat16
U32 = mybir.dt.uint32
ALU = mybir.AluOpType
ACT = mybir.ActivationFunctionType
AXIS_X = mybir.AxisListType.X

T = 100
D = 256
P = 128
KC = D // P
HEADS = 16
DH = D // HEADS
GROUPS = 4
HPG = HEADS // GROUPS
GW = HPG * T
LN_EPS = 1e-5
NEG = -1e30


def counts(U):

    def done(i, u, j=0, steps=1):
        return i * (U * steps) + (U * steps + U * j + u + 1)

    def before(i, u, j=0, steps=1):
        return i * (U * steps) + (U * j + u + 1)

    return done, before


def pipelined(eng, N, body):
    assert N >= 3
    with eng.Fori(0, N - 2) as i:
        body(i, 2)
    body(N - 2, 1)
    body(N - 1, 0)


class Links:

    def __init__(self, eng, sem, i, per_iter):
        self.eng, self.sem, self.i, self.per_iter, self.k = eng, sem, i, per_iter, 0

    def add(self, ins):
        self.k += 1
        ins.then_inc(self.sem, 1)

    def wait(self, back=0):
        self.eng.wait_ge(self.sem, self.i * self.per_iter + (self.k - back))

    def end(self):
        assert self.k == self.per_iter, f"links in one iteration: {self.k}"


class Store:

    def __init__(self, nc, ctx, stage, U):
        self.U = U
        self.nc, self.ctx, self.stage = nc, ctx, stage
        self.semaphores = []
        ctx.callback(self.end)

    def sb(self, name, shape, dt=F32):
        return self.ctx.enter_context(self.nc.sbuf_tensor(f"{self.stage}_{name}", shape, dt))

    def ps(self, name, shape, dt=F32):
        return self.ctx.enter_context(self.nc.psum_tensor(f"{self.stage}_{name}", shape, dt))

    def sem(self, name):
        self.semaphores.append(self.nc.alloc_semaphore(f"{self.stage}_{name}"))
        return self.semaphores[-1]

    def end(self):
        self.nc.clear_and_free_semaphores(self.semaphores)
        self.nc.all_engine_barrier()

    def sems(self, name):
        return [self.sem(f"{name}{u}") for u in range(self.U)]


class Norm:

    def __init__(self, s, nc, rows=T, tag="", lots=None):
        lots = lots or s.U
        self.U = s.U
        self.nc, self.rows = nc, rows
        tag = "ln" + tag + "_"
        self.stats = s.sb(tag + "stats", [rows, lots, 6])
        self.mv = s.sb(tag + "mv", [rows, lots, 2])
        self.spare = s.sb(tag + "spare", [rows, 1])
        self.var = s.sb(tag + "var", [rows, lots])
        self.rstd = s.sb(tag + "rstd", [rows, lots])
        self.power = s.sb(tag + "power", [rows, lots])
        self.var_ready = s.sem(tag + "var_ready")
        self.rstd_ready = s.sem(tag + "rstd_ready")
        self.power_set = s.sem(tag + "power_set")

    def set_power(self, pool):
        self.nc.gpsimd.memset(self.power[:], -0.5).then_inc(self.power_set, 1)
        pool.wait_ge(self.power_set, 1)

    def raise_power(self, pool, i):
        pool.wait_ge(self.var_ready, i + 1)
        self.nc.gpsimd.tensor_tensor(self.rstd[:], self.var[:], self.power[:], ALU.pow).then_inc(self.rstd_ready, 1)

    def steps_of(self, dve, links, i, sources, outs, out_ready):
        nc, mv = self.nc, self.mv
        for n, src in enumerate(sources):
            links.add(nc.vector.bn_stats(self.stats[:, n, :], src))
        links.wait()
        nc.vector.memset(self.spare[:], 0.0)
        for n in range(len(sources)):
            links.add(nc.vector.bn_aggr(mv[:, n, :], self.stats[:, n, :]))
        links.wait()
        nc.vector.tensor_scalar(self.var[:], mv[:, :, 1], LN_EPS, None, ALU.add).then_inc(self.var_ready, 1)
        dve.wait_ge(self.rstd_ready, i + 1)
        for n, (src, out) in enumerate(zip(sources, outs)):
            nc.vector.tensor_scalar(out, src, mv[:, n, 0:1], self.rstd[:, n:n + 1],
                                    ALU.subtract, ALU.mult).then_inc(out_ready, 1)

    def steps(self, dve, links, i, src, out, out_ready):
        self.steps_of(dve, links, i, [src[:, u, :] for u in range(self.U)], [out[:, u, :] for u in range(self.U)], out_ready)


def self_attention(nc, NB, x_in, x_out, w):
    with ExitStack() as ctx:
        U = 2
        done, before = counts(U)
        s = Store(nc, ctx, "sa", U)
        down = s.sb("down", [P, 3, HEADS // 2, D])
        up = s.sb("up", [P, 3, 2, 32])
        wq = s.sb("wq", [P, 2, KC, D])
        wk = s.sb("wk", [P, 2, KC, D])
        wv = s.sb("wv", [P, KC, D])
        wc = s.sb("wc", [P, KC, D])
        cosT = s.sb("cosT", [P, T])
        sinT = s.sb("sinT", [P, T])
        head_mask = s.sb("head_mask", [P, 8])
        head_mask2 = s.sb("head_mask2", [P, 4])
        ident = s.sb("ident", [P, P])
        identb = s.sb("identb", [P, P], BF16)
        causalf = s.sb("causalf", [T, T])
        causal = s.sb("causal", [T, HPG, T], BF16)
        neg1 = s.sb("neg1", [T, T], F32R)
        x_t = s.sb("x_t", [T, U, D])
        x_res = s.sb("x_res", [T, U, D])
        xT = s.sb("xT", [P, KC, U, T])
        q_c, k_c = s.sb("q_c", [P, KC, U, T]), s.sb("k_c", [P, KC, U, T])
        q_s, k_s = s.sb("q_s", [P, KC, U, T]), s.sb("k_s", [P, KC, U, T])
        kT = s.sb("kT", [P, KC, U, T])
        q_bd = s.sb("q_bd", [P, U, KC, 8, T])
        v1 = s.sb("v1", [T, U, GROUPS, P])
        mx = s.sb("mx", [T, U, GW])
        nmax = s.sb("nmax", [T, U, HPG])
        dmax = s.sb("dmax", [T, U, HPG, T], F32R)
        prob = s.sb("prob", [T, U, GW])
        own = s.sb("own", [P, U, GW])
        nd = s.sb("nd", [P, U, T])
        rec = s.sb("rec", [64, U, T])
        yT = s.sb("yT", [P, U, KC, T])
        r = s.sb("r", [T, U, D])
        norm = Norm(s, nc)
        x_o = s.sb("x_o", [T, U, D])
        S = [s.ps(f"S{u}", [P, 2, 512]) for u in range(U)]
        W = [s.ps(f"W{u}", [P, 512]) for u in range(U)]
        X = [s.ps(f"X{u}", [P, 512]) for u in range(U)]

        w_in = s.sem("weights_loaded")
        up_zero, up_ready = s.sem("up_zero"), s.sem("up_ready")
        fused = s.sem("fused_in_psum")
        fused_sb = s.sem("fused_in_sbuf")
        const_ready = s.sem("const_ready")
        x_loaded = s.sems("x_loaded")
        res_loaded = s.sems("res_loaded")
        stored = s.sems("stored")
        x_turned = s.sem("x_turned")
        xT_ready = s.sem("xT_ready")
        q_done, k_done = s.sem("q_done"), s.sem("k_done")
        q_rot, k_rot = s.sem("q_rot"), s.sem("k_rot")
        q_sum = s.sem("q_sum")
        k_ready = s.sem("k_ready")
        qbd_ready = s.sem("qbd_ready")
        v_done = s.sem("v_done")
        v_ready = s.sem("v_ready")
        scored = s.sem("scored")
        mx_copied = s.sem("mx_copied")
        mx_turned = s.sem("mx_turned")
        max_ready = s.sem("max_ready")
        shifted = s.sem("shifted")
        prob_ready = s.sem("prob_ready")
        av_done = s.sem("av_done")
        own_ready = s.sem("own_ready")
        nd_ready = s.sem("nd_ready")
        yT_ready = s.sem("yT_ready")
        y_done = s.sem("y_done")
        r_ready = s.sem("r_ready")
        out_ready = s.sem("out_ready")
        vlink = s.sem("dve_link")
        G = GROUPS
        N = NB // U

        slots = [(j, u) for j in range(G) for u in range(U)]
        LAST = len(slots) - 1

        def one_ahead(body):
            def run(eng):
                with eng.Fori(0, N - 1) as i:
                    body(i, True)
                body(N - 1, False)
            return run

        with nc.Block() as block:

            @block.sync
            def _(sp):
                for k, name in enumerate(("L0_attn_Wq_down", "L0_attn_Wk_down", "L0_attn_Wv_down")):
                    sp.dma_start(down[:, k, :, :], w[name].rearrange("(h l) c -> l h c", l=P)).then_inc(w_in, 16)
                sp.wait_ge(up_zero, 1)
                for head, rows in ((0, slice(0, 64)), (1, slice(64, 128))):
                    for k, (c_, e_) in enumerate((("Wq_up_c", "Wq_up_e"), ("Wk_up_c", "Wk_up_e"))):
                        sp.dma_start(up[rows, k, head, 0:8], w["L0_attn_" + c_]).then_inc(w_in, 16)
                        sp.dma_start(up[rows, k, head, 8:16], w["L0_attn_" + e_]).then_inc(w_in, 16)
                    sp.dma_start(up[rows, 2, head, 0:16], w["L0_attn_Wv_up"]).then_inc(w_in, 16)
                sp.dma_start(wc[:], w["L0_attn_Wc"].rearrange("(k p) n -> p k n", p=P)).then_inc(w_in, 16)
                sp.dma_start(cosT[:], w["cos_sa"]).then_inc(w_in, 16)
                sp.dma_start(sinT[:], w["sin_sa"]).then_inc(w_in, 16)
                sp.dma_start(head_mask[:], w["head_mask"]).then_inc(w_in, 16)
                sp.dma_start(head_mask2[:], w["head_mask2"]).then_inc(w_in, 16)
                sp.dma_start(ident[:], w["ident"]).then_inc(w_in, 16)
                sp.dma_start(causalf[:], w["causal"]).then_inc(w_in, 16)
                for u in range(U):
                    sp.sem_inc(stored[u], 16)

                def load(i):
                    for u in range(U):
                        sp.wait_ge(x_turned, i + 1)
                        sp.dma_start(x_t[:, u, :], x_in[U * i + u]).then_inc(x_loaded[u], 16)

                def load_again(i):
                    for u in range(U):
                        sp.wait_ge(r_ready, before(i, u))
                        sp.dma_start(x_res[:, u, :], x_in[U * i + u]).then_inc(res_loaded[u], 16)

                def body(i, coming):
                    if coming == 2:
                        load(i + 2)
                    if coming:
                        load_again(i + 1)
                    for u in range(U):
                        sp.wait_ge(out_ready, done(i, u))
                        sp.dma_start(x_out[U * i + u], x_o[:, u, :]).then_inc(stored[u], 16)

                load(0)
                load(1)
                load_again(0)
                pipelined(sp, N, body)
                for u in range(U):
                    sp.wait_ge(stored[u], 16 * N + 16)

            W_ALL = 16 * 20

            @block.tensor
            def _(pe):
                for sem, steps in ((v_done, 1), (scored, G), (mx_turned, G), (shifted, G), (av_done, G), (y_done, 1)):
                    pe.sem_inc(sem, U * steps)
                pe.sem_inc(x_turned, 1)
                pe.wait_ge(w_in, W_ALL)
                pe.wait_ge(up_ready, 1)
                for k in range(3):
                    n = 32 if k < 2 else 16
                    if k:
                        pe.wait_ge(fused_sb, k)
                    for c in range(KC):
                        for h in range(HEADS // 2):
                            last = nc.tensor.matmul(S[0][:, c, 2 * h * n:2 * (h + 1) * n], down[:, k, h, c * P:(c + 1) * P],
                                                    up[:, k, :, 0:n], start=True, stop=True)
                    last.then_inc(fused, 1)
                pe.wait_ge(fused_sb, 3)
                pe.wait_ge(const_ready, 1)

                def turn(i):
                    for u in range(U):
                        pe.wait_ge(x_loaded[u], 16 * i + 16)
                        pe.wait_ge(v_ready, before(i, u))
                        for c in range(KC):
                            last = nc.tensor.transpose(X[u][:, c * T:(c + 1) * T], x_t[:, u, c * P:(c + 1) * P], ident[:T, :T])
                    last.then_inc(x_turned, 1)

                def project(wm, turned, g, i, free, signal):
                    if turned == 0 and g == 0:
                        pe.wait_ge(free, i + 1)
                    for c in range(KC):
                        last = nc.tensor.matmul(X[turned][:, g * U * T:(g + 1) * U * T], wm[:, turned, c, g * P:(g + 1) * P],
                                                xT[:, c].rearrange("p u t -> p (u t)"), start=(c == 0), stop=(c == KC - 1))
                    if turned and g == KC - 1:
                        last.then_inc(signal, 1)

                def values(i):
                    pe.wait_ge(k_rot, i + 1)
                    for u in range(U):
                        for c in range(KC):
                            last = nc.tensor.matmul(X[u][:T, 0:D], xT[:, c, u, :], wv[:, c, :], start=(c == 0), stop=(c == KC - 1))
                        last.then_inc(v_done, 1)

                def score(i, j, u):
                    g, h0 = j // 2, 4 * (j % 2)
                    if h0 == 0:
                        pe.wait_ge(k_ready, KC * i + g + 1)
                        pe.wait_ge(qbd_ready, done(i, u, g, KC))
                    pe.wait_ge(prob_ready, done(i, u, j - 2, G) if j >= 2 else before(i, u, j + 2, G))
                    nc.tensor.matmul(S[u][:T, j % 2, 0:GW], kT[:, g, u, :],
                                     q_bd[:, u, g, h0:h0 + 4, :].rearrange("p h t -> p (h t)"), start=True, stop=False)
                    nc.tensor.matmul(S[u][:T, j % 2, 0:GW], identb[:T, :T],
                                     causal[:].rearrange("p h t -> p (h t)"), start=False, stop=True).then_inc(scored, 1)

                def turn_maxima(i, j, u):
                    pe.wait_ge(mx_copied, done(i, u, j, G))
                    if j:
                        pe.wait_ge(own_ready, done(i, u, j - 1, G))
                    else:
                        pe.wait_ge(r_ready, before(i, u))
                    for h in range(HPG):
                        last = nc.tensor.transpose(W[u][:T, h * P:h * P + T], mx[:, u, h * T:(h + 1) * T], ident[:T, :T])
                    last.then_inc(mx_turned, 1)

                def shift(i, j, u):
                    pe.wait_ge(max_ready, done(i, u, j, G))
                    nc.tensor.matmul(S[u][:T, j % 2, 0:GW], neg1[:], dmax[:, u, :, :].rearrange("p h t -> p (h t)"),
                                     start=False, stop=True, skip_group_check=True).then_inc(shifted, 1)

                def attend(i, j, u):
                    pe.wait_ge(prob_ready, done(i, u, j, G))
                    if j == 0:
                        pe.wait_ge(v_ready, done(i, u))
                    nc.tensor.matmul(W[u][:, 0:GW], v1[:, u, j, :], prob[:, u, :], start=True, stop=True).then_inc(av_done, 1)

                turn(0)
                for wm, free, signal in ((wq, xT_ready, q_done), (wk, q_rot, k_done)):
                    for turned in range(2):
                        for g in range(KC):
                            project(wm, turned, g, 0, free, signal)
                values(0)
                score(0, *slots[0])

                def body(i, coming):
                    queries = lambda turned, g: project(wq, turned, g, i + 1, xT_ready, q_done)
                    keys = lambda turned, g: project(wk, turned, g, i + 1, q_rot, k_done)
                    ahead = {1: (queries, 0), 2: (queries, 1), 4: (keys, 0), 5: (keys, 1)} if coming else {}
                    for k, (j, u) in enumerate(slots):
                        turn_maxima(i, j, u)
                        if k:
                            attend(i, *slots[k - 1])
                        if k < LAST:
                            score(i, *slots[k + 1])
                        if coming and k == 0:
                            turn(i + 1)
                        if k in ahead:
                            what, turned = ahead[k]
                            what(turned, 0)
                        shift(i, j, u)
                        if k in ahead:
                            what(turned, 1)
                    if coming:
                        values(i + 1)
                    attend(i, *slots[LAST])
                    if coming:
                        score(i + 1, *slots[0])
                    for u in range(U):
                        pe.wait_ge(yT_ready, done(i, u, G - 1, G))
                        for c in range(KC):
                            last = nc.tensor.matmul(W[u][:T, 0:D], yT[:, u, c, :], wc[:, c, :],
                                                    start=(c == 0), stop=(c == KC - 1))
                        last.then_inc(y_done, 1)

                one_ahead(body)(pe)

            @block.scalar
            def _(act):
                for sem, steps in ((v_ready, 1), (mx_copied, G), (prob_ready, G), (own_ready, G)):
                    act.sem_inc(sem, U * steps)
                for k in range(3):
                    act.wait_ge(fused, k + 1)
                    for c in range(KC):
                        if k < 2:
                            src = S[0][:, c, :].rearrange("p (h n) -> p h n", n=32)
                            dst = (wq, wk)[k]
                            for t in range(2):
                                last = nc.scalar.activation(dst[:, t, c, :].rearrange("p (h n) -> p h n", n=16),
                                                            src[:, :, 16 * t:16 * t + 16], ACT.Copy)
                        else:
                            last = nc.scalar.activation(wv[:, c, :], S[0][:, c, 0:D], ACT.Copy)
                    last.then_inc(fused_sb, 1)

                def copy_x(i):
                    act.wait_ge(x_turned, i + 2)
                    for u in range(U):
                        last = nc.scalar.activation(xT[:, :, u, :], X[u][:, 0:KC * T].rearrange("p (c t) -> p c t", t=T), ACT.Copy)
                    last.then_inc(xT_ready, 1)

                def copy_values(i):
                    for u in range(U):
                        act.wait_ge(v_done, done(i, u))
                        act.wait_ge(av_done, before(i, u, G - 1, G))
                        nc.scalar.activation(v1[:, u, :, 0:64], X[u][:T, 0:D].rearrange("p (g n) -> p g n", n=64),
                                             ACT.Copy).then_inc(v_ready, 1)

                def copy_scores(i, j, u):
                    act.wait_ge(scored, done(i, u, j, G))
                    nc.scalar.activation(mx[:, u, :], S[u][:T, j % 2, 0:GW], ACT.Copy).then_inc(mx_copied, 1)

                def pick_own(i, j, u):
                    act.wait_ge(av_done, done(i, u, j, G))
                    act.wait_ge(nd_ready, done(i, u, j - 1, G) if j else before(i, u, G - 1, G))
                    for h in range(HPG):
                        last = nc.scalar.activation(own[:, u, h * T:(h + 1) * T], W[u][:, h * T:(h + 1) * T], ACT.Copy,
                                                    scale=head_mask2[:, h:h + 1])
                    last.then_inc(own_ready, 1)

                act.wait_ge(w_in, W_ALL)
                copy_x(0)
                copy_values(0)
                copy_scores(0, *slots[0])

                def body(i, coming):
                    for k, (j, u) in enumerate(slots):
                        if k:
                            pick_own(i, *slots[k - 1])
                        if k < LAST:
                            copy_scores(i, *slots[k + 1])
                        if coming and k == 0:
                            copy_x(i + 1)
                        act.wait_ge(shifted, done(i, u, j, G))
                        nc.scalar.activation(prob[:, u, :], S[u][:T, j % 2, 0:GW], ACT.Exp,
                                             scale=float(DH) ** -0.5).then_inc(prob_ready, 1)
                    pick_own(i, *slots[LAST])
                    if coming:
                        copy_values(i + 1)
                        copy_scores(i + 1, *slots[0])

                one_ahead(body)(act)

            @block.gpsimd
            def _(pool):
                pool.sem_inc(qbd_ready, U * KC)
                norm.set_power(pool)
                pool.wait_ge(w_in, W_ALL)

                def sum_queries(i):
                    pool.wait_ge(q_rot, i + 1)
                    nc.gpsimd.tensor_tensor(q_c[:].rearrange("p c u t -> p (c u t)"), q_c[:].rearrange("p c u t -> p (c u t)"),
                                            q_s[:].rearrange("p c u t -> p (c u t)"), ALU.add).then_inc(q_sum, 1)

                def keys_and_queries(i, g):
                    pool.wait_ge(k_rot, i + 1)
                    pool.wait_ge(scored, before(i, U - 1, G - 1, G))
                    nc.gpsimd.tensor_tensor(kT[:, g].rearrange("p u t -> p (u t)"), k_c[:, g].rearrange("p u t -> p (u t)"),
                                            k_s[:, g].rearrange("p u t -> p (u t)"), ALU.add).then_inc(k_ready, 1)
                    pool.wait_ge(q_sum, i + 1)
                    for u in range(U):
                        nc.gpsimd.tensor_tensor(q_bd[:, u, g, :, :],
                                                q_c[:, g, u, :].unsqueeze(1).to_broadcast([P, 8, T]),
                                                head_mask[:].unsqueeze(2).to_broadcast([P, 8, T]),
                                                ALU.mult).then_inc(qbd_ready, 1)

                sum_queries(0)
                for g in range(KC):
                    keys_and_queries(0, g)

                def body(i, coming):
                    if coming:
                        sum_queries(i + 1)
                        keys_and_queries(i + 1, 0)
                    norm.raise_power(pool, i)
                    if coming:
                        keys_and_queries(i + 1, 1)

                one_ahead(body)(pool)

            @block.vector
            def _(dve):
                nc.vector.memset(up[:], 0.0).then_inc(up_zero, 1)
                nc.vector.memset(v1[:], 1.0)
                nc.vector.memset(neg1[:].bitcast(F32), -1.0)
                for sem, steps in ((max_ready, G), (nd_ready, G), (yT_ready, G), (r_ready, 1), (out_ready, 1)):
                    dve.sem_inc(sem, U * steps)
                dve.wait_ge(w_in, W_ALL)
                for k in range(2):
                    e = up[:, k, :, 8:16].rearrange("p h (n two) -> p h n two", two=2)
                    t = up[:, k, :, 24:32].rearrange("p h (n two) -> p h n two", two=2)
                    nc.vector.tensor_scalar(t[:, :, :, 0], e[:, :, :, 1], -1.0, None, ALU.mult)
                    last = nc.vector.tensor_copy(t[:, :, :, 1], e[:, :, :, 0])
                last.then_inc(up_ready, 1)
                nc.vector.tensor_copy(identb[:], ident[:])
                nc.vector.tensor_copy(causal[:], causalf[:].unsqueeze(1).to_broadcast([T, HPG, T])).then_inc(const_ready, 1)

                def rotate(i, signal, cos_part, sin_part, ready, free):
                    dve.wait_ge(signal, i + 1)
                    dve.wait_ge(qbd_ready, free)
                    for k, (dst, table) in enumerate(((cos_part, cosT), (sin_part, sinT))):
                        last = nc.vector.tensor_tensor(dst[:].rearrange("p g u t -> p (g u) t"),
                                                       X[k][:, 0:KC * U * T].rearrange("p (a t) -> p a t", t=T),
                                                       table[:].unsqueeze(1).to_broadcast([P, KC * U, T]), ALU.mult)
                    last.then_inc(ready, 1)

                def rotate_queries(i):
                    rotate(i, q_done, q_c, q_s, q_rot, before(i, U - 1, KC - 1, KC))

                def rotate_keys(i):
                    rotate(i, k_done, k_c, k_s, k_rot, before(i, U - 1, KC - 1, KC))

                def spread_maxima(i, j, u, links):
                    dve.wait_ge(mx_turned, done(i, u, j, G))
                    links.add(nc.vector.tensor_reduce(nmax[:, u, :], W[u][:T, :].rearrange("p (h t) -> p h t", t=P)[:, :, 0:T],
                                                      axis=AXIS_X, op=ALU.max))
                    links.wait()
                    nc.vector.tensor_tensor(dmax[:, u, :, :], ident[:T, :T].unsqueeze(1).to_broadcast([T, HPG, T]),
                                            nmax[:, u, :].unsqueeze(2).to_broadcast([T, HPG, T]),
                                            ALU.mult).then_inc(max_ready, 1)

                def gather_own(i, j, u):
                    dve.wait_ge(own_ready, done(i, u, j, G))
                    dve.wait_ge(yT_ready, done(i, u, j - 1, G) if j else before(i, u, G - 1, G))
                    nc.vector.tensor_reduce(nd[:, u, :], own[:, u, :].rearrange("p (h t) -> p t h", t=T),
                                            axis=AXIS_X, op=ALU.add).then_inc(nd_ready, 1)

                def invert(i, j, u, links):
                    dve.wait_ge(nd_ready, done(i, u, j, G))
                    links.add(nc.vector.reciprocal(rec[:, u, :], nd[64:128, u, :]))

                def normalise(i, j, u, links):
                    links.wait()
                    if j == 0:
                        dve.wait_ge(y_done, before(i, u))
                    o = 64 * (j % 2)
                    nc.vector.tensor_tensor(yT[o:o + 64, u, j // 2, :], nd[0:64, u, :], rec[:, u, :],
                                            ALU.mult).then_inc(yT_ready, 1)

                rotate_queries(0)
                rotate_keys(0)

                def body(i, coming):
                    links = Links(dve, vlink, i, 20)
                    for k, (j, u) in enumerate(slots):
                        spread_maxima(i, j, u, links)
                        if coming and k == 3:
                            rotate_queries(i + 1)
                        if coming and k == 6:
                            rotate_keys(i + 1)
                        if k >= 2:
                            invert(i, *slots[k - 2], links)
                        if k >= 1:
                            gather_own(i, *slots[k - 1])
                        if k >= 2:
                            normalise(i, *slots[k - 2], links)
                    invert(i, *slots[LAST - 1], links)
                    gather_own(i, *slots[LAST])
                    normalise(i, *slots[LAST - 1], links)
                    invert(i, *slots[LAST], links)
                    normalise(i, *slots[LAST], links)
                    for u in range(U):
                        dve.wait_ge(y_done, done(i, u))
                        dve.wait_ge(res_loaded[u], 16 * i + 16)
                        nc.vector.tensor_tensor(r[:, u, :], W[u][:T, 0:D], x_res[:, u, :], ALU.add).then_inc(r_ready, 1)
                    dve.wait_ge(r_ready, done(i, U - 1))
                    for u in range(U):
                        dve.wait_ge(stored[u], 16 * i + 16)
                    norm.steps(dve, links, i, r, x_o, out_ready)
                    links.end()

                one_ahead(body)(dve)


def cross_attention_strided(nc, NB, x_in, x_out, w, src_len, slot_rows):
    NH = 8
    HD = D // NH
    KPH = -(-src_len // NH)
    KFULL = src_len - (KPH - 1) * NH
    assert KFULL == 1
    SLOT = 64
    PAIRS = NH // 2
    VW = 96
    with ExitStack() as ctx:
        U = 4
        done, before = counts(U)
        s = Store(nc, ctx, "xs", U)
        wq = s.sb("wq", [P, KC, D])
        wk = s.sb("wk", [P, KC, D])
        wv = s.sb("wv", [P, KC, D + 64])
        wo = s.sb("wo", [P, KC, D])
        bq = s.sb("bq", [P, KC])
        bk = s.sb("bk", [P, KC])
        bv = s.sb("bv", [P, KC])
        bo = s.sb("bo", [T, D])
        ident = s.sb("ident", [P, P])
        head_mask = s.sb("head_mask", [P, 4])
        x_t = s.sb("x_t", [T, U, D])
        x_res = s.sb("x_res", [T, U, D])
        x_bo = s.sb("x_bo", [T, U, D])
        xT = s.sb("xT", [P, U, KC, T])
        ctxT = s.sb("ctxT", [P, U, KC, NH, SLOT])
        qT = s.sb("qT", [P, U, KC, T])
        q_bd = s.sb("q_bd", [P, U, KC, 4, T])
        kT = s.sb("kT", [P, U, KC, NH, KPH])
        v_bd = s.sb("v_bd", [P, U, PAIRS, VW])
        smax = s.sb("smax", [T, U, NH])
        prob = s.sb("prob", [T, U, NH, SLOT])
        pT = s.sb("pT", [P, U, PAIRS, T])
        rec = s.sb("rec", [T, U, NH])
        y = s.sb("y", [T, U, D])
        yT = s.sb("yT", [P, U, KC, T])
        r = s.sb("r", [T, U, D])
        x_o = s.sb("x_o", [T, U, D])
        norm = Norm(s, nc)
        B = [[s.ps(f"B{b}_{u}", [P, 512]) for b in range(2)] for u in range(U)]

        zero = s.sb("zero", [P, 8, D])
        zero_set, zeroed = s.sem("zero_set"), s.sem("slots_zeroed")
        w_in = s.sem("weights_loaded")
        const_ready = s.sem("const_ready")
        x_loaded, res_loaded, ctx_loaded, stored = s.sems("x_loaded"), s.sems("res_loaded"), s.sems("ctx_loaded"), s.sems("stored")
        x_turned, xT_ready = s.sem("x_turned"), s.sem("xT_ready")
        k_done, q_done, v_done = s.sem("k_done"), s.sem("q_done"), s.sem("v_done")
        q_ready, k_ready, v_ready = s.sem("q_ready"), s.sem("k_ready"), s.sem("v_ready")
        qbd_ready = s.sem("qbd_ready")
        xbo_ready = s.sem("xbo_ready")
        scored = s.sem("scored")
        less_ready = s.sem("less_ready")
        prob_ready = s.sem("prob_ready")
        p_turned, pT_ready = s.sem("p_turned"), s.sem("pT_ready")
        av_done = s.sem("av_done")
        y_ready = s.sem("y_ready")
        y_turned, yT_ready = s.sem("y_turned"), s.sem("yT_ready")
        o_done, r_ready, out_ready = s.sem("o_done"), s.sem("r_ready"), s.sem("out_ready")
        vlink = s.sem("dve_link")

        loads = [(wq[:], w["L0_xattn_Wq"].rearrange("(k p) n -> p k n", p=P)),
                 (wk[:], w["L0_xattn_Wk"].rearrange("(k p) n -> p k n", p=P)),
                 (wv[:, :, 0:D], w["L0_xattn_Wv"].rearrange("(k p) n -> p k n", p=P)),
                 (wo[:], w["L0_xattn_Wo"].rearrange("(k p) n -> p k n", p=P)),
                 (bq[:], w["L0_xattn_bq"]), (bk[:], w["L0_xattn_bk"]), (bv[:], w["L0_xattn_bv"]),
                 (bo[:], w["L0_xattn_bo"].to_broadcast([T, D])),
                 (ident[:], w["ident"]), (head_mask[:], w["head_mask4"]),
                 *[(v_bd[:, u], w["v_ones"]) for u in range(U)]]
        W_ALL = 16 * len(loads)
        SC = float(1.0 / np.sqrt(np.float32(HD)))

        with nc.Block() as block:

            @block.sync
            def _(sp):
                for dst, src in loads:
                    sp.dma_start(dst, src).then_inc(w_in, 16)
                for u in range(U):
                    sp.sem_inc(stored[u], 16)

                def load(i):
                    for u in range(U):
                        sp.wait_ge(x_turned, before(i, u))
                        sp.dma_start(x_t[:, u, :], x_in[U * i + u]).then_inc(x_loaded[u], 16)
                        sp.wait_ge(v_done, before(i, u))
                        sp.dma_start(ctxT[:, u].rearrange("p k h s -> p k (h s)"), w["ctxT"][U * i + u]).then_inc(ctx_loaded[u], 16)
                    for u in range(U):
                        sp.wait_ge(xbo_ready, before(i, u))
                        sp.dma_start(x_res[:, u, :], x_in[U * i + u]).then_inc(res_loaded[u], 16)

                def store(i):
                    for u in range(U):
                        sp.wait_ge(out_ready, done(i, u))
                        sp.dma_start(x_out[U * i + u], x_o[:, u, :]).then_inc(stored[u], 16)

                N = NB // U
                load(0)
                sp.wait_ge(zero_set, 1)
                z = slot_rows.rearrange("(n p r) d -> n p r d", p=P, r=8)
                for n in range(z.shape[0]):
                    sp.dma_start(z[n], zero[:]).then_inc(zeroed, 16)
                with sp.Fori(0, N - 1) as i:
                    load(i + 1)
                    store(i)
                store(N - 1)
                for u in range(U):
                    sp.wait_ge(stored[u], 16 * N + 16)
                sp.wait_ge(zeroed, 16 * z.shape[0])

            @block.tensor
            def _(pe):
                for sem in (x_turned, k_done, q_done, v_done, scored, p_turned, av_done, y_turned, o_done):
                    pe.sem_inc(sem, U)
                pe.wait_ge(w_in, W_ALL)
                pe.wait_ge(const_ready, 1)
                with pe.Fori(0, NB // U) as i:
                    for u in range(U):
                        pe.wait_ge(x_loaded[u], 16 * i + 16)
                        pe.wait_ge(r_ready, before(i, u))
                        for c in range(KC):
                            last = nc.tensor.transpose(B[u][1][:, c * T:(c + 1) * T], x_t[:, u, c * P:(c + 1) * P], ident[:T, :T])
                        last.then_inc(x_turned, 1)
                    for u in range(U):
                        pe.wait_ge(ctx_loaded[u], 16 * i + 16)
                        pe.wait_ge(xT_ready, done(i, u))
                        for g in range(KC):
                            for c in range(KC):
                                last = nc.tensor.matmul(B[u][g][:, 0:NH * KPH], wk[:, c, g * P:(g + 1) * P],
                                                        ctxT[:, u, c, :, 0:KPH], start=(c == 0), stop=(c == KC - 1))
                        last.then_inc(k_done, 1)
                    for u in range(U):
                        pe.wait_ge(k_ready, done(i, u))
                        for g in range(KC):
                            for c in range(KC):
                                last = nc.tensor.matmul(B[u][1][:, g * T:(g + 1) * T], wq[:, c, g * P:(g + 1) * P],
                                                        xT[:, u, c, :], start=(c == 0), stop=(c == KC - 1))
                        last.then_inc(q_done, 1)
                        for p in range(PAIRS):
                            for c in range(KC):
                                last = nc.tensor.matmul(B[u][0][:, p * P:(p + 1) * P],
                                                        ctxT[:, u, c, 2 * p:2 * p + 2, :].rearrange("p h s -> p (h s)"),
                                                        wv[:, c, 64 * p:64 * p + P], start=(c == 0), stop=(c == KC - 1))
                        last.then_inc(v_done, 1)
                    for u in range(U):
                        pe.wait_ge(qbd_ready, done(i, u))
                        for h in range(NH):
                            last = nc.tensor.matmul(B[u][1][:T, h * KPH:(h + 1) * KPH], q_bd[:, u, h // 4, h % 4, :],
                                                    kT[:, u, h // 4, h, :], start=True, stop=True)
                        last.then_inc(scored, 1)
                    for u in range(U):
                        pe.wait_ge(prob_ready, done(i, u))
                        pe.wait_ge(v_ready, done(i, u))
                        for p in range(PAIRS):
                            last = nc.tensor.transpose(B[u][0][:, p * T:(p + 1) * T],
                                                       prob[:, u, 2 * p:2 * p + 2, :].rearrange("p h s -> p (h s)"), ident[:T, :T])
                        last.then_inc(p_turned, 1)
                    for u in range(U):
                        pe.wait_ge(pT_ready, done(i, u))
                        for p in range(PAIRS):
                            last = nc.tensor.matmul(B[u][1][:T, p * VW:(p + 1) * VW], pT[:, u, p, :], v_bd[:, u, p, :],
                                                    start=True, stop=True)
                        last.then_inc(av_done, 1)
                    for u in range(U):
                        pe.wait_ge(y_ready, done(i, u))
                        for c in range(KC):
                            last = nc.tensor.transpose(B[u][0][:, c * T:(c + 1) * T], y[:, u, c * P:(c + 1) * P], ident[:T, :T])
                        last.then_inc(y_turned, 1)
                    for u in range(U):
                        pe.wait_ge(yT_ready, done(i, u))
                        for c in range(KC):
                            last = nc.tensor.matmul(B[u][1][:T, 0:D], yT[:, u, c, :], wo[:, c, :],
                                                    start=(c == 0), stop=(c == KC - 1))
                        last.then_inc(o_done, 1)

            @block.scalar
            def _(act):
                for sem in (xT_ready, q_ready, k_ready, v_ready, prob_ready, pT_ready, yT_ready):
                    act.sem_inc(sem, U)
                act.wait_ge(w_in, W_ALL)
                with act.Fori(0, NB // U) as i:
                    for u in range(U):
                        act.wait_ge(x_turned, done(i, u))
                        nc.scalar.activation(xT[:, u, :, :].rearrange("p c t -> p (c t)"), B[u][1][:, 0:KC * T],
                                             ACT.Copy).then_inc(xT_ready, 1)
                    for u in range(U):
                        act.wait_ge(k_done, done(i, u))
                        for g in range(KC):
                            last = nc.scalar.activation(kT[:, u, g, :, :].rearrange("p h s -> p (h s)"), B[u][g][:, 0:NH * KPH],
                                                        ACT.Identity, bias=bk[:, g:g + 1])
                        last.then_inc(k_ready, 1)
                    for u in range(U):
                        act.wait_ge(q_done, done(i, u))
                        act.wait_ge(qbd_ready, before(i, u))
                        for g in range(KC):
                            last = nc.scalar.activation(qT[:, u, g, :], B[u][1][:, g * T:(g + 1) * T], ACT.Identity, bias=bq[:, g:g + 1])
                        last.then_inc(q_ready, 1)
                        act.wait_ge(v_done, done(i, u))
                        v = B[u][0][:, :].rearrange("p (n f) -> p n f", f=P)
                        nc.scalar.activation(v_bd[0:KPH, u, :, 0:HD], v[0:KPH, :, 0:HD], ACT.Copy)
                        nc.scalar.activation(v_bd[SLOT:SLOT + KPH, u, :, HD + 1:2 * HD + 1], v[SLOT:SLOT + KPH, :, HD:2 * HD],
                                             ACT.Copy).then_inc(v_ready, 1)
                    for u in range(U):
                        act.wait_ge(less_ready, done(i, u))
                        nc.scalar.activation(prob[:, u, :, 0:KPH - 1], prob[:, u, :, 0:KPH - 1], ACT.Exp, scale=SC)
                        nc.scalar.activation(prob[:, u, 0, KPH - 1:KPH], prob[:, u, 0, KPH - 1:KPH], ACT.Exp,
                                             scale=SC).then_inc(prob_ready, 1)
                    for u in range(U):
                        act.wait_ge(p_turned, done(i, u))
                        nc.scalar.activation(pT[:, u, :, :].rearrange("p n t -> p (n t)"), B[u][0][:, 0:PAIRS * T],
                                             ACT.Copy).then_inc(pT_ready, 1)
                    for u in range(U):
                        act.wait_ge(y_turned, done(i, u))
                        for g in range(KC):
                            last = nc.scalar.activation(yT[:, u, g, :], B[u][0][:, g * T:(g + 1) * T], ACT.Identity, bias=bv[:, g:g + 1])
                        last.then_inc(yT_ready, 1)

            @block.gpsimd
            def _(pool):
                nc.gpsimd.memset(zero[:], 0.0).then_inc(zero_set, 1)
                nc.gpsimd.memset(wv[:, :, D:D + 64], 0.0)
                nc.gpsimd.memset(prob[:], 0.0).then_inc(const_ready, 1)
                pool.sem_inc(qbd_ready, U)
                pool.sem_inc(xbo_ready, U)
                norm.set_power(pool)
                pool.wait_ge(w_in, W_ALL)
                with pool.Fori(0, NB // U) as i:
                    for u in range(U):
                        pool.wait_ge(q_ready, done(i, u))
                        pool.wait_ge(scored, before(i, u))
                        for g in range(KC):
                            last = nc.gpsimd.tensor_tensor(q_bd[:, u, g, :, :],
                                                           qT[:, u, g, :].unsqueeze(1).to_broadcast([P, 4, T]),
                                                           head_mask[:].unsqueeze(2).to_broadcast([P, 4, T]), ALU.mult)
                        last.then_inc(qbd_ready, 1)
                    for u in range(U):
                        pool.wait_ge(res_loaded[u], 16 * i + 16)
                        pool.wait_ge(r_ready, before(i, u))
                        nc.gpsimd.tensor_tensor(x_bo[:, u, :], x_res[:, u, :], bo[:], ALU.add).then_inc(xbo_ready, 1)
                    norm.raise_power(pool, i)

            @block.vector
            def _(dve):
                for sem in (less_ready, y_ready, r_ready, out_ready):
                    dve.sem_inc(sem, U)
                dve.wait_ge(const_ready, 1)
                with dve.Fori(0, NB // U) as i:
                    links = Links(dve, vlink, i, 20)
                    for u in range(U):
                        dve.wait_ge(scored, done(i, u))
                        sc = B[u][1][:T, 0:NH * KPH].rearrange("p (h s) -> p h s", s=KPH)
                        links.add(nc.vector.tensor_reduce(smax[:, u, :], sc[:, :, 0:KPH - 1], axis=AXIS_X, op=ALU.max))
                    links.wait()
                    for u in range(U):
                        links.add(nc.vector.tensor_tensor(smax[:, u, 0:1], smax[:, u, 0:1], B[u][1][:T, KPH - 1:KPH], ALU.max))
                    links.wait()
                    for u in range(U):
                        sc = B[u][1][:T, 0:NH * KPH].rearrange("p (h s) -> p h s", s=KPH)
                        dve.wait_ge(p_turned, before(i, u))
                        nc.vector.tensor_tensor(prob[:, u, :, 0:KPH - 1], sc[:, :, 0:KPH - 1],
                                                smax[:, u, :].unsqueeze(2).to_broadcast([T, NH, KPH - 1]), ALU.subtract)
                        nc.vector.tensor_tensor(prob[:, u, 0, KPH - 1:KPH], sc[:, 0, KPH - 1:KPH], smax[:, u, 0:1],
                                                ALU.subtract).then_inc(less_ready, 1)
                    for u in range(U):
                        dve.wait_ge(av_done, done(i, u))
                        av = B[u][1][:T, 0:PAIRS * VW].rearrange("p (n c) -> p n c", c=VW)[:, :, 0:2 * (HD + 1)]\
                            .rearrange("p n (two c) -> p n two c", c=HD + 1)
                        links.add(nc.vector.reciprocal(rec[:, u, :].rearrange("p (n two) -> p n two", two=2), av[:, :, :, HD]))
                    links.wait()
                    for u in range(U):
                        av = B[u][1][:T, 0:PAIRS * VW].rearrange("p (n c) -> p n c", c=VW)[:, :, 0:2 * (HD + 1)]\
                            .rearrange("p n (two c) -> p n two c", c=HD + 1)
                        dve.wait_ge(y_turned, before(i, u))
                        nc.vector.tensor_tensor(y[:, u, :].rearrange("p (n two c) -> p n two c", two=2, c=HD), av[:, :, :, 0:HD],
                                                rec[:, u, :].rearrange("p (n two) -> p n two", two=2).unsqueeze(3).to_broadcast([T, PAIRS, 2, HD]),
                                                ALU.mult).then_inc(y_ready, 1)
                    for u in range(U):
                        dve.wait_ge(o_done, done(i, u))
                        dve.wait_ge(xbo_ready, done(i, u))
                        nc.vector.tensor_tensor(r[:, u, :], B[u][1][:T, 0:D], x_bo[:, u, :], ALU.add).then_inc(r_ready, 1)
                    dve.wait_ge(r_ready, done(i, U - 1))
                    for u in range(U):
                        dve.wait_ge(stored[u], 16 * i + 16)
                    norm.steps(dve, links, i, r, x_o, out_ready)
                    links.end()


EXPERTS = 64
TOPK = 6
CAP = 128
SLOTS = EXPERTS * CAP
FE = 176
FS = 352
HC = 88
FAR = 65536.0


def route(nc, NB, x_in, w, slot_rows, xz, slot_ids, slot_weights):
    with ExitStack() as ctx:
        U = 4
        done, before = counts(U)
        s = Store(nc, ctx, "rt", U)
        gate = s.sb("gate", [P, KC, EXPERTS])
        gate_b = s.sb("gate_b", [T, EXPERTS])
        ws1 = s.sb("ws1", [P, KC, FS])
        ws3 = s.sb("ws3", [P, KC, FS])
        ws2 = s.sb("ws2", [HC, FS // HC, D])
        ident = s.sb("ident", [P, P])
        earlier = s.sb("earlier", [T, T])
        ones = s.sb("ones", [T, T])
        expert_no = s.sb("expert_no", [T, EXPERTS])
        first_slot = s.sb("first_slot", [T, EXPERTS])
        x_t = s.sb("x_t", [T, U, D])
        x_again = s.sb("x_again", [T, U, D])
        xT = s.sb("xT", [P, U, KC, T])
        nmax = s.sb("nmax", [T, U])
        spare = s.sb("spare", [T, 1])
        esum = s.sb("esum", [T, U])
        rec = s.sb("rec", [T, U])
        e = s.sb("e", [T, U, EXPERTS])
        probs = s.sb("probs", [T, U, EXPERTS])
        biased = s.sb("biased", [T, U, EXPERTS])
        top = s.sb("top", [T, U, 8])
        top_i = s.sb("top_i", [T, U, 8], U32)
        top_f = s.sb("top_f", [T, U, TOPK])
        hot = s.sb("hot", [T, U, TOPK, EXPERTS])
        chosen = s.sb("chosen", [T, U, EXPERTS])
        sofar = s.sb("sofar", [T, U, EXPERTS])
        over = s.sb("over", [T, U, EXPERTS])
        slot_e = s.sb("slot_e", [T, U, EXPERTS])
        picked = s.sb("picked", [T, U, 2, TOPK, EXPERTS])
        slot_w = s.sb("slot_w", [T, U, 2, TOPK])
        slot_u = s.sb("slot_u", [T, U, TOPK], U32)
        gat_u = s.sb("gat_u", [T, U, TOPK], U32)
        w_keep = s.sb("w_keep", [T, U, TOPK])
        th = s.sb("th", [HC, U, 4 * T])
        h1 = s.sb("h1", [HC, U, 4 * T])
        hT = s.sb("hT", [HC, U, 4, T])
        x_z = s.sb("x_z", [T, U, D])
        B = [[s.ps(f"B{b}_{u}", [P, 512]) for b in range(2)] for u in range(U)]

        w_in = s.sem("weights_loaded")
        scatter_over, routes_seen = s.sem("scatter_over"), s.sem("routes_seen")
        ones_set = s.sem("ones_set")
        again_loaded = s.sems("again_loaded")
        x_loaded, scattered, kept, z_stored = s.sems("x_loaded"), s.sems("scattered"), s.sems("routes_kept"), s.sems("z_stored")
        x_turned, xT_ready = s.sem("x_turned"), s.sem("xT_ready")
        gated, up_done, ranked, z_done = s.sem("gated"), s.sem("up_done"), s.sem("ranked"), s.sem("z_done")
        nmax_ready, chosen_ready, h_ready, routes_ready = s.sem("nmax_ready"), s.sem("chosen_ready"), s.sem("h_ready"), s.sem("routes_ready")
        gate_read = s.sem("gate_read")
        slots_known = s.sem("slots_known")
        th_ready = s.sem("th_ready")
        xz_ready = s.sem("xz_ready")
        vlink = s.sem("dve_link")

        loads = [(gate[:], w["gate_wT"].rearrange("(k p) n -> p k n", p=P)),
                 (gate_b[:], w["gate_b"].to_broadcast([T, EXPERTS])),
                 (ws1[:], w["ws1T"].rearrange("(k p) n -> p k n", p=P)),
                 (ws3[:], w["ws3T"].rearrange("(k p) n -> p k n", p=P)),
                 (ws2[:], w["ws2T"].rearrange("(k p) n -> p k n", p=HC)),
                 (ident[:], w["ident"]), (earlier[:], w["earlier"]),
                 (expert_no[:], w["expert_no"]), (first_slot[:], w["first_slot"])]
        W_ALL = 16 * len(loads)

        with nc.Block() as block:

            @block.sync
            def _(sp):
                for u in range(U):
                    sp.sem_inc(z_stored[u], 16)
                    sp.sem_inc(kept[u], 32)

                def load_x(i):
                    for u in range(U):
                        sp.wait_ge(x_turned, before(i, u))
                        sp.dma_start(x_t[:, u, :], x_in[U * i + u]).then_inc(x_loaded[u], 16)

                def body(i, coming):
                    for u in range(U):
                        sp.wait_ge(xz_ready, before(i, u))
                        sp.wait_ge(scatter_over, before(i, u))
                        sp.dma_start(x_again[:, u, :], x_in[U * i + u]).then_inc(again_loaded[u], 16)
                    if coming:
                        load_x(i + 1)
                    for u in range(U):
                        sp.wait_ge(routes_ready, done(i, u))
                        sp.dma_start(slot_ids[U * i + u], gat_u[:, u, :]).then_inc(kept[u], 16)
                        sp.dma_start(slot_weights[U * i + u], w_keep[:, u, :]).then_inc(kept[u], 16)
                    for u in range(U):
                        sp.wait_ge(xz_ready, done(i, u))
                        sp.dma_start(xz[U * i + u], x_z[:, u, :]).then_inc(z_stored[u], 16)

                load_x(0)
                for dst, src in loads:
                    sp.dma_start(dst, src).then_inc(w_in, 16)
                with sp.Fori(0, NB // U - 1) as i:
                    body(i, 1)
                body(NB // U - 1, 0)
                for u in range(U):
                    sp.wait_ge(z_stored[u], 16 * (NB // U) + 16)
                    sp.wait_ge(kept[u], 32 * (NB // U) + 32)

            @block.tensor
            def _(pe):
                for sem in (x_turned, gated, up_done, ranked, z_done):
                    pe.sem_inc(sem, U)
                pe.wait_ge(w_in, W_ALL)
                pe.wait_ge(ones_set, 1)
                with pe.Fori(0, NB // U) as i:
                    for u in range(U):
                        pe.wait_ge(x_loaded[u], 16 * i + 16)
                        pe.wait_ge(slots_known, before(i, u))
                        for c in range(KC):
                            last = nc.tensor.transpose(B[u][1][:, c * T:(c + 1) * T], x_t[:, u, c * P:(c + 1) * P], ident[:T, :T])
                        last.then_inc(x_turned, 1)
                    for u in range(U):
                        pe.wait_ge(xT_ready, done(i, u))
                        pe.wait_ge(xz_ready, before(i, u))
                        for c in range(KC):
                            last = nc.tensor.matmul(B[u][0][:T, 0:EXPERTS], xT[:, u, c, :], gate[:, c, :],
                                                    start=(c == 0), stop=(c == KC - 1))
                        last.then_inc(gated, 1)
                    for u in range(U):
                        pe.wait_ge(gate_read, done(i, u))
                        for b, ws in ((0, ws1), (1, ws3)):
                            for m in range(FS // HC):
                                for c in range(KC):
                                    last = nc.tensor.matmul(B[u][b][:HC, m * T:(m + 1) * T], ws[:, c, m * HC:(m + 1) * HC],
                                                            xT[:, u, c, :], start=(c == 0), stop=(c == KC - 1))
                        last.then_inc(up_done, 1)
                    for u in range(U):
                        pe.wait_ge(h_ready, done(i, u))
                        pe.wait_ge(chosen_ready, done(i, u))
                        nc.tensor.matmul(B[u][1][:T, 0:EXPERTS], earlier[:], chosen[:, u, :], start=True, stop=False)
                        nc.tensor.matmul(B[u][1][:T, 0:EXPERTS], ones[:], sofar[:, u, :], start=False,
                                         stop=True).then_inc(ranked, 1)
                    for u in range(U):
                        for m in range(FS // HC):
                            last = nc.tensor.matmul(B[u][0][:T, 0:D], hT[:, u, m, :], ws2[:, m, :], start=(m == 0),
                                                    stop=(m == FS // HC - 1))
                        last.then_inc(z_done, 1)

            @block.scalar
            def _(act):
                for sem in (xT_ready, gate_read, th_ready):
                    act.sem_inc(sem, U)
                with act.Fori(0, NB // U) as i:
                    for u in range(U):
                        act.wait_ge(x_turned, done(i, u))
                        act.wait_ge(up_done, before(i, u))
                        nc.scalar.activation(xT[:, u, :, :].rearrange("p c t -> p (c t)"), B[u][1][:, 0:KC * T],
                                             ACT.Copy).then_inc(xT_ready, 1)
                    for u in range(U):
                        act.wait_ge(nmax_ready, done(i, u))
                        nc.scalar.activation(e[:, u, :], B[u][0][:T, 0:EXPERTS], ACT.Exp, bias=nmax[:, u:u + 1],
                                             accum_out=esum[:, u:u + 1]).then_inc(gate_read, 1)
                    for u in range(U):
                        act.wait_ge(up_done, done(i, u))
                        act.wait_ge(h_ready, before(i, u))
                        nc.scalar.activation(th[:, u, :], B[u][0][:HC, 0:4 * T], ACT.Tanh, scale=0.5).then_inc(th_ready, 1)

            @block.gpsimd
            def _(pool):
                pool.sem_inc(scatter_over, U)
                nc.gpsimd.memset(ones[:], 1.0).then_inc(ones_set, 1)
                with pool.Fori(0, NB // U) as i:
                    for u in range(U):
                        pool.wait_ge(routes_ready, done(i, u))
                        pool.wait_ge(again_loaded[u], 16 * i + 16)
                        pool.sem_inc(routes_seen, 1)
                        for k in range(TOPK):
                            nc.gpsimd.indirect_dma_start(slot_rows, bass.IndirectOffsetOnAxis(slot_u[:, u, k:k + 1], 0),
                                                         x_again[:, u, :], None, bounds_check=SLOTS - 1,
                                                         oob_is_err=False).then_inc(scattered[u], 16)
                    for u in range(U):
                        pool.wait_ge(scattered[u], 16 * TOPK * i + 16 * TOPK)
                        pool.sem_inc(scatter_over, 1)

            @block.vector
            def _(dve):
                for sem in (nmax_ready, chosen_ready, slots_known, h_ready, routes_ready, xz_ready):
                    dve.sem_inc(sem, U)
                nc.vector.memset(sofar[:], 0.0)
                dve.wait_ge(w_in, W_ALL)
                with dve.Fori(0, NB // U) as i:
                    links = Links(dve, vlink, i, 56)
                    for u in range(U):
                        dve.wait_ge(gated, done(i, u))
                        nc.vector.tensor_reduce(nmax[:, u:u + 1], B[u][0][:T, 0:EXPERTS], axis=AXIS_X, op=ALU.max,
                                                negate=True).then_inc(nmax_ready, 1)
                    for u in range(U):
                        dve.wait_ge(gate_read, done(i, u))
                        links.add(nc.vector.reciprocal(rec[:, u:u + 1], esum[:, u:u + 1]))
                    links.wait()
                    for u in range(U):
                        links.add(nc.vector.tensor_scalar(probs[:, u, :], e[:, u, :], rec[:, u:u + 1], None, ALU.mult))
                    links.wait()
                    for u in range(U):
                        links.add(nc.vector.tensor_tensor(biased[:, u, :], probs[:, u, :], gate_b[:], ALU.add))
                    links.wait()
                    nc.vector.memset(spare[:], 0.0)
                    for u in range(U):
                        links.add(nc.vector.max(top[:, u, :], biased[:, u, :]))
                    links.wait()
                    nc.vector.memset(spare[:], 0.0)
                    for u in range(U):
                        links.add(nc.vector.max_index(top_i[:, u, :], top[:, u, :], biased[:, u, :]))
                    links.wait()
                    for u in range(U):
                        links.add(nc.vector.tensor_copy(top_f[:, u, :], top_i[:, u, 0:TOPK]))
                    links.wait()
                    for u in range(U):
                        links.add(nc.vector.tensor_tensor(hot[:, u, :, :], expert_no[:].unsqueeze(1).to_broadcast([T, TOPK, EXPERTS]),
                                                          top_f[:, u, :].unsqueeze(2).to_broadcast([T, TOPK, EXPERTS]), ALU.is_equal))
                    links.wait()
                    dve.wait_ge(ranked, before(i, U - 1))
                    for u in range(U):
                        nc.vector.tensor_reduce(chosen[:, u, :], hot[:, u, :, :].rearrange("p k e -> p e k"), axis=AXIS_X,
                                                op=ALU.add).then_inc(chosen_ready, 1)
                    for u in range(U - 1):
                        dve.wait_ge(chosen_ready, done(i, u))
                        links.add(nc.vector.tensor_tensor(sofar[:, u + 1, :], sofar[:, u, :], chosen[:, u, :], ALU.add))
                        links.wait()
                    for u in range(U):
                        dve.wait_ge(th_ready, done(i, u))
                        links.add(nc.vector.scalar_tensor_tensor(h1[:, u, :], th[:, u, :], 1.0, B[u][0][:HC, 0:4 * T],
                                                                 ALU.add, ALU.mult))
                    links.wait()
                    for u in range(U):
                        dve.wait_ge(z_done, before(i, u))
                        nc.vector.scalar_tensor_tensor(hT[:, u, :, :].rearrange("p m t -> p (m t)"), h1[:, u, :], 0.5,
                                                       B[u][1][:HC, 0:4 * T], ALU.mult, ALU.mult).then_inc(h_ready, 1)
                    for u in range(U):
                        dve.wait_ge(ranked, done(i, u))
                        rank = B[u][1][:T, 0:EXPERTS]
                        links.add(nc.vector.tensor_scalar(over[:, u, :], rank, float(CAP), FAR, ALU.is_ge, ALU.mult))
                        nc.vector.tensor_tensor(slot_e[:, u, :], rank, first_slot[:], ALU.add).then_inc(slots_known, 1)
                    links.add(nc.vector.tensor_tensor(sofar[:, 0, :], sofar[:, U - 1, :], chosen[:, U - 1, :], ALU.add))
                    links.wait()
                    for u in range(U):
                        dve.wait_ge(slots_known, done(i, u))
                        links.add(nc.vector.tensor_tensor(slot_e[:, u, :], slot_e[:, u, :], over[:, u, :], ALU.add))
                    links.wait()
                    for u in range(U):
                        for k, what in ((0, slot_e), (1, probs)):
                            links.add(nc.vector.tensor_tensor(picked[:, u, k, :, :], hot[:, u, :, :],
                                                              what[:, u, :].unsqueeze(1).to_broadcast([T, TOPK, EXPERTS]), ALU.mult))
                    links.wait()
                    for u in range(U):
                        links.add(nc.vector.tensor_reduce(slot_w[:, u, :, :], picked[:, u, :, :, :], axis=AXIS_X, op=ALU.add))
                    links.wait()
                    for u in range(U):
                        dve.wait_ge(scatter_over, before(i, u))
                        dve.wait_ge(kept[u], 32 * i + 32)
                        nc.vector.tensor_copy(slot_u[:, u, :], slot_w[:, u, 0, :])
                        nc.vector.tensor_scalar(gat_u[:, u, :], slot_w[:, u, 0, :], float(SLOTS - 1), None, ALU.min)
                        nc.vector.scalar_tensor_tensor(w_keep[:, u, :], slot_w[:, u, 0, :], float(SLOTS), slot_w[:, u, 1, :],
                                                       ALU.is_lt, ALU.mult).then_inc(routes_ready, 1)
                    for u in range(U):
                        dve.wait_ge(z_done, done(i, u))
                        dve.wait_ge(again_loaded[u], 16 * i + 16)
                        dve.wait_ge(z_stored[u], 16 * i + 16)
                        nc.vector.tensor_tensor(x_z[:, u, :], B[u][0][:T, 0:D], x_again[:, u, :], ALU.add).then_inc(xz_ready, 1)
                    links.end()


def experts(nc, w, slot_rows, slot_out):
    with ExitStack() as ctx:
        U = 8
        done, before = counts(U)
        s = Store(nc, ctx, "ex", U)
        ident = s.sb("ident", [P, P])
        w13 = s.sb("w13", [P, U, KC, 2 * FE])
        w2 = s.sb("w2", [HC, U, 2, D])
        x_t = s.sb("x_t", [P, U, D])
        xT = s.sb("xT", [P, U, KC, P])
        th = s.sb("th", [P, U, FE])
        h1 = s.sb("h1", [P, U, FE])
        h = s.sb("h", [P, U, FE])
        hT = s.sb("hT", [HC, U, 2, P])
        y = s.sb("y", [P, U, D])
        B = [s.ps(f"B{u}", [P, 512]) for u in range(U)]

        ident_in = s.sem("ident_loaded")
        up_loaded, down_loaded, x_loaded, stored = s.sems("up_loaded"), s.sems("down_loaded"), s.sems("x_loaded"), s.sems("stored")
        x_turned, up_done, h_turned, y_done = s.sem("x_turned"), s.sem("up_done"), s.sem("h_turned"), s.sem("y_done")
        xT_ready, th_ready, y_ready = s.sem("xT_ready"), s.sem("th_ready"), s.sem("y_ready")
        h1_ready, h_ready, hT_ready = s.sem("h1_ready"), s.sem("h_ready"), s.sem("hT_ready")
        xs = slot_rows.rearrange("(e p) d -> e p d", p=P)
        ys = slot_out.rearrange("(e p) d -> e p d", p=P)

        with nc.Block() as block:

            @block.sync
            def _(sp):
                sp.dma_start(ident[:], w["ident"]).then_inc(ident_in, 16)
                for u in range(U):
                    sp.sem_inc(stored[u], 16)

                def load(i):
                    for u in range(U):
                        sp.wait_ge(x_turned, before(i, u))
                        sp.dma_start(x_t[:, u, :], xs[U * i + u]).then_inc(x_loaded[u], 16)
                    for u in range(U):
                        sp.wait_ge(up_done, before(i, u))
                        sp.dma_start(w13[:, u], w["w13T"][U * i + u].rearrange("(k p) n -> p k n", p=P)).then_inc(up_loaded[u], 16)
                    for u in range(U):
                        sp.wait_ge(y_done, before(i, u))
                        sp.dma_start(w2[:, u], w["w2T"][U * i + u].rearrange("(k p) n -> p k n", p=HC)).then_inc(down_loaded[u], 16)

                def body(i, coming):
                    if coming:
                        load(i + 1)
                    for u in range(U):
                        sp.wait_ge(y_ready, done(i, u))
                        sp.dma_start(ys[U * i + u], y[:, u, :]).then_inc(stored[u], 16)

                load(0)
                pipelined(sp, EXPERTS // U, body)
                for u in range(U):
                    sp.wait_ge(stored[u], 16 * (EXPERTS // U) + 16)

            @block.tensor
            def _(pe):
                for sem in (x_turned, up_done, h_turned, y_done):
                    pe.sem_inc(sem, U)
                pe.wait_ge(ident_in, 16)
                with pe.Fori(0, EXPERTS // U) as i:
                    for u in range(U):
                        pe.wait_ge(x_loaded[u], 16 * i + 16)
                        pe.wait_ge(y_ready, before(i, u))
                        for c in range(KC):
                            last = nc.tensor.transpose(B[u][:, c * P:(c + 1) * P], x_t[:, u, c * P:(c + 1) * P], ident[:])
                        last.then_inc(x_turned, 1)
                    for u in range(U):
                        pe.wait_ge(up_loaded[u], 16 * i + 16)
                        pe.wait_ge(xT_ready, done(i, u))
                        for c in range(KC):
                            last = nc.tensor.matmul(B[u][:, 0:2 * FE], xT[:, u, c, :], w13[:, u, c],
                                                    start=(c == 0), stop=(c == KC - 1))
                        last.then_inc(up_done, 1)
                    for u in range(U):
                        pe.wait_ge(h_ready, done(i, u))
                        for m in range(2):
                            last = nc.tensor.transpose(B[u][:HC, m * P:(m + 1) * P], h[:, u, m * HC:(m + 1) * HC], ident[:])
                        last.then_inc(h_turned, 1)
                    for u in range(U):
                        pe.wait_ge(down_loaded[u], 16 * i + 16)
                        pe.wait_ge(hT_ready, done(i, u))
                        for m in range(2):
                            last = nc.tensor.matmul(B[u][:, 0:D], hT[:, u, m, :], w2[:, u, m, :], start=(m == 0), stop=(m == 1))
                        last.then_inc(y_done, 1)

            @block.scalar
            def _(act):
                for sem in (xT_ready, th_ready, y_ready):
                    act.sem_inc(sem, U)
                with act.Fori(0, EXPERTS // U) as i:
                    for u in range(U):
                        act.wait_ge(x_turned, done(i, u))
                        nc.scalar.activation(xT[:, u].rearrange("p c t -> p (c t)"), B[u][:, 0:KC * P], ACT.Copy).then_inc(xT_ready, 1)
                    for u in range(U):
                        act.wait_ge(up_done, done(i, u))
                        nc.scalar.activation(th[:, u, :], B[u][:, 0:FE], ACT.Tanh, scale=0.5).then_inc(th_ready, 1)
                    for u in range(U):
                        act.wait_ge(y_done, done(i, u))
                        act.wait_ge(stored[u], 16 * i + 16)
                        nc.scalar.activation(y[:, u, :], B[u][:, 0:D], ACT.Copy).then_inc(y_ready, 1)

            @block.vector
            def _(dve):
                for sem in (h1_ready, h_ready, hT_ready):
                    dve.sem_inc(sem, U)
                with dve.Fori(0, EXPERTS // U) as i:
                    for u in range(U):
                        dve.wait_ge(th_ready, done(i, u))
                        nc.vector.scalar_tensor_tensor(h1[:, u, :], th[:, u, :], 1.0, B[u][:, 0:FE],
                                                       ALU.add, ALU.mult).then_inc(h1_ready, 1)
                        dve.wait_ge(h1_ready, done(i, u))
                        nc.vector.scalar_tensor_tensor(h[:, u, :], h1[:, u, :], 0.5, B[u][:, FE:2 * FE],
                                                       ALU.mult, ALU.mult).then_inc(h_ready, 1)
                    for u in range(U):
                        dve.wait_ge(h_turned, done(i, u))
                        nc.vector.tensor_copy(hT[:, u].rearrange("p m t -> p (m t)"), B[u][:HC, 0:2 * P]).then_inc(hT_ready, 1)


def linear_attention(nc, NB, xz, slot_out, slot_ids, slot_weights, x_out, w, n_out=None):
    EPS = 1e-6
    with ExitStack() as ctx:
        U = 4
        done, before = counts(U)
        s = Store(nc, ctx, "la", U)
        wqk = s.sb("wqk", [P, KC, 2 * D])
        wv = s.sb("wv", [P, KC, D])
        wo = s.sb("wo", [P, KC, D])
        bqk = s.sb("bqk", [T, 2 * D])
        bv = s.sb("bv", [T, D])
        bo = s.sb("bo", [T, D])
        ident = s.sb("ident", [P, P])
        ones = s.sb("ones", [T, T])
        block_mask = s.sb("block_mask", [P, P])
        ids = s.sb("ids", [T, U, TOPK], U32)
        wts = s.sb("wts", [T, U, TOPK])
        rows = s.sb("rows", [T, U, TOPK, D])
        acc = s.sb("acc", [T, U, 2, D])
        x_3 = s.sb("x_3", [T, U, D])
        x_bo = s.sb("x_bo", [T, U, D])
        xT = s.sb("xT", [P, U, KC, T])
        qk = s.sb("qk", [T, U, 2, D])
        qke = s.sb("qke", [T, U, 2, D])
        t1 = s.sb("t1", [T, U, 2, D])
        v = s.sb("v", [T, U, D])
        flow = s.sb("flow", [T, U, 2 * HEADS])
        kept = s.sb("kept", [T, U, 2 * HEADS])
        comp = s.sb("comp", [T, U, HEADS])
        ecs = s.sb("ecs", [T, U, HEADS])
        alloc = s.sb("alloc", [T, U, HEADS])
        qT = s.sb("qT", [P, U, KC, T])
        kv = s.sb("kv", [P, U, KC, P])
        y = s.sb("y", [T, U, D])
        yT = s.sb("yT", [P, U, KC, T])
        r = s.sb("r", [T, U, D])
        x_o = s.sb("x_o", [T, U, D])
        norm3 = Norm(s, nc, tag="3")
        norm = Norm(s, nc)
        B = [[s.ps(f"B{b}_{u}", [P, 512]) for b in range(2)] for u in range(U)]

        w_in, ones_set = s.sem("weights_loaded"), s.sem("ones_set")
        ids_loaded, wts_loaded, xz_loaded, gathered, stored = (s.sems(n) for n in (
            "ids_loaded", "wts_loaded", "xz_loaded", "gathered", "stored"))
        names = ["x3_ready", "x_turned", "xT_ready", "qkv_done", "biased", "th_ready", "qk_ready", "qke_ready", "summed",
                 "flows_ready", "flowed", "kept_ready", "ecs_ready", "esummed", "v_ready", "kv_done", "kv_ready", "q_turned",
                 "qT_ready", "attended", "y_ready", "y_turned", "yT_ready", "o_done", "r_ready", "out_ready", "xbo_ready"]
        (x3_ready, x_turned, xT_ready, qkv_done, biased, th_ready, qk_ready, qke_ready, summed, flows_ready, flowed, kept_ready,
         ecs_ready, esummed, v_ready, kv_done, kv_ready, q_turned, qT_ready, attended, y_ready, y_turned, yT_ready, o_done,
         r_ready, out_ready, xbo_ready) = (s.sem(n) for n in names)
        ids_seen = s.sem("ids_seen")
        vlink, vlink3 = s.sem("dve_link"), s.sem("dve_link_rows")

        kp = "(k p) n -> p k n"
        loads = [(wqk[:], w["L1_wqkT"].rearrange(kp, p=P)), (wv[:], w["L1_wvT"].rearrange(kp, p=P)),
                 (wo[:], w["L1_woT"].rearrange(kp, p=P)), (bqk[:], w["L1_bqk"].to_broadcast([T, 2 * D])),
                 (bv[:], w["L1_bv"].to_broadcast([T, D])), (bo[:], w["L1_bo"].to_broadcast([T, D])),
                 (ident[:], w["ident"]), (block_mask[:], w["block_mask"])]
        W_ALL = 16 * len(loads)
        N = NB // U
        EARLY = TOPK * U - 2

        with nc.Block() as block:

            @block.sync
            def _(sp):
                for u in range(U):
                    sp.sem_inc(stored[u], 16)

                def loads_of(i, again=True):
                    for u in range(U):
                        if again:
                            sp.wait_ge(gathered[u], 16 * TOPK * i)
                        sp.dma_start(ids[:, u, :], slot_ids[U * i + u]).then_inc(ids_loaded[u], 16)
                        sp.wait_ge(x3_ready, before(i, u))
                        sp.dma_start(wts[:, u, :], slot_weights[U * i + u]).then_inc(wts_loaded[u], 16)
                        sp.dma_start(acc[:, u, 0, :], xz[U * i + u]).then_inc(xz_loaded[u], 16)

                def body(i, coming):
                    if coming == 2:
                        loads_of(i + 2)
                    for u in range(U):
                        sp.wait_ge(out_ready, done(i, u))
                        sp.dma_start(x_out[U * i + u], x_o[:, u, :]).then_inc(stored[u], 16)

                loads_of(0, again=False)
                for dst, src in loads:
                    sp.dma_start(dst, src).then_inc(w_in, 16)
                loads_of(1)
                pipelined(sp, N, body)
                for u in range(U):
                    sp.wait_ge(stored[u], 16 * N + 16)

            @block.gpsimd
            def _(pool):
                pool.sem_inc(xbo_ready, U)
                nc.gpsimd.memset(ones[:], 1.0).then_inc(ones_set, 1)
                norm3.set_power(pool)
                norm.set_power(pool)

                def gather(i, steps):
                    for n in steps:
                        u, k = divmod(n, TOPK)
                        if k == 0:
                            pool.wait_ge(ids_loaded[u], 16 * i + 16)
                            pool.wait_ge(x3_ready, before(i, u))
                            pool.sem_inc(ids_seen, 1)
                        nc.gpsimd.indirect_dma_start(rows[:, u, k, :], None, slot_out,
                                                     bass.IndirectOffsetOnAxis(ids[:, u, k:k + 1], 0)).then_inc(gathered[u], 16)

                def body(i, coming):
                    for u in range(U):
                        pool.wait_ge(x3_ready, done(i, u))
                        pool.wait_ge(r_ready, before(i, u))
                        nc.gpsimd.tensor_tensor(x_bo[:, u, :], x_3[:, u, :], bo[:], ALU.add).then_inc(xbo_ready, 1)
                    if coming:
                        norm3.raise_power(pool, i + 1)
                    if coming == 2:
                        gather(i + 2, range(0, EARLY))
                    norm.raise_power(pool, i)
                    if coming == 2:
                        gather(i + 2, range(EARLY, TOPK * U))

                gather(0, range(TOPK * U))
                norm3.raise_power(pool, 0)
                gather(1, range(TOPK * U))
                pool.wait_ge(w_in, W_ALL)
                pipelined(pool, N, body)

            @block.tensor
            def _(pe):
                for sem in (x_turned, qkv_done, summed, flowed, esummed, kv_done, q_turned, attended, y_turned, o_done):
                    pe.sem_inc(sem, U)
                pe.wait_ge(w_in, W_ALL)
                pe.wait_ge(ones_set, 1)
                with pe.Fori(0, NB // U) as i:
                    for u in range(U):
                        pe.wait_ge(x3_ready, done(i, u))
                        pe.wait_ge(r_ready, before(i, u))
                        for c in range(KC):
                            last = nc.tensor.transpose(B[u][1][:, c * T:(c + 1) * T], x_3[:, u, c * P:(c + 1) * P], ident[:T, :T])
                        last.then_inc(x_turned, 1)
                    for u in range(U):
                        pe.wait_ge(xT_ready, done(i, u))
                        for c in range(KC):
                            nc.tensor.matmul(B[u][0][:T, :], xT[:, u, c, :], wqk[:, c, :], start=(c == 0), stop=(c == KC - 1))
                        for c in range(KC):
                            last = nc.tensor.matmul(B[u][1][:T, 0:D], xT[:, u, c, :], wv[:, c, :], start=(c == 0), stop=(c == KC - 1))
                        last.then_inc(qkv_done, 1)
                    for u in range(U):
                        pe.wait_ge(qk_ready, done(i, u))
                        nc.tensor.matmul(B[u][0][:T, :], ones[:], qk[:, u].rearrange("p a d -> p (a d)"), start=True,
                                         stop=True).then_inc(summed, 1)
                    for u in range(U):
                        for c in range(KC):
                            last = nc.tensor.transpose(B[u][1][:, c * T:(c + 1) * T], qk[:, u, 0, c * P:(c + 1) * P], ident[:T, :T])
                        last.then_inc(q_turned, 1)
                    for u in range(U):
                        pe.wait_ge(flows_ready, done(i, u))
                        nc.tensor.matmul(B[u][0][:T, :], ones[:], t1[:, u].rearrange("p a d -> p (a d)"), start=True,
                                         stop=True).then_inc(flowed, 1)
                    for u in range(U):
                        pe.wait_ge(ecs_ready, done(i, u))
                        pe.wait_ge(qT_ready, done(i, u))
                        nc.tensor.matmul(B[u][1][:T, 0:HEADS], ones[:], ecs[:, u, :], start=True, stop=True).then_inc(esummed, 1)
                    for u in range(U):
                        pe.wait_ge(v_ready, done(i, u))
                        for c in range(KC):
                            last = nc.tensor.matmul(B[u][0][:, c * P:(c + 1) * P], qk[:, u, 1, c * P:(c + 1) * P],
                                                    v[:, u, c * P:(c + 1) * P], start=True, stop=True)
                        last.then_inc(kv_done, 1)
                    for u in range(U):
                        pe.wait_ge(kv_ready, done(i, u))
                        for c in range(KC):
                            last = nc.tensor.matmul(B[u][1][:T, c * P:(c + 1) * P], qT[:, u, c, :], kv[:, u, c, :], start=True, stop=True)
                        last.then_inc(attended, 1)
                    for u in range(U):
                        pe.wait_ge(y_ready, done(i, u))
                        for c in range(KC):
                            last = nc.tensor.transpose(B[u][0][:, c * T:(c + 1) * T], y[:, u, c * P:(c + 1) * P], ident[:T, :T])
                        last.then_inc(y_turned, 1)
                    for u in range(U):
                        pe.wait_ge(yT_ready, done(i, u))
                        for c in range(KC):
                            last = nc.tensor.matmul(B[u][1][:T, 0:D], yT[:, u, c, :], wo[:, c, :], start=(c == 0), stop=(c == KC - 1))
                        last.then_inc(o_done, 1)

            @block.scalar
            def _(act):
                for sem in (xT_ready, th_ready, qk_ready, qke_ready, qT_ready, ecs_ready, yT_ready):
                    act.sem_inc(sem, U)
                with act.Fori(0, NB // U) as i:
                    for u in range(U):
                        act.wait_ge(x_turned, done(i, u))
                        nc.scalar.activation(xT[:, u].rearrange("p c t -> p (c t)"), B[u][1][:, 0:KC * T], ACT.Copy).then_inc(xT_ready, 1)
                    for u in range(U):
                        act.wait_ge(biased, done(i, u))
                        nc.scalar.activation(t1[:, u].rearrange("p a d -> p (a d)"), qke[:, u].rearrange("p a d -> p (a d)"),
                                             ACT.Tanh, scale=0.5).then_inc(th_ready, 1)
                        act.wait_ge(th_ready, done(i, u))
                        for dst, add, ready in ((qk, 0.5, qk_ready), (qke, 0.5 + EPS, qke_ready)):
                            nc.scalar.activation(dst[:, u].rearrange("p a d -> p (a d)"), t1[:, u].rearrange("p a d -> p (a d)"),
                                                 ACT.Copy, scale=0.5, bias=add).then_inc(ready, 1)
                    for u in range(U):
                        act.wait_ge(q_turned, done(i, u))
                        nc.scalar.activation(qT[:, u].rearrange("p c t -> p (c t)"), B[u][1][:, 0:KC * T], ACT.Copy).then_inc(qT_ready, 1)
                    for u in range(U):
                        act.wait_ge(kept_ready, done(i, u))
                        nc.scalar.activation(alloc[:, u, :], kept[:, u, 0:HEADS], ACT.Tanh, scale=0.5)
                        nc.scalar.activation(ecs[:, u, :], kept[:, u, HEADS:2 * HEADS], ACT.Exp).then_inc(ecs_ready, 1)
                    for u in range(U):
                        act.wait_ge(y_turned, done(i, u))
                        nc.scalar.activation(yT[:, u].rearrange("p c t -> p (c t)"), B[u][0][:, 0:KC * T], ACT.Copy).then_inc(yT_ready, 1)

            @block.vector
            def _(dve):
                for sem in (x3_ready, biased, flows_ready, kept_ready, v_ready, kv_ready, y_ready, r_ready, out_ready):
                    dve.sem_inc(sem, U)

                def heads(ap):
                    return ap.rearrange("p a (h d) -> p (a h) d", d=DH)

                def expert_rows(i, k, links):
                    for u in range(U):
                        if k == 0:
                            dve.wait_ge(gathered[u], 16 * TOPK * i + 16 * TOPK)
                            dve.wait_ge(wts_loaded[u], 16 * i + 16)
                            dve.wait_ge(xz_loaded[u], 16 * i + 16)
                        links.add(nc.vector.scalar_tensor_tensor(acc[:, u, (k + 1) % 2, :], rows[:, u, k, :], wts[:, u, k:k + 1],
                                                                 acc[:, u, k % 2, :], ALU.mult, ALU.add))
                    links.wait()

                def norm_rows(i, links):
                    dve.wait_ge(xbo_ready, before(i, U - 1))
                    dve.wait_ge(x_turned, before(i, U - 1))
                    norm3.steps(dve, links, i, acc[:, :, 0, :], x_3, x3_ready)
                    links.end()

                def body(i, coming):
                    links = Links(dve, vlink, i, 52)
                    ahead = Links(dve, vlink3, i + 1, TOPK * U + 2 * U)
                    for u in range(U):
                        dve.wait_ge(qkv_done, done(i, u))
                        nc.vector.tensor_tensor(v[:, u, :], B[u][1][:T, 0:D], bv[:], ALU.add)
                        nc.vector.tensor_tensor(qke[:, u].rearrange("p a d -> p (a d)"), B[u][0][:T, :], bqk[:], ALU.add).then_inc(biased, 1)
                        if coming and u < 3:
                            expert_rows(i + 1, u, ahead)
                    if coming:
                        expert_rows(i + 1, 3, ahead)
                        expert_rows(i + 1, 4, ahead)

                    def against_sums(sums, signal):
                        for u in range(U):
                            dve.wait_ge(signal, done(i, u))
                            dve.wait_ge(qke_ready, done(i, u))
                            for a in range(2):
                                links.add(nc.vector.scalar_tensor_tensor(t1[:, u, a, :], sums[u][:T, (1 - a) * D:(2 - a) * D], EPS,
                                                                         qke[:, u, a, :], ALU.add, ALU.mult))
                        links.wait()

                    against_sums([B[u][0] for u in range(U)], summed)
                    for u in range(U):
                        links.add(nc.vector.tensor_reduce(flow[:, u, :], heads(t1[:, u]), axis=AXIS_X, op=ALU.add))
                    links.wait()
                    for u in range(U):
                        links.add(nc.vector.reciprocal(flow[:, u, :], flow[:, u, :]))
                    links.wait()
                    for u in range(U):
                        nc.vector.tensor_tensor(heads(t1[:, u]), heads(qk[:, u]), flow[:, u, :].unsqueeze(2).to_broadcast([T, 2 * HEADS, DH]),
                                                ALU.mult).then_inc(flows_ready, 1)
                    if coming:
                        expert_rows(i + 1, 5, ahead)
                        norm_rows(i + 1, ahead)
                    against_sums([B[u][0] for u in range(U)], flowed)
                    for u in range(U):
                        links.add(nc.vector.tensor_reduce(kept[:, u, :], heads(t1[:, u]), axis=AXIS_X, op=ALU.add))
                    links.wait()
                    for u in range(U):
                        nc.vector.tensor_scalar(kept[:, u, HEADS:2 * HEADS], kept[:, u, HEADS:2 * HEADS], -1.0, 1.0,
                                                ALU.max, ALU.min).then_inc(kept_ready, 1)
                    for u in range(U):
                        dve.wait_ge(esummed, done(i, u))
                        links.add(nc.vector.reciprocal(comp[:, u, :], B[u][1][:T, 0:HEADS]))
                        links.add(nc.vector.tensor_scalar(alloc[:, u, :], alloc[:, u, :], 0.5, 0.5, ALU.mult, ALU.add))
                    links.wait()
                    for u in range(U):
                        links.add(nc.vector.tensor_tensor(comp[:, u, :], comp[:, u, :], ecs[:, u, :], ALU.mult))
                        links.add(nc.vector.tensor_tensor(alloc[:, u, :], alloc[:, u, :], flow[:, u, 0:HEADS], ALU.mult))
                    links.wait()
                    for u in range(U):
                        vh = v[:, u, :].rearrange("p (h d) -> p h d", d=DH)
                        nc.vector.scalar_tensor_tensor(vh, vh, float(T), comp[:, u, :].unsqueeze(2).to_broadcast([T, HEADS, DH]),
                                                       ALU.mult, ALU.mult).then_inc(v_ready, 1)
                    for u in range(U):
                        dve.wait_ge(kv_done, done(i, u))
                        nc.vector.tensor_tensor(kv[:, u], B[u][0][:, 0:KC * P].rearrange("p (c n) -> p c n", n=P),
                                                block_mask[:].unsqueeze(1).to_broadcast([P, KC, P]), ALU.mult).then_inc(kv_ready, 1)
                    for u in range(U):
                        dve.wait_ge(attended, done(i, u))
                        nc.vector.tensor_tensor(y[:, u, :].rearrange("p (h d) -> p h d", d=DH),
                                                B[u][1][:T, 0:D].rearrange("p (h d) -> p h d", d=DH),
                                                alloc[:, u, :].unsqueeze(2).to_broadcast([T, HEADS, DH]), ALU.mult).then_inc(y_ready, 1)
                    for u in range(U):
                        dve.wait_ge(o_done, done(i, u))
                        dve.wait_ge(xbo_ready, done(i, u))
                        nc.vector.tensor_tensor(r[:, u, :], B[u][1][:T, 0:D], x_bo[:, u, :], ALU.add).then_inc(r_ready, 1)
                    dve.wait_ge(r_ready, done(i, U - 1))
                    for u in range(U):
                        dve.wait_ge(stored[u], 16 * i + 16)
                    norm.steps(dve, links, i, r, x_o, out_ready)
                    links.end()

                first = Links(dve, vlink3, 0, TOPK * U + 2 * U)
                for k in range(TOPK):
                    expert_rows(0, k, first)
                norm_rows(0, first)
                dve.wait_ge(w_in, W_ALL)
                pipelined(dve, N, body)


def cross_attention(nc, NB, x_in, x_out, w, src_len):
    NCH = 3
    STEP = (src_len - 1) // NCH
    ROWS = STEP + 1
    assert STEP * NCH + 1 == src_len and ROWS <= P
    G = GROUPS
    with ExitStack() as ctx:
        U = 2
        done, before = counts(U)
        s = Store(nc, ctx, "xa", U)
        wq = s.sb("wq", [P, 2, KC, D])
        wk = s.sb("wk", [P, 2, KC, D])
        wv = s.sb("wv", [P, KC, D])
        wo = s.sb("wo", [P, KC, D])
        wg = s.sb("wg", [P, KC, D])
        bo = s.sb("bo", [T, D])
        bg = s.sb("bg", [T, D])
        gamma = s.sb("gamma", [P, KC])
        beta = s.sb("beta", [P, KC])
        cosT = s.sb("cosT", [P, src_len])
        sinT = s.sb("sinT", [P, src_len])
        bias = s.sb("bias", [ROWS, NCH - 1, T])
        exp_bias = s.sb("exp_bias", [ROWS, T])
        head_mask = s.sb("head_mask", [P, 8])
        head_mask2 = s.sb("head_mask2", [P, 4])
        ident = s.sb("ident", [P, P])
        neg1 = s.sb("neg1", [T, ROWS], F32R)
        x_t = s.sb("x_t", [T, U, D])
        x_res = s.sb("x_res", [T, U, D])
        x_2 = s.sb("x_2", [T, U, D])
        x_n = s.sb("x_n", [T, U, D])
        xT = s.sb("xT", [P, KC, U, T])
        c_t = s.sb("c_t", [ROWS, U, NCH, D])
        c_n = s.sb("c_n", [ROWS, U, NCH, D])
        cT = s.sb("cT", [P, U, KC, src_len])
        k_c = s.sb("k_c", [P, U, KC, src_len])
        k_s = s.sb("k_s", [P, U, KC, src_len])
        kT = s.sb("kT", [P, U, KC, src_len])
        q_c = s.sb("q_c", [P, KC, U, T])
        q_s = s.sb("q_s", [P, KC, U, T])
        q_bd = s.sb("q_bd", [P, U, KC, 8, T])
        v1 = s.sb("v1", [ROWS, U, NCH, G, P])
        mx = s.sb("mx", [ROWS, U, GW])
        nmax = s.sb("nmax", [T, U, HPG])
        dmax = s.sb("dmax", [T, U, HPG, T], F32R)
        prob = s.sb("prob", [ROWS, U, NCH, GW])
        own = s.sb("own", [P, U, GW])
        nd = s.sb("nd", [P, U, T])
        rec = s.sb("rec", [64, U, T])
        yT = s.sb("yT", [P, U, KC, T])
        att = s.sb("att", [T, U, D])
        aT = s.sb("aT", [P, U, KC, T])
        gl = s.sb("gl", [T, U, D])
        dif = s.sb("dif", [T, U, D])
        r = s.sb("r", [T, U, D])
        x_o = s.sb("x_o", [T, U, D])
        norm_q, norm_c, norm = Norm(s, nc, tag="q"), Norm(s, nc, ROWS, "c", lots=U * NCH), Norm(s, nc)
        S = [s.ps(f"S{u}", [P, 3, 512]) for u in range(U)]
        W = [s.ps(f"W{u}", [P, 512]) for u in range(U)]

        w_in, const_ready = s.sem("weights_loaded"), s.sem("const_ready")
        x_loaded, res_loaded, c_loaded, stored = (s.sems(n) for n in ("x_loaded", "res_loaded", "c_loaded", "stored"))
        xn_ready, cn_ready = s.sem("xn_ready"), s.sem("cn_ready")
        turned = s.sem("turned")
        xT_ready, cT_ready = s.sem("xT_ready"), s.sem("cT_ready")
        k_done, v_done = s.sem("k_done"), s.sem("v_done")
        q_done = s.sem("q_done")
        k_rot = s.sem("k_rot")
        q_rot = s.sem("q_rot")
        k_ready, qbd_ready = s.sem("k_ready"), s.sem("qbd_ready")
        q_sum = s.sem("q_sum")
        v_ready = s.sem("v_ready")
        scored, mx_turned, av_done = (s.sem(n) for n in ("scored", "mx_turned", "av_done"))
        shifted = s.sem("shifted")
        mx_ready, max_ready, nd_ready, yT_ready = (s.sem(n) for n in ("mx_ready", "max_ready", "nd_ready", "yT_ready"))
        less_ready = s.sem("less_ready")
        late_exp, late_ready = s.sem("late_exp"), s.sem("late_ready")
        own_ready = s.sem("own_ready")
        prob_ready = s.sem("prob_ready")
        o_done, a_turned, g_done = s.sem("o_done"), s.sem("a_turned"), s.sem("g_done")
        att_ready, gl_ready, r_ready, out_ready = (s.sem(n) for n in ("att_ready", "gl_ready", "r_ready", "out_ready"))
        aT_ready, th_ready = s.sem("aT_ready"), s.sem("th_ready")
        x2_ready = s.sem("x2_ready")
        vlink = s.sem("dve_link")
        vlink_norm = s.sem("dve_link_norm")

        kp = "(k p) n -> p k n"
        wqkv = w["L1x_wqkvT"].rearrange(kp, p=P)
        loads = [(wq[:, 0], wqkv[:, :, 0:D]), (wk[:, 0], wqkv[:, :, D:2 * D]), (wv[:], wqkv[:, :, 2 * D:3 * D]),
                 (wo[:], w["L1x_woT"].rearrange(kp, p=P)), (wg[:], w["L1x_wgT"].rearrange(kp, p=P)),
                 (bo[:], w["L1x_bo"].to_broadcast([T, D])), (bg[:], w["L1x_bg"].to_broadcast([T, D])),
                 (gamma[:], w["L1x_gamma"]), (beta[:], w["L1x_beta"]), (cosT[:], w["cos_xa"]), (sinT[:], w["sin_xa"]),
                 (bias[:], w["bias_xa"]), (exp_bias[:], w["exp_bias_xa"]), (head_mask[:], w["head_mask"]), (head_mask2[:], w["head_mask2"]), (ident[:], w["ident"])]
        W_ALL = 16 * len(loads)
        N = NB // U

        LATE = NCH - 1
        EARLY = range(NCH - 1)

        def part(i, u, j, n, parts):
            return (done(i, u, j, G) - 1) * parts + n + 1

        slots = [(j, u) for j in range(G) for u in range(U)]
        LAST = len(slots) - 1

        with nc.Block() as block:

            @block.sync
            def _(sp):

                def rows(i):
                    for u in range(U):
                        sp.wait_ge(xn_ready, before(i, u))
                        sp.dma_start(x_t[:, u, :], x_in[U * i + u]).then_inc(x_loaded[u], 16)
                        sp.wait_ge(cn_ready, before(i, u, NCH - 1, NCH))
                        for c in range(NCH):
                            sp.dma_start(c_t[:, u, c, :], w["ctx"][U * i + u, c * STEP:c * STEP + ROWS, :]).then_inc(c_loaded[u], 16)

                for u in range(U):
                    sp.sem_inc(stored[u], 16)
                rows(0)
                for dst, src in loads:
                    sp.dma_start(dst, src).then_inc(w_in, 16)
                rows(1)

                def residuals(i):
                    for u in range(U):
                        sp.wait_ge(r_ready, before(i, u))
                        sp.dma_start(x_res[:, u, :], x_in[U * i + u]).then_inc(res_loaded[u], 16)

                residuals(0)

                def body(i, coming):
                    if coming == 2:
                        rows(i + 2)
                    if coming:
                        residuals(i + 1)
                    for u in range(U):
                        sp.wait_ge(out_ready, done(i, u))
                        sp.dma_start(x_out[U * i + u], x_o[:, u, :]).then_inc(stored[u], 16)

                pipelined(sp, N, body)
                for u in range(U):
                    sp.wait_ge(stored[u], 16 * N + 16)

            @block.tensor
            def _(pe):
                for sem, steps in ((turned, 1), (k_done, KC), (v_done, 1), (scored, G), (mx_turned, G), (shifted, G * NCH),
                                   (av_done, G), (o_done, 1), (a_turned, 1), (g_done, 1)):
                    pe.sem_inc(sem, U * steps)
                pe.wait_ge(w_in, W_ALL)
                pe.wait_ge(const_ready, 1)

                def turn(i, u):
                    pe.wait_ge(xn_ready, done(i, u))
                    pe.wait_ge(cn_ready, done(i, u, NCH - 1, NCH))
                    pe.wait_ge(less_ready, before(i, u, G - 1, G) * len(EARLY))
                    pe.wait_ge(late_exp, before(i, u, G - 1, G))
                    for c in range(KC):
                        nc.tensor.transpose(S[u][:, 2, c * T:(c + 1) * T], x_n[:, u, c * P:(c + 1) * P], ident[:T, :T])
                    for c in range(KC):
                        for n in range(NCH):
                            last = nc.tensor.transpose(S[u][:, c, n * STEP:n * STEP + ROWS], c_n[:, u, n, c * P:(c + 1) * P],
                                                       ident[:ROWS, :ROWS])
                    last.then_inc(turned, 1)

                def keys(i, u, banks, signals):
                    for k in banks:
                        for c in range(KC):
                            last = nc.tensor.matmul(S[u][:, k % 3, 0:src_len], wk[:, k % 2, c, (k // 2) * P:(k // 2 + 1) * P],
                                                    cT[:, u, c, :], start=(c == 0), stop=(c == KC - 1))
                        if k in signals:
                            last.then_inc(k_done, 1)

                def queries(i):
                    for u in range(U):
                        pe.wait_ge(k_rot, done(i, u, 1, KC))
                        pe.wait_ge(xT_ready, done(i, u))
                    for turned_ in range(2):
                        for g in range(KC):
                            for c in range(KC):
                                last = nc.tensor.matmul(S[turned_][:, 2, g * U * T:(g + 1) * U * T],
                                                        wq[:, turned_, c, g * P:(g + 1) * P],
                                                        xT[:, c, :, :].rearrange("p u t -> p (u t)"),
                                                        start=(c == 0), stop=(c == KC - 1))
                    last.then_inc(q_done, 1)

                def values(i, u):
                    for n in range(NCH):
                        for c in range(KC):
                            last = nc.tensor.matmul(S[u][:ROWS, n // 2, (n % 2) * D:(n % 2) * D + D],
                                                    cT[:, u, c, n * STEP:n * STEP + ROWS], wv[:, c, :],
                                                    start=(c == 0), stop=(c == KC - 1))
                    last.then_inc(v_done, 1)

                def ahead(i):
                    for u in range(U):
                        turn(i, u)
                    for u in range(U):
                        pe.wait_ge(xT_ready, done(i, u))
                        pe.wait_ge(cT_ready, done(i, u))
                        keys(i, u, (0, 1, 2), (1,))
                    for u in range(U):
                        pe.wait_ge(k_rot, done(i, u, 0, KC))
                        keys(i, u, (3,), (3,))

                def score(i, j, u):
                    if j == 0:
                        pe.wait_ge(v_ready, done(i, u))
                        pe.wait_ge(q_rot, i + 1)
                    else:
                        pe.wait_ge(less_ready, part(i, u, j - 1, EARLY[-1], len(EARLY)))
                        pe.wait_ge(late_exp, done(i, u, j - 1, G))
                    g, h0 = j // 2, 4 * (j % 2)
                    if h0 == 0:
                        pe.wait_ge(k_ready, done(i, u, g, KC))
                        pe.wait_ge(qbd_ready, done(i, u, g, KC))
                    for n in range(NCH):
                        last = nc.tensor.matmul(S[u][:ROWS, n, 0:GW], kT[:, u, g, n * STEP:n * STEP + ROWS],
                                                q_bd[:, u, g, h0:h0 + 4, :].rearrange("p h t -> p (h t)"),
                                                start=True, stop=True)
                    last.then_inc(scored, 1)

                def attend(i, j, u, chunks):
                    for n in chunks:
                        if n in EARLY:
                            pe.wait_ge(prob_ready, part(i, u, j, n, len(EARLY)))
                        else:
                            pe.wait_ge(late_ready, done(i, u, j, G))
                        rows = ROWS if n == NCH - 1 else STEP
                        last = nc.tensor.matmul(W[u][:, 0:GW], v1[0:rows, u, n, j, :], prob[0:rows, u, n, :],
                                                start=(n == 0), stop=(n == NCH - 1))
                    if n == LATE:
                        last.then_inc(av_done, 1)

                def turn_maxima(i, j, u):
                    pe.wait_ge(mx_ready, done(i, u, j, G))
                    if j:
                        pe.wait_ge(own_ready, done(i, u, j - 1, G))
                    else:
                        pe.wait_ge(gl_ready, before(i, u))
                    for h in range(HPG):
                        last = nc.tensor.transpose(W[u][:T, h * P:h * P + ROWS], mx[:, u, h * T:(h + 1) * T],
                                                   ident[:ROWS, :ROWS])
                    last.then_inc(mx_turned, 1)

                def shift(i, j, u):
                    pe.wait_ge(max_ready, done(i, u, j, G))
                    for n in range(NCH):
                        nc.tensor.matmul(S[u][:ROWS, n, 0:GW], neg1[:], dmax[:, u, :, :].rearrange("p h t -> p (h t)"),
                                         start=False, stop=True, skip_group_check=True).then_inc(shifted, 1)

                def project(i, u):
                    pe.wait_ge(yT_ready, done(i, u, G - 1, G))
                    for c in range(KC):
                        last = nc.tensor.matmul(W[u][:T, 0:D], yT[:, u, c, :], wo[:, c, :], start=(c == 0), stop=(c == KC - 1))
                    last.then_inc(o_done, 1)

                def turn_attended(i, u):
                    pe.wait_ge(att_ready, done(i, u))
                    for c in range(KC):
                        last = nc.tensor.transpose(W[u][:, c * T:(c + 1) * T], att[:, u, c * P:(c + 1) * P], ident[:T, :T])
                    last.then_inc(a_turned, 1)

                def gate(i, u):
                    pe.wait_ge(aT_ready, done(i, u))
                    for c in range(KC):
                        last = nc.tensor.matmul(W[u][:T, 0:D], aT[:, u, c, :], wg[:, c, :], start=(c == 0), stop=(c == KC - 1))
                    last.then_inc(g_done, 1)

                def body(i, coming):
                    queries(i)
                    for u in range(U):
                        values(i, u)
                    score(i, *slots[0])
                    for k, (j, u) in enumerate(slots):
                        turn_maxima(i, j, u)
                        if k < LAST:
                            score(i, *slots[k + 1])
                        shift(i, j, u)
                        if k:
                            attend(i, *slots[k - 1], (LATE,))
                        if k == LAST and coming:
                            turn(i + 1, 0)
                        attend(i, j, u, EARLY)
                    attend(i, *slots[LAST], (LATE,))
                    if coming:
                        turn(i + 1, 1)
                    for u in range(U):
                        if coming:
                            pe.wait_ge(xT_ready, done(i + 1, u))
                            pe.wait_ge(cT_ready, done(i + 1, u))
                            keys(i + 1, u, (0, 1, 2), (1,))
                        project(i, u)
                    for u in range(U):
                        if coming:
                            pe.wait_ge(k_rot, done(i + 1, u, 0, KC))
                            keys(i + 1, u, (3,), (3,))
                        turn_attended(i, u)
                    for u in range(U):
                        gate(i, u)

                ahead(0)
                pipelined(pe, N, body)

            @block.scalar
            def _(act):
                for sem, steps in ((xT_ready, 1), (cT_ready, 1), (v_ready, 1), (prob_ready, G * len(EARLY)), (late_exp, G), (own_ready, G),
                                   (aT_ready, 1), (th_ready, 1)):
                    act.sem_inc(sem, U * steps)
                act.wait_ge(w_in, W_ALL)

                def ahead(i):
                    for u in range(U):
                        act.wait_ge(turned, done(i, u))
                        for c in range(KC):
                            last = nc.scalar.activation(xT[:, c, u, :], S[u][:, 2, c * T:(c + 1) * T], ACT.Identity,
                                                        scale=gamma[:, c:c + 1], bias=beta[:, c:c + 1])
                        last.then_inc(xT_ready, 1)
                        for c in range(KC):
                            last = nc.scalar.activation(cT[:, u, c, :], S[u][:, c, 0:src_len], ACT.Identity,
                                                        scale=gamma[:, c:c + 1], bias=beta[:, c:c + 1])
                        last.then_inc(cT_ready, 1)

                def pick_own(i, j, u):
                    act.wait_ge(av_done, done(i, u, j, G))
                    if j:
                        act.wait_ge(nd_ready, done(i, u, j - 1, G))
                    else:
                        act.wait_ge(nd_ready, before(i, u, G - 1, G))
                    for h in range(HPG):
                        last = nc.scalar.activation(own[:, u, h * T:(h + 1) * T], W[u][:, h * T:(h + 1) * T], ACT.Copy,
                                                    scale=head_mask2[:, h:h + 1])
                    last.then_inc(own_ready, 1)

                def body(i, coming):
                    for u in range(U):
                        act.wait_ge(v_done, done(i, u))
                        act.wait_ge(av_done, before(i, u, G - 1, G))
                        nc.scalar.activation(v1[:, u, 0:2, :, 0:64],
                                             S[u][:ROWS, 0, :].rearrange("p (n g f) -> p n g f", n=2, f=64), ACT.Copy)
                        nc.scalar.activation(v1[:, u, 2, :, 0:64], S[u][:ROWS, 1, 0:D].rearrange("p (g f) -> p g f", f=64),
                                             ACT.Copy).then_inc(v_ready, 1)
                    for k, (j, u) in enumerate(slots):
                        for n in EARLY:
                            act.wait_ge(less_ready, part(i, u, j, n, len(EARLY)))
                            nc.scalar.activation(prob[:, u, n, :], prob[:, u, n, :], ACT.Exp,
                                                 scale=float(DH) ** -0.5).then_inc(prob_ready, 1)
                        if k:
                            pick_own(i, *slots[k - 1])
                        act.wait_ge(shifted, part(i, u, j, LATE, NCH))
                        act.wait_ge(av_done, done(i, u, j - 1, G) if j else before(i, u, G - 1, G))
                        nc.scalar.activation(prob[:, u, LATE, :], S[u][:ROWS, LATE, 0:GW], ACT.Exp,
                                             scale=float(DH) ** -0.5).then_inc(late_exp, 1)
                    pick_own(i, *slots[LAST])
                    if coming:
                        ahead(i + 1)
                    for u in range(U):
                        act.wait_ge(a_turned, done(i, u))
                        nc.scalar.activation(aT[:, u].rearrange("p c t -> p (c t)"), W[u][:, 0:KC * T], ACT.Copy).then_inc(aT_ready, 1)
                    for u in range(U):
                        act.wait_ge(gl_ready, done(i, u))
                        nc.scalar.activation(gl[:, u, :], gl[:, u, :], ACT.Tanh, scale=0.5).then_inc(th_ready, 1)

                ahead(0)
                pipelined(act, N, body)

            @block.gpsimd
            def _(pool):
                for sem, steps in ((k_ready, KC), (qbd_ready, KC), (late_ready, G), (x2_ready, 1)):
                    pool.sem_inc(sem, U * steps)
                norm_q.set_power(pool)
                norm_c.set_power(pool)
                norm.set_power(pool)

                def norms_ahead(i):
                    norm_q.raise_power(pool, i)
                    norm_c.raise_power(pool, i)

                def keys_ahead(i):
                    for g in range(KC):
                        for u in range(U):
                            pool.wait_ge(k_rot, done(i, u, g, KC))
                            pool.wait_ge(scored, before(i, u, G - 1, G))
                            nc.gpsimd.tensor_tensor(kT[:, u, g, :], k_c[:, u, g, :], k_s[:, u, g, :], ALU.add).then_inc(k_ready, 1)

                def spread(i, g, u):
                    pool.wait_ge(scored, before(i, u, G - 1, G))
                    nc.gpsimd.tensor_tensor(q_bd[:, u, g, :, :],
                                            q_c[:, g, u, :].unsqueeze(1).to_broadcast([P, 8, T]),
                                            head_mask[:].unsqueeze(2).to_broadcast([P, 8, T]), ALU.mult).then_inc(qbd_ready, 1)

                def ahead(i):
                    norms_ahead(i)
                    pool.wait_ge(w_in, W_ALL)
                    keys_ahead(i)

                def body(i, coming):
                    pool.wait_ge(q_rot, i + 1)
                    for g in range(KC):
                        nc.gpsimd.tensor_tensor(q_c[:, g, :, :].rearrange("p u t -> p (u t)"),
                                                q_c[:, g, :, :].rearrange("p u t -> p (u t)"),
                                                q_s[:, g, :, :].rearrange("p u t -> p (u t)"), ALU.add).then_inc(q_sum, 1)
                    pool.wait_ge(q_sum, KC * i + KC)
                    for u in range(U):
                        spread(i, 0, u)
                    def late(j, u):
                        pool.wait_ge(late_exp, done(i, u, j, G))
                        chunk = prob[:, u, LATE, :].rearrange("p (h t) -> p h t", t=T)
                        nc.gpsimd.tensor_tensor(chunk, chunk, exp_bias[:].unsqueeze(1).to_broadcast([ROWS, HPG, T]),
                                                ALU.mult).then_inc(late_ready, 1)

                    for k, slot in enumerate(slots):
                        late(*slot)
                        if k < U:
                            spread(i, 1, k)
                    if coming == 2:
                        norms_ahead(i + 2)
                    if coming:
                        keys_ahead(i + 1)
                    for u in range(U):
                        pool.wait_ge(res_loaded[u], 16 * i + 16)
                        nc.gpsimd.tensor_tensor(x_2[:, u, :], x_res[:, u, :], x_res[:, u, :], ALU.add).then_inc(x2_ready, 1)
                    norm.raise_power(pool, i)

                ahead(0)
                norms_ahead(1)
                pipelined(pool, N, body)

            @block.vector
            def _(dve):
                nc.vector.memset(v1[:], 1.0)
                nc.vector.memset(neg1[:].bitcast(F32), -1.0)
                for sem, steps in ((xn_ready, 1), (cn_ready, NCH), (k_rot, KC), (mx_ready, G), (max_ready, G),
                                   (less_ready, G * len(EARLY)), (nd_ready, G), (yT_ready, G), (att_ready, 1), (gl_ready, 1),
                                   (r_ready, 1), (out_ready, 1)):
                    dve.sem_inc(sem, U * steps)

                def norms_ahead(i):
                    links = Links(dve, vlink_norm, i, 2 * (U + U * NCH))
                    for u in range(U):
                        dve.wait_ge(x_loaded[u], 16 * i + 16)
                    dve.wait_ge(turned, before(i, U - 1))
                    norm_q.steps(dve, links, i, x_t, x_n, xn_ready)
                    for u in range(U):
                        dve.wait_ge(c_loaded[u], 16 * NCH * i + 16 * NCH)
                    norm_c.steps_of(dve, links, i, [c_t[:, u, n, :] for n in range(NCH) for u in range(U)],
                                    [c_n[:, u, n, :] for n in range(NCH) for u in range(U)], cn_ready)
                    links.end()

                def rotate_keys(i, g, u):
                    dve.wait_ge(k_done, done(i, u, g, KC))
                    dve.wait_ge(k_ready, before(i, u, g, KC))
                    plain, turned_ = (2, 0) if g else (0, 1)
                    nc.vector.tensor_tensor(k_c[:, u, g, :], S[u][:, plain, 0:src_len], cosT[:], ALU.mult)
                    nc.vector.tensor_tensor(k_s[:, u, g, :], S[u][:, turned_, 0:src_len], sinT[:], ALU.mult).then_inc(k_rot, 1)

                def rotate_queries(i):
                    dve.wait_ge(q_done, i + 1)
                    for u in range(U):
                        dve.wait_ge(qbd_ready, before(i, u, KC - 1, KC))
                    for k, (dst, table) in enumerate(((q_c, cosT), (q_s, sinT))):
                        last = nc.vector.tensor_tensor(dst[:].rearrange("p g u t -> p (g u) t"),
                                                       S[k][:, 2, 0:KC * U * T].rearrange("p (a t) -> p a t", t=T),
                                                       table[:, 0:T].unsqueeze(1).to_broadcast([P, KC * U, T]), ALU.mult)
                    last.then_inc(q_rot, 1)

                def ahead(i):
                    for g in range(KC):
                        for u in range(U):
                            rotate_keys(i, g, u)

                def maxima(i, j, u):
                    dve.wait_ge(scored, done(i, u, j, G))
                    nc.vector.tensor_reduce(mx[:, u, :], S[u][:ROWS, :, 0:GW].rearrange("p n t -> p t n"),
                                            axis=AXIS_X, op=ALU.max).then_inc(mx_ready, 1)

                def spread_maxima(i, j, u, links):
                    dve.wait_ge(mx_turned, done(i, u, j, G))
                    links.add(nc.vector.tensor_reduce(nmax[:, u, :], W[u][:T, :].rearrange("p (h t) -> p h t", t=P)[:, :, 0:ROWS],
                                                      axis=AXIS_X, op=ALU.max))
                    links.wait()
                    nc.vector.tensor_tensor(dmax[:, u, :, :], ident[:T, :T].unsqueeze(1).to_broadcast([T, HPG, T]),
                                            nmax[:, u, :].unsqueeze(2).to_broadcast([T, HPG, T]),
                                            ALU.mult).then_inc(max_ready, 1)

                def add_bias(i, j, u):
                    if j:
                        dve.wait_ge(av_done, done(i, u, j - 1, G))
                    for n in EARLY:
                        dve.wait_ge(shifted, part(i, u, j, n, NCH))
                        nc.vector.tensor_tensor(prob[:, u, n, :].rearrange("p (h t) -> p h t", t=T),
                                                S[u][:ROWS, n, 0:GW].rearrange("p (h t) -> p h t", t=T),
                                                bias[:, n, :].unsqueeze(1).to_broadcast([ROWS, HPG, T]),
                                                ALU.add).then_inc(less_ready, 1)

                def gather_own(i, j, u):
                    dve.wait_ge(own_ready, done(i, u, j, G))
                    dve.wait_ge(yT_ready, done(i, u, j - 1, G) if j else before(i, u, G - 1, G))
                    nc.vector.tensor_reduce(nd[:, u, :], own[:, u, :].rearrange("p (h t) -> p t h", t=T),
                                            axis=AXIS_X, op=ALU.add).then_inc(nd_ready, 1)

                def invert(i, j, u, links):
                    dve.wait_ge(nd_ready, done(i, u, j, G))
                    links.add(nc.vector.reciprocal(rec[:, u, :], nd[64:128, u, :]))

                def normalise(i, j, u, links):
                    links.wait()
                    if j == 0:
                        dve.wait_ge(o_done, before(i, u))
                    o = 64 * (j % 2)
                    nc.vector.tensor_tensor(yT[o:o + 64, u, j // 2, :], nd[0:64, u, :], rec[:, u, :],
                                            ALU.mult).then_inc(yT_ready, 1)

                def body(i, coming):
                    links = Links(dve, vlink, i, 24)
                    rotate_queries(i)
                    maxima(i, *slots[0])
                    for k, (j, u) in enumerate(slots):
                        if k >= 2:
                            gather_own(i, *slots[k - 2])
                        spread_maxima(i, j, u, links)
                        if k >= 2:
                            invert(i, *slots[k - 2], links)
                            normalise(i, *slots[k - 2], links)
                        add_bias(i, j, u)
                        if k < LAST:
                            maxima(i, *slots[k + 1])
                    for k in (LAST - 1, LAST):
                        gather_own(i, *slots[k])
                        invert(i, *slots[k], links)
                        normalise(i, *slots[k], links)
                    if coming == 2:
                        norms_ahead(i + 2)
                    for u in range(U):
                        if coming:
                            rotate_keys(i + 1, 0, u)
                        dve.wait_ge(o_done, done(i, u))
                        nc.vector.tensor_tensor(att[:, u, :], W[u][:T, 0:D], bo[:], ALU.add).then_inc(att_ready, 1)
                    for u in range(U):
                        if coming:
                            rotate_keys(i + 1, 1, u)
                        dve.wait_ge(att_ready, done(i, u))
                        dve.wait_ge(res_loaded[u], 16 * i + 16)
                        links.add(nc.vector.tensor_tensor(dif[:, u, :], att[:, u, :], x_res[:, u, :], ALU.subtract))
                    for u in range(U):
                        dve.wait_ge(g_done, done(i, u))
                        nc.vector.tensor_tensor(gl[:, u, :], W[u][:T, 0:D], bg[:], ALU.add).then_inc(gl_ready, 1)
                    links.wait()
                    for u in range(U):
                        dve.wait_ge(th_ready, done(i, u))
                        links.add(nc.vector.scalar_tensor_tensor(dif[:, u, :], gl[:, u, :], 1.0, dif[:, u, :], ALU.add, ALU.mult))
                    links.wait()
                    for u in range(U):
                        dve.wait_ge(x2_ready, done(i, u))
                        nc.vector.scalar_tensor_tensor(r[:, u, :], dif[:, u, :], 0.5, x_2[:, u, :], ALU.mult, ALU.add).then_inc(r_ready, 1)
                    dve.wait_ge(r_ready, done(i, U - 1))
                    for u in range(U):
                        dve.wait_ge(stored[u], 16 * i + 16)
                    norm.steps(dve, links, i, r, x_o, out_ready)
                    links.end()

                norms_ahead(0)
                dve.wait_ge(w_in, W_ALL)
                H2 = DH // 2
                for wm in (wq, wk):
                    for c in range(KC):
                        a = wm[:, 0, c, :].rearrange("p (h two d) -> p h two d", two=2, d=H2)
                        t = wm[:, 1, c, :].rearrange("p (h two d) -> p h two d", two=2, d=H2)
                        nc.vector.tensor_scalar(t[:, :, 0, :], a[:, :, 1, :], -1.0, None, ALU.mult)
                        last = nc.vector.tensor_copy(t[:, :, 1, :], a[:, :, 0, :])
                last.then_inc(const_ready, 1)
                ahead(0)
                norms_ahead(1)
                pipelined(dve, N, body)


ROUND = 12582912.0


def bit_ffn(nc, NB, x_in, x_out, w):
    F = 1024
    FC = F // P
    EPS_N, EPS_Q = 1e-8, 1e-5
    with ExitStack() as ctx:
        U = 4
        done, before = counts(U)
        s = Store(nc, ctx, "bf", U)
        w1f = s.sb("w1f", [P, KC, F])
        w2f = s.sb("w2f", [P, FC, D])
        w1t = s.sb("w1t", [P, KC, F], BF16)
        w2t = s.sb("w2t", [P, FC, D], BF16)
        wsum = s.sb("wsum", [P, 2])
        wmean = s.sb("wmean", [P, 2])
        wscale = s.sb("wscale", [P, 2])
        ones = s.sb("ones", [P, P])
        n1 = s.sb("n1", [T, D])
        n2 = s.sb("n2", [T, F])
        a_s = s.sb("a_s", [T, 2])
        ident = s.sb("ident", [P, P])
        identb = s.sb("identb", [P, P], BF16)
        x_t = s.sb("x_t", [T, U, D])
        x_res = s.sb("x_res", [T, U, D])
        sq_x = s.sb("sq_x", [T, U, D])
        sq = s.sb("sq", [T, U, F])
        ss = s.sb("ss", [T, U, 2])
        ms = s.sb("ms", [T, U, 2])
        rms = s.sb("rms", [T, U, 2])
        power = s.sb("power", [T, U])
        xn = s.sb("xn", [T, U, D])
        amax = s.sb("amax", [T, U, 2])
        ascale = s.sb("ascale", [T, U, 2])
        back = s.sb("back", [T, U, 2])
        xq = s.sb("xq", [T, U, D])
        xi = s.sb("xi", [T, U, D], BF16)
        xiT = s.sb("xiT", [P, U, KC, T], BF16)
        h = s.sb("h", [T, U, F])
        hn = s.sb("hn", [T, U, F])
        hi = s.sb("hi", [T, U, F], BF16)
        hiT = s.sb("hiT", [P, U, FC, T], BF16)
        r = s.sb("r", [T, U, D])
        x_o = s.sb("x_o", [T, U, D])
        norm = Norm(s, nc)
        H = [s.ps(f"H{u}", [P, F]) for u in range(U)]
        TX = [H[u][:, 0:KC * T // 2].bitcast(BF16).rearrange("p (c t) -> p c t", t=T) for u in range(U)]
        TT = [H[u][:, 0:FC * T // 2].bitcast(BF16).rearrange("p (c t) -> p c t", t=T) for u in range(U)]
        Y = [H[u][:, 512:512 + D] for u in range(U)]

        w_in, summed_w, wsum_ready, ones_set, tern_ready, power_set = (s.sem(n) for n in (
            "weights_loaded", "weight_sums", "wsum_ready", "ones_set", "ternary_ready", "power_set"))
        x_loaded, res_loaded, stored = s.sems("x_loaded"), s.sems("res_loaded"), s.sems("stored")
        N = NB // U
        ss1_ready, h_relu, h_sq, ss2_ready = (s.sem(n) for n in ("ss1_ready", "h_relu", "h_sq", "ss2_ready"))
        ms1_ready, xi_ready, back1_ready, h_ready, ms2_ready, hi_ready, r_ready, out_ready = (s.sem(n) for n in (
            "ms1_ready", "xi_ready", "back1_ready", "h_ready", "ms2_ready", "hi_ready", "r_ready", "out_ready"))
        rms1_ready, rms2_ready = s.sem("rms1_ready"), s.sem("rms2_ready")
        x_turned, h_done, h_turned, y_done = (s.sem(n) for n in ("x_turned", "h_done", "h_turned", "y_done"))
        xiT_ready, hiT_ready = s.sem("xiT_ready"), s.sem("hiT_ready")
        vlink, alink = s.sem("dve_link"), s.sem("act_link")
        vlink_x = s.sem("dve_link_x")
        hn_ready = s.sem("hn_ready")

        kp = "(k p) n -> p k n"
        loads = [(w1f[:], w["ff_w1T"].rearrange(kp, p=P)), (w2f[:], w["ff_w2T"].rearrange(kp, p=P)),
                 (n1[:], w["ff_n1"].to_broadcast([T, D])), (n2[:], w["ff_n2"].to_broadcast([T, F])),
                 (a_s[:, 0:1], w["ff_as"].to_broadcast([T, 1])), (a_s[:, 1:2], w["ff_ab"].to_broadcast([T, 1])),
                 (ident[:], w["ident"])]
        W_ALL = 16 * len(loads)

        with nc.Block() as block:

            @block.sync
            def _(sp):
                for dst, src in loads:
                    sp.dma_start(dst, src).then_inc(w_in, 16)
                for u in range(U):
                    sp.sem_inc(stored[u], 16)

                def load(i):
                    for u in range(U):
                        sp.wait_ge(xi_ready, before(i, u))
                        sp.dma_start(x_t[:, u, :], x_in[U * i + u]).then_inc(x_loaded[u], 16)

                def load_again(i):
                    for u in range(U):
                        sp.wait_ge(r_ready, before(i, u))
                        sp.dma_start(x_res[:, u, :], x_in[U * i + u]).then_inc(res_loaded[u], 16)

                def body(i, coming):
                    if coming == 2:
                        load(i + 2)
                    if coming:
                        load_again(i + 1)
                    for u in range(U):
                        sp.wait_ge(out_ready, done(i, u))
                        sp.dma_start(x_out[U * i + u], x_o[:, u, :]).then_inc(stored[u], 16)

                load(0)
                load_again(0)
                load(1)
                pipelined(sp, N, body)
                for u in range(U):
                    sp.wait_ge(stored[u], 16 * N + 16)

            @block.gpsimd
            def _(pool):
                nc.gpsimd.memset(ones[:], 1.0).then_inc(ones_set, 1)
                nc.gpsimd.memset(power[:], -0.5).then_inc(power_set, 1)
                norm.set_power(pool)
                pool.wait_ge(power_set, 1)

                def root(i, k, there, ready):
                    pool.wait_ge(there, i + 1)
                    nc.gpsimd.tensor_tensor(rms[:, :, k], ms[:, :, k], power[:], ALU.pow).then_inc(ready, 1)

                def body(i, coming):
                    if coming:
                        root(i + 1, 0, ms1_ready, rms1_ready)
                    root(i, 1, ms2_ready, rms2_ready)
                    norm.raise_power(pool, i)

                root(0, 0, ms1_ready, rms1_ready)
                pipelined(pool, N, body)

            @block.tensor
            def _(pe):
                for sem in (x_turned, h_done, h_turned, y_done):
                    pe.sem_inc(sem, U)
                pe.wait_ge(ones_set, 1)
                pe.wait_ge(wsum_ready, 1)
                nc.tensor.matmul(Y[0][:, 0:2], ones[:], wsum[:], start=True, stop=True).then_inc(summed_w, 1)
                pe.wait_ge(tern_ready, 1)

                def turn_x(i):
                    for u in range(U):
                        pe.wait_ge(xi_ready, done(i, u))
                        pe.wait_ge(h_relu, before(i, u))
                        for c in range(KC):
                            last = nc.tensor.transpose(TX[u][:, c, :], xi[:, u, c * P:(c + 1) * P], identb[:T, :T])
                        last.then_inc(x_turned, 1)

                def hidden(i):
                    for u in range(U):
                        pe.wait_ge(xiT_ready, done(i, u))
                        for half in range(F // 512):
                            for c in range(KC):
                                last = nc.tensor.matmul(H[u][:T, half * 512:(half + 1) * 512], xiT[:, u, c, :],
                                                        w1t[:, c, half * 512:(half + 1) * 512], start=(c == 0), stop=(c == KC - 1))
                        last.then_inc(h_done, 1)

                def body(i, coming):
                    if coming:
                        turn_x(i + 1)
                        hidden(i + 1)
                    for u in range(U):
                        pe.wait_ge(hi_ready, done(i, u))
                        if coming:
                            pe.wait_ge(h_relu, done(i + 1, u))
                        for c in range(FC):
                            last = nc.tensor.transpose(TT[u][:, c, :], hi[:, u, c * P:(c + 1) * P], identb[:T, :T])
                        last.then_inc(h_turned, 1)
                    for u in range(U):
                        pe.wait_ge(hiT_ready, done(i, u))
                        for c in range(FC):
                            last = nc.tensor.matmul(Y[u][:T, :], hiT[:, u, c, :], w2t[:, c, :], start=(c == 0), stop=(c == FC - 1))
                        last.then_inc(y_done, 1)

                turn_x(0)
                hidden(0)
                pipelined(pe, N, body)

            @block.scalar
            def _(act):
                for sem in (ss1_ready, h_relu, h_sq, ss2_ready, xiT_ready, hiT_ready):
                    act.sem_inc(sem, U)

                def square_x(i):
                    for u in range(U):
                        act.wait_ge(x_loaded[u], 16 * i + 16)
                        nc.scalar.activation(sq_x[:, u, :], x_t[:, u, :], ACT.Square, accum_out=ss[:, u, 0:1]).then_inc(ss1_ready, 1)

                def copy_x(i):
                    for u in range(U):
                        act.wait_ge(x_turned, done(i, u))
                        act.wait_ge(h_done, before(i, u))
                        nc.scalar.activation(xiT[:, u], TX[u][:, :, :], ACT.Copy).then_inc(xiT_ready, 1)

                def activate(i):
                    for u in range(U):
                        act.wait_ge(h_done, done(i, u))
                        act.wait_ge(back1_ready, done(i, u))
                        act.wait_ge(hn_ready, before(i, u))
                        nc.scalar.activation(h[:, u, :], H[u][:T, :], ACT.Relu, scale=back[:, u, 0:1]).then_inc(h_relu, 1)
                    for u in range(U):
                        act.wait_ge(h_relu, done(i, u))
                        nc.scalar.activation(h[:, u, :], h[:, u, :], ACT.Square).then_inc(h_sq, 1)

                def square_hidden(i):
                    for u in range(U):
                        act.wait_ge(h_ready, done(i, u))
                        nc.scalar.activation(sq[:, u, :], h[:, u, :], ACT.Square, accum_out=ss[:, u, 1:2]).then_inc(ss2_ready, 1)

                def body(i, coming):
                    if coming:
                        copy_x(i + 1)
                        activate(i + 1)
                    if coming == 2:
                        square_x(i + 2)
                    for u in range(U):
                        act.wait_ge(h_turned, done(i, u))
                        act.wait_ge(y_done, before(i, u))
                        nc.scalar.activation(hiT[:, u], TT[u][:, :, :], ACT.Copy).then_inc(hiT_ready, 1)
                    if coming:
                        square_hidden(i + 1)

                square_x(0)
                copy_x(0)
                activate(0)
                square_x(1)
                square_hidden(0)
                pipelined(act, N, body)

            @block.vector
            def _(dve):
                for sem in (xi_ready, back1_ready, h_ready, hn_ready, hi_ready, r_ready, out_ready):
                    dve.sem_inc(sem, U)
                dve.wait_ge(w_in, W_ALL)
                count = 0

                def step(*instructions):
                    nonlocal count
                    for ins in instructions:
                        ins.then_inc(alink, 1)
                        count += 1
                    dve.wait_ge(alink, count)

                step(nc.vector.tensor_copy(identb[:], ident[:]))
                for k, wf in ((0, w1f), (1, w2f)):
                    last = nc.vector.tensor_reduce(wsum[:, k:k + 1], wf[:], axis=mybir.AxisListType.XY, op=ALU.add,
                                                   apply_absolute_value=True)
                last.then_inc(wsum_ready, 1)
                dve.wait_ge(summed_w, 1)
                step(nc.vector.tensor_scalar(wmean[:], Y[0][:, 0:2], 1.0 / (D * F), EPS_Q, ALU.mult, ALU.max))
                step(nc.vector.reciprocal(wscale[:], wmean[:]))
                for k, wf, wt in ((0, w1f, w1t), (1, w2f, w2t)):
                    step(nc.vector.tensor_scalar(wf[:], wf[:], wscale[:, k:k + 1], ROUND, ALU.mult, ALU.add))
                    step(nc.vector.tensor_scalar(wf[:], wf[:], ROUND, 1.0, ALU.subtract, ALU.min))
                    last = nc.vector.tensor_scalar(wt[:], wf[:], -1.0, None, ALU.max)
                last.then_inc(tern_ready, 1)

                def quantise(src, dst, k, scratch, ready, links):
                    for u in range(U):
                        links.add(nc.vector.tensor_reduce(amax[:, u, k:k + 1], src[:, u, :], axis=AXIS_X, op=ALU.max,
                                                          apply_absolute_value=True))
                    links.wait()
                    for u in range(U):
                        links.add(nc.vector.tensor_scalar(back[:, u, k:k + 1], amax[:, u, k:k + 1], EPS_Q, 1.0 / 127.0, ALU.max, ALU.mult))
                    links.wait()
                    for u in range(U):
                        links.add(nc.vector.reciprocal(ascale[:, u, k:k + 1], back[:, u, k:k + 1]))
                    links.wait()
                    for u in range(U):
                        links.add(nc.vector.tensor_scalar(scratch[:, u, :], src[:, u, :], ascale[:, u, k:k + 1], ROUND, ALU.mult, ALU.add))
                        if k == 0:
                            nc.vector.tensor_scalar(back[:, u, k:k + 1], back[:, u, k:k + 1], wmean[:T, k:k + 1], None,
                                                    ALU.mult).then_inc(back1_ready, 1)
                        else:
                            links.add(nc.vector.tensor_scalar(back[:, u, k:k + 1], back[:, u, k:k + 1], wmean[:T, k:k + 1], None, ALU.mult))
                    links.wait()
                    for u in range(U):
                        nc.vector.tensor_scalar(dst[:, u, :], scratch[:, u, :], ROUND, 127.0, ALU.subtract, ALU.min).then_inc(ready, 1)

                def front(i):
                    links = Links(dve, vlink_x, i, 5 * U)
                    dve.wait_ge(ss1_ready, done(i, U - 1))
                    nc.vector.tensor_scalar(ms[:, :, 0], ss[:, :, 0], 1.0 / D, EPS_N, ALU.mult, ALU.add).then_inc(ms1_ready, 1)
                    dve.wait_ge(rms1_ready, i + 1)
                    for u in range(U):
                        links.add(nc.vector.scalar_tensor_tensor(xn[:, u, :], x_t[:, u, :], rms[:, u, 0:1], n1[:], ALU.mult, ALU.mult))
                    links.wait()
                    dve.wait_ge(x_turned, before(i, U - 1))
                    dve.wait_ge(h_relu, before(i, U - 1))
                    quantise(xn, xi, 0, xq, xi_ready, links)
                    links.end()

                def scale_hidden(i):
                    for u in range(U):
                        dve.wait_ge(h_sq, done(i, u))
                        nc.vector.tensor_scalar(h[:, u, :], h[:, u, :], a_s[:, 0:1], a_s[:, 1:2], ALU.mult, ALU.add).then_inc(h_ready, 1)

                def body(i, coming):
                    links = Links(dve, vlink, i, 28)
                    if coming:
                        front(i + 1)
                    dve.wait_ge(ss2_ready, done(i, U - 1))
                    nc.vector.tensor_scalar(ms[:, :, 1], ss[:, :, 1], 1.0 / F, EPS_N, ALU.mult, ALU.add).then_inc(ms2_ready, 1)
                    dve.wait_ge(rms2_ready, i + 1)
                    for u in range(U):
                        nc.vector.scalar_tensor_tensor(hn[:, u, :], h[:, u, :], rms[:, u, 1:2], n2[:],
                                                       ALU.mult, ALU.mult).then_inc(hn_ready, 1)
                    dve.wait_ge(hn_ready, done(i, U - 1))
                    dve.wait_ge(h_turned, before(i, U - 1))
                    quantise(hn, hi, 1, hn, hi_ready, links)
                    if coming:
                        scale_hidden(i + 1)
                    for u in range(U):
                        dve.wait_ge(y_done, done(i, u))
                        dve.wait_ge(res_loaded[u], 16 * i + 16)
                        nc.vector.scalar_tensor_tensor(r[:, u, :], Y[u][:T, :], back[:, u, 1:2], x_res[:, u, :], ALU.mult, ALU.add).then_inc(r_ready, 1)
                    dve.wait_ge(r_ready, done(i, U - 1))
                    for u in range(U):
                        dve.wait_ge(stored[u], 16 * i + 16)
                    norm.steps(dve, links, i, r, x_o, out_ready)
                    links.end()

                front(0)
                scale_hidden(0)
                pipelined(dve, N, body)


def decoder(nc, x, out, w):
    NB = x.shape[0]
    src_len = w["ctx"].shape[1]

    def scratch(name, shape, dt=F32):
        return nc.dram_tensor(name, shape, dt, kind="Internal").ap()

    x1, x2, xz, x4, x5 = (scratch(n, [NB, T, D]) for n in ("x1", "x2", "x_plus_shared", "x4", "x5"))
    slot_rows = scratch("slot_rows", [SLOTS, D])
    slot_out = scratch("slot_out", [SLOTS, D])
    slot_ids = scratch("slot_ids", [NB, T, TOPK], U32)
    slot_weights = scratch("slot_weights", [NB, T, TOPK])
    self_attention(nc, NB, x, x1, w)
    cross_attention_strided(nc, NB, x1, x2, w, src_len, slot_rows)
    route(nc, NB, x2, w, slot_rows, xz, slot_ids, slot_weights)
    experts(nc, w, slot_rows, slot_out)
    linear_attention(nc, NB, xz, slot_out, slot_ids, slot_weights, x4, w)
    cross_attention(nc, NB, x4, x5, w, src_len)
    bit_ffn(nc, NB, x5, out, w)


def rope_tables(t, dim, theta):
    inv = (1.0 / theta ** (np.arange(0, dim, 2, dtype=np.float32) / np.float32(dim))).astype(np.float32)
    f = np.arange(t, dtype=np.float32)[:, None] * inv[None, :]
    e = np.concatenate((f, f), -1)
    return np.cos(e).astype(np.float32), np.sin(e).astype(np.float32)


def resize_matrix(n, m):
    inv = np.float32(n / m)
    k = max(float(inv), 1.0)
    f = (np.arange(m, dtype=np.float32) + np.float32(0.5)) * inv - np.float32(0.5)
    d = np.abs(f[None, :] - np.arange(n, dtype=np.float32)[:, None]) / np.float32(k)
    wt = np.maximum(np.float32(0), np.float32(1) - d)
    return (wt / wt.sum(0, keepdims=True)).astype(np.float32)


def position_bias(lq, lkv, length=128):
    pos = np.arange(length, dtype=np.float32)
    dist = np.abs(pos[None, :] - pos[:, None])
    bias = (np.exp(-dist * np.float32(0.1)) - dist * np.float32(0.05)).astype(np.float64)
    return (resize_matrix(length, lq).T.astype(np.float64) @ bias @ resize_matrix(length, lkv).astype(np.float64)).astype(np.float32)


def shape_constants(src_len):
    c = {}
    p = np.arange(P)
    t = np.arange(T)
    cos, sin = rope_tables(T, DH // 2, 10000.0)
    c["cos_sa"] = np.ones((P, T), np.float32)
    c["sin_sa"] = np.zeros((P, T), np.float32)
    for h in range(P // DH):
        c["cos_sa"][h * DH + DH // 2:(h + 1) * DH] = cos.T
        c["sin_sa"][h * DH + DH // 2:(h + 1) * DH] = sin.T
    cos, sin = rope_tables(src_len, DH, 10000.0)
    c["cos_xa"] = np.tile(cos.T, (P // DH, 1))
    c["sin_xa"] = np.tile(sin.T, (P // DH, 1))
    bias = position_bias(T, src_len)
    step = (src_len - 1) // 3
    c["bias_xa"] = np.stack([bias[:, step * n:step * n + step + 1].T for n in range(2)], 1) * np.float32(DH ** 0.5)
    c["exp_bias_xa"] = np.exp(bias[:, 2 * step:3 * step + 1].T.astype(np.float64)).astype(np.float32)
    c["head_mask"] = (p[:, None] // DH == np.arange(8)[None]).astype(np.float32)
    c["head_mask2"] = ((p[:, None] % 64) // DH == np.arange(4)[None]).astype(np.float32)
    c["head_mask4"] = (p[:, None] // 32 == np.arange(4)[None]).astype(np.float32)
    c["block_mask"] = (p[:, None] // DH == p[None] // DH).astype(np.float32)
    c["ident"] = np.eye(P, dtype=np.float32)
    c["causal"] = np.where(t[None, :] >= t[:, None], 0, NEG).astype(np.float32)
    c["earlier"] = (t[:, None] < t[None]).astype(np.float32)
    c["expert_no"] = np.tile(np.arange(EXPERTS, dtype=np.float32), (T, 1))
    c["first_slot"] = np.tile(np.arange(0, SLOTS, CAP, dtype=np.float32), (T, 1))
    keys = -(-src_len // 8)
    c["v_ones"] = np.zeros((P, 4, 96), np.float32)
    for h in range(8):
        row = 64 * (h % 2)
        c["v_ones"][row:row + len(range(h, src_len, 8)), h // 2, 33 * (h % 2) + 32] = 1
    assert keys <= 64
    return c


def layouts(x):
    o = {}
    for k in ("Wq_down", "Wk_down", "Wv_down"):
        o["L0_attn_" + k] = x["L0_attn_" + k].T
    for k in ("Wq_up_c", "Wq_up_e", "Wk_up_c", "Wk_up_e", "Wv_up", "Wc"):
        o["L0_attn_" + k] = x["L0_attn_" + k]
    for k in ("Wq", "Wk", "Wv", "Wo"):
        o["L0_xattn_" + k] = x["L0_xattn_" + k]
    for k in ("bq", "bk", "bv"):
        o["L0_xattn_" + k] = x["L0_xattn_" + k].reshape(KC, P).T
    o["L0_xattn_bo"] = x["L0_xattn_bo"].reshape(1, D)
    ctx = x["ctx_1024"]
    n, src_len, _ = ctx.shape
    strided = np.zeros((n, 8, 64, D), ctx.dtype)
    for h in range(8):
        strided[:, h, :len(range(h, src_len, 8))] = ctx[:, h::8]
    o["ctxT"] = strided.reshape(n, 512, KC, P).transpose(0, 3, 2, 1)
    o["ctx"] = ctx
    o["gate_wT"], o["gate_b"] = x["L0_ffn_gate_w"].T, x["L0_ffn_gate_b"].reshape(1, EXPERTS)
    o["ws1T"], o["ws2T"], o["ws3T"] = x["L0_ffn_ws1"].T, x["L0_ffn_ws2"].T, x["L0_ffn_ws3"].T
    o["w13T"] = np.concatenate([x["L0_ffn_w1"].transpose(0, 2, 1), x["L0_ffn_w3"].transpose(0, 2, 1)], axis=2)
    o["w2T"] = x["L0_ffn_w2"].transpose(0, 2, 1)
    o["L1_wqkT"] = np.concatenate([x["L1_attn_Wq"].T, x["L1_attn_Wk"].T], 1)
    o["L1_wvT"], o["L1_woT"] = x["L1_attn_Wv"].T, x["L1_attn_Wo"].T
    o["L1_bqk"] = np.concatenate([x["L1_attn_bq"], x["L1_attn_bk"]]).reshape(1, 2 * D)
    o["L1_bv"], o["L1_bo"] = x["L1_attn_bv"].reshape(1, D), x["L1_attn_bo"].reshape(1, D)
    o["L1x_wqkvT"], o["L1x_woT"], o["L1x_wgT"] = x["L1_xattn_Wqkv"].T, x["L1_xattn_Wout"].T, x["L1_xattn_Wgate"].T
    o["L1x_bo"], o["L1x_bg"] = x["L1_xattn_b_out"].reshape(1, D), x["L1_xattn_b_gate"].reshape(1, D)
    o["L1x_gamma"], o["L1x_beta"] = x["L1_xattn_gamma"].reshape(KC, P).T, x["L1_xattn_beta"].reshape(KC, P).T
    o["ff_w1T"], o["ff_w2T"] = x["L1_ffn_w1"].T, x["L1_ffn_w2"].T
    o["ff_n1"], o["ff_n2"] = x["L1_ffn_norm1_w"].reshape(1, -1), x["L1_ffn_norm2_w"].reshape(1, -1)
    o["ff_as"], o["ff_ab"] = x["L1_ffn_act_scale"].reshape(1, 1), x["L1_ffn_act_bias"].reshape(1, 1)
    return o


def kernel(**inputs):
    import concourse.bacc as _bacc
    from concourse.bass_utils import run_bass_kernel_spmd as _run

    x = {k: np.asarray(v) for k, v in inputs.items()}
    arrays = {"x_tokens": x["x"], **layouts(x), **shape_constants(x["ctx_1024"].shape[1])}
    arrays = {f"in_{k}": np.ascontiguousarray(v) for k, v in arrays.items()}
    nc = _bacc.Bacc("TRN2", target_bir_lowering=False, num_devices=1)
    w = {k[3:]: nc.dram_tensor(k, v.shape, mybir.dt.from_np(v.dtype), kind="ExternalInput").ap() for k, v in arrays.items()}
    out = nc.dram_tensor("out_0", list(x["x"].shape), F32, kind="ExternalOutput").ap()
    decoder(nc, w["x_tokens"], out, w)
    r = _run(nc, [arrays], core_ids=[0])
    return r.results[0]["out_0"]
```
